# Optimizing a Trainium2 kernel written in Bass

```python
import numpy as np
import jax
import jax.numpy as jnp

def _softmax(x, axis=-1):
    return jax.nn.softmax(x, axis=axis)

def _gelu(x):
    return jax.nn.gelu(x, approximate=True)

def _silu(x):
    return jax.nn.silu(x)

def _sigmoid(x):
    return jax.nn.sigmoid(x)

def _layernorm(x, axis=-1, eps=1e-05):
    m = jnp.mean(x, axis=axis, keepdims=True)
    v = jnp.var(x, axis=axis, keepdims=True)
    return (x - m) / jnp.sqrt(v + eps)

def _scatter_add(tgt, idx, src, axis=0):
    return tgt.at[idx].add(src)

def _segment_sum(src, seg, n):
    return jax.ops.segment_sum(src, seg, n)
kernel_name = 'mk_gps_d2_gnn_r16_7c58ec'

def setup_inputs(seed: int=0):
    np.random.seed(seed)
    _w = jnp.asarray

    def _rec_inputs():
        import jax
        import jax.numpy as jnp
        _gk = jax.random.key(seed)
        x = -0.0002117 + 1 * jax.random.normal(jax.random.fold_in(_gk, 1), (6250, 256), jnp.float32)
        src = jax.random.randint(jax.random.fold_in(_gk, 2), (100000,), 0, 6250, jnp.int32)
        dst = jax.random.randint(jax.random.fold_in(_gk, 3), (100000,), 0, 6250, jnp.int32)
        _o = jnp.argsort(dst, stable=True)
        src = src[_o]
        dst = dst[_o]
        edge_weight = jax.random.uniform(jax.random.fold_in(_gk, 14), (100000,), jnp.float32, 0.0, 1)
        return (x, src, dst, edge_weight)
    x, src, dst, edge_weight = _rec_inputs()

    def _L0_gnn_setup():
        import jax, jax.numpy as jnp
        import numpy as np
        BN_EPS = 1e-05

        def _batchnorm(h, gamma, beta):
            mean = jnp.mean(h, axis=0, keepdims=True)
            var = jnp.var(h, axis=0, keepdims=True)
            return (h - mean) * jax.lax.rsqrt(var + BN_EPS) * gamma + beta
        key = jax.random.key(seed)
        ks = jax.random.split(key, 10)
        N, E, D = (6250, 200000, 256)
        x = jax.random.normal(ks[0], (N, D), dtype=jnp.float32)
        edge_src = jax.random.randint(ks[1], (E,), 0, N, dtype=jnp.int32)
        edge_dst = jax.random.randint(ks[2], (E,), 0, N, dtype=jnp.int32)
        edge_vals = jnp.ones((E,), dtype=jnp.float32)
        n_norm = jax.random.uniform(ks[3], (N, 1), dtype=jnp.float32)
        s = 1.0 / np.sqrt(D)
        w1 = jax.random.uniform(ks[4], (D, D), jnp.float32, -s, s)
        gamma1 = jnp.ones((D,), jnp.float32)
        beta1 = jnp.zeros((D,), jnp.float32)
        w2 = jax.random.uniform(ks[5], (D, D), jnp.float32, -s, s)
        eps_weight = jnp.zeros((1,), jnp.float32)
        gamma_h = jnp.ones((D,), jnp.float32)
        beta_h = jnp.zeros((D,), jnp.float32)
        return {'x': x, 'edge_src': edge_src, 'edge_dst': edge_dst, 'edge_vals': edge_vals, 'n_norm': n_norm, 'w1': w1, 'gamma1': gamma1, 'beta1': beta1, 'w2': w2, 'eps_weight': eps_weight, 'gamma_h': gamma_h, 'beta_h': beta_h}
    _L0_gnn_all = _L0_gnn_setup()
    _L0_gnn_in = {k: v for k, v in _L0_gnn_all.items() if k in ('w1', 'gamma1', 'beta1', 'w2', 'eps_weight', 'gamma_h', 'beta_h')}
    del _L0_gnn_all

    def _L0_mix_setup():
        import jax, jax.numpy as jnp
        import numpy as np
        EMB, HEADS, DEPTH, SEQ, BATCH = (256, 8, 4, 512, 4)
        DH = EMB // HEADS
        FF = 4 * EMB
        EPS = 1e-05

        def _layernorm(x, g, b):
            mu = x.mean(-1, keepdims=True)
            var = ((x - mu) ** 2).mean(-1, keepdims=True)
            return (x - mu) * jax.lax.rsqrt(var + EPS) * g + b

        def _linear_attn(x, Wq, Wk, Wv, Wo, bo):
            b, n, dm = x.shape
            split = lambda t: t.reshape(b, n, HEADS, DH).transpose(0, 2, 1, 3)
            scale = DH ** (-0.25)
            q = jax.nn.softmax(split(x @ Wq) * scale, axis=-1)
            k = jax.nn.softmax(split(x @ Wk) * scale, axis=-2)
            v = split(x @ Wv)
            context = jnp.einsum('bhnd,bhne->bhde', k, v)
            out = jnp.einsum('bhnd,bhde->bhne', q, context)
            out = out.transpose(0, 2, 1, 3).reshape(b, n, dm)
            return out @ Wo + bo

        def _forward(x, Wq, Wk, Wv, Wo, bo, ln1_g, ln1_b, W1, b1, W2, b2, ln2_g, ln2_b):
            for i in range(DEPTH):
                h = _layernorm(x, ln1_g[i], ln1_b[i])
                x = x + _linear_attn(h, Wq[i], Wk[i], Wv[i], Wo[i], bo[i])
                h = _layernorm(x, ln2_g[i], ln2_b[i])
                x = x + (jax.nn.gelu(h @ W1[i] + b1[i], approximate=False) @ W2[i] + b2[i])
            return x
        key = jax.random.key(seed)
        ks = jax.random.split(key, 8)
        w = lambda k, shape: jax.random.normal(k, shape, dtype=jnp.float32) * 0.02
        D = DEPTH
        return {'x': jax.random.normal(ks[0], (BATCH, SEQ, EMB), dtype=jnp.float32), 'Wq': w(ks[1], (D, EMB, EMB)), 'Wk': w(ks[2], (D, EMB, EMB)), 'Wv': w(ks[3], (D, EMB, EMB)), 'Wo': w(ks[4], (D, EMB, EMB)), 'bo': jnp.zeros((D, EMB), jnp.float32), 'ln1_g': jnp.ones((D, EMB), jnp.float32), 'ln1_b': jnp.zeros((D, EMB), jnp.float32), 'W1': w(ks[5], (D, EMB, FF)), 'b1': jnp.zeros((D, FF), jnp.float32), 'W2': w(ks[6], (D, FF, EMB)), 'b2': jnp.zeros((D, EMB), jnp.float32), 'ln2_g': jnp.ones((D, EMB), jnp.float32), 'ln2_b': jnp.zeros((D, EMB), jnp.float32)}
    _L0_mix_all = _L0_mix_setup()
    _L0_mix_in = {k: v for k, v in _L0_mix_all.items() if k in ('Wq', 'Wk', 'Wv', 'Wo', 'bo', 'ln1_g', 'ln1_b', 'W1', 'b1', 'W2', 'b2', 'ln2_g', 'ln2_b')}
    del _L0_mix_all

    def _L0_ffn_setup():
        import jax, jax.numpy as jnp
        import numpy as np
        NUM_EXPERTS = 8
        TOP_K = 2
        B, S, D = (8, 512, 256)

        def _moe(tokens, router_w, w1, b1, w2, b2):
            N = tokens.shape[0]
            E = router_w.shape[0]
            logits = tokens.astype(jnp.float32) @ router_w.astype(jnp.float32).T
            probs = jax.nn.softmax(logits, axis=-1)
            rw, re = jax.lax.top_k(probs, TOP_K)
            if TOP_K > 1:
                rw = rw / jnp.maximum(rw.sum(-1, keepdims=True), 1e-12)
            rw = rw.astype(tokens.dtype)
            combine = jnp.zeros((N, E), tokens.dtype).at[jnp.arange(N)[:, None], re].set(rw)
            out = tokens
            for e in range(E):
                h = jax.nn.gelu(tokens @ w1[e] + b1[e], approximate=False)
                y = h @ w2[e] + b2[e]
                out = out + combine[:, e:e + 1] * y
            return out
        key = jax.random.key(seed)
        ks = jax.random.split(key, 4)
        scale = 1.0 / np.sqrt(D).astype(np.float32)
        return {'input_embeddings': jax.random.normal(ks[0], (B, S, D), jnp.float32), 'router_w': jax.random.normal(ks[1], (NUM_EXPERTS, D), jnp.float32) * scale, 'w1': jax.random.normal(ks[2], (NUM_EXPERTS, D, D), jnp.float32) * scale, 'b1': jnp.zeros((NUM_EXPERTS, D), jnp.float32), 'w2': jax.random.normal(ks[3], (NUM_EXPERTS, D, D), jnp.float32) * scale, 'b2': jnp.zeros((NUM_EXPERTS, D), jnp.float32)}
    _L0_ffn_all = _L0_ffn_setup()
    _L0_ffn_in = {k: v for k, v in _L0_ffn_all.items() if k in ('router_w', 'w1', 'b1', 'w2', 'b2')}
    del _L0_ffn_all

    def _L1_gnn_setup():
        import jax, jax.numpy as jnp
        import numpy as np
        N_NODES = 6250
        N_EDGES = 200000
        D_IN = 256
        D_OUT = 256
        LEAKY_SLOPE = 0.01
        key = jax.random.key(seed)
        ks = jax.random.split(key, 8)
        s_in = 1.0 / np.sqrt(D_IN)
        s_out = 1.0 / np.sqrt(D_OUT)
        return {'features': jax.random.normal(ks[0], (N_NODES, D_IN), dtype=jnp.float32), 'indices': jax.random.randint(ks[1], (2, N_EDGES), 0, N_NODES, dtype=jnp.int64), 'W_layer': jax.random.uniform(ks[2], (D_OUT, D_IN), jnp.float32, -s_in, s_in), 'b_layer': jax.random.uniform(ks[3], (D_OUT,), jnp.float32, -s_in, s_in), 'w_a1': jax.random.uniform(ks[4], (1, D_OUT), jnp.float32, -s_out, s_out), 'b_a1': jax.random.uniform(ks[5], (1,), jnp.float32, -s_out, s_out), 'w_a2': jax.random.uniform(ks[6], (1, D_OUT), jnp.float32, -s_out, s_out), 'b_a2': jax.random.uniform(ks[7], (1,), jnp.float32, -s_out, s_out)}
    _L1_gnn_all = _L1_gnn_setup()
    _L1_gnn_in = {k: v for k, v in _L1_gnn_all.items() if k in ('W_layer', 'b_layer', 'w_a1', 'b_a1', 'w_a2', 'b_a2')}
    del _L1_gnn_all

    def _L1_mix_setup():
        import jax, jax.numpy as jnp
        import numpy as np
        B, N, C = (8, 512, 256)
        HEADS, DH, KR = (8, 32, 4)
        INNER = HEADS * DH
        FF = 4 * C
        EPS = 1e-05

        def layernorm(x, g, b):
            mu = jnp.mean(x, axis=-1, keepdims=True)
            var = jnp.mean((x - mu) ** 2, axis=-1, keepdims=True)
            return (x - mu) * jax.lax.rsqrt(var + EPS) * g + b
        key = jax.random.key(seed)
        ks = jax.random.split(key, 16)
        s = 0.02
        return {'x': jax.random.normal(ks[0], (B, N, C), jnp.float32), 'ln1_g': jnp.ones((C,), jnp.float32), 'ln1_b': jnp.zeros((C,), jnp.float32), 'Wx': jax.random.normal(ks[1], (C, INNER), jnp.float32) * s, 'bx': jnp.zeros((INNER,), jnp.float32), 'Wq': jax.random.normal(ks[2], (DH, KR), jnp.float32) * s, 'Wk': jax.random.normal(ks[3], (DH, KR), jnp.float32) * s, 'Wv': jax.random.normal(ks[4], (DH, DH), jnp.float32) * s, 'Wo': jax.random.normal(ks[5], (INNER, C), jnp.float32) * s, 'bo': jnp.zeros((C,), jnp.float32), 'ln2_g': jnp.ones((C,), jnp.float32), 'ln2_b': jnp.zeros((C,), jnp.float32), 'W1': jax.random.normal(ks[6], (C, FF), jnp.float32) * s, 'b1': jnp.zeros((FF,), jnp.float32), 'W2': jax.random.normal(ks[7], (FF, C), jnp.float32) * s, 'b2': jnp.zeros((C,), jnp.float32)}
    _L1_mix_all = _L1_mix_setup()
    _L1_mix_in = {k: v for k, v in _L1_mix_all.items() if k in ('ln1_g', 'ln1_b', 'Wx', 'bx', 'Wq', 'Wk', 'Wv', 'Wo', 'bo', 'ln2_g', 'ln2_b', 'W1', 'b1', 'W2', 'b2')}
    del _L1_mix_all

    def _L1_ffn_setup():
        import jax, jax.numpy as jnp
        import numpy as np
        B, S, D = (8, 256, 256)
        H = 4 * D
        CAPACITY = 0.5
        key = jax.random.key(seed)
        ks = jax.random.split(key, 6)
        x = jax.random.normal(ks[0], (B, S, D), dtype=jnp.float32)
        attention_mask = jnp.zeros((B, 1, 1, S), dtype=jnp.float32)
        wr = jax.random.normal(ks[1], (D, 1), dtype=jnp.float32) * 0.02
        br = jnp.zeros((1,), dtype=jnp.float32)
        w1 = jax.random.normal(ks[2], (D, H), dtype=jnp.float32) * 0.02
        b1 = jnp.zeros((H,), dtype=jnp.float32)
        w2 = jax.random.normal(ks[3], (H, D), dtype=jnp.float32) * 0.02
        b2 = jnp.zeros((D,), dtype=jnp.float32)
        return {'x': x, 'attention_mask': attention_mask, 'wr': wr, 'br': br, 'w1': w1, 'b1': b1, 'w2': w2, 'b2': b2}
    _L1_ffn_all = _L1_ffn_setup()
    _L1_ffn_in = {k: v for k, v in _L1_ffn_all.items() if k in ('attention_mask', 'wr', 'br', 'w1', 'b1', 'w2', 'b2')}
    del _L1_ffn_all
    return {'x': x, 'src': src, 'dst': dst, 'edge_weight': edge_weight, 'L0_gnn_w1': _L0_gnn_in['w1'], 'L0_gnn_gamma1': _L0_gnn_in['gamma1'], 'L0_gnn_beta1': _L0_gnn_in['beta1'], 'L0_gnn_w2': _L0_gnn_in['w2'], 'L0_gnn_eps_weight': _L0_gnn_in['eps_weight'], 'L0_gnn_gamma_h': _L0_gnn_in['gamma_h'], 'L0_gnn_beta_h': _L0_gnn_in['beta_h'], 'L0_mix_Wq': _L0_mix_in['Wq'], 'L0_mix_Wk': _L0_mix_in['Wk'], 'L0_mix_Wv': _L0_mix_in['Wv'], 'L0_mix_Wo': _L0_mix_in['Wo'], 'L0_mix_bo': _L0_mix_in['bo'], 'L0_mix_ln1_g': _L0_mix_in['ln1_g'], 'L0_mix_ln1_b': _L0_mix_in['ln1_b'], 'L0_mix_W1': _L0_mix_in['W1'], 'L0_mix_b1': _L0_mix_in['b1'], 'L0_mix_W2': _L0_mix_in['W2'], 'L0_mix_b2': _L0_mix_in['b2'], 'L0_mix_ln2_g': _L0_mix_in['ln2_g'], 'L0_mix_ln2_b': _L0_mix_in['ln2_b'], 'L0_ffn_router_w': _L0_ffn_in['router_w'], 'L0_ffn_w1': _L0_ffn_in['w1'], 'L0_ffn_b1': _L0_ffn_in['b1'], 'L0_ffn_w2': _L0_ffn_in['w2'], 'L0_ffn_b2': _L0_ffn_in['b2'], 'L1_gnn_W_layer': _L1_gnn_in['W_layer'], 'L1_gnn_b_layer': _L1_gnn_in['b_layer'], 'L1_gnn_w_a1': _L1_gnn_in['w_a1'], 'L1_gnn_b_a1': _L1_gnn_in['b_a1'], 'L1_gnn_w_a2': _L1_gnn_in['w_a2'], 'L1_gnn_b_a2': _L1_gnn_in['b_a2'], 'L1_mix_ln1_g': _L1_mix_in['ln1_g'], 'L1_mix_ln1_b': _L1_mix_in['ln1_b'], 'L1_mix_Wx': _L1_mix_in['Wx'], 'L1_mix_bx': _L1_mix_in['bx'], 'L1_mix_Wq': _L1_mix_in['Wq'], 'L1_mix_Wk': _L1_mix_in['Wk'], 'L1_mix_Wv': _L1_mix_in['Wv'], 'L1_mix_Wo': _L1_mix_in['Wo'], 'L1_mix_bo': _L1_mix_in['bo'], 'L1_mix_ln2_g': _L1_mix_in['ln2_g'], 'L1_mix_ln2_b': _L1_mix_in['ln2_b'], 'L1_mix_W1': _L1_mix_in['W1'], 'L1_mix_b1': _L1_mix_in['b1'], 'L1_mix_W2': _L1_mix_in['W2'], 'L1_mix_b2': _L1_mix_in['b2'], 'L1_ffn_attention_mask': _L1_ffn_in['attention_mask'], 'L1_ffn_wr': _L1_ffn_in['wr'], 'L1_ffn_br': _L1_ffn_in['br'], 'L1_ffn_w1': _L1_ffn_in['w1'], 'L1_ffn_b1': _L1_ffn_in['b1'], 'L1_ffn_w2': _L1_ffn_in['w2'], 'L1_ffn_b2': _L1_ffn_in['b2']}

def reference(x, src, dst, edge_weight, L0_gnn_w1, L0_gnn_gamma1, L0_gnn_beta1, L0_gnn_w2, L0_gnn_eps_weight, L0_gnn_gamma_h, L0_gnn_beta_h, L0_mix_Wq, L0_mix_Wk, L0_mix_Wv, L0_mix_Wo, L0_mix_bo, L0_mix_ln1_g, L0_mix_ln1_b, L0_mix_W1, L0_mix_b1, L0_mix_W2, L0_mix_b2, L0_mix_ln2_g, L0_mix_ln2_b, L0_ffn_router_w, L0_ffn_w1, L0_ffn_b1, L0_ffn_w2, L0_ffn_b2, L1_gnn_W_layer, L1_gnn_b_layer, L1_gnn_w_a1, L1_gnn_b_a1, L1_gnn_w_a2, L1_gnn_b_a2, L1_mix_ln1_g, L1_mix_ln1_b, L1_mix_Wx, L1_mix_bx, L1_mix_Wq, L1_mix_Wk, L1_mix_Wv, L1_mix_Wo, L1_mix_bo, L1_mix_ln2_g, L1_mix_ln2_b, L1_mix_W1, L1_mix_b1, L1_mix_W2, L1_mix_b2, L1_ffn_attention_mask, L1_ffn_wr, L1_ffn_br, L1_ffn_w1, L1_ffn_b1, L1_ffn_w2, L1_ffn_b2):
    import jax
    import jax.numpy as jnp

    def _L0_gnn_ref(x, edge_src, edge_dst, edge_vals, n_norm, w1, gamma1, beta1, w2, eps_weight, gamma_h, beta_h):
        import jax, jax.numpy as jnp
        import numpy as np
        BN_EPS = 1e-05

        def _batchnorm(h, gamma, beta):
            mean = jnp.mean(h, axis=0, keepdims=True)
            var = jnp.var(h, axis=0, keepdims=True)
            return (h - mean) * jax.lax.rsqrt(var + BN_EPS) * gamma + beta
        N = x.shape[0]
        msgs = edge_vals[:, None] * x[edge_src]
        agg = jax.ops.segment_sum(msgs, edge_dst, num_segments=N)
        y = agg + eps_weight * x
        h = jax.nn.relu(_batchnorm(y @ w1.T, gamma1, beta1))
        y = h @ w2.T
        y = y * n_norm
        y = _batchnorm(y, gamma_h, beta_h)
        y = jax.nn.relu(y)
        y = y + x
        return y

    def _L0_mix_ref(x, Wq, Wk, Wv, Wo, bo, ln1_g, ln1_b, W1, b1, W2, b2, ln2_g, ln2_b):
        import jax, jax.numpy as jnp
        import numpy as np
        EMB, HEADS, DEPTH, SEQ, BATCH = (256, 8, 4, 512, 4)
        DH = EMB // HEADS
        FF = 4 * EMB
        EPS = 1e-05

        def _layernorm(x, g, b):
            mu = x.mean(-1, keepdims=True)
            var = ((x - mu) ** 2).mean(-1, keepdims=True)
            return (x - mu) * jax.lax.rsqrt(var + EPS) * g + b

        def _linear_attn(x, Wq, Wk, Wv, Wo, bo):
            b, n, dm = x.shape
            split = lambda t: t.reshape(b, n, HEADS, DH).transpose(0, 2, 1, 3)
            scale = DH ** (-0.25)
            q = jax.nn.softmax(split(x @ Wq) * scale, axis=-1)
            k = jax.nn.softmax(split(x @ Wk) * scale, axis=-2)
            v = split(x @ Wv)
            context = jnp.einsum('bhnd,bhne->bhde', k, v)
            out = jnp.einsum('bhnd,bhde->bhne', q, context)
            out = out.transpose(0, 2, 1, 3).reshape(b, n, dm)
            return out @ Wo + bo

        def _forward(x, Wq, Wk, Wv, Wo, bo, ln1_g, ln1_b, W1, b1, W2, b2, ln2_g, ln2_b):
            for i in range(DEPTH):
                h = _layernorm(x, ln1_g[i], ln1_b[i])
                x = x + _linear_attn(h, Wq[i], Wk[i], Wv[i], Wo[i], bo[i])
                h = _layernorm(x, ln2_g[i], ln2_b[i])
                x = x + (jax.nn.gelu(h @ W1[i] + b1[i], approximate=False) @ W2[i] + b2[i])
            return x
        return _forward(x, Wq, Wk, Wv, Wo, bo, ln1_g, ln1_b, W1, b1, W2, b2, ln2_g, ln2_b)

    def _L0_ffn_ref(input_embeddings, router_w, w1, b1, w2, b2):
        import jax, jax.numpy as jnp
        import numpy as np
        NUM_EXPERTS = 8
        TOP_K = 2
        B, S, D = (8, 512, 256)

        def _moe(tokens, router_w, w1, b1, w2, b2):
            N = tokens.shape[0]
            E = router_w.shape[0]
            logits = tokens.astype(jnp.float32) @ router_w.astype(jnp.float32).T
            probs = jax.nn.softmax(logits, axis=-1)
            rw, re = jax.lax.top_k(probs, TOP_K)
            if TOP_K > 1:
                rw = rw / jnp.maximum(rw.sum(-1, keepdims=True), 1e-12)
            rw = rw.astype(tokens.dtype)
            combine = jnp.zeros((N, E), tokens.dtype).at[jnp.arange(N)[:, None], re].set(rw)
            out = tokens
            for e in range(E):
                h = jax.nn.gelu(tokens @ w1[e] + b1[e], approximate=False)
                y = h @ w2[e] + b2[e]
                out = out + combine[:, e:e + 1] * y
            return out
        b, s, d = input_embeddings.shape
        tokens = input_embeddings.reshape(b * s, d)
        return _moe(tokens, router_w, w1, b1, w2, b2).reshape(b, s, d)

    def _L1_gnn_ref(features, indices, W_layer, b_layer, w_a1, b_a1, w_a2, b_a2):
        import jax, jax.numpy as jnp
        import numpy as np
        N_NODES = 6250
        N_EDGES = 200000
        D_IN = 256
        D_OUT = 256
        LEAKY_SLOPE = 0.01
        n = features.shape[0]
        h = features @ W_layer.T + b_layer
        a1 = (h @ w_a1.T + b_a1)[:, 0]
        a2 = (h @ w_a2.T + b_a2)[:, 0]
        row = indices[0]
        col = indices[1]
        v = jax.nn.leaky_relu(a1[row] + a2[col], negative_slope=LEAKY_SLOPE)
        m = jax.ops.segment_max(v, row, num_segments=n)
        ev = jnp.exp(v - m[row])
        s = jax.ops.segment_sum(ev, row, num_segments=n)
        att = ev / s[row]
        out = jax.ops.segment_sum(att[:, None] * h[col], row, num_segments=n)
        return out

    def _L1_mix_ref(x, ln1_g, ln1_b, Wx, bx, Wq, Wk, Wv, Wo, bo, ln2_g, ln2_b, W1, b1, W2, b2):
        import jax, jax.numpy as jnp
        import numpy as np
        B, N, C = (8, 512, 256)
        HEADS, DH, KR = (8, 32, 4)
        INNER = HEADS * DH
        FF = 4 * C
        EPS = 1e-05

        def layernorm(x, g, b):
            mu = jnp.mean(x, axis=-1, keepdims=True)
            var = jnp.mean((x - mu) ** 2, axis=-1, keepdims=True)
            return (x - mu) * jax.lax.rsqrt(var + EPS) * g + b
        b, n, c = x.shape
        h = layernorm(x, ln1_g, ln1_b)
        xm = h @ Wx + bx
        xm = xm.reshape(b, n, HEADS, DH).transpose(0, 2, 1, 3)
        q = jax.nn.softmax(xm @ Wq, axis=-1)
        k = jax.nn.softmax(xm @ Wk, axis=-2)
        v = xm @ Wv
        kv = jnp.einsum('bhnr,bhnd->bhrd', k, v)
        qkv = jnp.einsum('bhnr,bhrd->bhnd', q, kv)
        attn = qkv.transpose(0, 2, 1, 3).reshape(b, n, INNER) @ Wo + bo
        fx = attn + x
        h2 = layernorm(fx, ln2_g, ln2_b)
        m = jax.nn.gelu(h2 @ W1 + b1, approximate=False) @ W2 + b2
        return m + fx

    def _L1_ffn_ref(x, attention_mask, wr, br, w1, b1, w2, b2):
        import jax, jax.numpy as jnp
        import numpy as np
        B, S, D = (8, 256, 256)
        H = 4 * D
        CAPACITY = 0.5
        b, s, d = x.shape
        weights = (jnp.einsum('bsd,do->bso', x, wr) + br)[..., 0]
        k = max(1, int(CAPACITY * s))
        kk = k - 1 if k > 1 else 1
        _, idx = jax.lax.top_k(weights, k)
        sel_idx = idx[:, :kk]
        sel = jnp.take_along_axis(x, sel_idx[:, :, None], axis=1)
        h = jax.nn.gelu(jnp.einsum('bkd,dh->bkh', sel, w1) + b1)
        y = jnp.einsum('bkh,hd->bkd', h, w2) + b2
        w_sel = jnp.take_along_axis(weights, sel_idx, axis=1)
        y = y * w_sel[..., None]
        batch_idx = jnp.arange(b)[:, None]
        processed = jnp.zeros_like(x).at[batch_idx, sel_idx].set(y)
        return processed + x
    edge_index = jnp.stack([src, dst])
    deg = jnp.maximum(jax.ops.segment_sum(jnp.ones(dst.shape, jnp.float32), dst, num_segments=6250), 1.0)
    deg_isqrt = deg ** (-0.5)
    xn = _layernorm(x, axis=-1)
    x = x + _L0_gnn_ref(xn, src, dst, edge_weight, deg_isqrt[:, None], L0_gnn_w1, L0_gnn_gamma1, L0_gnn_beta1, L0_gnn_w2, L0_gnn_eps_weight, L0_gnn_gamma_h, L0_gnn_beta_h) + _L0_mix_ref(xn[None], L0_mix_Wq, L0_mix_Wk, L0_mix_Wv, L0_mix_Wo, L0_mix_bo, L0_mix_ln1_g, L0_mix_ln1_b, L0_mix_W1, L0_mix_b1, L0_mix_W2, L0_mix_b2, L0_mix_ln2_g, L0_mix_ln2_b)[0]
    x = x + _L0_ffn_ref(_layernorm(x, axis=-1)[None], L0_ffn_router_w, L0_ffn_w1, L0_ffn_b1, L0_ffn_w2, L0_ffn_b2)[0]
    xn = _layernorm(x, axis=-1)
    x = x + _L1_gnn_ref(xn, edge_index, L1_gnn_W_layer, L1_gnn_b_layer, L1_gnn_w_a1, L1_gnn_b_a1, L1_gnn_w_a2, L1_gnn_b_a2) + _L1_mix_ref(xn[None], L1_mix_ln1_g, L1_mix_ln1_b, L1_mix_Wx, L1_mix_bx, L1_mix_Wq, L1_mix_Wk, L1_mix_Wv, L1_mix_Wo, L1_mix_bo, L1_mix_ln2_g, L1_mix_ln2_b, L1_mix_W1, L1_mix_b1, L1_mix_W2, L1_mix_b2)[0]
    x = x + _L1_ffn_ref(_layernorm(x, axis=-1)[None], L1_ffn_attention_mask, L1_ffn_wr, L1_ffn_br, L1_ffn_w1, L1_ffn_b1, L1_ffn_w2, L1_ffn_b2)[0]
    return x

_drawn_inputs = setup_inputs


def setup_inputs(seed=0):
    import zlib

    import numpy as np

    out = dict(_drawn_inputs(seed))
    spreads = {'L0_gnn_gamma1': (1.0, 0.2),
     'L0_gnn_beta1': (0.0, 0.339),
     'L0_gnn_gamma_h': (1.0, 0.2),
     'L0_gnn_beta_h': (0.0, 0.294),
     'L0_mix_bo': (0.0, 0.1),
     'L0_mix_ln1_g': (1.0, 0.6),
     'L0_mix_ln1_b': (0.0, 0.717),
     'L0_mix_b1': (0.0, 0.279),
     'L0_mix_b2': (0.0, 0.1),
     'L0_mix_ln2_g': (1.0, 0.6),
     'L0_mix_ln2_b': (0.0, 0.756),
     'L0_ffn_b1': (0.0, 0.652),
     'L0_ffn_b2': (0.0, 0.438),
     'L1_mix_ln1_g': (1.0, 0.6),
     'L1_mix_ln1_b': (0.0, 0.8),
     'L1_mix_bx': (0.0, 0.8),
     'L1_mix_bo': (0.0, 0.397),
     'L1_mix_ln2_g': (1.0, 0.6),
     'L1_mix_ln2_b': (0.0, 0.8),
     'L1_mix_b1': (0.0, 0.8),
     'L1_mix_b2': (0.0, 0.411),
     'L1_ffn_b1': (0.0, 0.8),
     'L1_ffn_b2': (0.0, 0.8)}
    factors = {'L0_mix_Wq': 8.0,
     'L0_mix_Wk': 8.0,
     'L0_mix_Wv': 3.66,
     'L0_mix_Wo': 3.349,
     'L1_gnn_b_layer': 8.0,
     'L1_gnn_w_a1': 8.0,
     'L1_gnn_w_a2': 8.0,
     'L1_mix_Wx': 8.0,
     'L1_mix_Wq': 8.0,
     'L1_mix_Wk': 8.0,
     'L1_mix_Wv': 8.0,
     'L1_mix_Wo': 8.0,
     'L1_ffn_wr': 8.0,
     'L1_ffn_w1': 8.0,
     'L1_ffn_w2': 8.0}
    for name, (base, spread) in spreads.items():
        noise = np.random.default_rng([zlib.crc32(name.encode()), seed]).standard_normal(out[name].shape)
        drawn = base * np.exp(spread * noise) if base else spread * noise
        out[name] = jnp.asarray(drawn.astype(out[name].dtype))
    for name, factor in factors.items():
        out[name] = (out[name] * factor).astype(out[name].dtype)
    return out
```

```python
from contextlib import ExitStack, contextmanager
import numpy as np
import concourse.bass as bass
from concourse import mybir

F32 = mybir.dt.float32
I32 = mybir.dt.int32
BF16 = mybir.dt.bfloat16
ALU = mybir.AluOpType
ACT = mybir.ActivationFunctionType
AX_X = mybir.AxisListType.X
ds = bass.ds
P = 128

N = 6250
D = 256
H2 = D // P
E = 100000
TT = 125
CW = 2 * TT
NCH = N // CW
NT = N // TT
ET = 782
EP = ET * P
EB = 17
NEB = ET // EB
HI = 49
NODES = HI * P


START, NOW, PREV, OLD = 2, 3, 2, 1

CR = 2


class Phase:

    def __init__(self, nc, name):
        self.nc, self.name, self.ctx, self.sems = nc, name, ExitStack(), []
        self.loops = []

    def __enter__(self):
        self.ctx.__enter__()
        return self

    def sb(self, name, shape, dt=F32):
        return self.ctx.enter_context(self.nc.sbuf_tensor(f"{self.name}_{name}", shape, dt))

    def ps(self, name, shape, dt=F32):
        return self.ctx.enter_context(self.nc.psum_tensor(f"{self.name}_{name}", shape, dt))

    def sem(self, name):
        s = self.nc.alloc_semaphore(f"{self.name}_{name}")
        self.sems.append(s)
        return s

    def loop_sem(self, name):
        s = self.sem(name)
        self.loops.append(s)
        return s

    def block(self):
        for s in self.loops:
            self.nc.sync.sem_inc(s, START)
        self.nc.all_engine_barrier()
        return self.ctx.enter_context(self.nc.Block())

    def __exit__(self, *exc):
        self.ctx.__exit__(*exc)
        if exc[0] is None and self.sems:
            self.nc.clear_and_free_semaphores(self.sems)
            self.nc.all_engine_barrier()


def sort_edges(nc, name, keys, others, weights, iota, ident, identb, tri, upper, hist_d, base_d, sorted_d):
    with Phase(nc, name) as ph:
        kin, oin = ph.sb("kin", [P, ET], I32), ph.sb("oin", [P, ET], I32)
        hi_i, lo_i = ph.sb("hi_i", [P, ET], I32), ph.sb("lo_i", [P, ET], I32)
        meta = ph.sb("meta", [P, ET, 3])
        lo, hi = ph.sb("lo", [P, ET]), ph.sb("hi", [P, ET])
        iota_t, id_t, idb_t = ph.sb("iota", [P, P]), ph.sb("ident", [P, P]), ph.sb("identb", [P, P], BF16)
        tri_t, upper_t = ph.sb("tri", [P, P]), ph.sb("upper", [P, P])
        onelo, onehi = ph.sb("onelo", [P, 2, EB, P], BF16), ph.sb("onehi", [P, 2, EB, HI], BF16)
        hist, scan, base, part = (ph.sb(n, [HI, P]) for n in ("hist", "scan", "base", "part"))
        zero = ph.sb("zero", [P, P], BF16)
        rowsum = ph.sb("rowsum", [HI, 1])
        mb = [ph.sb(f"mb{b}", [P, EB, 3]) for b in range(2)]
        hiT = [ph.sb(f"hiT{b}", [HI, P]) for b in range(2)]
        hsnap = [ph.sb(f"hsnap{b}", [HI, P]) for b in range(2)]
        rank_in, rank_at = ph.sb("rank_in", [P, 2, EB]), ph.sb("rank_at", [P, 2, EB])
        place = [ph.sb(f"place{b}", [P, EB], I32) for b in range(2)]
        hist_ps, base_ps = ph.ps("hist_ps", [P, 512]), ph.ps("base_ps", [P, 512])
        krow_ps = [ph.ps(f"krow{b}", [P, 512]) for b in range(2)]
        hiT_ps = [ph.ps(f"hiT_ps{b}", [P, 1024], BF16) for b in range(2)]
        look_ps = [ph.ps(f"look{b}", [P, 512]) for b in range(2)]
        hist_acc = hist_ps[0:HI, 0:P]
        sem = ph.sem
        loaded, prep, onehot, counted, zeroed = sem("loaded"), sem("prep"), sem("onehot"), sem("counted"), sem("zeroed")
        hist_ready, based, rows_before, base_ready, saved = sem("hist_ready"), sem("based"), sem("rows_before"), sem("base_ready"), sem("saved")
        onehot2, krow, hi_turned, hi_copied, snapped, looked, added = (sem(n) for n in ("onehot2", "krow", "hi_turned", "hi_copied", "snapped", "looked", "added"))
        ranked_in, ranked_at, meta_b, placed = sem("ranked_in"), sem("ranked_at"), sem("meta_b"), sem("placed")
        left, gate = sem("left"), sem("gate")
        scattered = [sem(f"scattered{b}") for b in range(2)]
        block = ph.block()

        @block.sync
        def _(sp):
            for dst, src in ((kin, keys), (oin, others), (iota_t, iota), (id_t, ident), (idb_t, identb), (tri_t, tri), (upper_t, upper)):
                sp.dma_start(dst[:, :], src).then_inc(loaded, 16)
            sp.dma_start(meta[:, :, 2], weights, allow_slow_non_contiguous=True).then_inc(loaded, 16)
            sp.wait_ge(base_ready, 4)
            sp.dma_start(hist_d.rearrange("(h l) -> h l", l=P), hist[:, :]).then_inc(saved, 16)
            sp.dma_start(base_d.rearrange("(h l) -> h l", l=P), base[:, :]).then_inc(saved, 16)
            sp.wait_ge(saved, 32)

        @block.vector
        def _(dve):
            nc.vector.memset(zero[:, :], 0.0).then_inc(zeroed, 1)
            dve.wait_ge(loaded, 8 * 16)
            nc.vector.tensor_scalar(hi_i[:, :], kin[:, :], 7, None, ALU.logical_shift_right).then_inc(prep, 1)
            nc.vector.tensor_scalar(lo_i[:, :], kin[:, :], P - 1, None, ALU.bitwise_and).then_inc(prep, 1)
            nc.vector.tensor_copy(meta[:, :, 0], kin[:, :]).then_inc(prep, 1)
            nc.vector.tensor_scalar(meta[:, :, 1], oin[:, :], float(N - 1), None, ALU.min).then_inc(prep, 1)
            dve.wait_ge(prep, 4)
            nc.vector.tensor_copy(hi[:, :], hi_i[:, :]).then_inc(prep, 1)
            nc.vector.tensor_copy(lo[:, :], lo_i[:, :]).then_inc(prep, 1)
            dve.wait_ge(prep, 6)

            def one_hots(t0, b, done):
                nc.vector.tensor_tensor(
                    onelo[:, b, :, :], lo[:, ds(t0, EB)].unsqueeze(2).to_broadcast([P, EB, P]),
                    iota_t[:, None, :].to_broadcast([P, EB, P]), ALU.is_equal).then_inc(done, 1)
                nc.vector.tensor_tensor(
                    onehi[:, b, :, :], hi[:, ds(t0, EB)].unsqueeze(2).to_broadcast([P, EB, HI]),
                    iota_t[:, None, 0:HI].to_broadcast([P, EB, HI]), ALU.is_equal).then_inc(done, 1)

            with dve.Fori(0, NEB // 2) as i:
                for b in range(2):
                    dve.wait_ge(counted, i * 2 + (b + 1))
                    one_hots(i * (2 * EB) + b * EB, b, onehot)
            dve.wait_ge(counted, CR + NEB)
            nc.vector.tensor_copy(hist[:, :], hist_acc).then_inc(base_ready, 1)
            dve.wait_ge(base_ready, 1)
            nc.vector.tensor_tensor_scan(scan[:, :], hist[:, :], hist[:, :], 0.0, ALU.add, ALU.bypass).then_inc(base_ready, 1)
            dve.wait_ge(base_ready, 2)
            nc.vector.tensor_tensor(part[:, :], scan[:, :], hist[:, :], ALU.subtract).then_inc(base_ready, 1)
            dve.wait_ge(base_ready, 3)
            dve.wait_ge(rows_before, 1)
            nc.vector.tensor_scalar(base[:, :], part[:, :], base_ps[0:HI, 0:1], None, ALU.add).then_inc(base_ready, 1)
            dve.sem_inc(ranked_in, CR)
            dve.sem_inc(ranked_at, CR)
            with dve.Fori(0, NEB // 2) as i:
                for b in range(2):
                    t0 = i * (2 * EB) + b * EB
                    dve.wait_ge(added, t0 + CR)
                    dve.wait_ge(left, i * 2 + (b + 1))
                    one_hots(t0, b, onehot2)
                    nc.vector.tensor_copy(mb[b][:, :, :], meta[:, ds(t0, EB), :]).then_inc(meta_b, 1)
                    dve.wait_ge(meta_b, i * 2 + (b + 1))
                    for j in range(EB):
                        q = (b * EB + j) % 2
                        dve.wait_ge(krow, t0 + (j + 1))
                        nc.vector.scalar_tensor_tensor(
                            krow_ps[q][:, 0:P], krow_ps[q][:, 0:P], mb[b][:, j, 0:1], tri_t[:, :], ALU.is_equal, ALU.mult,
                            accum_out=rank_in[:, b, j:j + 1]).then_inc(ranked_in, 1)
                        dve.wait_ge(looked, t0 + (j + 1 + CR))
                        nc.vector.tensor_tensor_reduce(
                            look_ps[q][:, 0:P], look_ps[q][:, 0:P], onelo[:, b, j, :], 1.0, 0.0, ALU.mult, ALU.add,
                            rank_at[:, b, j:j + 1]).then_inc(ranked_at, 1)
                    dve.wait_ge(ranked_in, t0 + (EB + CR))
                    dve.wait_ge(ranked_at, t0 + (EB + CR))
                    nc.vector.tensor_tensor(place[b][:, :], rank_in[:, b, :], rank_at[:, b, :], ALU.add).then_inc(placed, 1)

        @block.tensor
        def _(pe):
            pe.wait_ge(zeroed, 1)
            nc.tensor.matmul(hist_acc, zero[:, 0:HI], zero[:, :], start=True, stop=False, skip_group_check=True)
            pe.sem_inc(counted, CR)
            with pe.Fori(0, NEB // 2) as i:
                for b in range(2):
                    pe.wait_ge(onehot, i * 4 + (b * 2 + 2))
                    for j in range(EB):
                        mm = nc.tensor.matmul(hist_acc, onehi[:, b, j, :], onelo[:, b, j, :], start=False, stop=False,
                                              skip_group_check=True)
                    mm.then_inc(counted, 1)
            pe.wait_ge(base_ready, 2)
            nc.tensor.matmul(base_ps[0:HI, 0:1], upper_t[0:HI, 0:HI], scan[:, P - 1:P], start=True, stop=True).then_inc(rows_before, 1)
            pe.wait_ge(base_ready, 4)
            nc.tensor.matmul(hist_acc, id_t[0:HI, 0:HI], base[:, :], start=True, stop=False, skip_group_check=True).then_inc(added, CR)
            pe.sem_inc(looked, CR)
            with pe.Fori(0, NEB // 2) as i:
                for b in range(2):
                    t0 = i * (2 * EB) + b * EB
                    pe.wait_ge(onehot2, i * 4 + (b * 2 + 2))
                    pe.wait_ge(meta_b, i * 2 + (b + 1))
                    for j in range(EB):
                        q = (b * EB + j) % 2
                        pe.wait_ge(ranked_in, t0 + (j + 1))
                        pe.wait_ge(hi_copied, t0 + (j + 1))
                        nc.tensor.transpose(krow_ps[q][:, 0:P], mb[b][:, j, 0:1].to_broadcast([P, P]), id_t[:, :]).then_inc(krow, 1)
                        nc.tensor.transpose(hiT_ps[q][0:HI, 0:P], onehi[:, b, j, :], idb_t[:, :]).then_inc(hi_turned, 1)
                        pe.wait_ge(hi_copied, t0 + (j + 1 + CR))
                        pe.wait_ge(snapped, t0 + (j + 1))
                        pe.wait_ge(ranked_at, t0 + (j + 1))
                        nc.tensor.matmul(look_ps[q][:, 0:P], hiT[q][:, :], hsnap[q][:, :], start=True, stop=True).then_inc(looked, 1)
                        nc.tensor.matmul(hist_acc, onehi[:, b, j, :], onelo[:, b, j, :], start=False, stop=False,
                                         skip_group_check=True).then_inc(added, 1)

        @block.scalar
        def _(act):
            act.sem_inc(hi_copied, CR)
            with act.Fori(0, NEB // 2) as i:
                for b in range(2):
                    t0 = i * (2 * EB) + b * EB
                    for j in range(EB):
                        q = (b * EB + j) % 2
                        act.wait_ge(looked, t0 + (j + 1))
                        act.wait_ge(hi_turned, t0 + (j + 1))
                        nc.scalar.activation(hiT[q][:, :], hiT_ps[q][0:HI, 0:P], ACT.Copy).then_inc(hi_copied, 1)
                        act.wait_ge(added, t0 + (j + CR))
                        nc.scalar.activation(hsnap[q][:, :], hist_acc, ACT.Copy).then_inc(snapped, 1)

        @block.gpsimd
        def _(pool):
            pool.sem_inc(left, CR)
            with pool.Fori(0, NEB // 2) as i:
                for b in range(2):
                    pool.wait_ge(placed, i * 2 + (b + 1))
                    pool.sem_inc(gate, 1)
                    for j in range(EB):
                        nc.gpsimd.indirect_dma_start(
                            sorted_d, bass.IndirectOffsetOnAxis(place[b][:, j:j + 1], 0), mb[b][:, j, :], None).then_inc(scattered[b], 16)
                for b in range(2):
                    pool.wait_ge(scattered[b], i * (16 * EB) + 16 * EB)
                    pool.sem_inc(left, 1)


def chunks(eng, body, ahead=True):
    with eng.Fori(0, NCH // 2) as i:
        for b in range(2):
            body(i * 2 + b, b, i, True)
    body(NCH - 1, 0, NCH // 2, False)


class Norm:

    def __init__(self, nc, ph, x, ones, used, gain=None, offset=None, eps=1e-5):
        self.nc, self.x, self.ones, self.eps, self.gain, self.offset, self.used = nc, x, ones, eps, gain, offset, used
        self.stat = [ph.ps(f"stat{b}", [P, 512]) for b in range(2)]
        self.cen = [ph.sb(f"cen{b}", [P, 2, CW]) for b in range(2)]
        self.sq = [ph.sb(f"sq{b}", [P, 2, CW]) for b in range(2)]
        self.dev = [ph.sb(f"dev{b}", [P, CW]) for b in range(2)]
        self.rstd = [ph.sb(f"rstd{b}", [P, CW]) for b in range(2)]
        self.eps_t = ph.sb("eps", [P, 1])
        self.nrm = [ph.sb(f"nrm{b}", [P, 2, CW]) for b in range(2)]
        self.out = self.nrm if gain is None else [ph.sb(f"out{b}", [P, 2, CW]) for b in range(2)]
        self.mean_ready, self.centred, self.squared, self.var_ready, self.rooted, self.inverted, self.normed, self.affine = (
            ph.loop_sem(n) for n in ("mean_ready", "centred", "squared", "var_ready", "rooted", "inverted", "normed", "affine"))
        self.eps_ready = ph.sem("eps_ready")
        self.ready = self.normed if gain is None else self.affine

    def pe_mean(self, pe, n, b):
        pe.wait_ge(self.centred, n + OLD)
        for h in range(2):
            mm = self.nc.tensor.matmul(self.stat[b][:, 0:CW], self.ones[:, :], self.x[b][:, h, :], start=(h == 0), stop=(h == 1))
        mm.then_inc(self.mean_ready, 1)

    def dve_centre(self, dve, n, b):
        dve.wait_ge(self.mean_ready, n + NOW)
        dve.wait_ge(self.squared, n + OLD)
        dve.wait_ge(self.normed, n + OLD)
        self.nc.vector.tensor_tensor(self.cen[b][:, :, :], self.x[b][:, :, :],
                                     self.stat[b][:, None, 0:CW].to_broadcast([P, 2, CW]), ALU.subtract).then_inc(self.centred, 1)

    def act_square(self, act, n, b):
        act.wait_ge(self.centred, n + NOW)
        act.wait_ge(self.var_ready, n + OLD)
        self.nc.scalar.activation(self.sq[b][:, :, :], self.cen[b][:, :, :], ACT.Square).then_inc(self.squared, 1)

    def pe_var(self, pe, n, b):
        pe.wait_ge(self.squared, n + NOW)
        pe.wait_ge(self.rooted, n + OLD)
        for h in range(2):
            mm = self.nc.tensor.matmul(self.stat[b][:, CW:2 * CW], self.ones[:, :], self.sq[b][:, h, :], start=(h == 0), stop=(h == 1))
        mm.then_inc(self.var_ready, 1)

    def dve_start(self, dve):
        self.nc.vector.memset(self.eps_t[:, :], self.eps).then_inc(self.eps_ready, 1)

    def act_root(self, act, n, b):
        if isinstance(n, int) and n == 0:
            act.wait_ge(self.eps_ready, 1)
        act.wait_ge(self.var_ready, n + NOW)
        act.wait_ge(self.inverted, n + OLD)
        self.nc.scalar.activation(self.dev[b][:, :], self.stat[b][:, CW:2 * CW], ACT.Sqrt, bias=self.eps_t[:, 0:1]).then_inc(self.rooted, 1)

    def dve_norm(self, dve, n, b):
        dve.wait_ge(self.rooted, n + NOW)
        dve.wait_ge(self.normed, n + OLD)
        self.nc.vector.reciprocal(self.rstd[b][:, :], self.dev[b][:, :]).then_inc(self.inverted, 1)
        dve.wait_ge(self.inverted, n + NOW)
        for s in [self.affine] if self.gain is not None else self.used:
            dve.wait_ge(s, n + OLD)
        self.nc.vector.tensor_tensor(self.nrm[b][:, :, :], self.cen[b][:, :, :],
                                     self.rstd[b][:, None, :].to_broadcast([P, 2, CW]), ALU.mult).then_inc(self.normed, 1)

    def act_affine(self, act, n, b):
        act.wait_ge(self.normed, n + NOW)
        for s in self.used:
            act.wait_ge(s, n + OLD)
        for h in range(2):
            last = self.nc.scalar.activation(self.out[b][:, h, :], self.nrm[b][:, h, :], ACT.Identity,
                                             bias=self.offset[:, h:h + 1], scale=self.gain[:, h:h + 1])
        last.then_inc(self.affine, 1)


def attend_first(nc, name, KH, KP, R, scale, x_d, qT_d, mixer, c_d, gain_d, offset_d, wq_d, wk_d, wv_d, wo_d, wx_d=None, bx_d=None):
    EW = D // KH
    QW = KH * KP
    NQ = QW // R
    proj = wx_d is not None
    with Phase(nc, name) as ph:
        x = [ph.sb(f"x{b}", [P, 2, CW]) for b in range(2)]
        ones, ident = ph.sb("ones", [P, P]), ph.sb("ident", [P, P])
        blocks = ph.sb("blocks", [KP, KH, EW])
        gain, offset = ph.sb("gain", [P, 2]), ph.sb("offset", [P, 2])
        wq, wk, wv, wo = ph.sb("wq", [P, 2, QW]), ph.sb("wk", [P, 2, QW]), ph.sb("wv", [P, 2, D]), ph.sb("wo", [P, 2, D])
        if proj:
            wx, bx = ph.sb("wx", [P, 2, D]), ph.sb("bx", [P, 2])
            xm = [ph.sb(f"xm{b}", [P, 2, CW]) for b in range(2)]
        ek = [ph.sb(f"ek{b}", [KP, KH, CW]) for b in range(2)]
        ekT = [ph.sb(f"ekT{b}", [TT, 2, QW]) for b in range(2)]
        v = [ph.sb(f"v{b}", [TT, 2, D]) for b in range(2)]
        kmax, run, nbias, fade, ksum = ([ph.sb(f"{n}{b}", [KP, KH]) for b in range(2)] for n in ("kmax", "run", "nbias", "fade", "ksum"))
        total, rtotal = ph.sb("total", [KP, KH]), ph.sb("rtotal", [KP, KH])
        ctxt, ctxn = ph.sb("context", [KP, KH, EW]), ph.sb("contextn", [KP, KH, EW])
        ctxT = ph.sb("contextT", [P, 2, KP])
        qmax, qsum, qrec = ([ph.sb(f"{n}{b}", [TT, 2 * NQ]) for b in range(2)] for n in ("qmax", "qsum", "qrec"))
        qs, qe, qn = ([ph.sb(f"{n}{b}", [TT, 2 * NQ, R]) for b in range(2)] for n in ("qs", "qe", "qn"))
        qT = [ph.sb(f"qT{b}", [KP, KH, CW]) for b in range(2)]
        k_ps, q_ps, v_ps, ekT_ps, qT_ps, ctx_ps = (ph.ps(n, [P, 512]) for n in ("k_ps", "q_ps", "v_ps", "ekT_ps", "qT_ps", "ctx_ps"))
        kps = k_ps[0:KP, 0:KH * CW].rearrange("p (h c) -> p h c", h=KH)
        if proj:
            ekps = k_ps[0:TT, 256:256 + 2 * QW].rearrange("p (t c) -> p t c", t=2)
            xm_ps = ekT_ps[:, 0:2 * CW].rearrange("p (h c) -> p h c", h=2)
        else:
            ekps = ekT_ps[0:TT, 0:2 * QW].rearrange("p (t c) -> p t c", t=2)
        qps = q_ps[0:TT, 0:2 * QW].rearrange("p (g r) -> p g r", r=R)
        vps = v_ps[0:TT, 0:2 * D].rearrange("p (t c) -> p t c", t=2)
        qTps = qT_ps[0:KP, 0:KH * CW].rearrange("p (h c) -> p h c", h=KH)
        cps = ctx_ps[0:KP, 0:KH * EW].rearrange("p (h e) -> p h e", h=KH)
        weights = ph.sem("weights")
        x_loaded = [ph.sem(f"x_loaded{b}") for b in range(2)]
        q_saved = [ph.sem(f"q_saved{b}") for b in range(2)]
        (xm_made, xm_copied, k_made, v_made, q_made, ekT_made, ctx_made, qT_made, k_maxed, k_run, k_bias, q_maxed, q_less, q_exp,
         q_summed, q_rec, q_normed, k_exp, faded, v_copied, ekT_copied, qT_copied, ctx_added, total_added) = (ph.loop_sem(n) for n in (
             "xm_made", "xm_copied", "k_made", "v_made", "q_made", "ekT_made", "ctx_made", "qT_made", "k_maxed", "k_run", "k_bias",
             "q_maxed", "q_less", "q_exp", "q_summed", "q_rec", "q_normed", "k_exp", "faded", "v_copied", "ekT_copied", "qT_copied",
             "ctx_added", "total_added"))
        started, ended, turned, turned_copied, mixed, kept = (ph.sem(n) for n in ("started", "ended", "turned", "turned_copied", "mixed", "kept"))
        ln = Norm(nc, ph, x, ones, [xm_made] if proj else [q_made], gain, offset)
        loads = [(ones, c_d["mean"]), (ident, c_d["ident"]), (blocks, c_d[f"blocks{KH}"]), (gain, gain_d), (offset, offset_d),
                 (wo, wo_d)] + ([(wx, wx_d), (bx, bx_d)] if proj else [(wq, wq_d), (wk, wk_d), (wv, wv_d)])
        by_head, keys_gate = ph.sem("by_head"), ph.sem("keys_gate")
        if proj:
            for w, w_d in ((wq, wq_d), (wk, wk_d), (wv, wv_d)):
                rows, cols = w_d.shape
                for n in range(D // rows):
                    p0 = n * rows % P
                    loads.append((w[p0:p0 + rows, n * rows // P, n * cols:(n + 1) * cols], w_d))
        block = ph.block()

        @block.sync
        def _(sp):
            for b in range(2):
                sp.sem_inc(q_saved[b], 16)
            if proj:
                sp.wait_ge(by_head, 3)
            for dst, src in loads:
                sp.dma_start(dst[:], src).then_inc(weights, 16)
            sp.dma_start(x[0][:, :, :], x_d[:, :, 0:CW]).then_inc(x_loaded[0], 16)

            def body(c, b, r, more):
                if more:
                    sp.wait_ge(ln.centred, c + PREV)
                    sp.dma_start(x[1 - b][:, :, :], x_d[:, :, ds((c + 1) * CW, CW)]).then_inc(x_loaded[1 - b], 16)
                sp.wait_ge(qT_copied, c + NOW)
                sp.dma_start(qT_d[:, :, ds(c * CW, CW)], qT[b][:, :, :]).then_inc(q_saved[b], 16)
            chunks(sp, body)
            for b in range(2):
                sp.wait_ge(q_saved[b], 16 * ((NCH + 1 - b) // 2) + 16)

        @block.tensor
        def _(pe):
            pe.wait_ge(weights, 16 * len(loads))
            pe.wait_ge(x_loaded[0], 16)
            ln.pe_mean(pe, 0, 0)
            ln.pe_var(pe, 0, 0)

            def body(c, b, r, more):
                src = xm[b] if proj else ln.out[b]
                if more:
                    pe.wait_ge(x_loaded[1 - b], r * 16 + (b * 16 + 16))
                    ln.pe_mean(pe, c + 1, 1 - b)
                pe.wait_ge(ln.affine, c + NOW)
                if proj:
                    pe.wait_ge(xm_copied, c + PREV)
                    for h in range(2):
                        for k in range(2):
                            mm = nc.tensor.matmul(xm_ps[:, h, :], wx[:, k, h * P:(h + 1) * P], ln.out[b][:, k, :], start=(k == 0), stop=(k == 1))
                    mm.then_inc(xm_made, 1)
                    pe.wait_ge(xm_copied, c + NOW)
                pe.wait_ge(k_exp, c + PREV)
                pe.wait_ge(ekT_copied, c + PREV)
                for h in range(KH):
                    for k in range(2):
                        mm = nc.tensor.matmul(kps[:, h, :], wk[:, k, h * KP:(h + 1) * KP], src[:, k, :], start=(k == 0), stop=(k == 1))
                mm.then_inc(k_made, 1)
                pe.wait_ge(v_copied, c + PREV)
                for t in range(2):
                    for k in range(2):
                        mm = nc.tensor.matmul(vps[:, t, :], src[:, k, t * TT:(t + 1) * TT], wv[:, k, :], start=(k == 0), stop=(k == 1))
                mm.then_inc(v_made, 1)
                pe.wait_ge(q_less, c + PREV)
                for t in range(2):
                    for k in range(2):
                        mm = nc.tensor.matmul(q_ps[0:TT, t * QW:(t + 1) * QW], src[:, k, t * TT:(t + 1) * TT], wq[:, k, :],
                                              start=(k == 0), stop=(k == 1))
                mm.then_inc(q_made, 1)
                if more:
                    ln.pe_var(pe, c + 1, 1 - b)
                pe.wait_ge(k_exp, c + NOW)
                pe.sem_inc(keys_gate, 1)
                for t in range(2):
                    for h in range(KH):
                        mm = nc.tensor.transpose(ekps[:, t, h * KP:(h + 1) * KP], ek[b][:, h, t * TT:(t + 1) * TT], ident[0:KP, 0:KP])
                mm.then_inc(ekT_made, 1)
                pe.wait_ge(ekT_copied, c + NOW)
                pe.wait_ge(v_copied, c + NOW)
                pe.wait_ge(ctx_added, c + PREV)
                for h in range(KH):
                    for t in range(2):
                        mm = nc.tensor.matmul(cps[:, h, :], ekT[b][:, t, h * KP:(h + 1) * KP], v[b][:, t, h * EW:(h + 1) * EW],
                                              start=(t == 0), stop=(t == 1))
                mm.then_inc(ctx_made, 1)
                pe.wait_ge(q_normed, c + NOW)
                pe.wait_ge(qT_copied, c + PREV)
                for t in range(2):
                    for h in range(KH):
                        mm = nc.tensor.transpose(qTps[:, h, t * TT:(t + 1) * TT],
                                                 qn[b][:, t * NQ:(t + 1) * NQ, :].rearrange("p g r -> p (g r)")[:, h * KP:(h + 1) * KP],
                                                 ident[0:TT, 0:TT])
                mm.then_inc(qT_made, 1)
            chunks(pe, body)
            pe.wait_ge(ended, 3)
            for h in range(2):
                src = ctxn[:, h, :] if KH == 2 else ctxn[:, 0, h * P:(h + 1) * P]
                mm = nc.tensor.transpose(q_ps[:, h * P:h * P + KP], src, ident[0:KP, 0:KP])
            mm.then_inc(turned, 1)
            pe.wait_ge(turned_copied, 1)
            for h in range(2):
                mm = nc.tensor.matmul(v_ps[0:KP, h * D:(h + 1) * D] if KH == 2 else v_ps[0:KP, 0:D], ctxT[:, h, :], wo[:, h, :],
                                      start=(KH == 2 or h == 0), stop=(KH == 2 or h == 1))
            mm.then_inc(mixed, 1)

        @block.scalar
        def _(act):
            act.wait_ge(weights, 16 * len(loads))
            ln.act_square(act, 0, 0)
            ln.act_root(act, 0, 0)
            ln.act_affine(act, 0, 0)

            def body(c, b, r, more):
                if proj:
                    act.wait_ge(xm_made, c + NOW)
                    act.wait_ge(q_made, c + OLD)
                    for h in range(2):
                        last = nc.scalar.activation(xm[b][:, h, :], xm_ps[:, h, :], ACT.Identity, bias=bx[:, h:h + 1])
                    last.then_inc(xm_copied, 1)
                if more:
                    ln.act_square(act, c + 1, 1 - b)
                act.wait_ge(v_made, c + NOW)
                act.wait_ge(ctx_made, c + OLD)
                nc.scalar.activation(v[b][:, :, :], vps, ACT.Copy).then_inc(v_copied, 1)
                act.wait_ge(k_bias, c + NOW)
                act.wait_ge(ekT_made, c + OLD)
                act.wait_ge(total_added, c + OLD)
                for h in range(KH):
                    last = nc.scalar.activation(ek[b][:, h, :], kps[:, h, :], ACT.Exp, bias=nbias[b][:, h:h + 1], scale=scale,
                                                accum_out=ksum[b][:, h:h + 1])
                last.then_inc(k_exp, 1)
                act.wait_ge(ctx_added, c + OLD)
                for h in range(KH):
                    last = nc.scalar.activation(fade[b][:, h:h + 1], run[1 - b][:, h:h + 1], ACT.Exp, bias=nbias[b][:, h:h + 1], scale=scale)
                last.then_inc(faded, 1)
                act.wait_ge(q_less, c + NOW)
                act.wait_ge(q_normed, c + OLD)
                nc.scalar.activation(qe[b][:], qs[b][:], ACT.Exp, scale=scale).then_inc(q_exp, 1)
                act.wait_ge(ekT_made, c + NOW)
                act.wait_ge(ctx_made, c + OLD)
                nc.scalar.activation(ekT[b][:, :, :], ekps, ACT.Copy).then_inc(ekT_copied, 1)
                if more:
                    ln.act_root(act, c + 1, 1 - b)
                    ln.act_affine(act, c + 1, 1 - b)
                act.wait_ge(qT_made, c + NOW)
                act.wait_ge(q_saved[b], r * 16 + 16)
                nc.scalar.activation(qT[b][:, :, :], qTps, ACT.Copy).then_inc(qT_copied, 1)
            chunks(act, body)
            act.wait_ge(turned, 1)
            nc.scalar.activation(ctxT[:, :, :], q_ps[:, 0:2 * P].rearrange("p (h k) -> p h k", h=2)[:, :, 0:KP], ACT.Copy).then_inc(turned_copied, 1)
            act.wait_ge(mixed, 1)
            nc.scalar.activation(mixer[0:KP, 0:KH, :], v_ps[0:KP, 0:KH * D].rearrange("p (h e) -> p h e", h=KH), ACT.Copy).then_inc(kept, 1)
            act.wait_ge(kept, 1)

        @block.vector
        def _(dve):
            if proj:
                for w in (wq, wk, wv):
                    nc.vector.memset(w[:, :, :], 0.0).then_inc(by_head, 1)
            nc.vector.memset(run[1][:, :], -1e30).then_inc(started, 1)
            nc.vector.memset(total[:, :], 0.0).then_inc(started, 1)
            nc.vector.memset(ctxt[:, :, :], 0.0).then_inc(started, 1)
            dve.wait_ge(started, 3)
            ln.dve_start(dve)
            dve.wait_ge(weights, 16 * len(loads))
            dve.wait_ge(x_loaded[0], 16)
            ln.dve_centre(dve, 0, 0)
            ln.dve_norm(dve, 0, 0)

            def body(c, b, r, more):
                if more:
                    dve.wait_ge(x_loaded[1 - b], r * 16 + (b * 16 + 16))
                    ln.dve_centre(dve, c + 1, 1 - b)
                dve.wait_ge(k_made, c + NOW)
                dve.wait_ge(k_run, c + OLD)
                nc.vector.tensor_reduce(kmax[b][:, :], kps, AX_X, ALU.max).then_inc(k_maxed, 1)
                dve.wait_ge(k_maxed, c + NOW)
                dve.wait_ge(k_run, c + PREV)
                dve.wait_ge(faded, c + PREV)
                dve.wait_ge(k_bias, c + OLD)
                nc.vector.tensor_tensor(run[b][:, :], run[1 - b][:, :], kmax[b][:, :], ALU.max).then_inc(k_run, 1)
                dve.wait_ge(k_run, c + NOW)
                nc.vector.tensor_scalar(nbias[b][:, :], run[b][:, :], -scale, None, ALU.mult).then_inc(k_bias, 1)
                dve.wait_ge(q_made, c + NOW)
                dve.wait_ge(q_less, c + OLD)
                nc.vector.tensor_reduce(qmax[b][:, :], qps, AX_X, ALU.max).then_inc(q_maxed, 1)
                dve.wait_ge(q_maxed, c + NOW)
                dve.wait_ge(q_exp, c + OLD)
                nc.vector.tensor_tensor(qs[b][:], qps, qmax[b][:, :].unsqueeze(2).to_broadcast([TT, 2 * NQ, R]), ALU.subtract).then_inc(q_less, 1)
                dve.wait_ge(q_exp, c + NOW)
                dve.wait_ge(q_rec, c + OLD)
                nc.vector.tensor_reduce(qsum[b][:, :], qe[b][:], AX_X, ALU.add).then_inc(q_summed, 1)
                dve.wait_ge(q_summed, c + NOW)
                dve.wait_ge(q_normed, c + OLD)
                nc.vector.reciprocal(qrec[b][:, :], qsum[b][:, :]).then_inc(q_rec, 1)
                dve.wait_ge(q_rec, c + NOW)
                dve.wait_ge(qT_made, c + OLD)
                nc.vector.tensor_tensor(qn[b][:], qe[b][:], qrec[b][:, :].unsqueeze(2).to_broadcast([TT, 2 * NQ, R]), ALU.mult).then_inc(q_normed, 1)
                dve.wait_ge(faded, c + NOW)
                dve.wait_ge(total_added, c + PREV)
                for h in range(KH):
                    last = nc.vector.scalar_tensor_tensor(total[:, h:h + 1], total[:, h:h + 1], fade[b][:, h:h + 1], ksum[b][:, h:h + 1],
                                                          ALU.mult, ALU.add)
                last.then_inc(total_added, 1)
                if more:
                    ln.dve_norm(dve, c + 1, 1 - b)
                dve.wait_ge(ctx_made, c + NOW)
                dve.wait_ge(ctx_added, c + PREV)
                for h in range(KH):
                    last = nc.vector.scalar_tensor_tensor(ctxt[:, h, :], ctxt[:, h, :], fade[b][:, h:h + 1], cps[:, h, :], ALU.mult, ALU.add)
                last.then_inc(ctx_added, 1)
            chunks(dve, body)
            dve.wait_ge(total_added, NCH - 1 + NOW)
            nc.vector.reciprocal(rtotal[:, :], total[:, :]).then_inc(ended, 1)
            dve.wait_ge(ended, 1)
            dve.wait_ge(ctx_added, NCH - 1 + NOW)
            nc.vector.tensor_tensor(ctxt[:, :, :], ctxt[:, :, :], rtotal[:, :].unsqueeze(2).to_broadcast([KP, KH, EW]), ALU.mult).then_inc(ended, 1)
            dve.wait_ge(ended, 2)
            nc.vector.tensor_tensor(ctxn[:, :, :], ctxt[:, :, :], blocks[:, :, :], ALU.mult).then_inc(ended, 1)


def attend_second(nc, name, KH, KP, x_d, qT_d, mixer, out_d, c_d, bo_d, gain_d, offset_d, w1_d, b1_d, w2_d, b2_d, add_d=()):
    F = 4 * D
    FG = F // P
    with Phase(nc, name) as ph:
        xin = [ph.sb(f"xin{b}", [P, 2, CW]) for b in range(2)]
        q = [ph.sb(f"q{b}", [KP, KH, CW]) for b in range(2)]
        more_in = [[ph.sb(f"add{n}_{b}", [P, 2, CW]) for b in range(2)] for n in range(len(add_d))]
        x = [ph.sb(f"x{b}", [P, 2, CW]) for b in range(2)]
        g = [ph.sb(f"g{b}", [P, FG, CW]) for b in range(2)]
        y = [ph.sb(f"y{b}", [P, 2, CW]) for b in range(2)]
        ones = ph.sb("ones", [P, P])
        bo, gain, offset, b2 = (ph.sb(n, [P, 2]) for n in ("bo", "gain", "offset", "b2"))
        b1 = ph.sb("b1", [P, FG])
        w1, w2 = ph.sb("w1", [P, 2, F]), ph.sb("w2", [P, FG, D])
        a_ps, y_ps = ph.ps("a_ps", [P, 512]), ph.ps("y_ps", [P, 512])
        f_ps = [ph.ps(f"f_ps{i}", [P, 512]) for i in range(4)]
        aps = a_ps[:, 0:2 * CW].rearrange("p (h c) -> p h c", h=2)
        yps = y_ps[:, 0:2 * CW].rearrange("p (h c) -> p h c", h=2)
        weights = ph.sem("weights")
        loaded = [ph.sem(f"loaded{b}") for b in range(2)]
        saved = [ph.sem(f"saved{b}") for b in range(2)]
        a_made, a_added, y_made, y_added = (ph.loop_sem(n) for n in ("a_made", "a_added", "y_made", "y_added"))
        more_added = [ph.loop_sem(f"more_added{n}") for n in range(len(add_d))]
        done = more_added[-1] if add_d else y_added
        up = [ph.loop_sem(f"up{m}") for m in range(FG // 2)]
        gelu = [ph.loop_sem(f"gelu{m}") for m in range(FG // 2)]
        ln = Norm(nc, ph, x, ones, [up[FG // 2 - 1]], gain, offset)
        loads = [(ones, c_d["mean"]), (bo, bo_d), (gain, gain_d), (offset, offset_d), (w1, w1_d), (b1, b1_d), (w2, w2_d), (b2, b2_d)]
        block = ph.block()
        NL = 2 + len(add_d)

        @block.sync
        def _(sp):
            for b in range(2):
                sp.sem_inc(saved[b], 16)

            def load(c, b):
                for dst, src in [(xin, x_d), (q, qT_d)] + list(zip(more_in, add_d)):
                    sp.dma_start(dst[b][:, :, :], src[:, :, ds(c * CW, CW)]).then_inc(loaded[b], 16)
            load(0, 0)
            for dst, src in loads:
                sp.dma_start(dst[:], src).then_inc(weights, 16)

            def body(c, b, r, more):
                if more:
                    sp.wait_ge(a_added, c + PREV)
                    sp.wait_ge(done, c + PREV)
                    load(c + 1, 1 - b)
                sp.wait_ge(done, c + NOW)
                sp.dma_start(out_d[:, :, ds(c * CW, CW)], y[b][:, :, :]).then_inc(saved[b], 16)
            chunks(sp, body)
            for b in range(2):
                sp.wait_ge(saved[b], 16 * ((NCH + 1 - b) // 2) + 16)

        @block.tensor
        def _(pe):
            def attention(c, b, r):
                pe.wait_ge(loaded[b], r * (16 * NL) + 16 * NL)
                pe.wait_ge(a_added, c + PREV)
                for h in range(2):
                    for k in range(KH):
                        mm = nc.tensor.matmul(aps[:, h, :], mixer[0:KP, k, h * P:(h + 1) * P], q[b][:, k, :], start=(k == 0), stop=(k == KH - 1))
                mm.then_inc(a_made, 1)
                pe.wait_ge(a_added, c + NOW)
                ln.pe_mean(pe, c, b)

            pe.wait_ge(weights, 16 * len(loads))
            attention(0, 0, 0)
            ln.pe_var(pe, 0, 0)

            def body(c, b, r, more):
                pe.wait_ge(ln.affine, c + NOW)
                for m in range(FG // 2):
                    pe.wait_ge(gelu[m], c + PREV)
                    for h in range(2):
                        for k in range(2):
                            g0 = (2 * m + h) * P
                            mm = nc.tensor.matmul(f_ps[m][:, h * CW:(h + 1) * CW], w1[:, k, g0:g0 + P], ln.out[b][:, k, :],
                                                  start=(k == 0), stop=(k == 1))
                    mm.then_inc(up[m], 1)
                    if m == 1 and more:
                        attention(c + 1, 1 - b, r + b)
                if more:
                    ln.pe_var(pe, c + 1, 1 - b)
                pe.wait_ge(y_added, c + PREV)
                for m in range(FG // 2):
                    pe.wait_ge(gelu[m], c + NOW)
                for h in range(2):
                    for m in range(FG):
                        mm = nc.tensor.matmul(yps[:, h, :], w2[:, m, h * P:(h + 1) * P], g[b][:, m, :], start=(m == 0), stop=(m == FG - 1))
                mm.then_inc(y_made, 1)
            chunks(pe, body)

        @block.scalar
        def _(act):
            act.wait_ge(weights, 16 * len(loads))
            ln.act_square(act, 0, 0)
            ln.act_root(act, 0, 0)
            ln.act_affine(act, 0, 0)

            def body(c, b, r, more):
                act.wait_ge(y_made, c + OLD)
                for m in range(FG // 2):
                    act.wait_ge(up[m], c + NOW)
                    for h in range(2):
                        last = nc.scalar.activation(g[b][:, 2 * m + h, :], f_ps[m][:, h * CW:(h + 1) * CW], ACT.Gelu, bias=b1[:, 2 * m + h:2 * m + h + 1])
                    last.then_inc(gelu[m], 1)
                    if m == 2 and more:
                        ln.act_square(act, c + 1, 1 - b)
                if more:
                    ln.act_root(act, c + 1, 1 - b)
                    ln.act_affine(act, c + 1, 1 - b)
            chunks(act, body)

        @block.vector
        def _(dve):
            def attention(c, b, r):
                dve.wait_ge(loaded[b], r * (16 * NL) + 16 * NL)
                dve.wait_ge(a_made, c + NOW)
                dve.wait_ge(ln.mean_ready, c + OLD)
                dve.wait_ge(y_added, c + OLD)
                dve.wait_ge(ln.centred, c + OLD)
                for h in range(2):
                    last = nc.vector.scalar_tensor_tensor(x[b][:, h, :], aps[:, h, :], bo[:, h:h + 1], xin[b][:, h, :], ALU.add, ALU.add)
                last.then_inc(a_added, 1)
                dve.wait_ge(a_added, c + NOW)
                ln.dve_centre(dve, c, b)

            ln.dve_start(dve)
            dve.wait_ge(weights, 16 * len(loads))
            attention(0, 0, 0)
            ln.dve_norm(dve, 0, 0)

            def body(c, b, r, more):
                if more:
                    attention(c + 1, 1 - b, r + b)
                    ln.dve_norm(dve, c + 1, 1 - b)
                dve.wait_ge(y_made, c + NOW)
                dve.wait_ge(saved[b], r * 16 + 16)
                for h in range(2):
                    last = nc.vector.scalar_tensor_tensor(y[b][:, h, :], yps[:, h, :], b2[:, h:h + 1], x[b][:, h, :], ALU.add, ALU.add)
                last.then_inc(y_added, 1)
                before = y_added
                for n, s in enumerate(more_added):
                    dve.wait_ge(before, c + NOW)
                    nc.vector.tensor_tensor(y[b][:, :, :], y[b][:, :, :], more_in[n][b][:, :, :], ALU.add).then_inc(s, 1)
                    before = s
            chunks(dve, body)


def feature_major(p, c0=0, n=CW):
    return p[:, c0:c0 + 2 * n].rearrange("p (h c) -> p h c", h=2)


def norm_table(nc, name, x_d, out_d, table_d, c_d, w_d=None, b_d=None, wa_d=None, ba_d=None, a_d=None):
    proj = w_d is not None
    with Phase(nc, name) as ph:
        x = [ph.sb(f"x{b}", [P, 2, CW]) for b in range(2)]
        row = [ph.sb(f"row{b}", [TT, 2, D]) for b in range(2)]
        ones, ident = ph.sb("ones", [P, P]), ph.sb("ident", [P, P])
        r_ps = [ph.ps(f"r_ps{b}", [P, 512]) for b in range(2)]
        if proj:
            w, bias, wa = ph.sb("w", [P, 2, D]), ph.sb("bias", [TT, D]), ph.sb("wa", [TT, 2, D])
            ba = ph.sb("ba", [TT, 2])
            prod = [ph.sb(f"prod{b}", [TT, 4, D]) for b in range(2)]
            dots = [ph.sb(f"dots{b}", [TT, 2, 2]) for b in range(2)]
        weights = ph.sem("weights")
        loaded, saved, a_saved = ([ph.sem(f"{n}{b}") for b in range(2)] for n in ("loaded", "saved", "a_saved"))
        rows_made, rows_copied, dotted, out_sent = (ph.loop_sem(n) for n in ("rows_made", "rows_copied", "dotted", "out_sent"))
        out_saved = [ph.sem(f"out_saved{b}") for b in range(2)]
        ln = Norm(nc, ph, x, ones, [rows_made, out_sent])
        loads = [(ones, c_d["mean"]), (ident, c_d["ident"])] + ([(w, w_d), (bias, b_d.partition_broadcast(TT)), (wa, wa_d.partition_broadcast(TT)),
                                                                 (ba, ba_d.partition_broadcast(TT))] if proj else [])
        block = ph.block()

        @block.sync
        def _(sp):
            for b in range(2):
                sp.sem_inc(saved[b], 16)
                sp.sem_inc(a_saved[b], 32)
            sp.dma_start(x[0][:, :, :], x_d[:, :, 0:CW]).then_inc(loaded[0], 16)
            for dst, src in loads:
                sp.dma_start(dst[:], src).then_inc(weights, 16)

            def body(c, b, r, more):
                if more:
                    sp.wait_ge(ln.centred, c + PREV)
                    sp.dma_start(x[1 - b][:, :, :], x_d[:, :, ds((c + 1) * CW, CW)]).then_inc(loaded[1 - b], 16)
                sp.wait_ge(ln.normed, c + NOW)
                sp.dma_start(out_d[:, :, ds(c * CW, CW)], ln.out[b][:, :, :]).then_inc(out_saved[b], 16)
                sp.wait_ge(rows_copied, c + NOW)
                sp.dma_start(table_d[ds(c * CW, CW), :].rearrange("(t p) d -> p t d", t=2), row[b][:, :, :]).then_inc(saved[b], 16)
                if proj:
                    sp.wait_ge(dotted, c + NOW)
                    for n in range(2):
                        sp.dma_start(a_d[n, ds(c * CW, CW)].rearrange("(t p) -> p t", t=2), dots[b][:, :, n],
                                     allow_slow_non_contiguous=True).then_inc(a_saved[b], 16)
                sp.wait_ge(out_saved[b], r * 16 + 16)
                sp.sem_inc(out_sent, 1)
            chunks(sp, body)
            for b in range(2):
                sp.wait_ge(saved[b], 16 * ((NCH + 1 - b) // 2) + 16)
                if proj:
                    sp.wait_ge(a_saved[b], 32 * ((NCH + 1 - b) // 2) + 32)

        @block.tensor
        def _(pe):
            pe.wait_ge(weights, 16 * len(loads))
            pe.wait_ge(loaded[0], 16)
            ln.pe_mean(pe, 0, 0)
            ln.pe_var(pe, 0, 0)

            def body(c, b, r, more):
                if more:
                    pe.wait_ge(loaded[1 - b], r * 16 + (b * 16 + 16))
                    ln.pe_mean(pe, c + 1, 1 - b)
                pe.wait_ge(ln.normed, c + NOW)
                pe.wait_ge(rows_copied, c + OLD)
                for t in range(2):
                    for k in range(2):
                        cols = ln.out[b][:, k, t * TT:(t + 1) * TT]
                        if proj:
                            mm = nc.tensor.matmul(r_ps[b][0:TT, t * D:(t + 1) * D], cols, w[:, k, :], start=(k == 0), stop=(k == 1))
                        else:
                            mm = nc.tensor.transpose(r_ps[b][0:TT, t * D + k * P:t * D + (k + 1) * P], cols, ident[:, :])
                mm.then_inc(rows_made, 1)
                if more:
                    ln.pe_var(pe, c + 1, 1 - b)
            chunks(pe, body)

        @block.scalar
        def _(act):
            ln.act_square(act, 0, 0)
            ln.act_root(act, 0, 0)

            def body(c, b, r, more):
                if more:
                    ln.act_square(act, c + 1, 1 - b)
                if not proj:
                    act.wait_ge(rows_made, c + NOW)
                    act.wait_ge(saved[b], r * 16 + 16)
                    nc.scalar.activation(row[b][:, :, :], r_ps[b][0:TT, :].rearrange("p (t d) -> p t d", t=2), ACT.Copy).then_inc(rows_copied, 1)
                if more:
                    ln.act_root(act, c + 1, 1 - b)
            chunks(act, body)

        @block.vector
        def _(dve):
            ln.dve_start(dve)
            dve.wait_ge(weights, 16 * len(loads))
            dve.wait_ge(loaded[0], 16)
            ln.dve_centre(dve, 0, 0)
            ln.dve_norm(dve, 0, 0)

            def body(c, b, r, more):
                if more:
                    dve.wait_ge(loaded[1 - b], r * 16 + (b * 16 + 16))
                    ln.dve_centre(dve, c + 1, 1 - b)
                if proj:
                    dve.wait_ge(rows_made, c + NOW)
                    dve.wait_ge(saved[b], r * 16 + 16)
                    dve.wait_ge(dotted, c + OLD)
                    nc.vector.tensor_tensor(row[b][:, :, :], r_ps[b][0:TT, :].rearrange("p (t d) -> p t d", t=2),
                                            bias[:, None, :].to_broadcast([TT, 2, D]), ALU.add).then_inc(rows_copied, 1)
                    dve.wait_ge(rows_copied, c + NOW)
                    dve.wait_ge(a_saved[b], r * 32 + 32)
                    for t in range(2):
                        for n in range(2):
                            last = nc.vector.tensor_tensor_reduce(prod[b][:, 2 * t + n, :], row[b][:, t, :], wa[:, n, :], 1.0, ba[:, n:n + 1], ALU.mult, ALU.add,
                                                                  dots[b][:, t, n:n + 1])
                    last.then_inc(dotted, 1)
                if more:
                    ln.dve_norm(dve, c + 1, 1 - b)
            chunks(dve, body)


RB = -(-ET // P)


def sum_edges(nc, name, sorted_d, weight_d, table_d, running_d, W, c_d):
    own = weight_d is None
    with Phase(nc, name) as ph:
        ident, last_row = ph.sb("ident", [P, P]), ph.sb("last_row", [P, 1])
        rows = [ph.sb(f"rows{b}", [P, P, 3]) for b in range(2)]
        wrows = [ph.sb(f"wrows{b}", [P, P]) for b in range(2)]
        key, wgt = ph.sb("key", [P, ET + 1]), ph.sb("wgt", [P, ET])
        idx = ph.sb("idx", [P, ET], I32)
        kb, wb = [ph.sb(f"kb{b}", [P, EB + 1]) for b in range(2)], [ph.sb(f"wb{b}", [P, EB]) for b in range(2)]
        ib = [ph.sb(f"ib{b}", [P, EB], I32) for b in range(2)]
        g = [ph.sb(f"g{b}", [P, EB, W]) for b in range(2)]
        run = [ph.sb(f"run{b}", [P, EB, W]) for b in range(2)]
        same, carry = ph.sb("same", [P, 4, P]), ph.sb("carry", [P, 4, P])
        t_ps = [ph.ps(f"t_ps{b}", [P, 512]) for b in range(2)]
        krow_ps = [ph.ps(f"krow_ps{n}", [P, 512]) for n in range(4)]
        s_ps = [ph.ps(f"s_ps{b}", [P, 512]) for b in range(2)]
        consts, edge0, gate = ph.sem("consts"), ph.sem("edge0"), ph.sem("gate")
        rows_in = [ph.sem(f"rows_in{b}") for b in range(2)]
        turned, taken = ph.sem("turned"), ph.sem("taken")
        landed = [[ph.sem(f"landed{b}_{j}") for j in range(EB)] for b in range(2)]
        batch_in, batch_summed = ph.loop_sem("batch_in"), ph.loop_sem("batch_summed")
        krow, selected, summed, kept = (ph.loop_sem(n) for n in ("krow", "selected", "summed", "kept"))
        saved = [ph.sem(f"saved{b}") for b in range(2)]
        parts = 3 if own else 2
        per = 1 if own else 2
        blocks = [(n * P, min(P, ET - n * P)) for n in range(RB)]
        block = ph.block()

        @block.sync
        def _(sp):
            for b in range(2):
                sp.sem_inc(saved[b], 16)
            sp.dma_start(ident[:, :], c_d["ident"]).then_inc(consts, 16)
            sp.dma_start(last_row[:, :], c_d["last_row"]).then_inc(consts, 16)
            for n, (t0, nt) in enumerate(blocks):
                if n >= 2:
                    sp.wait_ge(turned, n - 1)
                sp.dma_start(rows[n % 2][0:nt, :, :], sorted_d.rearrange("(t p) c -> t p c", p=P)[t0:t0 + nt]).then_inc(rows_in[n % 2], 16)
                if not own:
                    sp.dma_start(wrows[n % 2][0:nt, :], weight_d.rearrange("(t p) -> t p", p=P)[t0:t0 + nt]).then_inc(rows_in[n % 2], 16)
            out = running_d.rearrange("(t p) w -> p t w", p=P)
            with sp.Fori(0, NEB // 2) as i:
                for b in range(2):
                    t0 = i * (2 * EB) + b * EB
                    sp.wait_ge(kept, t0 + (EB - 1 + NOW))
                    sp.dma_start(out[:, ds(t0, EB), :], run[b][:, :, :]).then_inc(saved[b], 16)
            for b in range(2):
                sp.wait_ge(saved[b], 16 * (NEB // 2) + 16)

        @block.gpsimd
        def _(pool):
            with pool.Fori(0, NEB // 2) as i:
                for b in range(2):
                    pool.wait_ge(batch_in, i * 2 + (b + NOW))
                    pool.wait_ge(batch_summed, i * 2 + (b + OLD))
                    pool.sem_inc(gate, 1)
                    for j in range(EB):
                        nc.gpsimd.indirect_dma_start(g[b][:, j, 0:D], None, table_d, bass.IndirectOffsetOnAxis(ib[b][:, j:j + 1], 0)).then_inc(landed[b][j], 16)

        @block.tensor
        def _(pe):
            pe.wait_ge(consts, 32)
            for n, (t0, nt) in enumerate(blocks):
                pe.wait_ge(rows_in[n % 2], 16 * per * (n // 2 + 1))
                if n >= 2:
                    pe.wait_ge(taken, n - 1)
                for k in range(3):
                    src = rows[n % 2][0:nt, :, k] if k < 2 or own else wrows[n % 2][0:nt, :]
                    mm = nc.tensor.transpose(t_ps[n % 2][:, k * P:k * P + nt], src, ident[0:nt, 0:nt])
                mm.then_inc(turned, 1)

            def keys_along(t0, b, j):
                pe.wait_ge(selected, t0 + (max(j - 4, -1) + NOW))
                nc.tensor.transpose(krow_ps[j % 4][:, 0:P], kb[b][:, j + 1:j + 2].to_broadcast([P, P]), ident[:, :]).then_inc(krow, 1)

            with pe.Fori(0, NEB // 2) as i:
                for b in range(2):
                    t0 = i * (2 * EB) + b * EB
                    pe.wait_ge(batch_in, i * 2 + (b + NOW))
                    for j in range(3):
                        keys_along(t0, b, j)
                    for j in range(EB):
                        q = (b * EB + j) % 2
                        if j + 3 < EB:
                            keys_along(t0, b, j + 3)
                        pe.wait_ge(selected, t0 + (j + NOW))
                        pe.wait_ge(kept, t0 + (j + OLD))
                        pe.wait_ge(landed[b][j], i * 16 + 16)
                        nc.tensor.matmul(s_ps[q][:, 0:W], same[:, j % 4, :], g[b][:, j, :], start=True, stop=False)
                        pe.wait_ge(kept, t0 + (j + PREV))
                        before = run[b][96:P, j - 1, :] if j else run[1 - b][96:P, EB - 1, :]
                        mm = nc.tensor.matmul(s_ps[q][:, 0:W], carry[96:P, j % 4, :], before, start=False, stop=True)
                        mm.then_inc(summed, 1)
                    nc.tensor.transpose(t_ps[0][:, 0:P], ident[:, :], ident[:, :]).then_inc(batch_summed, 1)

        @block.scalar
        def _(act):
            with act.Fori(0, NEB // 2) as i:
                for b in range(2):
                    t0 = i * (2 * EB) + b * EB
                    act.wait_ge(saved[b], i * 16 + 16)
                    for j in range(EB):
                        q = (b * EB + j) % 2
                        act.wait_ge(summed, t0 + (j + NOW))
                        nc.scalar.activation(run[b][:, j, :], s_ps[q][:, 0:W], ACT.Copy).then_inc(kept, 1)

        @block.vector
        def _(dve):
            nc.vector.memset(key[:, 0:1], -1.0).then_inc(edge0, 1)
            nc.vector.memset(run[1][:, EB - 1, :], 0.0).then_inc(edge0, 1)
            for b in range(2):
                if W > D:
                    nc.vector.memset(g[b][:, :, D:W], 1.0).then_inc(edge0, 1)
            dve.wait_ge(consts, 32)
            for n, (t0, nt) in enumerate(blocks):
                dve.wait_ge(turned, n + 1)
                nc.vector.tensor_copy(key[:, 1 + t0:1 + t0 + nt], t_ps[n % 2][:, 0:nt])
                nc.vector.tensor_copy(idx[:, t0:t0 + nt], t_ps[n % 2][:, P:P + nt])
                nc.vector.tensor_copy(wgt[:, t0:t0 + nt], t_ps[n % 2][:, 2 * P:2 * P + nt]).then_inc(taken, 1)
            dve.wait_ge(taken, RB)
            dve.wait_ge(edge0, 4 if W > D else 2)
            with dve.Fori(0, NEB // 2) as i:
                for b in range(2):
                    t0 = i * (2 * EB) + b * EB
                    dve.wait_ge(batch_summed, i * 2 + (b + OLD))
                    dve.wait_ge(selected, t0 + (-1 + NOW))
                    nc.vector.tensor_copy(kb[b][:, :], key[:, ds(t0, EB + 1)])
                    nc.vector.tensor_copy(wb[b][:, :], wgt[:, ds(t0, EB)])
                    nc.vector.tensor_copy(ib[b][:, :], idx[:, ds(t0, EB)]).then_inc(batch_in, 1)
                    dve.wait_ge(batch_in, i * 2 + (b + NOW))
                    for j in range(EB):
                        k4 = krow_ps[j % 4][:, 0:P]
                        dve.wait_ge(krow, t0 + (j + NOW))
                        dve.wait_ge(summed, t0 + (max(j - 4, -1) + NOW))
                        nc.vector.tensor_scalar(same[:, j % 4, :], k4, kb[b][:, j + 1:j + 2], wb[b][:, j:j + 1], ALU.is_equal, ALU.mult)
                        nc.vector.tensor_scalar(carry[96:P, j % 4, :], k4[96:P, :], kb[b][96:P, j:j + 1], last_row[96:P, 0:1], ALU.is_equal,
                                                ALU.mult).then_inc(selected, 1)


def node_ends(nc, dve, ph, base, hist, first, ends, mask, sem):
    nc.vector.tensor_scalar(mask[:, :], hist[:, :], 1.0, None, ALU.min).then_inc(sem, 1)
    nc.vector.tensor_tensor(first[:, :], base[:, :], hist[:, :], ALU.add).then_inc(sem, 1)
    dve.wait_ge(sem, 2)
    nc.vector.tensor_scalar(ends[:, :], first[:, :], -1.0, 0.0, ALU.add, ALU.max).then_inc(sem, 1)
    dve.wait_ge(sem, 3)


def node_rows(nc, name, running_d, W, hist_d, base_d, out_d, c_d):
    with Phase(nc, name) as ph:
        ident = ph.sb("ident", [P, P])
        base, hist, first, mask = (ph.sb(n, [TT, NT]) for n in ("base", "hist", "first", "mask"))
        ends = ph.sb("ends", [TT, NT], I32)
        eb = [ph.sb(f"eb{b}", [TT, 2], I32) for b in range(2)]
        row = [ph.sb(f"row{b}", [TT, 2, W]) for b in range(2)]
        fac, floor = ([ph.sb(f"{n}{b}", [TT, 2]) for b in range(2)] for n in ("fac", "floor"))
        inv = [ph.sb(f"inv{b}", [TT, 2]) for b in range(2)]
        scaled = [ph.sb(f"scaled{b}", [TT, 2, D]) for b in range(2)]
        out = [ph.sb(f"out{b}", [P, 2, CW]) for b in range(2)]
        o_ps = [ph.ps(f"o_ps{b}", [P, 512]) for b in range(2)]
        loaded, prep, gate = ph.sem("loaded"), ph.sem("prep"), ph.sem("gate")
        landed = [[ph.sem(f"landed{b}{t}") for t in range(2)] for b in range(2)]
        saved = [ph.sem(f"saved{b}") for b in range(2)]
        index_in, s1, s2, factored, scaled_s, turned, copied = (ph.loop_sem(n) for n in ("index_in", "floored", "inverted", "factored", "scaled", "turned", "copied"))
        block = ph.block()

        @block.sync
        def _(sp):
            for b in range(2):
                sp.sem_inc(saved[b], 16)
            sp.dma_start(ident[:, :], c_d["ident"]).then_inc(loaded, 16)
            sp.dma_start(base[:, :], base_d[0:N].rearrange("(t p) -> p t", p=TT), allow_slow_non_contiguous=True).then_inc(loaded, 16)
            sp.dma_start(hist[:, :], hist_d[0:N].rearrange("(t p) -> p t", p=TT), allow_slow_non_contiguous=True).then_inc(loaded, 16)

            def body(c, b, r, more):
                sp.wait_ge(copied, c + NOW)
                sp.dma_start(out_d[:, :, ds(c * CW, CW)], out[b][:, :, :]).then_inc(saved[b], 16)
            chunks(sp, body)
            for b in range(2):
                sp.wait_ge(saved[b], 16 * ((NCH + 1 - b) // 2) + 16)

        @block.gpsimd
        def _(pool):
            def body(c, b, r, more):
                pool.wait_ge(index_in, c + NOW)
                pool.wait_ge(scaled_s, c + OLD)
                pool.sem_inc(gate, 1)
                for t in range(2):
                    nc.gpsimd.indirect_dma_start(row[b][:, t, :], None, running_d, bass.IndirectOffsetOnAxis(eb[b][:, t:t + 1], 0)).then_inc(landed[b][t], 16)
            chunks(pool, body)

        @block.vector
        def _(dve):
            dve.wait_ge(loaded, 48)
            node_ends(nc, dve, ph, base, hist, first, ends, mask, prep)

            def indices(c, b):
                dve.wait_ge(scaled_s, c + OLD)
                nc.vector.tensor_copy(eb[b][:, :], ends[:, ds(c * 2, 2)]).then_inc(index_in, 1)
            indices(0, 0)

            def body(c, b, r, more):
                if more:
                    indices(c + 1, 1 - b)
                for t in range(2):
                    dve.wait_ge(landed[b][t], r * 16 + 16)
                if W > D:
                    nc.vector.tensor_scalar(floor[b][:, :], row[b][:, :, D], 1e-30, None, ALU.max).then_inc(s1, 1)
                    dve.wait_ge(s1, c + NOW)
                    nc.vector.reciprocal(inv[b][:, :], floor[b][:, :]).then_inc(s2, 1)
                    dve.wait_ge(s2, c + NOW)
                    dve.wait_ge(scaled_s, c + OLD)
                    nc.vector.tensor_tensor(fac[b][:, :], inv[b][:, :], mask[:, ds(c * 2, 2)], ALU.mult).then_inc(factored, 1)
                else:
                    dve.wait_ge(scaled_s, c + OLD)
                    nc.vector.tensor_copy(fac[b][:, :], mask[:, ds(c * 2, 2)]).then_inc(factored, 1)
                dve.wait_ge(factored, c + NOW)
                dve.wait_ge(turned, c + OLD)
                nc.vector.tensor_tensor(scaled[b][:, :, :], row[b][:, :, 0:D], fac[b][:, :].unsqueeze(2).to_broadcast([TT, 2, D]), ALU.mult).then_inc(scaled_s, 1)
            chunks(dve, body)

        @block.tensor
        def _(pe):
            pe.wait_ge(loaded, 48)

            def body(c, b, r, more):
                pe.wait_ge(scaled_s, c + NOW)
                pe.wait_ge(copied, c + OLD)
                for t in range(2):
                    for h in range(2):
                        mm = nc.tensor.transpose(o_ps[b][:, h * CW + t * TT:h * CW + (t + 1) * TT], scaled[b][:, t, h * P:(h + 1) * P], ident[0:TT, 0:TT])
                mm.then_inc(turned, 1)
            chunks(pe, body)

        @block.scalar
        def _(act):
            def body(c, b, r, more):
                act.wait_ge(turned, c + NOW)
                act.wait_ge(saved[b], r * 16 + 16)
                nc.scalar.activation(out[b][:, :, :], feature_major(o_ps[b]), ACT.Copy).then_inc(copied, 1)
            chunks(act, body)


def batchnorm_factors(nc, dve, act, stats, mv, gain, offset, scale, shift, dev, inv, t, eps_t, sem, root):
    def on_dve():
        for h in range(2):
            nc.vector.bn_aggr(mv[:, h, :], stats[:, h, :, :].rearrange("p c s -> p (c s)")).then_inc(sem, 1)
        dve.wait_ge(root, 1)
        nc.vector.reciprocal(inv[:, :], dev[:, :]).then_inc(sem, 1)
        dve.wait_ge(sem, 3)
        nc.vector.tensor_tensor(scale[:, :], inv[:, :], gain[:, :], ALU.mult).then_inc(sem, 1)
        dve.wait_ge(sem, 4)
        nc.vector.tensor_tensor(t[:, :], mv[:, :, 0], scale[:, :], ALU.mult).then_inc(sem, 1)
        dve.wait_ge(sem, 5)
        nc.vector.tensor_tensor(shift[:, :], offset[:, :], t[:, :], ALU.subtract).then_inc(sem, 1)
        dve.wait_ge(sem, 6)

    def on_act():
        act.wait_ge(sem, 2)
        nc.scalar.activation(dev[:, :], mv[:, :, 1], ACT.Sqrt, bias=eps_t[:, 0:1]).then_inc(root, 1)
    return on_dve, on_act


def message_layer(nc, name, agg_d, x_d, xn_d, mix_d, out_d, z_d, u_d, hist_d, c_d, eps_d, w1_d, w2_d, g1_d, o1_d, g2_d, o2_d):
    common = ("gain1", "offset1", "gain2", "offset2", "scale1", "shift1", "scale2", "shift2", "dev", "inv", "t")
    with Phase(nc, name) as keep:
        tiles = {n: keep.sb(n, [P, 2]) for n in common}
        mv = keep.sb("mv", [P, 2, 2])
        stats = keep.sb("stats", [P, 2, NCH, 6])
        w1, w2, epsw, eps_t = keep.sb("w1", [P, 2, D]), keep.sb("w2", [P, 2, D]), keep.sb("epsw", [P, 1]), keep.sb("eps", [P, 1])
        for step in range(3):
            with Phase(nc, f"{name}{step}") as ph:
                srcs = [(agg_d, xn_d), (z_d,), (u_d, xn_d, x_d, mix_d)][step]
                ins = [[ph.sb(f"in{n}_{b}", [P, 2, CW]) for b in range(2)] for n in range(len(srcs))]
                y, res = ([ph.sb(f"{n}{b}", [P, 2, CW]) for b in range(2)] for n in ("y", "res"))
                deg, dsq, nn = ([ph.sb(f"{n}{b}", [P, CW]) for b in range(2)] for n in ("deg", "dsq", "nn"))
                m_ps = [ph.ps(f"m_ps{b}", [P, 512]) for b in range(2)]
                loaded, saved = ([ph.sem(f"{n}{b}") for b in range(2)] for n in ("loaded", "saved"))
                y_made, mult, res_made, statted, degs, rooted, nn_made, s3, s4, s5 = (ph.loop_sem(n) for n in (
                    "y_made", "mult", "res_made", "statted", "degs", "rooted", "nn_made", "plus_xn", "plus_x", "plus_mix"))
                weights, agg_s, root = ph.sem("weights"), ph.sem("aggregated"), ph.sem("root")
                n_in = len(srcs) + (1 if step == 1 else 0)
                loads = [] if step else [(tiles["gain1"], g1_d), (tiles["offset1"], o1_d), (tiles["gain2"], g2_d), (tiles["offset2"], o2_d),
                                         (w1, w1_d), (w2, w2_d), (epsw, eps_d.partition_broadcast(P))]
                dst = (z_d, u_d, out_d)[step]
                last_sem = (res_made, res_made, s5)[step]
                block = ph.block()

                @block.sync
                def _(sp):
                    for b in range(2):
                        sp.sem_inc(saved[b], 16)
                    for to, src in loads:
                        sp.dma_start(to[:], src).then_inc(weights, 16)

                    def load(c, b):
                        for n, src in enumerate(srcs):
                            sp.dma_start(ins[n][b][:, :, :], src[:, :, ds(c * CW, CW)]).then_inc(loaded[b], 16)
                        if step == 1:
                            sp.dma_start(deg[b][:, :], hist_d[ds(c * CW, CW)].partition_broadcast(P)).then_inc(loaded[b], 16)
                    load(0, 0)

                    def body(c, b, r, more):
                        if more:
                            sp.wait_ge(last_sem, c + PREV)
                            load(c + 1, 1 - b)
                        sp.wait_ge(last_sem, c + NOW)
                        sp.dma_start(dst[:, :, ds(c * CW, CW)], res[b][:, :, :]).then_inc(saved[b], 16)
                    chunks(sp, body)
                    for b in range(2):
                        sp.wait_ge(saved[b], 16 * ((NCH + 1 - b) // 2) + 16)

                @block.vector
                def _(dve):
                    if step == 0:
                        nc.vector.memset(eps_t[:, :], 1e-5).then_inc(weights, 1)
                        dve.wait_ge(weights, 16 * len(loads) + 1)

                    def body(c, b, r, more):
                        dve.wait_ge(loaded[b], r * (16 * n_in) + 16 * n_in)
                        if step == 0:
                            dve.wait_ge(mult, c + OLD)
                            nc.vector.scalar_tensor_tensor(y[b][:, :, :], ins[1][b][:, :, :], epsw[:, 0:1], ins[0][b][:, :, :], ALU.mult,
                                                           ALU.add).then_inc(y_made, 1)
                        if step == 1:
                            dve.wait_ge(rooted, c + OLD)
                            nc.vector.tensor_scalar(dsq[b][:, :], deg[b][:, :], 1.0, None, ALU.max).then_inc(degs, 1)
                            dve.wait_ge(rooted, c + NOW)
                            dve.wait_ge(res_made, c + OLD)
                            nc.vector.reciprocal(nn[b][:, :], deg[b][:, :]).then_inc(nn_made, 1)
                        if step < 2:
                            dve.wait_ge(mult, c + NOW)
                            dve.wait_ge(saved[b], r * 16 + 16)
                            dve.wait_ge(statted, c + OLD)
                        if step == 0:
                            nc.vector.tensor_copy(res[b][:, :, :], feature_major(m_ps[b])).then_inc(res_made, 1)
                        if step == 1:
                            dve.wait_ge(nn_made, c + NOW)
                            nc.vector.tensor_tensor(res[b][:, :, :], feature_major(m_ps[b]), nn[b][:, None, :].to_broadcast([P, 2, CW]),
                                                    ALU.mult).then_inc(res_made, 1)
                        if step < 2:
                            dve.wait_ge(res_made, c + NOW)
                            for h in range(2):
                                last = nc.vector.bn_stats(stats[:, h, ds(c, 1), :].rearrange("p c s -> p (c s)"), res[b][:, h, :])
                            last.then_inc(statted, 1)
                        if step == 2:
                            dve.wait_ge(y_made, c + NOW)
                            dve.wait_ge(saved[b], r * 16 + 16)
                            for n, (a, s) in enumerate(((y, s3), (res, s4), (res, s5))):
                                if n:
                                    dve.wait_ge((s3, s4)[n - 1], c + NOW)
                                nc.vector.tensor_tensor(res[b][:, :, :], a[b][:, :, :], ins[n + 1][b][:, :, :], ALU.add).then_inc(s, 1)
                    chunks(dve, body)
                    if step < 2:
                        dve.wait_ge(statted, NCH - 1 + NOW)
                        batchnorm_factors(nc, dve, None, stats, mv, tiles[f"gain{step + 1}"], tiles[f"offset{step + 1}"], tiles[f"scale{step + 1}"],
                                          tiles[f"shift{step + 1}"], tiles["dev"], tiles["inv"], tiles["t"], eps_t, agg_s, root)[0]()

                @block.scalar
                def _(act):
                    def body(c, b, r, more):
                        if step == 1:
                            act.wait_ge(degs, c + NOW)
                            nc.scalar.activation(deg[b][:, :], dsq[b][:, :], ACT.Sqrt).then_inc(rooted, 1)
                        if step:
                            act.wait_ge(loaded[b], r * (16 * n_in) + 16 * n_in)
                            act.wait_ge(mult if step == 1 else s3, c + OLD)
                            for h in range(2):
                                last = nc.scalar.activation(y[b][:, h, :], ins[0][b][:, h, :], ACT.Relu, bias=tiles[f"shift{step}"][:, h:h + 1],
                                                            scale=tiles[f"scale{step}"][:, h:h + 1])
                            last.then_inc(y_made, 1)
                    if step:
                        chunks(act, body)
                    if step < 2:
                        batchnorm_factors(nc, None, act, stats, mv, None, None, None, None, tiles["dev"], None, None, eps_t, agg_s, root)[1]()

                if step < 2:
                    @block.tensor
                    def _(pe):
                        w = (w1, w2)[step]
                        if step == 0:
                            pe.wait_ge(weights, 16 * len(loads) + 1)

                        def body(c, b, r, more):
                            pe.wait_ge(y_made, c + NOW)
                            pe.wait_ge(res_made, c + OLD)
                            for h in range(2):
                                for k in range(2):
                                    mm = nc.tensor.matmul(m_ps[b][:, h * CW:(h + 1) * CW], w[:, k, h * P:(h + 1) * P], y[b][:, k, :], start=(k == 0), stop=(k == 1))
                            mm.then_inc(mult, 1)
                        chunks(pe, body)


def experts(nc, name, x_d, out_d, c_d, router_d, w1_d, b1_d, w2_d, b2_d):
    NE = 8
    with Phase(nc, name) as ph:
        x = [ph.sb(f"x{b}", [P, 2, CW]) for b in range(2)]
        ones, ident = ph.sb("ones", [P, P]), ph.sb("ident", [P, P])
        router, pick = ph.sb("router", [P, 2, NE]), ph.sb("pick", [NE, NE, P])
        before = ph.sb("before", [TT, NE, NE])
        w1, w2 = ph.sb("w1", [P, NE, 2, D]), ph.sb("w2", [P, NE, 2, D])
        b1, b2 = ph.sb("b1", [P, NE, 2]), ph.sb("b2", [NE, D])
        lg, lmax, les, ex, esum, erec, pr, cnt, eq, sel, psel, ps, pg, pgr, comb = (
            [ph.sb(f"{n}{b}", s) for b in range(2)] for n, s in (
                ("lg", [TT, 2, NE]), ("lmax", [TT, 2]), ("les", [TT, 2, NE]), ("ex", [TT, 2, NE]), ("esum", [TT, 2]), ("erec", [TT, 2]),
                ("pr", [TT, 2, NE]), ("cnt", [TT, 2 * NE, NE]), ("eq", [TT, 2 * NE, NE]), ("sel", [TT, 2, NE]), ("psel", [TT, 2, NE]),
                ("ps", [TT, 2]), ("pg", [TT, 2]), ("pgr", [TT, 2]), ("comb", [TT, 2, NE])))
        combT = [ph.sb(f"combT{b}", [NE, CW]) for b in range(2)]
        g = [ph.sb(f"g{n}", [P, 2, CW]) for n in range(2)]
        gw = [ph.sb(f"gw{n}", [P, 2, CW]) for n in range(2)]
        t1, y = ([ph.sb(f"{n}{b}", [P, 2, CW]) for b in range(2)] for n in ("t1_", "y"))
        h_ps = [ph.ps(f"h_ps{n}", [P, 512]) for n in range(2)]
        o_ps = [ph.ps(f"o_ps{h}", [P, 512]) for h in range(2)]
        l_ps, c_ps = ph.ps("l_ps", [P, 512]), ph.ps("c_ps", [P, 512])
        weights = ph.sem("weights")
        loaded, saved = ([ph.sem(f"{n}{b}") for b in range(2)] for n in ("loaded", "saved"))
        logits, l_read, comb_ready, combT_made, combT_copied, y_made, summed_x = (ph.loop_sem(n) for n in (
            "logits", "l_read", "comb_ready", "combT_made", "combT_copied", "y_made", "summed_x"))
        route = [ph.loop_sem(f"route{n}") for n in range(16)]
        e_up, e_gelu, e_cb, e_weighted, e_down = (ph.loop_sem(n) for n in ("e_up", "e_gelu", "e_cb", "e_weighted", "e_down"))
        exped = ph.loop_sem("exped")
        ln = Norm(nc, ph, x, ones, [y_made, summed_x])
        loads = [(ones, c_d["mean"]), (ident, c_d["ident"]), (pick, c_d["pick"]), (before, c_d["before"]), (router, router_d),
                 (w1, w1_d), (b1, b1_d), (w2, w2_d), (b2, b2_d)]
        block = ph.block()

        @block.sync
        def _(sp):
            for b in range(2):
                sp.sem_inc(saved[b], 16)
            sp.dma_start(x[0][:, :, :], x_d[:, :, 0:CW]).then_inc(loaded[0], 16)
            for dst, src in loads:
                sp.dma_start(dst[:], src).then_inc(weights, 16)

            def body(c, b, r, more):
                if more:
                    sp.wait_ge(ln.centred, c + PREV)
                    sp.wait_ge(summed_x, c + PREV)
                    sp.dma_start(x[1 - b][:, :, :], x_d[:, :, ds((c + 1) * CW, CW)]).then_inc(loaded[1 - b], 16)
                sp.wait_ge(y_made, c + NOW)
                sp.dma_start(out_d[:, :, ds(c * CW, CW)], y[b][:, :, :]).then_inc(saved[b], 16)
            chunks(sp, body)
            for b in range(2):
                sp.wait_ge(saved[b], 16 * ((NCH + 1 - b) // 2) + 16)

        @block.tensor
        def _(pe):
            def scores(c, b):
                pe.wait_ge(ln.normed, c + NOW)
                pe.wait_ge(l_read, c + PREV)
                pe.wait_ge(combT_copied, c + PREV)
                for t in range(2):
                    for k in range(2):
                        mm = nc.tensor.matmul(l_ps[0:TT, t * NE:(t + 1) * NE], ln.out[b][:, k, t * TT:(t + 1) * TT], router[:, k, :], start=(k == 0), stop=(k == 1))
                mm.then_inc(logits, 1)

            def turn(c, b):
                pe.wait_ge(comb_ready, c + NOW)
                for t in range(2):
                    mm = nc.tensor.transpose(l_ps[0:NE, 256 + t * TT:256 + (t + 1) * TT], comb[b][:, t, :], ident[0:TT, 0:TT])
                mm.then_inc(combT_made, 1)

            def up(c, b, e):
                n = c * NE + e
                pe.wait_ge(e_gelu, n + OLD)
                for h in range(2):
                    for k in range(2):
                        mm = nc.tensor.matmul(h_ps[e % 2][:, h * CW:(h + 1) * CW], w1[:, e, k, h * P:(h + 1) * P], ln.out[b][:, k, :], start=(k == 0), stop=(k == 1))
                mm.then_inc(e_up, 1)
                pe.wait_ge(e_weighted, n + PREV)
                nc.tensor.matmul(c_ps[:, 0:CW], pick[:, e, :], combT[b][:, :], start=True, stop=True).then_inc(e_cb, 1)

            def down(c, b, e):
                pe.wait_ge(e_weighted, c * NE + (e + NOW))
                for h in range(2):
                    for k in range(2):
                        mm = nc.tensor.matmul(o_ps[h][:, 0:CW], w2[:, e, k, h * P:(h + 1) * P], gw[e % 2][:, k, :], start=False, stop=(e == NE - 1 and k == 1),
                                              skip_group_check=True)
                mm.then_inc(e_down, 1)

            pe.wait_ge(weights, 16 * len(loads))
            pe.wait_ge(loaded[0], 16)
            ln.pe_mean(pe, 0, 0)
            ln.pe_var(pe, 0, 0)
            scores(0, 0)
            turn(0, 0)

            def body(c, b, r, more):
                pe.wait_ge(combT_copied, c + NOW)
                pe.wait_ge(y_made, c + PREV)
                for e in range(NE):
                    up(c, b, e)
                    if e == 0:
                        for h in range(2):
                            nc.tensor.matmul(o_ps[h][:, 0:CW], b2[:, h * P:(h + 1) * P], combT[b][:, :], start=True, stop=False, skip_group_check=True)
                    else:
                        down(c, b, e - 1)
                    if more:
                        if e == 1:
                            pe.wait_ge(loaded[1 - b], r * 16 + (b * 16 + 16))
                            ln.pe_mean(pe, c + 1, 1 - b)
                        if e == 3:
                            ln.pe_var(pe, c + 1, 1 - b)
                        if e == 5:
                            scores(c + 1, 1 - b)
                        if e == 7:
                            turn(c + 1, 1 - b)
                down(c, b, NE - 1)
            chunks(pe, body)

        @block.scalar
        def _(act):
            def softmax_exp(c, b):
                act.wait_ge(route[1], c + NOW)
                act.wait_ge(route[3], c + OLD)
                act.wait_ge(route[4], c + OLD)
                nc.scalar.activation(ex[b][:, :, :], les[b][:, :, :], ACT.Exp).then_inc(exped, 1)

            def copy_turned(c, b):
                act.wait_ge(combT_made, c + NOW)
                act.wait_ge(y_made, c + OLD)
                nc.scalar.activation(combT[b][:, :], l_ps[0:NE, 256:256 + CW], ACT.Copy).then_inc(combT_copied, 1)

            act.wait_ge(weights, 16 * len(loads))
            ln.act_square(act, 0, 0)
            ln.act_root(act, 0, 0)
            softmax_exp(0, 0)
            copy_turned(0, 0)

            def body(c, b, r, more):
                for e in range(NE):
                    n = c * NE + e
                    act.wait_ge(e_up, n + NOW)
                    act.wait_ge(e_weighted, n + OLD)
                    for h in range(2):
                        last = nc.scalar.activation(g[e % 2][:, h, :], h_ps[e % 2][:, h * CW:(h + 1) * CW], ACT.Gelu, bias=b1[:, e, h:h + 1])
                    last.then_inc(e_gelu, 1)
                    if more:
                        if e == 2:
                            ln.act_square(act, c + 1, 1 - b)
                        if e == 4:
                            ln.act_root(act, c + 1, 1 - b)
                        if e == 6:
                            softmax_exp(c + 1, 1 - b)
                if more:
                    copy_turned(c + 1, 1 - b)
            chunks(act, body)

        @block.vector
        def _(dve):
            def step(c, n, ins):
                ins.then_inc(route[n], 1)
                dve.wait_ge(route[n], c + NOW)

            def routing1(c, b):
                dve.wait_ge(logits, c + NOW)
                dve.wait_ge(comb_ready, c + OLD)
                dve.wait_ge(exped, c + OLD)
                nc.vector.tensor_copy(lg[b][:, :, :], l_ps[0:TT, 0:2 * NE].rearrange("p (t e) -> p t e", t=2)).then_inc(l_read, 1)
                dve.wait_ge(l_read, c + NOW)
                step(c, 0, nc.vector.tensor_reduce(lmax[b][:, :], lg[b][:, :, :], AX_X, ALU.max))
                step(c, 1, nc.vector.tensor_tensor(les[b][:, :, :], lg[b][:, :, :], lmax[b][:, :].unsqueeze(2).to_broadcast([TT, 2, NE]), ALU.subtract))

            def routing2(c, b):
                dve.wait_ge(exped, c + NOW)
                step(c, 3, nc.vector.tensor_reduce(esum[b][:, :], ex[b][:, :, :], AX_X, ALU.add))
                step(c, 2, nc.vector.reciprocal(erec[b][:, :], esum[b][:, :]))
                step(c, 4, nc.vector.tensor_tensor(pr[b][:, :, :], ex[b][:, :, :], erec[b][:, :].unsqueeze(2).to_broadcast([TT, 2, NE]), ALU.mult))
                for t in range(2):
                    own = pr[b][:, t, :].unsqueeze(2).to_broadcast([TT, NE, NE])
                    others = pr[b][:, t, None, :].to_broadcast([TT, NE, NE])
                    nc.vector.tensor_tensor(cnt[b][:, t * NE:(t + 1) * NE, :], others, own, ALU.is_gt)
                    last = nc.vector.tensor_tensor(eq[b][:, t * NE:(t + 1) * NE, :], others, own, ALU.is_equal)
                step(c, 5, last)
                for t in range(2):
                    last = nc.vector.tensor_tensor(eq[b][:, t * NE:(t + 1) * NE, :], eq[b][:, t * NE:(t + 1) * NE, :], before[:, :, :], ALU.mult)
                step(c, 6, last)
                step(c, 7, nc.vector.tensor_tensor(cnt[b][:], cnt[b][:], eq[b][:], ALU.add))
                step(c, 8, nc.vector.tensor_reduce(sel[b][:].rearrange("p t e -> p (t e)"), cnt[b][:], AX_X, ALU.add))
                step(c, 9, nc.vector.scalar_tensor_tensor(psel[b][:], sel[b][:], 2.0, pr[b][:], ALU.is_lt, ALU.mult))
                step(c, 10, nc.vector.tensor_reduce(ps[b][:, :], psel[b][:], AX_X, ALU.add))
                step(c, 11, nc.vector.tensor_scalar(pg[b][:, :], ps[b][:, :], 1e-12, None, ALU.max))
                step(c, 12, nc.vector.reciprocal(pgr[b][:, :], pg[b][:, :]))
                dve.wait_ge(combT_made, c + OLD)
                nc.vector.tensor_tensor(comb[b][:], psel[b][:], pgr[b][:, :].unsqueeze(2).to_broadcast([TT, 2, NE]), ALU.mult).then_inc(comb_ready, 1)

            ln.dve_start(dve)
            dve.wait_ge(weights, 16 * len(loads))
            dve.wait_ge(loaded[0], 16)
            ln.dve_centre(dve, 0, 0)
            ln.dve_norm(dve, 0, 0)
            routing1(0, 0)
            routing2(0, 0)

            def body(c, b, r, more):
                for e in range(NE):
                    n = c * NE + e
                    dve.wait_ge(e_gelu, n + NOW)
                    dve.wait_ge(e_cb, n + NOW)
                    dve.wait_ge(e_down, n + OLD)
                    nc.vector.tensor_tensor(gw[e % 2][:, :, :], g[e % 2][:, :, :], c_ps[:, None, 0:CW].to_broadcast([P, 2, CW]), ALU.mult).then_inc(e_weighted, 1)
                    if more:
                        if e == 1:
                            dve.wait_ge(loaded[1 - b], r * 16 + (b * 16 + 16))
                            ln.dve_centre(dve, c + 1, 1 - b)
                        if e == 4:
                            ln.dve_norm(dve, c + 1, 1 - b)
                        if e == 5:
                            routing1(c + 1, 1 - b)
                        if e == 6:
                            routing2(c + 1, 1 - b)
                dve.wait_ge(y_made, c + OLD)
                nc.vector.tensor_tensor(t1[b][:, :, :], x[b][:, :, :], ln.out[b][:, :, :], ALU.add).then_inc(summed_x, 1)
                dve.wait_ge(summed_x, c + NOW)
                dve.wait_ge(e_down, c * NE + (NE - 1 + NOW))
                dve.wait_ge(saved[b], r * 16 + 16)
                for h in range(2):
                    last = nc.vector.tensor_tensor(y[b][:, h, :], t1[b][:, h, :], o_ps[h][:, 0:CW], ALU.add)
                last.then_inc(y_made, 1)
            chunks(dve, body)


def token_weights(nc, name, x_d, t_d, row_d, c_d, wr_d, br_d):
    with Phase(nc, name) as ph:
        x = [ph.sb(f"x{b}", [P, 2, CW]) for b in range(2)]
        ones, wr, wrb, br = ph.sb("ones", [P, P]), ph.sb("wr", [P, 2]), ph.sb("wrb", [P, 2, 32]), ph.sb("br", [32, 1])
        row = [ph.sb(f"row{b}", [32, CW]) for b in range(2)]
        r_ps = [ph.ps(f"r_ps{b}", [P, 512]) for b in range(2)]
        weights, wide = ph.sem("weights"), ph.sem("wide")
        loaded, saved, out_saved = ([ph.sem(f"{n}{b}") for b in range(2)] for n in ("loaded", "saved", "out_saved"))
        made, copied, out_sent = (ph.loop_sem(n) for n in ("made", "copied", "out_sent"))
        ln = Norm(nc, ph, x, ones, [made, out_sent])
        loads = [(ones, c_d["mean"]), (wr, wr_d), (br, br_d.partition_broadcast(32))]
        block = ph.block()

        @block.sync
        def _(sp):
            for b in range(2):
                sp.sem_inc(saved[b], 16)
            sp.dma_start(x[0][:, :, :], x_d[:, :, 0:CW]).then_inc(loaded[0], 16)
            for dst, src in loads:
                sp.dma_start(dst[:], src).then_inc(weights, 16)

            def body(c, b, r, more):
                if more:
                    sp.wait_ge(ln.centred, c + PREV)
                    sp.dma_start(x[1 - b][:, :, :], x_d[:, :, ds((c + 1) * CW, CW)]).then_inc(loaded[1 - b], 16)
                sp.wait_ge(ln.normed, c + NOW)
                sp.dma_start(t_d[:, :, ds(c * CW, CW)], ln.out[b][:, :, :]).then_inc(out_saved[b], 16)
                sp.wait_ge(copied, c + NOW)
                sp.dma_start(row_d[ds(c * CW, CW)].rearrange("(o n) -> o n", o=1), row[b][0:1, :]).then_inc(saved[b], 16)
                sp.wait_ge(out_saved[b], r * 16 + 16)
                sp.sem_inc(out_sent, 1)
            chunks(sp, body)
            for b in range(2):
                sp.wait_ge(saved[b], 16 * ((NCH + 1 - b) // 2) + 16)

        @block.tensor
        def _(pe):
            pe.wait_ge(weights, 16 * len(loads))
            pe.wait_ge(loaded[0], 16)
            ln.pe_mean(pe, 0, 0)
            ln.pe_var(pe, 0, 0)
            pe.wait_ge(wide, 1)

            def body(c, b, r, more):
                if more:
                    pe.wait_ge(loaded[1 - b], r * 16 + (b * 16 + 16))
                    ln.pe_mean(pe, c + 1, 1 - b)
                pe.wait_ge(ln.normed, c + NOW)
                pe.wait_ge(copied, c + OLD)
                for k in range(2):
                    mm = nc.tensor.matmul(r_ps[b][0:32, 0:CW], wrb[:, k, :], ln.out[b][:, k, :], start=(k == 0), stop=(k == 1))
                mm.then_inc(made, 1)
                if more:
                    ln.pe_var(pe, c + 1, 1 - b)
            chunks(pe, body)

        @block.scalar
        def _(act):
            act.wait_ge(weights, 16 * len(loads))
            ln.act_square(act, 0, 0)
            ln.act_root(act, 0, 0)

            def body(c, b, r, more):
                if more:
                    ln.act_square(act, c + 1, 1 - b)
                act.wait_ge(made, c + NOW)
                act.wait_ge(saved[b], r * 16 + 16)
                nc.scalar.activation(row[b][:, :], r_ps[b][0:32, 0:CW], ACT.Identity, bias=br[:, 0:1]).then_inc(copied, 1)
                if more:
                    ln.act_root(act, c + 1, 1 - b)
            chunks(act, body)

        @block.vector
        def _(dve):
            ln.dve_start(dve)
            dve.wait_ge(weights, 16 * len(loads))
            nc.vector.tensor_copy(wrb[:, :, :], wr[:, :].unsqueeze(2).to_broadcast([P, 2, 32])).then_inc(wide, 1)
            dve.wait_ge(loaded[0], 16)
            ln.dve_centre(dve, 0, 0)
            ln.dve_norm(dve, 0, 0)

            def body(c, b, r, more):
                if more:
                    dve.wait_ge(loaded[1 - b], r * 16 + (b * 16 + 16))
                    ln.dve_centre(dve, c + 1, 1 - b)
                    ln.dve_norm(dve, c + 1, 1 - b)
            chunks(dve, body)


KEPT = N // 2 - 1


def choose_tokens(nc, name, row_d, factor_d, c_d):
    with Phase(nc, name) as ph:
        row, col = ph.sb("row", [TT, N]), ph.sb("col", [TT, NT])
        tri = ph.sb("tri", [TT, TT])
        junk = [ph.sb(f"junk{b}", [TT, N]) for b in range(2)]
        diag = [ph.sb(f"diag{b}", [TT, TT]) for b in range(2)]
        parts = ph.sb("parts", [TT, 4, NT])
        total, factor = ph.sb("total", [TT, 3, NT]), ph.sb("factor", [TT, NT])
        loaded, step, saved, done = ph.sem("loaded"), ph.sem("step"), ph.sem("saved"), ph.sem("compared")
        block = ph.block()

        @block.sync
        def _(sp):
            sp.dma_start(row[:, :], row_d.partition_broadcast(TT)).then_inc(loaded, 16)
            sp.dma_start(col[:, :], row_d.rearrange("(t p) -> p t", p=TT), allow_slow_non_contiguous=True).then_inc(loaded, 16)
            sp.dma_start(tri[:, :], c_d["tri"][0:TT, 0:TT]).then_inc(loaded, 16)
            sp.wait_ge(step, 5)
            sp.dma_start(factor_d.rearrange("(t p) -> p t", p=TT), factor[:, :], allow_slow_non_contiguous=True).then_inc(saved, 16)
            sp.wait_ge(saved, 16)

        @block.vector
        def _(dve):
            dve.wait_ge(loaded, 48)
            nc.vector.memset(parts[:, :, :], 0.0).then_inc(step, 1)
            dve.wait_ge(step, 1)
            for t in range(NT):
                a, z = t * TT, (t + 1) * TT
                own = col[:, t:t + 1]
                if t >= 2:
                    dve.wait_ge(done, t - 1)
                if t:
                    nc.vector.tensor_scalar(junk[t % 2][:, 0:a], row[:, 0:a], own, 0.0, ALU.is_ge, ALU.add, accum_out=parts[:, 0, t:t + 1])
                if z < N:
                    nc.vector.tensor_scalar(junk[t % 2][:, z:N], row[:, z:N], own, 0.0, ALU.is_gt, ALU.add, accum_out=parts[:, 1, t:t + 1])
                nc.vector.tensor_scalar(junk[t % 2][:, a:z], row[:, a:z], own, 0.0, ALU.is_gt, ALU.add, accum_out=parts[:, 2, t:t + 1])
                nc.vector.scalar_tensor_tensor(diag[t % 2][:, :], row[:, a:z], own, tri[:, :], ALU.is_equal, ALU.mult,
                                               accum_out=parts[:, 3, t:t + 1]).then_inc(done, 1)
            dve.wait_ge(done, NT)
            nc.vector.tensor_tensor(total[:, 0, :], parts[:, 0, :], parts[:, 1, :], ALU.add).then_inc(step, 1)
            nc.vector.tensor_tensor(total[:, 1, :], parts[:, 2, :], parts[:, 3, :], ALU.add).then_inc(step, 1)
            dve.wait_ge(step, 3)
            nc.vector.tensor_tensor(total[:, 2, :], total[:, 0, :], total[:, 1, :], ALU.add).then_inc(step, 1)
            dve.wait_ge(step, 4)
            nc.vector.scalar_tensor_tensor(factor[:, :], total[:, 2, :], float(KEPT), col[:, :], ALU.is_lt, ALU.mult).then_inc(step, 1)


def chosen_forward(nc, name, t_d, x_d, factor_d, out_d, w1_d, b1_d, w2_d, b2_d):
    F = 4 * D
    FG = F // P
    with Phase(nc, name) as ph:
        t, x, y = ([ph.sb(f"{n}{b}", [P, 2, CW]) for b in range(2)] for n in ("t", "x", "y"))
        fac = [ph.sb(f"fac{b}", [P, CW]) for b in range(2)]
        g = [ph.sb(f"g{b}", [P, FG, CW]) for b in range(2)]
        w1, w2, b1, b2 = ph.sb("w1", [P, 2, F]), ph.sb("w2", [P, FG, D]), ph.sb("b1", [P, FG]), ph.sb("b2", [P, 2])
        f_ps = [ph.ps(f"f_ps{i}", [P, 512]) for i in range(4)]
        y_ps = [ph.ps(f"y_ps{b}", [P, 512]) for b in range(2)]
        weights = ph.sem("weights")
        loaded, saved = ([ph.sem(f"{n}{b}") for b in range(2)] for n in ("loaded", "saved"))
        y_made, y_scaled, y_t, y_x = (ph.loop_sem(n) for n in ("y_made", "y_scaled", "plus_t", "plus_x"))
        up = [ph.loop_sem(f"up{m}") for m in range(4)]
        gelu = [ph.loop_sem(f"gelu{m}") for m in range(4)]
        loads = [(w1, w1_d), (b1, b1_d), (w2, w2_d), (b2, b2_d)]
        block = ph.block()

        @block.sync
        def _(sp):
            for b in range(2):
                sp.sem_inc(saved[b], 16)

            def load(c, b):
                sp.dma_start(t[b][:, :, :], t_d[:, :, ds(c * CW, CW)]).then_inc(loaded[b], 16)
                sp.dma_start(x[b][:, :, :], x_d[:, :, ds(c * CW, CW)]).then_inc(loaded[b], 16)
                sp.dma_start(fac[b][:, :], factor_d[ds(c * CW, CW)].partition_broadcast(P)).then_inc(loaded[b], 16)
            load(0, 0)
            for dst, src in loads:
                sp.dma_start(dst[:], src).then_inc(weights, 16)

            def body(c, b, r, more):
                if more:
                    sp.wait_ge(y_x, c + PREV)
                    load(c + 1, 1 - b)
                sp.wait_ge(y_x, c + NOW)
                sp.dma_start(out_d[:, :, ds(c * CW, CW)], y[b][:, :, :]).then_inc(saved[b], 16)
            chunks(sp, body)
            for b in range(2):
                sp.wait_ge(saved[b], 16 * ((NCH + 1 - b) // 2) + 16)

        @block.tensor
        def _(pe):
            pe.wait_ge(weights, 16 * len(loads))

            def body(c, b, r, more):
                pe.wait_ge(loaded[b], r * 48 + 48)
                for m in range(4):
                    pe.wait_ge(gelu[m], c + PREV)
                    for h in range(2):
                        for k in range(2):
                            g0 = (2 * m + h) * P
                            mm = nc.tensor.matmul(f_ps[m][:, h * CW:(h + 1) * CW], w1[:, k, g0:g0 + P], t[b][:, k, :], start=(k == 0), stop=(k == 1))
                    mm.then_inc(up[m], 1)
                pe.wait_ge(y_scaled, c + OLD)
                for m in range(4):
                    pe.wait_ge(gelu[m], c + NOW)
                for h in range(2):
                    for m in range(FG):
                        mm = nc.tensor.matmul(y_ps[b][:, h * CW:(h + 1) * CW], w2[:, m, h * P:(h + 1) * P], g[b][:, m, :], start=(m == 0), stop=(m == FG - 1))
                mm.then_inc(y_made, 1)
            chunks(pe, body)

        @block.scalar
        def _(act):
            act.wait_ge(weights, 16 * len(loads))

            def body(c, b, r, more):
                act.wait_ge(y_made, c + OLD)
                for m in range(4):
                    act.wait_ge(up[m], c + NOW)
                    for h in range(2):
                        last = nc.scalar.activation(g[b][:, 2 * m + h, :], f_ps[m][:, h * CW:(h + 1) * CW], ACT.Gelu_apprx_tanh,
                                                    bias=b1[:, 2 * m + h:2 * m + h + 1])
                    last.then_inc(gelu[m], 1)
            chunks(act, body)

        @block.vector
        def _(dve):
            dve.wait_ge(weights, 16 * len(loads))

            def body(c, b, r, more):
                dve.wait_ge(y_made, c + NOW)
                dve.wait_ge(loaded[b], r * 48 + 48)
                dve.wait_ge(saved[b], r * 16 + 16)
                for h in range(2):
                    last = nc.vector.scalar_tensor_tensor(y[b][:, h, :], y_ps[b][:, h * CW:(h + 1) * CW], b2[:, h:h + 1], fac[b][:, :], ALU.add, ALU.mult)
                last.then_inc(y_scaled, 1)
                dve.wait_ge(y_scaled, c + NOW)
                nc.vector.tensor_tensor(y[b][:, :, :], y[b][:, :, :], t[b][:, :, :], ALU.add).then_inc(y_t, 1)
                dve.wait_ge(y_t, c + NOW)
                nc.vector.tensor_tensor(y[b][:, :, :], y[b][:, :, :], x[b][:, :, :], ALU.add).then_inc(y_x, 1)
            chunks(dve, body)


def attention_weights(nc, name, sorted_d, prev_d, a_d, hist_d, base_d, max_d, pair_d, ev_d, c_d):
    FAR = -1e30
    with Phase(nc, name) as ph:
        ident = ph.sb("ident", [P, P])
        meta, pair = ph.sb("meta", [P, ET, 3]), ph.sb("pair", [P, ET, 2])
        prev, same, pen = ph.sb("prev", [P, ET]), ph.sb("same", [P, ET]), ph.sb("pen", [P, ET])
        idx = ph.sb("idx", [P, ET], I32)
        a1 = ph.sb("a1", [P, ET])
        zero = ph.sb("zero", [P, ET])
        loc, acc, mx = ph.sb("loc", [P, ET]), ph.sb("acc", [P, ET]), ph.sb("mx", [P, ET])
        fill = [ph.sb(f"fill{n}", [P, ET]) for n in range(2)]
        v, vl, d, dm, ev = (ph.sb(n, [P, ET]) for n in ("v", "vl", "d", "dm", "ev"))
        edge, rowp, rows = ph.sb("edge", [P, 2]), ph.sb("rowp", [1, 2, P]), ph.sb("rows", [1, 4, P + 1])
        cin = ph.sb("cin", [P, 3])
        ib = [ph.sb(f"ib{b}", [P, EB], I32) for b in range(2)]
        gb = [ph.sb(f"gb{b}", [P, EB]) for b in range(2)]
        base, hist, first, mask, at, amax, a0, s, sl = (ph.sb(n, [TT, NT]) for n in ("base", "hist", "first", "mask", "at", "amax", "a0", "s", "sl"))
        ends, put = ph.sb("ends", [TT, NT], I32), ph.sb("put", [TT, NT], I32)
        nodes = ph.sb("nodes", [TT, NT, 2])
        x_ps = ph.ps("x_ps", [P, 512])
        c_ps = ph.ps("c_ps", [P, 512])
        loaded, prep, gate, batches, saved = (ph.sem(n) for n in ("loaded", "prep", "gate", "batches", "saved"))
        landed = [ph.sem(f"landed{b}") for b in range(2)]
        index_in, values_out = ph.loop_sem("index_in"), ph.loop_sem("values_out")
        max_saved, max_got, put_ready, placed, pair_in, ends_ready = (ph.sem(n) for n in ("max_saved", "max_got", "put_ready", "placed", "pair_in", "ends_ready"))
        ends_of_parts = ph.sem("ends_of_parts")
        turned, line, back, carried, dv = (ph.sem(n) for n in ("turned", "line", "back", "carried", "dv"))
        exped, max_ready, ev_ready = ph.sem("exped"), ph.sem("max_ready"), ph.sem("ev_ready")
        block = ph.block()

        @block.sync
        def _(sp):
            sp.dma_start(ident[:, :], c_d["ident"]).then_inc(loaded, 16)
            sp.dma_start(meta[:, :, :], sorted_d.rearrange("(p j) c -> p j c", j=ET)).then_inc(loaded, 16)
            sp.dma_start(base[:, :], base_d[0:N].rearrange("(t p) -> p t", p=TT), allow_slow_non_contiguous=True).then_inc(loaded, 16)
            sp.dma_start(hist[:, :], hist_d[0:N].rearrange("(t p) -> p t", p=TT), allow_slow_non_contiguous=True).then_inc(loaded, 16)
            sp.dma_start(a0[:, :], a_d[1].rearrange("(t p) -> p t", p=TT), allow_slow_non_contiguous=True).then_inc(loaded, 16)
            sp.wait_ge(dv, 1)
            sp.dma_start(prev_d[1:1 + EP].rearrange("(p j) -> p j", j=ET), loc[:, :]).then_inc(saved, 16)
            sp.wait_ge(dv, 2)
            sp.dma_start(prev_d[0:1].rearrange("(a o) -> a o", a=1), cin[0:1, 0:1]).then_inc(saved, 16)
            for n in range(2):
                sp.dma_start(pair_d.rearrange("(p j) c -> p (j c)", j=ET)[:, n * ET:(n + 1) * ET], zero[:, :]).then_inc(saved, 16)
            sp.wait_ge(saved, 64)
            sp.dma_start(prev[:, :], prev_d[0:EP].rearrange("(p j) -> p j", j=ET)).then_inc(loaded, 16)
            sp.wait_ge(max_ready, 1)
            sp.dma_start(max_d.rearrange("(p j) -> p j", j=ET), mx[:, :]).then_inc(max_saved, 16)
            sp.wait_ge(placed, 16 * NT)
            sp.dma_start(pair[:, :, :], pair_d.rearrange("(p j) c -> p j c", j=ET)).then_inc(pair_in, 16)
            sp.wait_ge(ev_ready, 1)
            sp.dma_start(ev_d.rearrange("(p j) -> p j", j=ET), ev[:, :]).then_inc(pair_in, 16)
            sp.wait_ge(pair_in, 32)

        @block.gpsimd
        def _(pool):
            with pool.Fori(0, NEB // 2) as i:
                for b in range(2):
                    pool.wait_ge(index_in, i * 2 + (b + NOW))
                    pool.wait_ge(values_out, i * 2 + (b + OLD))
                    pool.sem_inc(gate, 1)
                    for j in range(EB):
                        nc.gpsimd.indirect_dma_start(gb[b][:, j:j + 1], None, a_d[0].rearrange("(n o) -> n o", o=1),
                                                     bass.IndirectOffsetOnAxis(ib[b][:, j:j + 1], 0)).then_inc(landed[b], 16)
            pool.wait_ge(max_saved, 16)
            pool.wait_ge(ends_ready, 1)
            for t in range(NT):
                nc.gpsimd.indirect_dma_start(amax[:, t:t + 1], None, max_d.rearrange("(n o) -> n o", o=1),
                                             bass.IndirectOffsetOnAxis(ends[:, t:t + 1], 0)).then_inc(max_got, 16)
            pool.wait_ge(put_ready, 1)
            pool.wait_ge(saved, 64)
            for t in range(NT):
                nc.gpsimd.indirect_dma_start(pair_d, bass.IndirectOffsetOnAxis(put[:, t:t + 1], 0), nodes[:, t, :], None,
                                             bounds_check=EP - 1, oob_is_err=False).then_inc(placed, 16)
            pool.wait_ge(placed, 16 * NT)

        @block.tensor
        def _(pe):
            pe.wait_ge(loaded, 80)
            for n in range(3):
                pe.wait_ge(ends_of_parts, n + 1)
                for k in range(2):
                    mm = nc.tensor.transpose(x_ps[0:1, k * P:(k + 1) * P], edge[:, k:k + 1], ident[:, :])
                mm.then_inc(turned, 1)
                pe.wait_ge(line, n + 1)
                nc.tensor.transpose(c_ps[:, 0:1], rows[0:1, n, 0:P], ident[0:1, 0:1]).then_inc(back, 1)

        @block.vector
        def _(dve):
            count = [0]

            def step(ins):
                count[0] += 1
                ins.then_inc(dv, 1)
                dve.wait_ge(dv, count[0])

            def join(n, op0, op1, start, change, end):
                nc.vector.tensor_copy(edge[:, 0:1], change[:, ET - 1:ET])
                nc.vector.tensor_copy(edge[:, 1:2], end[:, ET - 1:ET]).then_inc(ends_of_parts, 1)
                dve.wait_ge(turned, n + 1)
                step(nc.vector.tensor_copy(rowp[0:1, :, :], x_ps[0:1, 0:2 * P].rearrange("p (k c) -> p k c", k=2)))
                step(nc.vector.memset(rows[0:1, n, 0:1], start))
                nc.vector.tensor_tensor_scan(rows[0:1, n, 1:P + 1], rowp[0:1, 0, :], rowp[0:1, 1, :], start, op0, op1).then_inc(line, 1)
                dve.wait_ge(back, n + 1)
                step(nc.vector.tensor_copy(cin[:, n:n + 1], c_ps[:, 0:1]))

            dve.wait_ge(loaded, 80)
            nc.vector.memset(zero[:, :], 0.0)
            step(nc.vector.tensor_copy(loc[:, :], meta[:, :, 0]))
            step(nc.vector.memset(cin[:, :], -1.0))
            nc.vector.tensor_copy(idx[:, :], meta[:, :, 1]).then_inc(batches, 1)
            with dve.Fori(0, NEB // 2) as i:
                for b in range(2):
                    dve.wait_ge(landed[b], i * (16 * EB) + 16 * EB)
                    nc.vector.tensor_copy(a1[:, ds(i * (2 * EB) + b * EB, EB)], gb[b][:, :]).then_inc(values_out, 1)
            dve.wait_ge(values_out, NEB - 1 + NOW)
            dve.wait_ge(loaded, 96)
            step(nc.vector.tensor_tensor(same[:, :], meta[:, :, 0], prev[:, :], ALU.is_equal))
            step(nc.vector.tensor_scalar(pen[:, :], same[:, :], -FAR, FAR, ALU.mult, ALU.add))
            nc.vector.tensor_tensor_scan(acc[:, :], pen[:, :], pen[:, :], 0.0, ALU.add, ALU.bypass)
            nc.vector.tensor_tensor_scan(loc[:, :], pen[:, :], a1[:, :], FAR, ALU.add, ALU.max).then_inc(carried, 1)
            dve.wait_ge(carried, 1)
            join(0, ALU.add, ALU.max, FAR, acc, loc)
            nc.vector.scalar_tensor_tensor(mx[:, :], acc[:, :], cin[:, 0:1], loc[:, :], ALU.add, ALU.max).then_inc(max_ready, 1)
            step(nc.vector.tensor_scalar(mask[:, :], hist[:, :], 1.0, None, ALU.min))
            step(nc.vector.tensor_tensor(first[:, :], base[:, :], hist[:, :], ALU.add))
            nc.vector.tensor_scalar(ends[:, :], first[:, :], -1.0, 0.0, ALU.add, ALU.max).then_inc(ends_ready, 1)
            step(nc.vector.tensor_scalar(at[:, :], mask[:, :], -float(2 * EP), float(2 * EP), ALU.mult, ALU.add))
            step(nc.vector.tensor_tensor(put[:, :], at[:, :], base[:, :], ALU.add))
            dve.wait_ge(max_got, 16 * NT)
            step(nc.vector.tensor_tensor(s[:, :], amax[:, :], a0[:, :], ALU.add))
            step(nc.vector.tensor_scalar(sl[:, :], s[:, :], 0.01, None, ALU.mult))
            step(nc.vector.tensor_tensor(nodes[:, :, 1], s[:, :], sl[:, :], ALU.max))
            nc.vector.tensor_copy(nodes[:, :, 0], a0[:, :]).then_inc(put_ready, 1)
            dve.wait_ge(pair_in, 16)
            step(nc.vector.tensor_tensor_scan(acc[:, :], same[:, :], same[:, :], 1.0, ALU.mult, ALU.bypass))
            for n in range(2):
                step(nc.vector.tensor_copy(loc[:, :], pair[:, :, n]))
                step(nc.vector.tensor_tensor_scan(d[:, :], same[:, :], loc[:, :], 0.0, ALU.mult, ALU.add))
                join(n + 1, ALU.mult, ALU.add, 0.0, acc, d)
                step(nc.vector.scalar_tensor_tensor(fill[n][:, :], acc[:, :], cin[:, n + 1:n + 2], d[:, :], ALU.mult, ALU.add))
            step(nc.vector.tensor_tensor(v[:, :], fill[0][:, :], a1[:, :], ALU.add))
            step(nc.vector.tensor_scalar(vl[:, :], v[:, :], 0.01, None, ALU.mult))
            step(nc.vector.tensor_tensor(v[:, :], v[:, :], vl[:, :], ALU.max))
            step(nc.vector.tensor_tensor(dm[:, :], v[:, :], fill[1][:, :], ALU.subtract))
            nc.vector.tensor_scalar(dm[:, :], dm[:, :], 0.0, None, ALU.min).then_inc(exped, 1)

        @block.scalar
        def _(act):
            act.wait_ge(batches, 1)
            with act.Fori(0, NEB // 2) as i:
                for b in range(2):
                    act.wait_ge(values_out, i * 2 + (b + OLD))
                    nc.scalar.activation(ib[b][:, :], idx[:, ds(i * (2 * EB) + b * EB, EB)], ACT.Copy).then_inc(index_in, 1)
            act.wait_ge(exped, 1)
            nc.scalar.activation(ev[:, :], dm[:, :], ACT.Exp).then_inc(ev_ready, 1)


def network(nc, a, out_d, parts=None):
    parts = parts or {}

    def dram(name, shape):
        return parts.get(name) or nc.dram_tensor(name, shape, F32).ap()
    fm = [P, 2, N]
    c_d = {n: a[f"c_{n}"] for n in ("mean", "ident", "blocks1", "blocks2", "last_row", "tri", "pick", "before")}
    xn, xn_rows = dram("xn", fm), dram("xn_rows", [N, D])
    norm_table(nc, "norm0", a["x"], xn, xn_rows, c_d)
    orders = {}
    for name, key, other in (("dst", "dst", "src"), ("src", "src", "dst")):
        o = orders[name] = [dram(f"hist_{name}", [NODES]), dram(f"first_{name}", [NODES]), dram(f"sorted_{name}", [EP, 3])]
        sort_edges(nc, f"sort_{name}", a[key], a[other], a["edge_weight"], a["c_iota"], a["c_ident"], a["c_identb"], a["c_tri"], a["c_upper"], *o)

    hist, first, by_dst = orders["dst"]
    running, agg = nc.dram_tensor("running0", [EP, D], F32).ap(), dram("agg", fm)
    sum_edges(nc, "sum0", by_dst, None, xn_rows, running, D, c_d)
    node_rows(nc, "rows0", running, D, hist, first, agg, c_d)

    xs, qT = dram("mix0", fm), dram("qT0", fm)
    with Phase(nc, "copy") as ph:
        copied = ph.sem("copied")
        block = ph.block()

        @block.sync
        def _(sp):
            sp.dma_start(xs, xn).then_inc(copied, 16)
            sp.wait_ge(copied, 16)
    mixer = nc.alloc_sbuf_tensor("mixer", [P, 2, D], F32)
    with nc.Fori(0, 4) as layer:
        def of(name):
            w = a[f"L0_mix_{name}"][ds(layer, 1)]
            return w.rearrange("l p h c -> (l p) h c" if len(w.shape) == 4 else "l p h -> (l p) h")
        attend_first(nc, "attend0", 2, P, 32, 32 ** -0.25, xs, qT, mixer, c_d, of("ln1_g"), of("ln1_b"), of("Wq"), of("Wk"), of("Wv"), of("Wo"))
        attend_second(nc, "forward0", 2, P, xs, qT, mixer, xs, c_d, of("bo"), of("ln2_g"), of("ln2_b"), of("W1"), of("b1"), of("W2"), of("b2"))
    x1 = dram("x1", fm)
    g = {n: a[f"L0_gnn_{n}"] for n in ("eps_weight", "w1", "w2", "gamma1", "beta1", "gamma_h", "beta_h")}
    message_layer(nc, "message0", agg, a["x"], xn, xs, x1, dram("z", fm), dram("u", fm), hist, c_d, g["eps_weight"], g["w1"], g["w2"],
                  g["gamma1"], g["beta1"], g["gamma_h"], g["beta_h"])
    x2 = dram("x2", fm)
    experts(nc, "experts", x1, x2, c_d, *(a[f"L0_ffn_{n}"] for n in ("router_w", "w1", "b1", "w2", "b2")))

    hist, first, by_src = orders["src"]
    xn1, h_rows, scores = dram("xn1", fm), dram("h_rows", [N, D]), dram("scores", [2, N])
    norm_table(nc, "norm1", x2, xn1, h_rows, c_d, a["L1_gnn_W_layer"], a["L1_gnn_b_layer"], a["L1_gnn_w_a"], a["L1_gnn_b_a"], scores)
    ev, g1 = dram("ev", [EP]), dram("g1", fm)
    attention_weights(nc, "edges1", by_src, nc.dram_tensor("prev", [EP + 1], F32).ap(), scores, hist, first, nc.dram_tensor("maxs", [EP], F32).ap(),
                      nc.dram_tensor("pairs", [EP, 2], F32).ap(), ev, c_d)
    running = nc.dram_tensor("running1", [EP, D + 1], F32).ap()
    sum_edges(nc, "sum1", by_src, ev, h_rows, running, D + 1, c_d)
    node_rows(nc, "rows1", running, D + 1, hist, first, g1, c_d)

    m = {n[7:]: v for n, v in a.items() if n.startswith("L1_mix_")}
    qT1, x3 = dram("qT1", [32, 1, N]), dram("x3", fm)
    attend_first(nc, "attend1", 1, 32, 4, 1.0, xn1, qT1, mixer, c_d, m["ln1_g"], m["ln1_b"], m["Wq"], m["Wk"], m["Wv"], m["Wo"], m["Wx"], m["bx"])
    attend_second(nc, "forward1", 1, 32, xn1, qT1, mixer, x3, c_d, m["bo"], m["ln2_g"], m["ln2_b"], m["W1"], m["b1"], m["W2"], m["b2"], (x2, g1))
    t, row, factor = dram("t", fm), dram("row", [N]), dram("factor", [N])
    token_weights(nc, "tokens", x3, t, row, c_d, a["L1_ffn_wr"], a["L1_ffn_br"])
    choose_tokens(nc, "choose", row, factor, c_d)
    chosen_forward(nc, "chosen", t, x3, factor, out_d, *(a[f"L1_ffn_{n}"] for n in ("w1", "b1", "w2", "b2")))


def laid_out(inputs):
    x = {k: np.asarray(v) for k, v in inputs.items()}

    def wide(v):
        return v.reshape(*v.shape[:-2], -1, P, v.shape[-1]).swapaxes(-3, -2)

    def per_channel(v):
        return v.reshape(*v.shape[:-1], -1, P).swapaxes(-2, -1)

    def edges(v, pad):
        return np.concatenate([v, np.full(EP - E, pad, v.dtype)]).reshape(ET, P).T

    a = {"x": wide(x["x"].T), "edge_weight": edges(x["edge_weight"], 0)}
    a["src"], a["dst"] = edges(x["src"], N), edges(x["dst"], N)
    for n in ("w1", "w2"):
        a[f"L0_gnn_{n}"] = wide(x[f"L0_gnn_{n}"].T)
    for n in ("gamma1", "beta1", "gamma_h", "beta_h"):
        a[f"L0_gnn_{n}"] = per_channel(x[f"L0_gnn_{n}"])
    a["L0_gnn_eps_weight"] = x["L0_gnn_eps_weight"]
    for n in ("Wq", "Wk", "Wv", "Wo", "W1", "W2"):
        a[f"L0_mix_{n}"] = wide(x[f"L0_mix_{n}"])
    for n in ("bo", "ln1_g", "ln1_b", "b1", "b2", "ln2_g", "ln2_b"):
        a[f"L0_mix_{n}"] = per_channel(x[f"L0_mix_{n}"])
        a[f"L1_mix_{n}"] = per_channel(x[f"L1_mix_{n}"])
    a["L0_ffn_router_w"] = wide(x["L0_ffn_router_w"].T)
    for n in ("w1", "w2"):
        a[f"L0_ffn_{n}"] = wide(x[f"L0_ffn_{n}"]).transpose(1, 0, 2, 3)
    a["L0_ffn_b1"] = per_channel(x["L0_ffn_b1"]).transpose(1, 0, 2)
    a["L0_ffn_b2"] = x["L0_ffn_b2"]
    a["L1_gnn_W_layer"] = wide(x["L1_gnn_W_layer"].T)
    a["L1_gnn_b_layer"] = x["L1_gnn_b_layer"]
    a["L1_gnn_w_a"] = np.concatenate([x["L1_gnn_w_a2"], x["L1_gnn_w_a1"]])
    a["L1_gnn_b_a"] = np.concatenate([x["L1_gnn_b_a2"], x["L1_gnn_b_a1"]])
    for n in ("Wx", "Wo", "W1", "W2"):
        a[f"L1_mix_{n}"] = wide(x[f"L1_mix_{n}"])
    for n in ("Wq", "Wk", "Wv"):
        a[f"L1_mix_{n}"] = x[f"L1_mix_{n}"]
    a["L1_mix_bx"] = per_channel(x["L1_mix_bx"])
    a["L1_ffn_wr"] = per_channel(x["L1_ffn_wr"][:, 0])
    a["L1_ffn_br"] = x["L1_ffn_br"]
    for n in ("w1", "w2"):
        a[f"L1_ffn_{n}"] = wide(x[f"L1_ffn_{n}"])
    for n in ("b1", "b2"):
        a[f"L1_ffn_{n}"] = per_channel(x[f"L1_ffn_{n}"])
    p, q = np.arange(P)[:, None], np.arange(P)[None, :]
    f = np.float32
    head = (p // 32 == q // 32).astype(f)
    a["c_mean"] = np.full((P, P), 1 / D, f)
    a["c_ident"] = np.eye(P, dtype=f)
    a["c_identb"] = np.eye(P).astype(_mybir_bf16())
    a["c_iota"] = np.broadcast_to(q, (P, P)).astype(f)
    a["c_tri"], a["c_upper"] = (q < p).astype(f), (p < q).astype(f)
    a["c_blocks2"] = np.stack([head, head], 1)
    a["c_blocks1"] = (np.arange(32)[:, None] // 4 == np.arange(D)[None, :] // 32).astype(f)[:, None, :]
    a["c_last_row"] = (p == P - 1).astype(f)
    e8 = np.arange(8)
    a["c_pick"] = np.broadcast_to((e8[:, None] == e8[None, :])[:, :, None], (8, 8, P)).astype(f)
    a["c_before"] = np.broadcast_to((e8[None, :] < e8[:, None])[None], (TT, 8, 8)).astype(f)
    return {k: np.ascontiguousarray(v) for k, v in a.items()}


def _mybir_bf16():
    return mybir.dt.np(BF16)


def kernel(**inputs):
    import concourse.bacc as bacc
    from concourse.bass_utils import run_bass_kernel_spmd

    nc = bacc.Bacc("TRN2", target_bir_lowering=False, num_devices=1)
    arrays = {f"in_{k}": v for k, v in laid_out(inputs).items()}
    aps = {k[3:]: nc.dram_tensor(k, v.shape, mybir.dt.from_np(v.dtype), kind="ExternalInput").ap() for k, v in arrays.items()}
    out = nc.dram_tensor("out", [P, 2, N], F32, kind="ExternalOutput").ap()
    network(nc, aps, out)
    r = run_bass_kernel_spmd(nc, [arrays], core_ids=[0])
    return r.results[0]["out"].transpose(1, 0, 2).reshape(D, N).T
```

```python
from contextlib import ExitStack, contextmanager
import numpy as np
import concourse.bass as bass
from concourse import mybir

F32 = mybir.dt.float32
I32 = mybir.dt.int32
BF16 = mybir.dt.bfloat16
ALU = mybir.AluOpType
ACT = mybir.ActivationFunctionType
AX_X = mybir.AxisListType.X
ds = bass.ds
P = 128

N = 6250
D = 256
H2 = D // P
E = 100000
TT = 125
CW = 2 * TT
NCH = N // CW
NT = N // TT
ET = 784
EP = ET * P
EB = 14
NEB = ET // EB
HI = 49
NODES = HI * P


START, NOW, PREV, OLD = 2, 3, 2, 1

CR = 2


class Phase:

    def __init__(self, nc, name):
        self.nc, self.name, self.ctx, self.sems = nc, name, ExitStack(), []
        self.loops = []

    def __enter__(self):
        self.ctx.__enter__()
        return self

    def sb(self, name, shape, dt=F32):
        return self.ctx.enter_context(self.nc.sbuf_tensor(f"{self.name}_{name}", shape, dt))

    def ps(self, name, shape, dt=F32):
        return self.ctx.enter_context(self.nc.psum_tensor(f"{self.name}_{name}", shape, dt))

    def sem(self, name):
        s = self.nc.alloc_semaphore(f"{self.name}_{name}")
        self.sems.append(s)
        return s

    def loop_sem(self, name):
        s = self.sem(name)
        self.loops.append(s)
        return s

    def block(self):
        for s in self.loops:
            self.nc.sync.sem_inc(s, START)
        self.nc.all_engine_barrier()
        return self.ctx.enter_context(self.nc.Block())

    def __exit__(self, *exc):
        self.ctx.__exit__(*exc)
        if exc[0] is None and self.sems:
            self.nc.clear_and_free_semaphores(self.sems)
            self.nc.all_engine_barrier()


MB = 4


def sort_edges(nc, name, keys, weights, orders, c_d):
    S = range(2)
    with Phase(nc, name) as ph:
        kin = [ph.sb(f"kin{s}", [P, ET], I32) for s in S]
        hi_i, lo_i = ([ph.sb(f"{n}{s}", [P, ET], I32) for s in S] for n in ("hi_i", "lo_i"))
        meta = [ph.sb(f"meta{s}", [P, ET + EB, 3]) for s in S]
        lo, hi = ([ph.sb(f"{n}{s}", [P, ET + EB], BF16) for s in S] for n in ("lo", "hi"))
        iota_f, iota_t, id_t, idb_t = ph.sb("iota_f", [P, P]), ph.sb("iota", [P, P], BF16), ph.sb("ident", [P, P]), ph.sb("identb", [P, P], BF16)
        tri_t, upper_t = ph.sb("tri", [P, P]), ph.sb("upper", [P, P])
        onelo = [ph.sb(f"onelo{s}", [P, 2, EB, P], BF16) for s in S]
        onehi = [ph.sb(f"onehi{s}", [P, 2, EB, HI], BF16) for s in S]
        hist, scan, base, part = ([ph.sb(f"{n}{s}", [HI, P]) for s in S] for n in ("hist", "scan", "base", "part"))
        zero = ph.sb("zero", [P, P], BF16)
        mb = [[ph.sb(f"mb{s}_{k}", [P, EB, 3]) for k in range(MB)] for s in S]
        place = [[ph.sb(f"place{s}_{k}", [P, EB], I32) for k in range(MB)] for s in S]
        rank_in, rank_at = ([ph.sb(f"{n}{s}", [P, MB, EB]) for s in S] for n in ("rank_in", "rank_at"))
        hiT, hsnap = ([[ph.sb(f"{n}{s}_{q}", [HI, P]) for q in range(2)] for s in S] for n in ("hiT", "hsnap"))
        hist_ps, krow_ps, look_ps = ([ph.ps(f"{n}{s}", [P, 512]) for s in S] for n in ("hist_ps", "krow_ps", "look_ps"))
        hiT_ps = [ph.ps(f"hiT_ps{s}", [P, 1024], BF16) for s in S]
        hist_acc = [hist_ps[s][0:HI, 0:P] for s in S]
        rows_ps = [look_ps[s][0:HI, 256:257] for s in S]
        pair = lambda n: [ph.sem(f"{n}{s}") for s in S]
        loaded, zeroed, saved, gate = ph.sem("loaded"), ph.sem("zeroed"), ph.sem("saved"), ph.sem("gate")
        prep, onehot, counted, rows_before, base_ready = (pair(n) for n in ("prep", "onehot", "counted", "rows_before", "base_ready"))
        onehot2, krow, hi_turned, hi_copied, snapped, looked, added = (pair(n) for n in (
            "onehot2", "krow", "hi_turned", "hi_copied", "snapped", "looked", "added"))
        ranked_in, ranked_at, meta_b, placed, left = (pair(n) for n in ("ranked_in", "ranked_at", "meta_b", "placed", "left"))
        scattered = [[ph.sem(f"scattered{s}_{k}") for k in range(MB)] for s in S]
        block = ph.block()

        def tiles(eng, step):
            with eng.Fori(0, NEB // MB) as i:
                for k in range(MB):
                    for j in range(EB):
                        for s in S:
                            step(s, i * (MB * EB) + (k * EB + j), i * MB + k, k, j)

        @block.sync
        def _(sp):
            loads = [(kin[0], keys[0]), (kin[1], keys[1]), (iota_f, c_d["iota"]), (id_t, c_d["ident"]), (idb_t, c_d["identb"]), (tri_t, c_d["tri"]),
                     (upper_t, c_d["upper"])]
            for dst, src in loads:
                sp.dma_start(dst[:, :], src).then_inc(loaded, 16)
            for s in S:
                sp.dma_start(meta[s][:, 0:ET, 2], weights, allow_slow_non_contiguous=True).then_inc(loaded, 16)
            for s in S:
                hist_d, base_d, _ = orders[s]
                sp.wait_ge(base_ready[s], 4)
                sp.dma_start(hist_d.rearrange("(h l) -> h l", l=P), hist[s][:, :]).then_inc(saved, 16)
                sp.dma_start(base_d.rearrange("(h l) -> h l", l=P), base[s][:, :]).then_inc(saved, 16)
            sp.wait_ge(saved, 64)

        @block.vector
        def _(dve):
            nc.vector.memset(zero[:, :], 0.0).then_inc(zeroed, 1)
            for s in S:
                nc.vector.memset(meta[s][:, ET:ET + EB, :], 0.0).then_inc(zeroed, 1)
                nc.vector.memset(lo[s][:, ET:ET + EB], 0.0).then_inc(zeroed, 1)
                nc.vector.memset(hi[s][:, ET:ET + EB], 0.0).then_inc(zeroed, 1)
            dve.wait_ge(zeroed, 7)
            dve.wait_ge(loaded, 9 * 16)
            for s in S:
                nc.vector.tensor_scalar(hi_i[s][:, :], kin[s][:, :], 7, None, ALU.logical_shift_right).then_inc(prep[s], 1)
                nc.vector.tensor_scalar(lo_i[s][:, :], kin[s][:, :], P - 1, None, ALU.bitwise_and).then_inc(prep[s], 1)
                nc.vector.tensor_copy(meta[s][:, 0:ET, 0], kin[s][:, :]).then_inc(prep[s], 1)
                nc.vector.tensor_scalar(meta[s][:, 0:ET, 1], kin[1 - s][:, :], float(N - 1), None, ALU.min).then_inc(prep[s], 1)
            nc.vector.tensor_copy(iota_t[:, :], iota_f[:, :]).then_inc(zeroed, 1)
            dve.wait_ge(zeroed, 8)
            for s in S:
                dve.wait_ge(prep[s], 4)
                nc.vector.tensor_copy(hi[s][:, 0:ET], hi_i[s][:, :]).then_inc(prep[s], 1)
                nc.vector.tensor_copy(lo[s][:, 0:ET], lo_i[s][:, :]).then_inc(prep[s], 1)
            for s in S:
                dve.wait_ge(prep[s], 6)

            def one_hots(s, t0, b, done):
                nc.vector.tensor_tensor(
                    onelo[s][:, b, :, :], lo[s][:, ds(t0, EB)].unsqueeze(2).to_broadcast([P, EB, P]),
                    iota_t[:, None, :].to_broadcast([P, EB, P]), ALU.is_equal).then_inc(done, 1)
                nc.vector.tensor_tensor(
                    onehi[s][:, b, :, :], hi[s][:, ds(t0, EB)].unsqueeze(2).to_broadcast([P, EB, HI]),
                    iota_t[:, None, 0:HI].to_broadcast([P, EB, HI]), ALU.is_equal).then_inc(done, 1)

            with dve.Fori(0, NEB // 2) as i:
                for b in range(2):
                    for s in S:
                        dve.wait_ge(counted[s], i * 2 + (b + 1))
                        one_hots(s, i * (2 * EB) + b * EB, b, onehot[s])
            for s in S:
                dve.wait_ge(counted[s], CR + NEB)
                nc.vector.tensor_copy(hist[s][:, :], hist_acc[s]).then_inc(base_ready[s], 1)
                dve.wait_ge(base_ready[s], 1)
                nc.vector.tensor_tensor_scan(scan[s][:, :], hist[s][:, :], hist[s][:, :], 0.0, ALU.add, ALU.bypass).then_inc(base_ready[s], 1)
                dve.wait_ge(base_ready[s], 2)
                nc.vector.tensor_tensor(part[s][:, :], scan[s][:, :], hist[s][:, :], ALU.subtract).then_inc(base_ready[s], 1)
                dve.wait_ge(base_ready[s], 3)
                dve.wait_ge(rows_before[s], 1)
                nc.vector.tensor_scalar(base[s][:, :], part[s][:, :], rows_ps[s], None, ALU.add).then_inc(base_ready[s], 1)

            def ahead(s, t0, b, k):
                one_hots(s, t0, b, onehot2[s])
                nc.vector.tensor_copy(mb[s][k][:, :, :], meta[s][:, ds(t0, EB), :]).then_inc(meta_b[s], 1)

            def rank_inside(s, n, k, j):
                dve.wait_ge(krow[s], n)
                nc.vector.scalar_tensor_tensor(
                    krow_ps[s][:, 0:P], krow_ps[s][:, 0:P], mb[s][k][:, j, 0:1], tri_t[:, :], ALU.is_equal, ALU.mult,
                    accum_out=rank_in[s][:, k, j:j + 1]).then_inc(ranked_in[s], 1)

            for s in S:
                ahead(s, 0, 0, 0)
                dve.wait_ge(meta_b[s], 1)
                rank_inside(s, 1, 0, 0)

            def step(s, n, B, k, j):
                if j == 2:
                    dve.wait_ge(added[s], B * EB + 1)
                    dve.wait_ge(ranked_at[s], B * EB + 1)
                    dve.wait_ge(left[s], B + 2)
                    ahead(s, B * EB + EB, (k + 1) % 2, (k + 1) % MB)
                j1, k1 = (j + 1, k) if j + 1 < EB else (0, (k + 1) % MB)
                if j1 == 0:
                    dve.wait_ge(meta_b[s], B + 2)
                rank_inside(s, n + 2, k1, j1)
                dve.wait_ge(looked[s], n + 3)
                nc.vector.tensor_tensor_reduce(
                    look_ps[s][:, 0:P], look_ps[s][:, 0:P], onelo[s][:, k % 2, j, :], 1.0, 0.0, ALU.mult, ALU.add,
                    rank_at[s][:, k, j:j + 1]).then_inc(ranked_at[s], 1)
                if j == EB - 1:
                    dve.wait_ge(ranked_in[s], n + 1)
                    dve.wait_ge(ranked_at[s], n + 2)
                    nc.vector.tensor_tensor(place[s][k][:, :], rank_in[s][:, k, :], rank_at[s][:, k, :], ALU.add).then_inc(placed[s], 1)
            tiles(dve, step)

        @block.tensor
        def _(pe):
            pe.wait_ge(zeroed, 1)
            for s in S:
                nc.tensor.matmul(hist_acc[s], zero[:, 0:HI], zero[:, :], start=True, stop=False, skip_group_check=True)
                pe.sem_inc(counted[s], CR)
            with pe.Fori(0, NEB // 2) as i:
                for b in range(2):
                    for s in S:
                        pe.wait_ge(onehot[s], i * 4 + (b * 2 + 2))
                        for j in range(EB):
                            mm = nc.tensor.matmul(hist_acc[s], onehi[s][:, b, j, :], onelo[s][:, b, j, :], start=False, stop=False,
                                                  skip_group_check=True)
                        mm.then_inc(counted[s], 1)
            for s in S:
                pe.wait_ge(base_ready[s], 2)
                nc.tensor.matmul(rows_ps[s], upper_t[0:HI, 0:HI], scan[s][:, P - 1:P], start=True, stop=True).then_inc(rows_before[s], 1)
            for s in S:
                pe.wait_ge(base_ready[s], 4)
                nc.tensor.matmul(hist_acc[s], id_t[0:HI, 0:HI], base[s][:, :], start=True, stop=False, skip_group_check=True).then_inc(added[s], 1)
                pe.sem_inc(looked[s], CR)
                pe.sem_inc(ranked_at[s], 1)

            def turn(s, k, j):
                nc.tensor.transpose(krow_ps[s][:, 0:P], mb[s][k][:, j, 0:1].to_broadcast([P, P]), id_t[:, :]).then_inc(krow[s], 1)
                nc.tensor.transpose(hiT_ps[s][0:HI, 0:P], onehi[s][:, k % 2, j, :], idb_t[:, :]).then_inc(hi_turned[s], 1)

            for s in S:
                pe.wait_ge(onehot2[s], 2)
                pe.wait_ge(meta_b[s], 1)
                turn(s, 0, 0)

            def step(s, n, B, k, j):
                j1, k1 = (j + 1, k) if j + 1 < EB else (0, (k + 1) % MB)
                if j1 == 0:
                    pe.wait_ge(onehot2[s], B * 2 + 4)
                    pe.wait_ge(meta_b[s], B + 2)
                pe.wait_ge(ranked_in[s], n + 1)
                pe.wait_ge(hi_copied[s], n + 1)
                turn(s, k1, j1)
                pe.wait_ge(snapped[s], n + 1)
                pe.wait_ge(ranked_at[s], n + 1)
                nc.tensor.matmul(look_ps[s][:, 0:P], hiT[s][j % 2][:, :], hsnap[s][j % 2][:, :], start=True, stop=True).then_inc(looked[s], 1)
                nc.tensor.matmul(hist_acc[s], onehi[s][:, k % 2, j, :], onelo[s][:, k % 2, j, :], start=False, stop=False,
                                 skip_group_check=True).then_inc(added[s], 1)
            tiles(pe, step)

        @block.scalar
        def _(act):
            def copy_high(s, n, q):
                act.wait_ge(hi_turned[s], n)
                act.wait_ge(looked[s], n)
                nc.scalar.activation(hiT[s][q][:, :], hiT_ps[s][0:HI, 0:P], ACT.Copy).then_inc(hi_copied[s], 1)
            for s in S:
                copy_high(s, 1, 0)

            def step(s, n, B, k, j):
                act.wait_ge(looked[s], n + 1)
                act.wait_ge(added[s], n + 1)
                nc.scalar.activation(hsnap[s][j % 2][:, :], hist_acc[s], ACT.Copy).then_inc(snapped[s], 1)
                copy_high(s, n + 2, (j + 1) % 2)
            tiles(act, step)

        @block.gpsimd
        def _(pool):
            for s in S:
                pool.sem_inc(left[s], MB)
            with pool.Fori(0, NEB // MB) as i:
                for k in range(MB):
                    for s in S:
                        pool.wait_ge(placed[s], i * MB + (k + 1))
                        pool.sem_inc(gate, 1)
                        for j in range(EB):
                            nc.gpsimd.indirect_dma_start(
                                orders[s][2], bass.IndirectOffsetOnAxis(place[s][k][:, j:j + 1], 0), mb[s][k][:, j, :], None).then_inc(scattered[s][k], 16)
                    for s in S:
                        for kk in ([], [0], [1], [2, 3])[k]:
                            pool.wait_ge(scattered[s][kk], i * (16 * EB) + 16 * EB)
                            pool.sem_inc(left[s], 1)


def chunks(eng, body, ahead=1):
    pairs = (NCH - ahead) // 2
    with eng.Fori(0, pairs) as i:
        for b in range(2):
            body(i * 2 + b, b, i, True)
    for c in range(2 * pairs, NCH):
        body(c, c % 2, c // 2, c + ahead < NCH)


def chunks_behind(eng, body, behind):
    def second(c, b, r):
        return lambda n: behind(c, b, r, n)
    body(0, 0, 0, True, lambda n: None)
    with eng.Fori(0, (NCH - 3) // 2) as i:
        body(i * 2 + 1, 1, i, True, second(i * 2, 0, i))
        body(i * 2 + 2, 0, i + 1, True, second(i * 2 + 1, 1, i))
    body(NCH - 2, 1, (NCH - 3) // 2, True, second(NCH - 3, 0, (NCH - 3) // 2))
    body(NCH - 1, 0, NCH // 2, False, second(NCH - 2, 1, (NCH - 3) // 2))
    for n in range(3):
        behind(NCH - 1, 0, NCH // 2, n)


class Norm:

    def __init__(self, nc, ph, x, ones, used, gain=None, offset=None, eps=1e-5):
        self.nc, self.x, self.ones, self.eps, self.gain, self.offset, self.used = nc, x, ones, eps, gain, offset, used
        self.stat = [ph.ps(f"stat{b}", [P, 512]) for b in range(2)]
        self.cen = [ph.sb(f"cen{b}", [P, 2, CW]) for b in range(2)]
        self.sq = [ph.sb(f"sq{b}", [P, 2, CW]) for b in range(2)]
        self.dev = [ph.sb(f"dev{b}", [P, CW]) for b in range(2)]
        self.rstd = [ph.sb(f"rstd{b}", [P, CW]) for b in range(2)]
        self.eps_t = ph.sb("eps", [P, 1])
        self.nrm = [ph.sb(f"nrm{b}", [P, 2, CW]) for b in range(2)]
        self.out = self.nrm if gain is None else [ph.sb(f"out{b}", [P, 2, CW]) for b in range(2)]
        self.mean_ready, self.centred, self.squared, self.var_ready, self.rooted, self.inverted, self.normed, self.affine = (
            ph.loop_sem(n) for n in ("mean_ready", "centred", "squared", "var_ready", "rooted", "inverted", "normed", "affine"))
        self.eps_ready = ph.sem("eps_ready")
        self.ready = self.normed if gain is None else self.affine

    def pe_mean(self, pe, n, b):
        pe.wait_ge(self.centred, n + OLD)
        for h in range(2):
            mm = self.nc.tensor.matmul(self.stat[b][:, 0:CW], self.ones[:, :], self.x[b][:, h, :], start=(h == 0), stop=(h == 1))
        mm.then_inc(self.mean_ready, 1)

    def dve_centre(self, dve, n, b):
        dve.wait_ge(self.mean_ready, n + NOW)
        dve.wait_ge(self.squared, n + OLD)
        dve.wait_ge(self.normed, n + OLD)
        self.nc.vector.tensor_tensor(self.cen[b][:, :, :], self.x[b][:, :, :],
                                     self.stat[b][:, None, 0:CW].to_broadcast([P, 2, CW]), ALU.subtract).then_inc(self.centred, 1)

    def act_square(self, act, n, b):
        act.wait_ge(self.centred, n + NOW)
        act.wait_ge(self.var_ready, n + OLD)
        self.nc.scalar.activation(self.sq[b][:, :, :], self.cen[b][:, :, :], ACT.Square).then_inc(self.squared, 1)

    def pe_var(self, pe, n, b):
        pe.wait_ge(self.squared, n + NOW)
        pe.wait_ge(self.rooted, n + OLD)
        for h in range(2):
            mm = self.nc.tensor.matmul(self.stat[b][:, CW:2 * CW], self.ones[:, :], self.sq[b][:, h, :], start=(h == 0), stop=(h == 1))
        mm.then_inc(self.var_ready, 1)

    def dve_start(self, dve):
        self.nc.vector.memset(self.eps_t[:, :], self.eps).then_inc(self.eps_ready, 1)

    def act_root(self, act, n, b):
        if isinstance(n, int) and n == 0:
            act.wait_ge(self.eps_ready, 1)
        act.wait_ge(self.var_ready, n + NOW)
        act.wait_ge(self.inverted, n + OLD)
        self.nc.scalar.activation(self.dev[b][:, :], self.stat[b][:, CW:2 * CW], ACT.Sqrt, bias=self.eps_t[:, 0:1]).then_inc(self.rooted, 1)

    def dve_norm(self, dve, n, b):
        dve.wait_ge(self.rooted, n + NOW)
        dve.wait_ge(self.normed, n + OLD)
        self.nc.vector.reciprocal(self.rstd[b][:, :], self.dev[b][:, :]).then_inc(self.inverted, 1)
        dve.wait_ge(self.inverted, n + NOW)
        for s in [self.affine] if self.gain is not None else self.used:
            dve.wait_ge(s, n + OLD)
        self.nc.vector.tensor_tensor(self.nrm[b][:, :, :], self.cen[b][:, :, :],
                                     self.rstd[b][:, None, :].to_broadcast([P, 2, CW]), ALU.mult).then_inc(self.normed, 1)

    def act_affine(self, act, n, b):
        act.wait_ge(self.normed, n + NOW)
        for s in self.used:
            act.wait_ge(s, n + OLD)
        for h in range(2):
            last = self.nc.scalar.activation(self.out[b][:, h, :], self.nrm[b][:, h, :], ACT.Identity,
                                             bias=self.offset[:, h:h + 1], scale=self.gain[:, h:h + 1])
        last.then_inc(self.affine, 1)


def attend_first(nc, name, KH, KP, R, scale, x_d, qT_d, mixer, c_d, gain_d, offset_d, wq_d, wk_d, wv_d, wo_d, wx_d=None, bx_d=None):
    EW = D // KH
    QW = KH * KP
    NQ = QW // R
    proj = wx_d is not None
    with Phase(nc, name) as ph:
        x = [ph.sb(f"x{b}", [P, 2, CW]) for b in range(2)]
        ones, ident = ph.sb("ones", [P, P]), ph.sb("ident", [P, P])
        blocks = ph.sb("blocks", [KP, KH, EW])
        gain, offset = ph.sb("gain", [P, 2]), ph.sb("offset", [P, 2])
        wq, wk, wv, wo = ph.sb("wq", [P, 2, QW]), ph.sb("wk", [P, 2, QW]), ph.sb("wv", [P, 2, D]), ph.sb("wo", [P, 2, D])
        if proj:
            wx, bx = ph.sb("wx", [P, 2, D]), ph.sb("bx", [P, 2])
            xm = [ph.sb(f"xm{b}", [P, 2, CW]) for b in range(2)]
        ek = [ph.sb(f"ek{b}", [KP, KH, CW]) for b in range(2)]
        ekT = [ph.sb(f"ekT{b}", [TT, 2, QW]) for b in range(2)]
        v = [ph.sb(f"v{b}", [TT, 2, D]) for b in range(2)]
        kmax, run, nbias, fade, ksum = ([ph.sb(f"{n}{b}", [KP, KH]) for b in range(2)] for n in ("kmax", "run", "nbias", "fade", "ksum"))
        total, rtotal = ph.sb("total", [KP, KH]), ph.sb("rtotal", [KP, KH])
        ctxt, ctxn = ph.sb("context", [KP, KH, EW]), ph.sb("contextn", [KP, KH, EW])
        ctxT = ph.sb("contextT", [P, 2, KP])
        qmax, qsum, qrec = ([ph.sb(f"{n}{b}", [TT, 2 * NQ]) for b in range(2)] for n in ("qmax", "qsum", "qrec"))
        qs, qe, qn = ([ph.sb(f"{n}{b}", [TT, 2 * NQ, R]) for b in range(2)] for n in ("qs", "qe", "qn"))
        qT = [ph.sb(f"qT{b}", [KP, KH, CW]) for b in range(2)]
        k_ps, q_ps, v_ps, ekT_ps, qT_ps, ctx_ps = (ph.ps(n, [P, 512]) for n in ("k_ps", "q_ps", "v_ps", "ekT_ps", "qT_ps", "ctx_ps"))
        kps = k_ps[0:KP, 0:KH * CW].rearrange("p (h c) -> p h c", h=KH)
        if proj:
            ekps = qT_ps[0:TT, 256:256 + 2 * QW].rearrange("p (t c) -> p t c", t=2)
            xm_ps = ekT_ps[:, 0:2 * CW].rearrange("p (h c) -> p h c", h=2)
        else:
            ekps = ekT_ps[0:TT, 0:2 * QW].rearrange("p (t c) -> p t c", t=2)
        qps = q_ps[0:TT, 0:2 * QW].rearrange("p (g r) -> p g r", r=R)
        vps = v_ps[0:TT, 0:2 * D].rearrange("p (t c) -> p t c", t=2)
        qTps = qT_ps[0:KP, 0:KH * CW].rearrange("p (h c) -> p h c", h=KH)
        cps = ctx_ps[0:KP, 0:KH * EW].rearrange("p (h e) -> p h e", h=KH)
        weights = ph.sem("weights")
        x_loaded = [ph.sem(f"x_loaded{b}") for b in range(2)]
        q_saved = [ph.sem(f"q_saved{b}") for b in range(2)]
        (xm_made, xm_copied, k_made, v_made, q_made, ekT_made, ctx_made, qT_made, k_maxed, k_run, k_bias, q_maxed, q_less, q_exp,
         q_summed, q_rec, q_normed, k_exp, faded, v_copied, ekT_copied, qT_copied, ctx_added, total_added) = (ph.loop_sem(n) for n in (
             "xm_made", "xm_copied", "k_made", "v_made", "q_made", "ekT_made", "ctx_made", "qT_made", "k_maxed", "k_run", "k_bias",
             "q_maxed", "q_less", "q_exp", "q_summed", "q_rec", "q_normed", "k_exp", "faded", "v_copied", "ekT_copied", "qT_copied",
             "ctx_added", "total_added"))
        started, ended, turned, turned_copied, mixed, kept = (ph.sem(n) for n in ("started", "ended", "turned", "turned_copied", "mixed", "kept"))
        ln = Norm(nc, ph, x, ones, [xm_made] if proj else [q_made], gain, offset)
        loads = [(ones, c_d["mean"]), (ident, c_d["ident"]), (blocks, c_d[f"blocks{KH}"]), (gain, gain_d), (offset, offset_d),
                 (wo, wo_d)] + ([(wx, wx_d), (bx, bx_d)] if proj else [(wq, wq_d), (wk, wk_d), (wv, wv_d)])
        by_head, keys_gate = ph.sem("by_head"), ph.sem("keys_gate")
        if proj:
            for w, w_d in ((wq, wq_d), (wk, wk_d), (wv, wv_d)):
                rows, cols = w_d.shape
                for n in range(D // rows):
                    p0 = n * rows % P
                    loads.append((w[p0:p0 + rows, n * rows // P, n * cols:(n + 1) * cols], w_d))
        block = ph.block()

        @block.sync
        def _(sp):
            for b in range(2):
                sp.sem_inc(q_saved[b], 16)
            if proj:
                sp.wait_ge(by_head, 3)
            for dst, src in loads:
                sp.dma_start(dst[:], src).then_inc(weights, 16)
            for b in range(2):
                sp.dma_start(x[b][:, :, :], x_d[:, :, b * CW:(b + 1) * CW]).then_inc(x_loaded[b], 16)

            def body(c, b, r, more, behind):
                if not isinstance(c, int) or c + 2 < NCH:
                    sp.wait_ge(ln.centred, c + NOW)
                    sp.dma_start(x[b][:, :, :], x_d[:, :, ds((c + 2) * CW, CW)]).then_inc(x_loaded[b], 16)
                behind(0)

            def save(c, b, r, n):
                if n == 0:
                    sp.wait_ge(qT_copied, c + NOW)
                    sp.dma_start(qT_d[:, :, ds(c * CW, CW)], qT[b][:, :, :]).then_inc(q_saved[b], 16)
            chunks_behind(sp, body, save)
            for b in range(2):
                sp.wait_ge(q_saved[b], 16 * ((NCH + 1 - b) // 2) + 16)

        @block.tensor
        def _(pe):
            pe.wait_ge(weights, 16 * len(loads))
            pe.wait_ge(x_loaded[0], 16)
            ln.pe_mean(pe, 0, 0)
            ln.pe_var(pe, 0, 0)

            def body(c, b, r, more, behind):
                src = xm[b] if proj else ln.out[b]
                if more:
                    pe.wait_ge(x_loaded[1 - b], r * 16 + (b * 16 + 16))
                    ln.pe_mean(pe, c + 1, 1 - b)
                pe.wait_ge(ln.affine, c + NOW)
                if proj:
                    pe.wait_ge(xm_copied, c + PREV)
                    for h in range(2):
                        for k in range(2):
                            mm = nc.tensor.matmul(xm_ps[:, h, :], wx[:, k, h * P:(h + 1) * P], ln.out[b][:, k, :], start=(k == 0), stop=(k == 1))
                    mm.then_inc(xm_made, 1)
                behind(0)
                if proj:
                    pe.wait_ge(xm_copied, c + NOW)
                pe.wait_ge(k_exp, c + PREV)
                for h in range(KH):
                    for k in range(2):
                        mm = nc.tensor.matmul(kps[:, h, :], wk[:, k, h * KP:(h + 1) * KP], src[:, k, :], start=(k == 0), stop=(k == 1))
                mm.then_inc(k_made, 1)
                pe.wait_ge(v_copied, c + PREV)
                for t in range(2):
                    for k in range(2):
                        mm = nc.tensor.matmul(vps[:, t, :], src[:, k, t * TT:(t + 1) * TT], wv[:, k, :], start=(k == 0), stop=(k == 1))
                mm.then_inc(v_made, 1)
                if more:
                    ln.pe_var(pe, c + 1, 1 - b)
                behind(1)
                pe.wait_ge(q_less, c + PREV)
                for t in range(2):
                    for k in range(2):
                        mm = nc.tensor.matmul(q_ps[0:TT, t * QW:(t + 1) * QW], src[:, k, t * TT:(t + 1) * TT], wq[:, k, :],
                                              start=(k == 0), stop=(k == 1))
                mm.then_inc(q_made, 1)
                behind(2)

            def context_part(c, b, r, n):
                if n == 0:
                    pe.wait_ge(ekT_copied, c + PREV)
                    if proj:
                        pe.wait_ge(qT_copied, c + PREV)
                    pe.wait_ge(k_exp, c + NOW)
                    pe.sem_inc(keys_gate, 1)
                    for t in range(2):
                        for h in range(KH):
                            mm = nc.tensor.transpose(ekps[:, t, h * KP:(h + 1) * KP], ek[b][:, h, t * TT:(t + 1) * TT], ident[0:KP, 0:KP])
                    mm.then_inc(ekT_made, 1)
                if n == 1:
                    pe.wait_ge(ekT_copied, c + NOW)
                    pe.wait_ge(v_copied, c + NOW)
                    pe.wait_ge(ctx_added, c + PREV)
                    for h in range(KH):
                        for t in range(2):
                            mm = nc.tensor.matmul(cps[:, h, :], ekT[b][:, t, h * KP:(h + 1) * KP], v[b][:, t, h * EW:(h + 1) * EW],
                                                  start=(t == 0), stop=(t == 1))
                    mm.then_inc(ctx_made, 1)
                if n == 2:
                    pe.wait_ge(q_normed, c + NOW)
                    pe.wait_ge(qT_copied, c + PREV)
                    for t in range(2):
                        for h in range(KH):
                            mm = nc.tensor.transpose(qTps[:, h, t * TT:(t + 1) * TT],
                                                     qn[b][:, t * NQ:(t + 1) * NQ, :].rearrange("p g r -> p (g r)")[:, h * KP:(h + 1) * KP],
                                                     ident[0:TT, 0:TT])
                    mm.then_inc(qT_made, 1)
            chunks_behind(pe, body, context_part)
            pe.wait_ge(ended, 3)
            for h in range(2):
                src = ctxn[:, h, :] if KH == 2 else ctxn[:, 0, h * P:(h + 1) * P]
                mm = nc.tensor.transpose(q_ps[:, h * P:h * P + KP], src, ident[0:KP, 0:KP])
            mm.then_inc(turned, 1)
            pe.wait_ge(turned_copied, 1)
            for h in range(2):
                mm = nc.tensor.matmul(v_ps[0:KP, h * D:(h + 1) * D] if KH == 2 else v_ps[0:KP, 0:D], ctxT[:, h, :], wo[:, h, :],
                                      start=(KH == 2 or h == 0), stop=(KH == 2 or h == 1))
            mm.then_inc(mixed, 1)

        @block.scalar
        def _(act):
            act.wait_ge(weights, 16 * len(loads))
            ln.act_square(act, 0, 0)
            ln.act_root(act, 0, 0)
            ln.act_affine(act, 0, 0)

            def body(c, b, r, more, behind):
                if proj:
                    act.wait_ge(xm_made, c + NOW)
                    act.wait_ge(q_made, c + OLD)
                    for h in range(2):
                        last = nc.scalar.activation(xm[b][:, h, :], xm_ps[:, h, :], ACT.Identity, bias=bx[:, h:h + 1])
                    last.then_inc(xm_copied, 1)
                if more:
                    ln.act_square(act, c + 1, 1 - b)
                behind(0)
                act.wait_ge(v_made, c + NOW)
                act.wait_ge(ctx_made, c + OLD)
                nc.scalar.activation(v[b][:, :, :], vps, ACT.Copy).then_inc(v_copied, 1)
                if more:
                    ln.act_root(act, c + 1, 1 - b)
                act.wait_ge(k_bias, c + NOW)
                act.wait_ge(ekT_made, c + OLD)
                act.wait_ge(total_added, c + OLD)
                for h in range(KH):
                    last = nc.scalar.activation(ek[b][:, h, :], kps[:, h, :], ACT.Exp, bias=nbias[b][:, h:h + 1], scale=scale,
                                                accum_out=ksum[b][:, h:h + 1])
                last.then_inc(k_exp, 1)
                act.wait_ge(ctx_added, c + OLD)
                for h in range(KH):
                    last = nc.scalar.activation(fade[b][:, h:h + 1], run[1 - b][:, h:h + 1], ACT.Exp, bias=nbias[b][:, h:h + 1], scale=scale)
                last.then_inc(faded, 1)
                if more:
                    ln.act_affine(act, c + 1, 1 - b)
                act.wait_ge(q_less, c + NOW)
                act.wait_ge(q_normed, c + OLD)
                nc.scalar.activation(qe[b][:], qs[b][:], ACT.Exp, scale=scale).then_inc(q_exp, 1)
                behind(1)

            def context_part(c, b, r, n):
                if n == 0:
                    act.wait_ge(ekT_made, c + NOW)
                    act.wait_ge(ctx_made, c + OLD)
                    nc.scalar.activation(ekT[b][:, :, :], ekps, ACT.Copy).then_inc(ekT_copied, 1)
                if n == 1:
                    act.wait_ge(qT_made, c + NOW)
                    act.wait_ge(q_saved[b], r * 16 + 16)
                    nc.scalar.activation(qT[b][:, :, :], qTps, ACT.Copy).then_inc(qT_copied, 1)
            chunks_behind(act, body, context_part)
            act.wait_ge(turned, 1)
            nc.scalar.activation(ctxT[:, :, :], q_ps[:, 0:2 * P].rearrange("p (h k) -> p h k", h=2)[:, :, 0:KP], ACT.Copy).then_inc(turned_copied, 1)
            act.wait_ge(mixed, 1)
            nc.scalar.activation(mixer[0:KP, 0:KH, :], v_ps[0:KP, 0:KH * D].rearrange("p (h e) -> p h e", h=KH), ACT.Copy).then_inc(kept, 1)
            act.wait_ge(kept, 1)

        @block.vector
        def _(dve):
            if proj:
                for w in (wq, wk, wv):
                    nc.vector.memset(w[:, :, :], 0.0).then_inc(by_head, 1)
            nc.vector.memset(run[1][:, :], -1e30).then_inc(started, 1)
            nc.vector.memset(total[:, :], 0.0).then_inc(started, 1)
            nc.vector.memset(ctxt[:, :, :], 0.0).then_inc(started, 1)
            dve.wait_ge(started, 3)
            ln.dve_start(dve)
            dve.wait_ge(weights, 16 * len(loads))
            dve.wait_ge(x_loaded[0], 16)
            ln.dve_centre(dve, 0, 0)
            ln.dve_norm(dve, 0, 0)

            def body(c, b, r, more, behind):
                if more:
                    dve.wait_ge(x_loaded[1 - b], r * 16 + (b * 16 + 16))
                    ln.dve_centre(dve, c + 1, 1 - b)
                dve.wait_ge(k_made, c + NOW)
                dve.wait_ge(k_run, c + OLD)
                nc.vector.tensor_reduce(kmax[b][:, :], kps, AX_X, ALU.max).then_inc(k_maxed, 1)
                dve.wait_ge(k_maxed, c + NOW)
                dve.wait_ge(k_run, c + PREV)
                dve.wait_ge(faded, c + PREV)
                dve.wait_ge(k_bias, c + OLD)
                nc.vector.tensor_tensor(run[b][:, :], run[1 - b][:, :], kmax[b][:, :], ALU.max).then_inc(k_run, 1)
                dve.wait_ge(k_run, c + NOW)
                nc.vector.tensor_scalar(nbias[b][:, :], run[b][:, :], -scale, None, ALU.mult).then_inc(k_bias, 1)
                if more:
                    ln.dve_norm(dve, c + 1, 1 - b)
                dve.wait_ge(q_made, c + NOW)
                dve.wait_ge(q_less, c + OLD)
                nc.vector.tensor_reduce(qmax[b][:, :], qps, AX_X, ALU.max).then_inc(q_maxed, 1)
                dve.wait_ge(q_maxed, c + NOW)
                dve.wait_ge(q_exp, c + OLD)
                nc.vector.tensor_tensor(qs[b][:], qps, qmax[b][:, :].unsqueeze(2).to_broadcast([TT, 2 * NQ, R]), ALU.subtract).then_inc(q_less, 1)
                dve.wait_ge(q_exp, c + NOW)
                dve.wait_ge(q_rec, c + OLD)
                nc.vector.tensor_reduce(qsum[b][:, :], qe[b][:], AX_X, ALU.add).then_inc(q_summed, 1)
                dve.wait_ge(q_summed, c + NOW)
                dve.wait_ge(q_normed, c + OLD)
                nc.vector.reciprocal(qrec[b][:, :], qsum[b][:, :]).then_inc(q_rec, 1)
                dve.wait_ge(q_rec, c + NOW)
                dve.wait_ge(qT_made, c + OLD)
                nc.vector.tensor_tensor(qn[b][:], qe[b][:], qrec[b][:, :].unsqueeze(2).to_broadcast([TT, 2 * NQ, R]), ALU.mult).then_inc(q_normed, 1)
                dve.wait_ge(faded, c + NOW)
                dve.wait_ge(total_added, c + PREV)
                for h in range(KH):
                    last = nc.vector.scalar_tensor_tensor(total[:, h:h + 1], total[:, h:h + 1], fade[b][:, h:h + 1], ksum[b][:, h:h + 1],
                                                          ALU.mult, ALU.add)
                last.then_inc(total_added, 1)
                behind(0)

            def context_part(c, b, r, n):
                if n:
                    return
                dve.wait_ge(ctx_made, c + NOW)
                dve.wait_ge(ctx_added, c + PREV)
                for h in range(KH):
                    last = nc.vector.scalar_tensor_tensor(ctxt[:, h, :], ctxt[:, h, :], fade[b][:, h:h + 1], cps[:, h, :], ALU.mult, ALU.add)
                last.then_inc(ctx_added, 1)
            chunks_behind(dve, body, context_part)
            dve.wait_ge(total_added, NCH - 1 + NOW)
            nc.vector.reciprocal(rtotal[:, :], total[:, :]).then_inc(ended, 1)
            dve.wait_ge(ended, 1)
            dve.wait_ge(ctx_added, NCH - 1 + NOW)
            nc.vector.tensor_tensor(ctxt[:, :, :], ctxt[:, :, :], rtotal[:, :].unsqueeze(2).to_broadcast([KP, KH, EW]), ALU.mult).then_inc(ended, 1)
            dve.wait_ge(ended, 2)
            nc.vector.tensor_tensor(ctxn[:, :, :], ctxt[:, :, :], blocks[:, :, :], ALU.mult).then_inc(ended, 1)


def attend_second(nc, name, KH, KP, x_d, qT_d, mixer, out_d, c_d, bo_d, gain_d, offset_d, w1_d, b1_d, w2_d, b2_d, add_d=()):
    F = 4 * D
    FG = F // P
    with Phase(nc, name) as ph:
        xin = [ph.sb(f"xin{b}", [P, 2, CW]) for b in range(2)]
        q = [ph.sb(f"q{b}", [KP, KH, CW]) for b in range(2)]
        more_in = [[ph.sb(f"add{n}_{b}", [P, 2, CW]) for b in range(2)] for n in range(len(add_d))]
        x = [ph.sb(f"x{b}", [P, 2, CW]) for b in range(2)]
        g = [ph.sb(f"g{b}", [P, FG, CW]) for b in range(2)]
        y = [ph.sb(f"y{b}", [P, 2, CW]) for b in range(2)]
        ones = ph.sb("ones", [P, P])
        bo, gain, offset, b2 = (ph.sb(n, [P, 2]) for n in ("bo", "gain", "offset", "b2"))
        b1 = ph.sb("b1", [P, FG])
        w1, w2 = ph.sb("w1", [P, 2, F]), ph.sb("w2", [P, FG, D])
        a_ps, y_ps = ph.ps("a_ps", [P, 512]), ph.ps("y_ps", [P, 512])
        f_ps = [ph.ps(f"f_ps{i}", [P, 512]) for i in range(4)]
        aps = a_ps[:, 0:2 * CW].rearrange("p (h c) -> p h c", h=2)
        yps = y_ps[:, 0:2 * CW].rearrange("p (h c) -> p h c", h=2)
        weights = ph.sem("weights")
        loaded, more_loaded, saved = ([ph.sem(f"{n}{b}") for b in range(2)] for n in ("loaded", "more_loaded", "saved"))
        a_made, a_added, y_made, y_added = (ph.loop_sem(n) for n in ("a_made", "a_added", "y_made", "y_added"))
        more_added = [ph.loop_sem(f"more_added{n}") for n in range(len(add_d))]
        done = more_added[-1] if add_d else y_added
        up = [ph.loop_sem(f"up{m}") for m in range(FG // 2)]
        gelu = [ph.loop_sem(f"gelu{m}") for m in range(FG // 2)]
        ln = Norm(nc, ph, x, ones, [up[FG // 2 - 1]], gain, offset)
        loads = [(ones, c_d["mean"]), (bo, bo_d), (gain, gain_d), (offset, offset_d), (w1, w1_d), (b1, b1_d), (w2, w2_d), (b2, b2_d)]
        block = ph.block()
        NL, NA = 2, len(add_d)

        @block.sync
        def _(sp):
            for b in range(2):
                sp.sem_inc(saved[b], 16)

            def load(c, b):
                for dst, src in [(xin, x_d), (q, qT_d)]:
                    sp.dma_start(dst[b][:, :, :], src[:, :, ds(c * CW, CW)]).then_inc(loaded[b], 16)

            def load_more(c, b):
                for dst, src in zip(more_in, add_d):
                    sp.dma_start(dst[b][:, :, :], src[:, :, ds(c * CW, CW)]).then_inc(more_loaded[b], 16)
            for b in range(2):
                load(b, b)
                load_more(b, b)
            for dst, src in loads:
                sp.dma_start(dst[:], src).then_inc(weights, 16)

            def body(c, b, r, more):
                if more:
                    sp.wait_ge(a_added, c + NOW)
                    load(c + 2, b)
                sp.wait_ge(done, c + NOW)
                sp.dma_start(out_d[:, :, ds(c * CW, CW)], y[b][:, :, :]).then_inc(saved[b], 16)
                if more:
                    load_more(c + 2, b)
            chunks(sp, body, 2)
            for b in range(2):
                sp.wait_ge(saved[b], 16 * ((NCH + 1 - b) // 2) + 16)

        @block.tensor
        def _(pe):
            def attention(c, b, r):
                pe.wait_ge(loaded[b], r * (16 * NL) + 16 * NL)
                pe.wait_ge(a_added, c + PREV)
                for h in range(2):
                    for k in range(KH):
                        mm = nc.tensor.matmul(aps[:, h, :], mixer[0:KP, k, h * P:(h + 1) * P], q[b][:, k, :], start=(k == 0), stop=(k == KH - 1))
                mm.then_inc(a_made, 1)
                pe.wait_ge(a_added, c + NOW)
                ln.pe_mean(pe, c, b)

            pe.wait_ge(weights, 16 * len(loads))
            attention(0, 0, 0)
            ln.pe_var(pe, 0, 0)

            def body(c, b, r, more):
                pe.wait_ge(ln.affine, c + NOW)
                for m in range(FG // 2):
                    pe.wait_ge(gelu[m], c + PREV)
                    for h in range(2):
                        for k in range(2):
                            g0 = (2 * m + h) * P
                            mm = nc.tensor.matmul(f_ps[m][:, h * CW:(h + 1) * CW], w1[:, k, g0:g0 + P], ln.out[b][:, k, :],
                                                  start=(k == 0), stop=(k == 1))
                    mm.then_inc(up[m], 1)
                    if m == 0 and more:
                        attention(c + 1, 1 - b, r + b)
                    if m == 2 and more:
                        ln.pe_var(pe, c + 1, 1 - b)
                pe.wait_ge(y_added, c + PREV)
                for h in range(2):
                    for m in range(FG):
                        if h == 0 and m % 2 == 0:
                            pe.wait_ge(gelu[m // 2], c + NOW)
                        mm = nc.tensor.matmul(yps[:, h, :], w2[:, m, h * P:(h + 1) * P], g[b][:, m, :], start=(m == 0), stop=(m == FG - 1))
                mm.then_inc(y_made, 1)
            chunks(pe, body)

        @block.scalar
        def _(act):
            act.wait_ge(weights, 16 * len(loads))
            ln.act_square(act, 0, 0)
            ln.act_root(act, 0, 0)
            ln.act_affine(act, 0, 0)

            def body(c, b, r, more):
                act.wait_ge(y_made, c + OLD)
                for m in range(FG // 2):
                    act.wait_ge(up[m], c + NOW)
                    for h in range(2):
                        last = nc.scalar.activation(g[b][:, 2 * m + h, :], f_ps[m][:, h * CW:(h + 1) * CW], ACT.Gelu, bias=b1[:, 2 * m + h:2 * m + h + 1])
                    last.then_inc(gelu[m], 1)
                    if m == 1 and more:
                        ln.act_square(act, c + 1, 1 - b)
                if more:
                    ln.act_root(act, c + 1, 1 - b)
                    ln.act_affine(act, c + 1, 1 - b)
            chunks(act, body)

        @block.vector
        def _(dve):
            def attention(c, b, r):
                dve.wait_ge(loaded[b], r * (16 * NL) + 16 * NL)
                dve.wait_ge(a_made, c + NOW)
                dve.wait_ge(ln.mean_ready, c + OLD)
                dve.wait_ge(y_added, c + OLD)
                dve.wait_ge(ln.centred, c + OLD)
                for h in range(2):
                    last = nc.vector.scalar_tensor_tensor(x[b][:, h, :], aps[:, h, :], bo[:, h:h + 1], xin[b][:, h, :], ALU.add, ALU.add)
                last.then_inc(a_added, 1)
                dve.wait_ge(a_added, c + NOW)
                ln.dve_centre(dve, c, b)

            ln.dve_start(dve)
            dve.wait_ge(weights, 16 * len(loads))
            attention(0, 0, 0)
            ln.dve_norm(dve, 0, 0)

            def body(c, b, r, more):
                if more:
                    attention(c + 1, 1 - b, r + b)
                    ln.dve_norm(dve, c + 1, 1 - b)
                dve.wait_ge(y_made, c + NOW)
                dve.wait_ge(saved[b], r * 16 + 16)
                for h in range(2):
                    last = nc.vector.scalar_tensor_tensor(y[b][:, h, :], yps[:, h, :], b2[:, h:h + 1], x[b][:, h, :], ALU.add, ALU.add)
                last.then_inc(y_added, 1)
                before = y_added
                if NA:
                    dve.wait_ge(more_loaded[b], r * (16 * NA) + 16 * NA)
                for n, s in enumerate(more_added):
                    dve.wait_ge(before, c + NOW)
                    nc.vector.tensor_tensor(y[b][:, :, :], y[b][:, :, :], more_in[n][b][:, :, :], ALU.add).then_inc(s, 1)
                    before = s
            chunks(dve, body)


def feature_major(p, c0=0, n=CW):
    return p[:, c0:c0 + 2 * n].rearrange("p (h c) -> p h c", h=2)


def norm_table(nc, name, x_d, out_d, table_d, c_d, w_d=None, b_d=None, wa_d=None, ba_d=None, a_d=None):
    proj = w_d is not None
    with Phase(nc, name) as ph:
        x = [ph.sb(f"x{b}", [P, 2, CW]) for b in range(2)]
        row = [ph.sb(f"row{b}", [TT, 2, D]) for b in range(2)]
        ones, ident = ph.sb("ones", [P, P]), ph.sb("ident", [P, P])
        r_ps = [ph.ps(f"r_ps{b}", [P, 512]) for b in range(2)]
        if proj:
            w, bias, wa = ph.sb("w", [P, 2, D]), ph.sb("bias", [TT, D]), ph.sb("wa", [TT, 2, D])
            ba = ph.sb("ba", [TT, 2])
            prod = [ph.sb(f"prod{b}", [TT, 4, D]) for b in range(2)]
            dots = [ph.sb(f"dots{b}", [TT, 2, 2]) for b in range(2)]
        weights = ph.sem("weights")
        loaded, saved, a_saved = ([ph.sem(f"{n}{b}") for b in range(2)] for n in ("loaded", "saved", "a_saved"))
        rows_made, rows_copied, dotted = (ph.loop_sem(n) for n in ("rows_made", "rows_copied", "dotted"))
        out_sent = ph.sem("out_sent")
        out_saved = [ph.sem(f"out_saved{b}") for b in range(2)]
        ln = Norm(nc, ph, x, ones, [rows_made, out_sent])
        loads = [(ones, c_d["mean"]), (ident, c_d["ident"])] + ([(w, w_d), (bias, b_d.partition_broadcast(TT)), (wa, wa_d.partition_broadcast(TT)),
                                                                 (ba, ba_d.partition_broadcast(TT))] if proj else [])
        nc.sync.sem_inc(out_sent, START - 1)
        block = ph.block()

        @block.sync
        def _(sp):
            for b in range(2):
                sp.sem_inc(saved[b], 16)
                sp.sem_inc(a_saved[b], 32)
                sp.sem_inc(out_saved[b], 16)
                sp.dma_start(x[b][:, :, :], x_d[:, :, b * CW:(b + 1) * CW]).then_inc(loaded[b], 16)
            for dst, src in loads:
                sp.dma_start(dst[:], src).then_inc(weights, 16)

            def body(c, b, r, more):
                if more:
                    sp.wait_ge(ln.centred, c + NOW)
                    sp.dma_start(x[b][:, :, :], x_d[:, :, ds((c + 2) * CW, CW)]).then_inc(loaded[b], 16)
                sp.wait_ge(out_saved[1 - b], r * 16 + (b * 16 + 16))
                sp.sem_inc(out_sent, 1)
                sp.wait_ge(ln.normed, c + NOW)
                sp.dma_start(out_d[:, :, ds(c * CW, CW)], ln.out[b][:, :, :]).then_inc(out_saved[b], 16)
                sp.wait_ge(rows_copied, c + NOW)
                sp.dma_start(table_d[ds(c * CW, CW), :].rearrange("(t p) d -> p t d", t=2), row[b][:, :, :]).then_inc(saved[b], 16)
                if proj:
                    sp.wait_ge(dotted, c + NOW)
                    for n in range(2):
                        sp.dma_start(a_d[n, ds(c * CW, CW)].rearrange("(t p) -> p t", t=2), dots[b][:, :, n],
                                     allow_slow_non_contiguous=True).then_inc(a_saved[b], 16)
            chunks(sp, body, 2)
            for b in range(2):
                sp.wait_ge(out_saved[b], 16 * ((NCH + 1 - b) // 2) + 16)
                sp.wait_ge(saved[b], 16 * ((NCH + 1 - b) // 2) + 16)
                if proj:
                    sp.wait_ge(a_saved[b], 32 * ((NCH + 1 - b) // 2) + 32)

        @block.tensor
        def _(pe):
            pe.wait_ge(weights, 16 * len(loads))
            pe.wait_ge(loaded[0], 16)
            ln.pe_mean(pe, 0, 0)
            ln.pe_var(pe, 0, 0)

            def body(c, b, r, more):
                if more:
                    pe.wait_ge(loaded[1 - b], r * 16 + (b * 16 + 16))
                    ln.pe_mean(pe, c + 1, 1 - b)
                pe.wait_ge(ln.normed, c + NOW)
                pe.wait_ge(rows_copied, c + OLD)
                for t in range(2):
                    for k in range(2):
                        cols = ln.out[b][:, k, t * TT:(t + 1) * TT]
                        if proj:
                            mm = nc.tensor.matmul(r_ps[b][0:TT, t * D:(t + 1) * D], cols, w[:, k, :], start=(k == 0), stop=(k == 1))
                        else:
                            mm = nc.tensor.transpose(r_ps[b][0:TT, t * D + k * P:t * D + (k + 1) * P], cols, ident[:, :])
                mm.then_inc(rows_made, 1)
                if more:
                    ln.pe_var(pe, c + 1, 1 - b)
            chunks(pe, body)

        @block.scalar
        def _(act):
            ln.act_square(act, 0, 0)
            ln.act_root(act, 0, 0)

            def body(c, b, r, more):
                if more:
                    ln.act_square(act, c + 1, 1 - b)
                if not proj:
                    act.wait_ge(rows_made, c + NOW)
                    act.wait_ge(saved[b], r * 16 + 16)
                    nc.scalar.activation(row[b][:, :, :], r_ps[b][0:TT, :].rearrange("p (t d) -> p t d", t=2), ACT.Copy).then_inc(rows_copied, 1)
                if more:
                    ln.act_root(act, c + 1, 1 - b)
            chunks(act, body)

        @block.vector
        def _(dve):
            ln.dve_start(dve)
            dve.wait_ge(weights, 16 * len(loads))
            dve.wait_ge(loaded[0], 16)
            ln.dve_centre(dve, 0, 0)
            ln.dve_norm(dve, 0, 0)

            def body(c, b, r, more):
                if more:
                    dve.wait_ge(loaded[1 - b], r * 16 + (b * 16 + 16))
                    ln.dve_centre(dve, c + 1, 1 - b)
                if proj:
                    dve.wait_ge(rows_made, c + NOW)
                    dve.wait_ge(saved[b], r * 16 + 16)
                    dve.wait_ge(dotted, c + OLD)
                    nc.vector.tensor_tensor(row[b][:, :, :], r_ps[b][0:TT, :].rearrange("p (t d) -> p t d", t=2),
                                            bias[:, None, :].to_broadcast([TT, 2, D]), ALU.add).then_inc(rows_copied, 1)
                    dve.wait_ge(rows_copied, c + NOW)
                    dve.wait_ge(a_saved[b], r * 32 + 32)
                    for t in range(2):
                        for n in range(2):
                            last = nc.vector.tensor_tensor_reduce(prod[b][:, 2 * t + n, :], row[b][:, t, :], wa[:, n, :], 1.0, ba[:, n:n + 1], ALU.mult, ALU.add,
                                                                  dots[b][:, t, n:n + 1])
                    last.then_inc(dotted, 1)
                if more:
                    ln.dve_norm(dve, c + 1, 1 - b)
            chunks(dve, body)


RB = -(-ET // P)


def sum_edges(nc, name, sorted_d, weight_d, table_d, running_d, W, c_d):
    own = weight_d is None
    with Phase(nc, name) as ph:
        ident = ph.sb("ident", [P, P])
        rows = [ph.sb(f"rows{b}", [P, P, 3]) for b in range(2)]
        wrows = [ph.sb(f"wrows{b}", [P, P]) for b in range(2)]
        key, wgt = ph.sb("key", [P, ET + EB]), ph.sb("wgt", [P, ET + EB])
        idx = ph.sb("idx", [P, ET + EB], I32)
        kb, wb = [ph.sb(f"kb{b}", [P, EB]) for b in range(2)], [ph.sb(f"wb{b}", [P, EB]) for b in range(2)]
        ib = [ph.sb(f"ib{b}", [P, EB], I32) for b in range(2)]
        g = [ph.sb(f"g{b}", [P, EB, W]) for b in range(2)]
        run = [ph.sb(f"run{b}", [P, EB, W]) for b in range(2)]
        same = ph.sb("same", [P, 4, P])
        t_ps = [ph.ps(f"t_ps{b}", [P, 512]) for b in range(2)]
        krow_ps = [ph.ps(f"krow_ps{n}", [P, 512]) for n in range(4)]
        s_ps = [ph.ps(f"s_ps{b}", [P, 512]) for b in range(2)]
        consts, edge0, gate = ph.sem("consts"), ph.sem("edge0"), ph.sem("gate")
        rows_in = [ph.sem(f"rows_in{b}") for b in range(2)]
        turned, taken = ph.sem("turned"), ph.sem("taken")
        landed = [[ph.sem(f"landed{b}_{j}") for j in range(EB)] for b in range(2)]
        batch_in, batch_summed = ph.loop_sem("batch_in"), ph.loop_sem("batch_summed")
        krow, selected, summed, kept = (ph.loop_sem(n) for n in ("krow", "selected", "summed", "kept"))
        saved = [ph.sem(f"saved{b}") for b in range(2)]
        parts = 3 if own else 2
        per = 1 if own else 2
        blocks = [(n * P, min(P, ET - n * P)) for n in range(RB)]
        block = ph.block()

        @block.sync
        def _(sp):
            for b in range(2):
                sp.sem_inc(saved[b], 16)
            sp.dma_start(ident[:, :], c_d["ident"]).then_inc(consts, 16)
            for n, (t0, nt) in enumerate(blocks):
                if n >= 2:
                    sp.wait_ge(turned, n - 1)
                sp.dma_start(rows[n % 2][0:nt, :, :], sorted_d.rearrange("(t p) c -> t p c", p=P)[t0:t0 + nt]).then_inc(rows_in[n % 2], 16)
                if not own:
                    sp.dma_start(wrows[n % 2][0:nt, :], weight_d.rearrange("(t p) -> t p", p=P)[t0:t0 + nt]).then_inc(rows_in[n % 2], 16)
            out = running_d.rearrange("(t p) w -> p t w", p=P)
            with sp.Fori(0, NEB // 2) as i:
                for b in range(2):
                    t0 = i * (2 * EB) + b * EB
                    sp.wait_ge(kept, t0 + (EB - 1 + NOW))
                    sp.dma_start(out[:, ds(t0, EB), :], run[b][:, :, :]).then_inc(saved[b], 16)
            for b in range(2):
                sp.wait_ge(saved[b], 16 * (NEB // 2) + 16)

        @block.gpsimd
        def _(pool):
            with pool.Fori(0, NEB // 2) as i:
                for b in range(2):
                    pool.wait_ge(batch_in, i * 2 + (b + NOW))
                    pool.wait_ge(batch_summed, i * 2 + (b + OLD))
                    pool.sem_inc(gate, 1)
                    for j in range(EB):
                        nc.gpsimd.indirect_dma_start(g[b][:, j, 0:D], None, table_d, bass.IndirectOffsetOnAxis(ib[b][:, j:j + 1], 0)).then_inc(landed[b][j], 16)

        @block.tensor
        def _(pe):
            pe.wait_ge(consts, 16)
            for n, (t0, nt) in enumerate(blocks):
                pe.wait_ge(rows_in[n % 2], 16 * per * (n // 2 + 1))
                if n >= 2:
                    pe.wait_ge(taken, n - 1)
                for k in range(3):
                    src = rows[n % 2][0:nt, :, k] if k < 2 or own else wrows[n % 2][0:nt, :]
                    mm = nc.tensor.transpose(t_ps[n % 2][:, k * P:k * P + nt], src, ident[0:nt, 0:nt])
                mm.then_inc(turned, 1)

            def keys_along(t0, b, j):
                pe.wait_ge(selected, t0 + (max(j - 4, -1) + NOW))
                nc.tensor.transpose(krow_ps[j % 4][:, 0:P], kb[b][:, j:j + 1].to_broadcast([P, P]), ident[:, :]).then_inc(krow, 1)

            with pe.Fori(0, NEB // 2) as i:
                for b in range(2):
                    t0 = i * (2 * EB) + b * EB
                    pe.wait_ge(batch_in, i * 2 + (b + NOW))
                    for j in range(3):
                        keys_along(t0, b, j)
                    for j in range(EB):
                        q = (b * EB + j) % 2
                        if j + 3 < EB:
                            keys_along(t0, b, j + 3)
                        pe.wait_ge(selected, t0 + (j + NOW))
                        pe.wait_ge(kept, t0 + (j + OLD))
                        pe.wait_ge(landed[b][j], i * 16 + 16)
                        nc.tensor.matmul(s_ps[q][:, 0:W], same[:, j % 4, :], g[b][:, j, :], start=True, stop=True).then_inc(summed, 1)
                    nc.tensor.transpose(t_ps[0][:, 0:P], ident[:, :], ident[:, :]).then_inc(batch_summed, 1)

        @block.scalar
        def _(act):
            with act.Fori(0, NEB // 2) as i:
                for b in range(2):
                    t0 = i * (2 * EB) + b * EB
                    act.wait_ge(saved[b], i * 16 + 16)
                    for j in range(EB):
                        q = (b * EB + j) % 2
                        act.wait_ge(summed, t0 + (j + NOW))
                        nc.scalar.activation(run[b][:, j, :], s_ps[q][:, 0:W], ACT.Copy).then_inc(kept, 1)

        @block.vector
        def _(dve):
            for b in range(2):
                if W > D:
                    nc.vector.memset(g[b][:, :, D:W], 1.0).then_inc(edge0, 1)
            dve.wait_ge(consts, 16)
            for n, (t0, nt) in enumerate(blocks):
                dve.wait_ge(turned, n + 1)
                nc.vector.tensor_copy(key[:, t0:t0 + nt], t_ps[n % 2][:, 0:nt])
                nc.vector.tensor_copy(idx[:, t0:t0 + nt], t_ps[n % 2][:, P:P + nt])
                nc.vector.tensor_copy(wgt[:, t0:t0 + nt], t_ps[n % 2][:, 2 * P:2 * P + nt]).then_inc(taken, 1)
            dve.wait_ge(taken, RB)
            for tile in (key, wgt, idx):
                nc.vector.memset(tile[:, ET:ET + EB], 0.0).then_inc(edge0, 1)
            dve.wait_ge(edge0, 5 if W > D else 3)

            def take(B, b):
                dve.wait_ge(batch_summed, B + OLD)
                dve.wait_ge(selected, B * EB + (-EB - 1 + NOW) if not isinstance(B, int) else START)
                nc.vector.tensor_copy(kb[b][:, :], key[:, ds(B * EB, EB)])
                nc.vector.tensor_copy(wb[b][:, :], wgt[:, ds(B * EB, EB)])
                nc.vector.tensor_copy(ib[b][:, :], idx[:, ds(B * EB, EB)]).then_inc(batch_in, 1)
            take(0, 0)
            with dve.Fori(0, NEB // 2) as i:
                for b in range(2):
                    t0 = i * (2 * EB) + b * EB
                    dve.wait_ge(batch_in, i * 2 + (b + NOW))
                    for j in range(EB):
                        if j == EB // 2:
                            take(i * 2 + (b + 1), 1 - b)
                        k4 = krow_ps[j % 4][:, 0:P]
                        dve.wait_ge(krow, t0 + (j + NOW))
                        dve.wait_ge(summed, t0 + (max(j - 4, -1) + NOW))
                        nc.vector.tensor_scalar(same[:, j % 4, :], k4, kb[b][:, j:j + 1], wb[b][:, j:j + 1], ALU.is_equal, ALU.mult).then_inc(selected, 1)


def tile_carries(nc, name, sorted_d, running_d, carry_d, W, c_d):
    blocks = [(n * P, min(P, ET - n * P)) for n in range(RB)]
    groups = [(0, P), (P, P)] + ([(D, W - D)] if W > D else [])
    with Phase(nc, name) as ph:
        ident = ph.sb("ident", [P, P])
        keys = ph.sb("keys", [P, RB])
        last = ph.sb("last", [P, RB, W])
        endkey, goes_on = ph.sb("endkey", [P, ET + 1]), ph.sb("goes_on", [P, ET])
        lastT, sumT = ph.sb("lastT", [P, len(groups), ET]), ph.sb("sumT", [P, len(groups), ET])
        rows, zero = ph.sb("rows", [P, RB, W]), ph.sb("zero", [1, W])
        k_ps = [ph.ps(f"k_ps{b}", [P, 512]) for b in range(2)]
        t_ps = [ph.ps(f"t_ps{b}", [P, 512]) for b in range(2)]
        r_ps = [ph.ps(f"r_ps{b}", [P, 512]) for b in range(2)]
        loaded, cleared, along, key_taken, turned, taken, scanned, back, copied, saved = (ph.sem(n) for n in (
            "loaded", "cleared", "along", "key_taken", "turned", "taken", "scanned", "back", "copied", "saved"))
        block = ph.block()

        @block.sync
        def _(sp):
            sp.dma_start(ident[:, :], c_d["ident"]).then_inc(loaded, 16)
            for n, (t0, nt) in enumerate(blocks):
                sp.dma_start(last[0:nt, n, :], running_d.rearrange("(t p) w -> t p w", p=P)[t0:t0 + nt, P - 1, :]).then_inc(loaded, 16)
                sp.dma_start(keys[0:nt, n:n + 1], sorted_d.rearrange("(t p) c -> t p c", p=P)[t0:t0 + nt, P - 1, 0:1],
                             allow_slow_non_contiguous=True).then_inc(loaded, 16)
            for n, (t0, nt) in enumerate(blocks):
                sp.wait_ge(copied, n + 1)
                nt = min(nt, ET - 1 - t0)
                sp.dma_start(carry_d[1 + t0:1 + t0 + nt, :], rows[0:nt, n, :]).then_inc(saved, 16)
            sp.wait_ge(cleared, 1)
            sp.dma_start(carry_d[0:1, :], zero[0:1, :]).then_inc(saved, 16)
            sp.wait_ge(saved, 16 * (RB + 1))

        @block.tensor
        def _(pe):
            pe.wait_ge(loaded, 16 * (1 + 2 * RB))
            for n, (t0, nt) in enumerate(blocks):
                if n >= 2:
                    pe.wait_ge(key_taken, n - 1)
                nc.tensor.transpose(k_ps[n % 2][:, 0:nt], keys[0:nt, n:n + 1].to_broadcast([nt, P]), ident[0:nt, 0:nt]).then_inc(along, 1)
            for n, (t0, nt) in enumerate(blocks):
                if n >= 2:
                    pe.wait_ge(taken, n - 1)
                for g, (c0, cw) in enumerate(groups):
                    mm = nc.tensor.transpose(t_ps[n % 2][0:cw, g * P:g * P + nt], last[0:nt, n, c0:c0 + cw], ident[0:nt, 0:nt])
                mm.then_inc(turned, 1)
            pe.wait_ge(scanned, 1)
            for n, (t0, nt) in enumerate(blocks):
                if n >= 2:
                    pe.wait_ge(copied, n - 1)
                for g, (c0, cw) in enumerate(groups):
                    mm = nc.tensor.transpose(r_ps[n % 2][0:nt, c0:c0 + cw], sumT[0:cw, g, t0:t0 + nt], ident[0:cw, 0:cw])
                mm.then_inc(back, 1)

        @block.scalar
        def _(act):
            for n, (t0, nt) in enumerate(blocks):
                act.wait_ge(back, n + 1)
                nc.scalar.activation(rows[0:nt, n, :], r_ps[n % 2][0:nt, 0:W], ACT.Copy).then_inc(copied, 1)

        @block.vector
        def _(dve):
            nc.vector.memset(zero[:, :], 0.0).then_inc(cleared, 1)
            nc.vector.memset(endkey[:, 0:1], -1.0).then_inc(cleared, 1)
            for n, (t0, nt) in enumerate(blocks):
                dve.wait_ge(along, n + 1)
                nc.vector.tensor_copy(endkey[:, 1 + t0:1 + t0 + nt], k_ps[n % 2][:, 0:nt]).then_inc(key_taken, 1)
            dve.wait_ge(cleared, 2)
            dve.wait_ge(key_taken, RB)
            nc.vector.tensor_tensor(goes_on[:, :], endkey[:, 1:ET + 1], endkey[:, 0:ET], ALU.is_equal).then_inc(key_taken, 1)
            for n, (t0, nt) in enumerate(blocks):
                dve.wait_ge(turned, n + 1)
                for g, (c0, cw) in enumerate(groups):
                    mm = nc.vector.tensor_copy(lastT[0:cw, g, t0:t0 + nt], t_ps[n % 2][0:cw, g * P:g * P + nt])
                mm.then_inc(taken, 1)
            dve.wait_ge(key_taken, RB + 1)
            dve.wait_ge(taken, RB)
            for g, (c0, cw) in enumerate(groups):
                mm = nc.vector.tensor_tensor_scan(sumT[0:cw, g, :], goes_on[0:cw, :], lastT[0:cw, g, :], 0.0, ALU.mult, ALU.add)
            mm.then_inc(scanned, 1)


def node_ends(nc, dve, ph, base, hist, first, ends, mask, sem):
    nc.vector.tensor_scalar(mask[:, :], hist[:, :], 1.0, None, ALU.min).then_inc(sem, 1)
    nc.vector.tensor_tensor(first[:, :], base[:, :], hist[:, :], ALU.add).then_inc(sem, 1)
    dve.wait_ge(sem, 2)
    nc.vector.tensor_scalar(ends[:, :], first[:, :], -1.0, 0.0, ALU.add, ALU.max).then_inc(sem, 1)
    dve.wait_ge(sem, 3)


def node_rows(nc, name, running_d, carry_d, W, hist_d, base_d, out_d, c_d):
    with Phase(nc, name) as ph:
        ident = ph.sb("ident", [P, P])
        base, hist, first, mask = (ph.sb(n, [TT, NT]) for n in ("base", "hist", "first", "mask"))
        ends, tile = ph.sb("ends", [TT, NT], I32), ph.sb("tile", [TT, NT], I32)
        tile_f, cross = ph.sb("tile_f", [TT, NT]), ph.sb("cross", [TT, NT])
        eb, tb = ([ph.sb(f"{n}{b}", [TT, 2], I32) for b in range(2)] for n in ("eb", "tb"))
        cb = [ph.sb(f"cb{b}", [TT, 2]) for b in range(2)]
        last, before, row = ([ph.sb(f"{n}{b}", [TT, 2, W]) for b in range(2)] for n in ("last", "before", "row"))
        fac, floor = ([ph.sb(f"{n}{b}", [TT, 2]) for b in range(2)] for n in ("fac", "floor"))
        inv = [ph.sb(f"inv{b}", [TT, 2]) for b in range(2)]
        scaled = [ph.sb(f"scaled{b}", [TT, 2, D]) for b in range(2)]
        out = [ph.sb(f"out{b}", [P, 2, CW]) for b in range(2)]
        o_ps = [ph.ps(f"o_ps{b}", [P, 512]) for b in range(2)]
        loaded, prep, gate = ph.sem("loaded"), ph.sem("prep"), ph.sem("gate")
        landed = [[ph.sem(f"landed{b}{t}") for t in range(2)] for b in range(2)]
        saved = [ph.sem(f"saved{b}") for b in range(2)]
        index_in, joined, s1, s2, factored, scaled_s, turned, copied = (ph.loop_sem(n) for n in (
            "index_in", "joined", "floored", "inverted", "factored", "scaled", "turned", "copied"))
        block = ph.block()

        @block.sync
        def _(sp):
            for b in range(2):
                sp.sem_inc(saved[b], 16)
            sp.dma_start(ident[:, :], c_d["ident"]).then_inc(loaded, 16)
            sp.dma_start(base[:, :], base_d[0:N].rearrange("(t p) -> p t", p=TT), allow_slow_non_contiguous=True).then_inc(loaded, 16)
            sp.dma_start(hist[:, :], hist_d[0:N].rearrange("(t p) -> p t", p=TT), allow_slow_non_contiguous=True).then_inc(loaded, 16)

            def body(c, b, r, more):
                sp.wait_ge(copied, c + NOW)
                sp.dma_start(out_d[:, :, ds(c * CW, CW)], out[b][:, :, :]).then_inc(saved[b], 16)
            chunks(sp, body)
            for b in range(2):
                sp.wait_ge(saved[b], 16 * ((NCH + 1 - b) // 2) + 16)

        @block.gpsimd
        def _(pool):
            def body(c, b, r, more):
                pool.wait_ge(index_in, c + NOW)
                pool.wait_ge(scaled_s, c + OLD)
                pool.sem_inc(gate, 1)
                for t in range(2):
                    nc.gpsimd.indirect_dma_start(last[b][:, t, :], None, running_d, bass.IndirectOffsetOnAxis(eb[b][:, t:t + 1], 0)).then_inc(landed[b][t], 16)
                    nc.gpsimd.indirect_dma_start(before[b][:, t, :], None, carry_d, bass.IndirectOffsetOnAxis(tb[b][:, t:t + 1], 0)).then_inc(landed[b][t], 16)
            chunks(pool, body)

        @block.vector
        def _(dve):
            dve.wait_ge(loaded, 48)
            node_ends(nc, dve, ph, base, hist, first, ends, mask, prep)
            nc.vector.tensor_scalar(tile[:, :], ends[:, :], 7, None, ALU.logical_shift_right).then_inc(prep, 1)
            dve.wait_ge(prep, 4)
            nc.vector.tensor_copy(tile_f[:, :], tile[:, :]).then_inc(prep, 1)
            dve.wait_ge(prep, 5)
            nc.vector.scalar_tensor_tensor(cross[:, :], tile_f[:, :], float(P), base[:, :], ALU.mult, ALU.is_gt).then_inc(prep, 1)
            dve.wait_ge(prep, 6)

            def indices(c, b):
                dve.wait_ge(scaled_s, c + OLD)
                nc.vector.tensor_copy(eb[b][:, :], ends[:, ds(c * 2, 2)])
                nc.vector.tensor_copy(cb[b][:, :], cross[:, ds(c * 2, 2)])
                nc.vector.tensor_copy(tb[b][:, :], tile[:, ds(c * 2, 2)]).then_inc(index_in, 1)
            indices(0, 0)

            def body(c, b, r, more):
                if more:
                    indices(c + 1, 1 - b)
                dve.wait_ge(index_in, c + NOW)
                for t in range(2):
                    dve.wait_ge(landed[b][t], r * 32 + 32)
                    ins = nc.vector.scalar_tensor_tensor(row[b][:, t, :], before[b][:, t, :], cb[b][:, t:t + 1], last[b][:, t, :], ALU.mult, ALU.add)
                ins.then_inc(joined, 1)
                dve.wait_ge(joined, c + NOW)
                if W > D:
                    nc.vector.tensor_scalar(floor[b][:, :], row[b][:, :, D], 1e-30, None, ALU.max).then_inc(s1, 1)
                    dve.wait_ge(s1, c + NOW)
                    nc.vector.reciprocal(inv[b][:, :], floor[b][:, :]).then_inc(s2, 1)
                    dve.wait_ge(s2, c + NOW)
                    dve.wait_ge(scaled_s, c + OLD)
                    nc.vector.tensor_tensor(fac[b][:, :], inv[b][:, :], mask[:, ds(c * 2, 2)], ALU.mult).then_inc(factored, 1)
                else:
                    dve.wait_ge(scaled_s, c + OLD)
                    nc.vector.tensor_copy(fac[b][:, :], mask[:, ds(c * 2, 2)]).then_inc(factored, 1)
                dve.wait_ge(factored, c + NOW)
                dve.wait_ge(turned, c + OLD)
                nc.vector.tensor_tensor(scaled[b][:, :, :], row[b][:, :, 0:D], fac[b][:, :].unsqueeze(2).to_broadcast([TT, 2, D]), ALU.mult).then_inc(scaled_s, 1)
            chunks(dve, body)

        @block.tensor
        def _(pe):
            pe.wait_ge(loaded, 48)

            def body(c, b, r, more):
                pe.wait_ge(scaled_s, c + NOW)
                pe.wait_ge(copied, c + OLD)
                for t in range(2):
                    for h in range(2):
                        mm = nc.tensor.transpose(o_ps[b][:, h * CW + t * TT:h * CW + (t + 1) * TT], scaled[b][:, t, h * P:(h + 1) * P], ident[0:TT, 0:TT])
                mm.then_inc(turned, 1)
            chunks(pe, body)

        @block.scalar
        def _(act):
            def body(c, b, r, more):
                act.wait_ge(turned, c + NOW)
                act.wait_ge(saved[b], r * 16 + 16)
                nc.scalar.activation(out[b][:, :, :], feature_major(o_ps[b]), ACT.Copy).then_inc(copied, 1)
            chunks(act, body)


def batchnorm_factors(nc, dve, act, stats, mv, gain, offset, scale, shift, dev, inv, t, eps_t, sem, root):
    def on_dve():
        for h in range(2):
            nc.vector.bn_aggr(mv[:, h, :], stats[:, h, :, :].rearrange("p c s -> p (c s)")).then_inc(sem, 1)
        dve.wait_ge(root, 1)
        nc.vector.reciprocal(inv[:, :], dev[:, :]).then_inc(sem, 1)
        dve.wait_ge(sem, 3)
        nc.vector.tensor_tensor(scale[:, :], inv[:, :], gain[:, :], ALU.mult).then_inc(sem, 1)
        dve.wait_ge(sem, 4)
        nc.vector.tensor_tensor(t[:, :], mv[:, :, 0], scale[:, :], ALU.mult).then_inc(sem, 1)
        dve.wait_ge(sem, 5)
        nc.vector.tensor_tensor(shift[:, :], offset[:, :], t[:, :], ALU.subtract).then_inc(sem, 1)
        dve.wait_ge(sem, 6)

    def on_act():
        act.wait_ge(sem, 2)
        nc.scalar.activation(dev[:, :], mv[:, :, 1], ACT.Sqrt, bias=eps_t[:, 0:1]).then_inc(root, 1)
    return on_dve, on_act


def message_layer(nc, name, agg_d, x_d, xn_d, mix_d, out_d, z_d, u_d, hist_d, c_d, eps_d, w1_d, w2_d, g1_d, o1_d, g2_d, o2_d):
    common = ("gain1", "offset1", "gain2", "offset2", "scale1", "shift1", "scale2", "shift2", "dev", "inv", "t")
    with Phase(nc, name) as keep:
        tiles = {n: keep.sb(n, [P, 2]) for n in common}
        mv = keep.sb("mv", [P, 2, 2])
        stats = keep.sb("stats", [P, 2, NCH, 6])
        w1, w2, epsw, eps_t = keep.sb("w1", [P, 2, D]), keep.sb("w2", [P, 2, D]), keep.sb("epsw", [P, 1]), keep.sb("eps", [P, 1])
        for step in range(3):
            with Phase(nc, f"{name}{step}") as ph:
                srcs = [(agg_d, xn_d), (z_d,), (u_d, xn_d, x_d, mix_d)][step]
                ins = [[ph.sb(f"in{n}_{b}", [P, 2, CW]) for b in range(2)] for n in range(len(srcs))]
                y, res = ([ph.sb(f"{n}{b}", [P, 2, CW]) for b in range(2)] for n in ("y", "res"))
                deg, dsq, nn = ([ph.sb(f"{n}{b}", [P, CW]) for b in range(2)] for n in ("deg", "dsq", "nn"))
                m_ps = [ph.ps(f"m_ps{b}", [P, 512]) for b in range(2)]
                loaded, saved = ([ph.sem(f"{n}{b}") for b in range(2)] for n in ("loaded", "saved"))
                y_made, mult, res_made, statted, degs, rooted, nn_made, s3, s4, s5 = (ph.loop_sem(n) for n in (
                    "y_made", "mult", "res_made", "statted", "degs", "rooted", "nn_made", "plus_xn", "plus_x", "plus_mix"))
                weights, agg_s, root = ph.sem("weights"), ph.sem("aggregated"), ph.sem("root")
                n_in = len(srcs) + (1 if step == 1 else 0)
                loads = [] if step else [(tiles["gain1"], g1_d), (tiles["offset1"], o1_d), (tiles["gain2"], g2_d), (tiles["offset2"], o2_d),
                                         (w1, w1_d), (w2, w2_d), (epsw, eps_d.partition_broadcast(P))]
                dst = (z_d, u_d, out_d)[step]
                last_sem = (res_made, res_made, s5)[step]
                block = ph.block()

                @block.sync
                def _(sp):
                    for b in range(2):
                        sp.sem_inc(saved[b], 16)
                    for to, src in loads:
                        sp.dma_start(to[:], src).then_inc(weights, 16)

                    def load(c, b):
                        for n, src in enumerate(srcs):
                            sp.dma_start(ins[n][b][:, :, :], src[:, :, ds(c * CW, CW)]).then_inc(loaded[b], 16)
                        if step == 1:
                            sp.dma_start(deg[b][:, :], hist_d[ds(c * CW, CW)].partition_broadcast(P)).then_inc(loaded[b], 16)
                    load(0, 0)

                    def body(c, b, r, more):
                        if more:
                            sp.wait_ge(last_sem, c + PREV)
                            load(c + 1, 1 - b)
                        sp.wait_ge(last_sem, c + NOW)
                        sp.dma_start(dst[:, :, ds(c * CW, CW)], res[b][:, :, :]).then_inc(saved[b], 16)
                    chunks(sp, body)
                    for b in range(2):
                        sp.wait_ge(saved[b], 16 * ((NCH + 1 - b) // 2) + 16)

                @block.vector
                def _(dve):
                    if step == 0:
                        nc.vector.memset(eps_t[:, :], 1e-5).then_inc(weights, 1)
                        dve.wait_ge(weights, 16 * len(loads) + 1)

                    def body(c, b, r, more):
                        dve.wait_ge(loaded[b], r * (16 * n_in) + 16 * n_in)
                        if step == 0:
                            dve.wait_ge(mult, c + OLD)
                            nc.vector.scalar_tensor_tensor(y[b][:, :, :], ins[1][b][:, :, :], epsw[:, 0:1], ins[0][b][:, :, :], ALU.mult,
                                                           ALU.add).then_inc(y_made, 1)
                        if step == 1:
                            dve.wait_ge(rooted, c + OLD)
                            nc.vector.tensor_scalar(dsq[b][:, :], deg[b][:, :], 1.0, None, ALU.max).then_inc(degs, 1)
                            dve.wait_ge(rooted, c + NOW)
                            dve.wait_ge(res_made, c + OLD)
                            nc.vector.reciprocal(nn[b][:, :], deg[b][:, :]).then_inc(nn_made, 1)
                        if step < 2:
                            dve.wait_ge(mult, c + NOW)
                            dve.wait_ge(saved[b], r * 16 + 16)
                            dve.wait_ge(statted, c + OLD)
                        if step == 0:
                            nc.vector.tensor_copy(res[b][:, :, :], feature_major(m_ps[b])).then_inc(res_made, 1)
                        if step == 1:
                            dve.wait_ge(nn_made, c + NOW)
                            nc.vector.tensor_tensor(res[b][:, :, :], feature_major(m_ps[b]), nn[b][:, None, :].to_broadcast([P, 2, CW]),
                                                    ALU.mult).then_inc(res_made, 1)
                        if step < 2:
                            dve.wait_ge(res_made, c + NOW)
                            for h in range(2):
                                last = nc.vector.bn_stats(stats[:, h, ds(c, 1), :].rearrange("p c s -> p (c s)"), res[b][:, h, :])
                            last.then_inc(statted, 1)
                        if step == 2:
                            dve.wait_ge(y_made, c + NOW)
                            dve.wait_ge(saved[b], r * 16 + 16)
                            for n, (a, s) in enumerate(((y, s3), (res, s4), (res, s5))):
                                if n:
                                    dve.wait_ge((s3, s4)[n - 1], c + NOW)
                                nc.vector.tensor_tensor(res[b][:, :, :], a[b][:, :, :], ins[n + 1][b][:, :, :], ALU.add).then_inc(s, 1)
                    chunks(dve, body)
                    if step < 2:
                        dve.wait_ge(statted, NCH - 1 + NOW)
                        batchnorm_factors(nc, dve, None, stats, mv, tiles[f"gain{step + 1}"], tiles[f"offset{step + 1}"], tiles[f"scale{step + 1}"],
                                          tiles[f"shift{step + 1}"], tiles["dev"], tiles["inv"], tiles["t"], eps_t, agg_s, root)[0]()

                @block.scalar
                def _(act):
                    def body(c, b, r, more):
                        if step == 1:
                            act.wait_ge(degs, c + NOW)
                            nc.scalar.activation(deg[b][:, :], dsq[b][:, :], ACT.Sqrt).then_inc(rooted, 1)
                        if step:
                            act.wait_ge(loaded[b], r * (16 * n_in) + 16 * n_in)
                            act.wait_ge(mult if step == 1 else s3, c + OLD)
                            for h in range(2):
                                last = nc.scalar.activation(y[b][:, h, :], ins[0][b][:, h, :], ACT.Relu, bias=tiles[f"shift{step}"][:, h:h + 1],
                                                            scale=tiles[f"scale{step}"][:, h:h + 1])
                            last.then_inc(y_made, 1)
                    if step:
                        chunks(act, body)
                    if step < 2:
                        batchnorm_factors(nc, None, act, stats, mv, None, None, None, None, tiles["dev"], None, None, eps_t, agg_s, root)[1]()

                if step < 2:
                    @block.tensor
                    def _(pe):
                        w = (w1, w2)[step]
                        if step == 0:
                            pe.wait_ge(weights, 16 * len(loads) + 1)

                        def body(c, b, r, more):
                            pe.wait_ge(y_made, c + NOW)
                            pe.wait_ge(res_made, c + OLD)
                            for h in range(2):
                                for k in range(2):
                                    mm = nc.tensor.matmul(m_ps[b][:, h * CW:(h + 1) * CW], w[:, k, h * P:(h + 1) * P], y[b][:, k, :], start=(k == 0), stop=(k == 1))
                            mm.then_inc(mult, 1)
                        chunks(pe, body)


def experts(nc, name, x_d, out_d, c_d, router_d, w1_d, b1_d, w2_d, b2_d):
    NE = 8
    with Phase(nc, name) as ph:
        x = [ph.sb(f"x{b}", [P, 2, CW]) for b in range(2)]
        ones, ident = ph.sb("ones", [P, P]), ph.sb("ident", [P, P])
        router, pick = ph.sb("router", [P, 2, NE]), ph.sb("pick", [NE, NE, P])
        before = ph.sb("before", [TT, NE, NE])
        w1, w2 = ph.sb("w1", [P, NE, 2, D]), ph.sb("w2", [P, NE, 2, D])
        b1, b2 = ph.sb("b1", [P, NE, 2]), ph.sb("b2", [NE, D])
        lg, lmax, les, ex, esum, erec, pr, cnt, eq, sel, psel, ps, pg, pgr, comb = (
            [ph.sb(f"{n}{b}", s) for b in range(2)] for n, s in (
                ("lg", [TT, 2, NE]), ("lmax", [TT, 2]), ("les", [TT, 2, NE]), ("ex", [TT, 2, NE]), ("esum", [TT, 2]), ("erec", [TT, 2]),
                ("pr", [TT, 2, NE]), ("cnt", [TT, 2 * NE, NE]), ("eq", [TT, 2 * NE, NE]), ("sel", [TT, 2, NE]), ("psel", [TT, 2, NE]),
                ("ps", [TT, 2]), ("pg", [TT, 2]), ("pgr", [TT, 2]), ("comb", [TT, 2, NE])))
        combT = [ph.sb(f"combT{b}", [NE, CW]) for b in range(2)]
        g = [ph.sb(f"g{n}", [P, 2, CW]) for n in range(2)]
        gw = [ph.sb(f"gw{n}", [P, 2, CW]) for n in range(2)]
        t1, y = ([ph.sb(f"{n}{b}", [P, 2, CW]) for b in range(2)] for n in ("t1_", "y"))
        h_ps = [ph.ps(f"h_ps{n}", [P, 512]) for n in range(2)]
        o_ps = [ph.ps(f"o_ps{h}", [P, 512]) for h in range(2)]
        l_ps, c_ps = ph.ps("l_ps", [P, 512]), ph.ps("c_ps", [P, 512])
        weights = ph.sem("weights")
        loaded, saved = ([ph.sem(f"{n}{b}") for b in range(2)] for n in ("loaded", "saved"))
        logits, l_read, comb_ready, combT_made, combT_copied, y_made, summed_x = (ph.loop_sem(n) for n in (
            "logits", "l_read", "comb_ready", "combT_made", "combT_copied", "y_made", "summed_x"))
        route = [ph.loop_sem(f"route{n}") for n in range(16)]
        e_up, e_gelu, e_cb, e_weighted, e_down = (ph.loop_sem(n) for n in ("e_up", "e_gelu", "e_cb", "e_weighted", "e_down"))
        exped = ph.loop_sem("exped")
        ln = Norm(nc, ph, x, ones, [y_made, summed_x])
        loads = [(ones, c_d["mean"]), (ident, c_d["ident"]), (pick, c_d["pick"]), (before, c_d["before"]), (router, router_d),
                 (w1, w1_d), (b1, b1_d), (w2, w2_d), (b2, b2_d)]
        block = ph.block()

        @block.sync
        def _(sp):
            for b in range(2):
                sp.sem_inc(saved[b], 16)
            sp.dma_start(x[0][:, :, :], x_d[:, :, 0:CW]).then_inc(loaded[0], 16)
            for dst, src in loads:
                sp.dma_start(dst[:], src).then_inc(weights, 16)

            def body(c, b, r, more):
                if more:
                    sp.wait_ge(ln.centred, c + PREV)
                    sp.wait_ge(summed_x, c + PREV)
                    sp.dma_start(x[1 - b][:, :, :], x_d[:, :, ds((c + 1) * CW, CW)]).then_inc(loaded[1 - b], 16)
                sp.wait_ge(y_made, c + NOW)
                sp.dma_start(out_d[:, :, ds(c * CW, CW)], y[b][:, :, :]).then_inc(saved[b], 16)
            chunks(sp, body)
            for b in range(2):
                sp.wait_ge(saved[b], 16 * ((NCH + 1 - b) // 2) + 16)

        @block.tensor
        def _(pe):
            def scores(c, b):
                pe.wait_ge(ln.normed, c + NOW)
                pe.wait_ge(l_read, c + PREV)
                pe.wait_ge(combT_copied, c + PREV)
                for t in range(2):
                    for k in range(2):
                        mm = nc.tensor.matmul(l_ps[0:TT, t * NE:(t + 1) * NE], ln.out[b][:, k, t * TT:(t + 1) * TT], router[:, k, :], start=(k == 0), stop=(k == 1))
                mm.then_inc(logits, 1)

            def turn(c, b):
                pe.wait_ge(comb_ready, c + NOW)
                for t in range(2):
                    mm = nc.tensor.transpose(l_ps[0:NE, 256 + t * TT:256 + (t + 1) * TT], comb[b][:, t, :], ident[0:TT, 0:TT])
                mm.then_inc(combT_made, 1)

            def up(c, b, e):
                n = c * NE + e
                pe.wait_ge(e_gelu, n + OLD)
                for h in range(2):
                    for k in range(2):
                        mm = nc.tensor.matmul(h_ps[e % 2][:, h * CW:(h + 1) * CW], w1[:, e, k, h * P:(h + 1) * P], ln.out[b][:, k, :], start=(k == 0), stop=(k == 1))
                mm.then_inc(e_up, 1)
                pe.wait_ge(e_weighted, n + PREV)
                nc.tensor.matmul(c_ps[:, 0:CW], pick[:, e, :], combT[b][:, :], start=True, stop=True).then_inc(e_cb, 1)

            def down(c, b, e):
                pe.wait_ge(e_weighted, c * NE + (e + NOW))
                for h in range(2):
                    for k in range(2):
                        mm = nc.tensor.matmul(o_ps[h][:, 0:CW], w2[:, e, k, h * P:(h + 1) * P], gw[e % 2][:, k, :], start=False, stop=(e == NE - 1 and k == 1),
                                              skip_group_check=True)
                mm.then_inc(e_down, 1)

            pe.wait_ge(weights, 16 * len(loads))
            pe.wait_ge(loaded[0], 16)
            ln.pe_mean(pe, 0, 0)
            ln.pe_var(pe, 0, 0)
            scores(0, 0)
            turn(0, 0)

            def body(c, b, r, more):
                pe.wait_ge(combT_copied, c + NOW)
                pe.wait_ge(y_made, c + PREV)
                for e in range(NE):
                    up(c, b, e)
                    if e == 0:
                        for h in range(2):
                            nc.tensor.matmul(o_ps[h][:, 0:CW], b2[:, h * P:(h + 1) * P], combT[b][:, :], start=True, stop=False, skip_group_check=True)
                    else:
                        down(c, b, e - 1)
                    if more:
                        if e == 1:
                            pe.wait_ge(loaded[1 - b], r * 16 + (b * 16 + 16))
                            ln.pe_mean(pe, c + 1, 1 - b)
                        if e == 3:
                            ln.pe_var(pe, c + 1, 1 - b)
                        if e == 5:
                            scores(c + 1, 1 - b)
                        if e == 7:
                            turn(c + 1, 1 - b)
                down(c, b, NE - 1)
            chunks(pe, body)

        @block.scalar
        def _(act):
            def softmax_exp(c, b):
                act.wait_ge(route[1], c + NOW)
                act.wait_ge(route[3], c + OLD)
                act.wait_ge(route[4], c + OLD)
                nc.scalar.activation(ex[b][:, :, :], les[b][:, :, :], ACT.Exp).then_inc(exped, 1)

            def copy_turned(c, b):
                act.wait_ge(combT_made, c + NOW)
                act.wait_ge(y_made, c + OLD)
                nc.scalar.activation(combT[b][:, :], l_ps[0:NE, 256:256 + CW], ACT.Copy).then_inc(combT_copied, 1)

            act.wait_ge(weights, 16 * len(loads))
            ln.act_square(act, 0, 0)
            ln.act_root(act, 0, 0)
            softmax_exp(0, 0)
            copy_turned(0, 0)

            def body(c, b, r, more):
                for e in range(NE):
                    n = c * NE + e
                    act.wait_ge(e_up, n + NOW)
                    act.wait_ge(e_weighted, n + OLD)
                    for h in range(2):
                        last = nc.scalar.activation(g[e % 2][:, h, :], h_ps[e % 2][:, h * CW:(h + 1) * CW], ACT.Gelu, bias=b1[:, e, h:h + 1])
                    last.then_inc(e_gelu, 1)
                    if more:
                        if e == 2:
                            ln.act_square(act, c + 1, 1 - b)
                        if e == 4:
                            ln.act_root(act, c + 1, 1 - b)
                        if e == 6:
                            softmax_exp(c + 1, 1 - b)
                if more:
                    copy_turned(c + 1, 1 - b)
            chunks(act, body)

        @block.vector
        def _(dve):
            def step(c, n, ins):
                ins.then_inc(route[n], 1)
                dve.wait_ge(route[n], c + NOW)

            def routing1(c, b):
                dve.wait_ge(logits, c + NOW)
                dve.wait_ge(comb_ready, c + OLD)
                dve.wait_ge(exped, c + OLD)
                nc.vector.tensor_copy(lg[b][:, :, :], l_ps[0:TT, 0:2 * NE].rearrange("p (t e) -> p t e", t=2)).then_inc(l_read, 1)
                dve.wait_ge(l_read, c + NOW)
                step(c, 0, nc.vector.tensor_reduce(lmax[b][:, :], lg[b][:, :, :], AX_X, ALU.max))
                step(c, 1, nc.vector.tensor_tensor(les[b][:, :, :], lg[b][:, :, :], lmax[b][:, :].unsqueeze(2).to_broadcast([TT, 2, NE]), ALU.subtract))

            def routing2(c, b):
                dve.wait_ge(exped, c + NOW)
                step(c, 3, nc.vector.tensor_reduce(esum[b][:, :], ex[b][:, :, :], AX_X, ALU.add))
                step(c, 2, nc.vector.reciprocal(erec[b][:, :], esum[b][:, :]))
                step(c, 4, nc.vector.tensor_tensor(pr[b][:, :, :], ex[b][:, :, :], erec[b][:, :].unsqueeze(2).to_broadcast([TT, 2, NE]), ALU.mult))
                for t in range(2):
                    own = pr[b][:, t, :].unsqueeze(2).to_broadcast([TT, NE, NE])
                    others = pr[b][:, t, None, :].to_broadcast([TT, NE, NE])
                    nc.vector.tensor_tensor(cnt[b][:, t * NE:(t + 1) * NE, :], others, own, ALU.is_gt)
                    last = nc.vector.tensor_tensor(eq[b][:, t * NE:(t + 1) * NE, :], others, own, ALU.is_equal)
                step(c, 5, last)
                for t in range(2):
                    last = nc.vector.tensor_tensor(eq[b][:, t * NE:(t + 1) * NE, :], eq[b][:, t * NE:(t + 1) * NE, :], before[:, :, :], ALU.mult)
                step(c, 6, last)
                step(c, 7, nc.vector.tensor_tensor(cnt[b][:], cnt[b][:], eq[b][:], ALU.add))
                step(c, 8, nc.vector.tensor_reduce(sel[b][:].rearrange("p t e -> p (t e)"), cnt[b][:], AX_X, ALU.add))
                step(c, 9, nc.vector.scalar_tensor_tensor(psel[b][:], sel[b][:], 2.0, pr[b][:], ALU.is_lt, ALU.mult))
                step(c, 10, nc.vector.tensor_reduce(ps[b][:, :], psel[b][:], AX_X, ALU.add))
                step(c, 11, nc.vector.tensor_scalar(pg[b][:, :], ps[b][:, :], 1e-12, None, ALU.max))
                step(c, 12, nc.vector.reciprocal(pgr[b][:, :], pg[b][:, :]))
                dve.wait_ge(combT_made, c + OLD)
                nc.vector.tensor_tensor(comb[b][:], psel[b][:], pgr[b][:, :].unsqueeze(2).to_broadcast([TT, 2, NE]), ALU.mult).then_inc(comb_ready, 1)

            ln.dve_start(dve)
            dve.wait_ge(weights, 16 * len(loads))
            dve.wait_ge(loaded[0], 16)
            ln.dve_centre(dve, 0, 0)
            ln.dve_norm(dve, 0, 0)
            routing1(0, 0)
            routing2(0, 0)

            def body(c, b, r, more):
                for e in range(NE):
                    n = c * NE + e
                    dve.wait_ge(e_gelu, n + NOW)
                    dve.wait_ge(e_cb, n + NOW)
                    dve.wait_ge(e_down, n + OLD)
                    nc.vector.tensor_tensor(gw[e % 2][:, :, :], g[e % 2][:, :, :], c_ps[:, None, 0:CW].to_broadcast([P, 2, CW]), ALU.mult).then_inc(e_weighted, 1)
                    if more:
                        if e == 1:
                            dve.wait_ge(loaded[1 - b], r * 16 + (b * 16 + 16))
                            ln.dve_centre(dve, c + 1, 1 - b)
                        if e == 4:
                            ln.dve_norm(dve, c + 1, 1 - b)
                        if e == 5:
                            routing1(c + 1, 1 - b)
                        if e == 6:
                            routing2(c + 1, 1 - b)
                dve.wait_ge(y_made, c + OLD)
                nc.vector.tensor_tensor(t1[b][:, :, :], x[b][:, :, :], ln.out[b][:, :, :], ALU.add).then_inc(summed_x, 1)
                dve.wait_ge(summed_x, c + NOW)
                dve.wait_ge(e_down, c * NE + (NE - 1 + NOW))
                dve.wait_ge(saved[b], r * 16 + 16)
                for h in range(2):
                    last = nc.vector.tensor_tensor(y[b][:, h, :], t1[b][:, h, :], o_ps[h][:, 0:CW], ALU.add)
                last.then_inc(y_made, 1)
            chunks(dve, body)


def token_weights(nc, name, x_d, t_d, row_d, c_d, wr_d, br_d):
    with Phase(nc, name) as ph:
        x = [ph.sb(f"x{b}", [P, 2, CW]) for b in range(2)]
        ones, wr, wrb, br = ph.sb("ones", [P, P]), ph.sb("wr", [P, 2]), ph.sb("wrb", [P, 2, 32]), ph.sb("br", [32, 1])
        row = [ph.sb(f"row{b}", [32, CW]) for b in range(2)]
        r_ps = [ph.ps(f"r_ps{b}", [P, 512]) for b in range(2)]
        weights, wide = ph.sem("weights"), ph.sem("wide")
        loaded, saved, out_saved = ([ph.sem(f"{n}{b}") for b in range(2)] for n in ("loaded", "saved", "out_saved"))
        made, copied = (ph.loop_sem(n) for n in ("made", "copied"))
        out_sent = ph.sem("out_sent")
        ln = Norm(nc, ph, x, ones, [made, out_sent])
        loads = [(ones, c_d["mean"]), (wr, wr_d), (br, br_d.partition_broadcast(32))]
        nc.sync.sem_inc(out_sent, START - 1)
        block = ph.block()

        @block.sync
        def _(sp):
            for b in range(2):
                sp.sem_inc(saved[b], 16)
                sp.sem_inc(out_saved[b], 16)
                sp.dma_start(x[b][:, :, :], x_d[:, :, b * CW:(b + 1) * CW]).then_inc(loaded[b], 16)
            for dst, src in loads:
                sp.dma_start(dst[:], src).then_inc(weights, 16)

            def body(c, b, r, more):
                if more:
                    sp.wait_ge(ln.centred, c + NOW)
                    sp.dma_start(x[b][:, :, :], x_d[:, :, ds((c + 2) * CW, CW)]).then_inc(loaded[b], 16)
                sp.wait_ge(out_saved[1 - b], r * 16 + (b * 16 + 16))
                sp.sem_inc(out_sent, 1)
                sp.wait_ge(ln.normed, c + NOW)
                sp.dma_start(t_d[:, :, ds(c * CW, CW)], ln.out[b][:, :, :]).then_inc(out_saved[b], 16)
                sp.wait_ge(copied, c + NOW)
                sp.dma_start(row_d[ds(c * CW, CW)].rearrange("(o n) -> o n", o=1), row[b][0:1, :]).then_inc(saved[b], 16)
            chunks(sp, body, 2)
            for b in range(2):
                sp.wait_ge(out_saved[b], 16 * ((NCH + 1 - b) // 2) + 16)
                sp.wait_ge(saved[b], 16 * ((NCH + 1 - b) // 2) + 16)

        @block.tensor
        def _(pe):
            pe.wait_ge(weights, 16 * len(loads))
            pe.wait_ge(loaded[0], 16)
            ln.pe_mean(pe, 0, 0)
            ln.pe_var(pe, 0, 0)
            pe.wait_ge(wide, 1)

            def body(c, b, r, more):
                if more:
                    pe.wait_ge(loaded[1 - b], r * 16 + (b * 16 + 16))
                    ln.pe_mean(pe, c + 1, 1 - b)
                pe.wait_ge(ln.normed, c + NOW)
                pe.wait_ge(copied, c + OLD)
                for k in range(2):
                    mm = nc.tensor.matmul(r_ps[b][0:32, 0:CW], wrb[:, k, :], ln.out[b][:, k, :], start=(k == 0), stop=(k == 1))
                mm.then_inc(made, 1)
                if more:
                    ln.pe_var(pe, c + 1, 1 - b)
            chunks(pe, body)

        @block.scalar
        def _(act):
            act.wait_ge(weights, 16 * len(loads))
            ln.act_square(act, 0, 0)
            ln.act_root(act, 0, 0)

            def body(c, b, r, more):
                if more:
                    ln.act_square(act, c + 1, 1 - b)
                act.wait_ge(made, c + NOW)
                act.wait_ge(saved[b], r * 16 + 16)
                nc.scalar.activation(row[b][:, :], r_ps[b][0:32, 0:CW], ACT.Identity, bias=br[:, 0:1]).then_inc(copied, 1)
                if more:
                    ln.act_root(act, c + 1, 1 - b)
            chunks(act, body)

        @block.vector
        def _(dve):
            ln.dve_start(dve)
            dve.wait_ge(weights, 16 * len(loads))
            nc.vector.tensor_copy(wrb[:, :, :], wr[:, :].unsqueeze(2).to_broadcast([P, 2, 32])).then_inc(wide, 1)
            dve.wait_ge(loaded[0], 16)
            ln.dve_centre(dve, 0, 0)
            ln.dve_norm(dve, 0, 0)

            def body(c, b, r, more):
                if more:
                    dve.wait_ge(loaded[1 - b], r * 16 + (b * 16 + 16))
                    ln.dve_centre(dve, c + 1, 1 - b)
                    ln.dve_norm(dve, c + 1, 1 - b)
            chunks(dve, body)


KEPT = N // 2 - 1


def choose_tokens(nc, name, row_d, factor_d, c_d):
    with Phase(nc, name) as ph:
        row, col = ph.sb("row", [TT, N]), ph.sb("col", [TT, NT])
        tri = ph.sb("tri", [TT, TT])
        junk = [ph.sb(f"junk{b}", [TT, N]) for b in range(2)]
        diag = [ph.sb(f"diag{b}", [TT, TT]) for b in range(2)]
        parts = ph.sb("parts", [TT, 4, NT])
        total, factor = ph.sb("total", [TT, 3, NT]), ph.sb("factor", [TT, NT])
        loaded, step, saved, done = ph.sem("loaded"), ph.sem("step"), ph.sem("saved"), ph.sem("compared")
        block = ph.block()

        @block.sync
        def _(sp):
            sp.dma_start(row[:, :], row_d.partition_broadcast(TT)).then_inc(loaded, 16)
            sp.dma_start(col[:, :], row_d.rearrange("(t p) -> p t", p=TT), allow_slow_non_contiguous=True).then_inc(loaded, 16)
            sp.dma_start(tri[:, :], c_d["tri"][0:TT, 0:TT]).then_inc(loaded, 16)
            sp.wait_ge(step, 5)
            sp.dma_start(factor_d.rearrange("(t p) -> p t", p=TT), factor[:, :], allow_slow_non_contiguous=True).then_inc(saved, 16)
            sp.wait_ge(saved, 16)

        @block.vector
        def _(dve):
            dve.wait_ge(loaded, 48)
            nc.vector.memset(parts[:, :, :], 0.0).then_inc(step, 1)
            dve.wait_ge(step, 1)
            for t in range(NT):
                a, z = t * TT, (t + 1) * TT
                own = col[:, t:t + 1]
                if t >= 2:
                    dve.wait_ge(done, t - 1)
                if t:
                    nc.vector.tensor_scalar(junk[t % 2][:, 0:a], row[:, 0:a], own, 0.0, ALU.is_ge, ALU.add, accum_out=parts[:, 0, t:t + 1])
                if z < N:
                    nc.vector.tensor_scalar(junk[t % 2][:, z:N], row[:, z:N], own, 0.0, ALU.is_gt, ALU.add, accum_out=parts[:, 1, t:t + 1])
                nc.vector.tensor_scalar(junk[t % 2][:, a:z], row[:, a:z], own, 0.0, ALU.is_gt, ALU.add, accum_out=parts[:, 2, t:t + 1])
                nc.vector.scalar_tensor_tensor(diag[t % 2][:, :], row[:, a:z], own, tri[:, :], ALU.is_equal, ALU.mult,
                                               accum_out=parts[:, 3, t:t + 1]).then_inc(done, 1)
            dve.wait_ge(done, NT)
            nc.vector.tensor_tensor(total[:, 0, :], parts[:, 0, :], parts[:, 1, :], ALU.add).then_inc(step, 1)
            nc.vector.tensor_tensor(total[:, 1, :], parts[:, 2, :], parts[:, 3, :], ALU.add).then_inc(step, 1)
            dve.wait_ge(step, 3)
            nc.vector.tensor_tensor(total[:, 2, :], total[:, 0, :], total[:, 1, :], ALU.add).then_inc(step, 1)
            dve.wait_ge(step, 4)
            nc.vector.scalar_tensor_tensor(factor[:, :], total[:, 2, :], float(KEPT), col[:, :], ALU.is_lt, ALU.mult).then_inc(step, 1)


def chosen_forward(nc, name, t_d, x_d, factor_d, out_d, w1_d, b1_d, w2_d, b2_d):
    F = 4 * D
    FG = F // P
    with Phase(nc, name) as ph:
        t, x, y = ([ph.sb(f"{n}{b}", [P, 2, CW]) for b in range(2)] for n in ("t", "x", "y"))
        fac = [ph.sb(f"fac{b}", [P, CW]) for b in range(2)]
        g = [ph.sb(f"g{b}", [P, FG, CW]) for b in range(2)]
        w1, w2, b1, b2 = ph.sb("w1", [P, 2, F]), ph.sb("w2", [P, FG, D]), ph.sb("b1", [P, FG]), ph.sb("b2", [P, 2])
        f_ps = [ph.ps(f"f_ps{i}", [P, 512]) for i in range(4)]
        y_ps = [ph.ps(f"y_ps{b}", [P, 512]) for b in range(2)]
        weights = ph.sem("weights")
        loaded, saved = ([ph.sem(f"{n}{b}") for b in range(2)] for n in ("loaded", "saved"))
        y_made, y_scaled, y_t, y_x = (ph.loop_sem(n) for n in ("y_made", "y_scaled", "plus_t", "plus_x"))
        up = [ph.loop_sem(f"up{m}") for m in range(4)]
        gelu = [ph.loop_sem(f"gelu{m}") for m in range(4)]
        loads = [(w1, w1_d), (b1, b1_d), (w2, w2_d), (b2, b2_d)]
        block = ph.block()

        @block.sync
        def _(sp):
            for b in range(2):
                sp.sem_inc(saved[b], 16)

            def load(c, b):
                sp.dma_start(t[b][:, :, :], t_d[:, :, ds(c * CW, CW)]).then_inc(loaded[b], 16)
                sp.dma_start(x[b][:, :, :], x_d[:, :, ds(c * CW, CW)]).then_inc(loaded[b], 16)
                sp.dma_start(fac[b][:, :], factor_d[ds(c * CW, CW)].partition_broadcast(P)).then_inc(loaded[b], 16)
            load(0, 0)
            for dst, src in loads:
                sp.dma_start(dst[:], src).then_inc(weights, 16)

            def body(c, b, r, more):
                if more:
                    sp.wait_ge(y_x, c + PREV)
                    load(c + 1, 1 - b)
                sp.wait_ge(y_x, c + NOW)
                sp.dma_start(out_d[:, :, ds(c * CW, CW)], y[b][:, :, :]).then_inc(saved[b], 16)
            chunks(sp, body)
            for b in range(2):
                sp.wait_ge(saved[b], 16 * ((NCH + 1 - b) // 2) + 16)

        @block.tensor
        def _(pe):
            pe.wait_ge(weights, 16 * len(loads))

            def body(c, b, r, more):
                pe.wait_ge(loaded[b], r * 48 + 48)
                for m in range(4):
                    pe.wait_ge(gelu[m], c + PREV)
                    for h in range(2):
                        for k in range(2):
                            g0 = (2 * m + h) * P
                            mm = nc.tensor.matmul(f_ps[m][:, h * CW:(h + 1) * CW], w1[:, k, g0:g0 + P], t[b][:, k, :], start=(k == 0), stop=(k == 1))
                    mm.then_inc(up[m], 1)
                pe.wait_ge(y_scaled, c + OLD)
                for m in range(4):
                    pe.wait_ge(gelu[m], c + NOW)
                for h in range(2):
                    for m in range(FG):
                        mm = nc.tensor.matmul(y_ps[b][:, h * CW:(h + 1) * CW], w2[:, m, h * P:(h + 1) * P], g[b][:, m, :], start=(m == 0), stop=(m == FG - 1))
                mm.then_inc(y_made, 1)
            chunks(pe, body)

        @block.scalar
        def _(act):
            act.wait_ge(weights, 16 * len(loads))

            def body(c, b, r, more):
                act.wait_ge(y_made, c + OLD)
                for m in range(4):
                    act.wait_ge(up[m], c + NOW)
                    for h in range(2):
                        last = nc.scalar.activation(g[b][:, 2 * m + h, :], f_ps[m][:, h * CW:(h + 1) * CW], ACT.Gelu_apprx_tanh,
                                                    bias=b1[:, 2 * m + h:2 * m + h + 1])
                    last.then_inc(gelu[m], 1)
            chunks(act, body)

        @block.vector
        def _(dve):
            dve.wait_ge(weights, 16 * len(loads))

            def body(c, b, r, more):
                dve.wait_ge(y_made, c + NOW)
                dve.wait_ge(loaded[b], r * 48 + 48)
                dve.wait_ge(saved[b], r * 16 + 16)
                for h in range(2):
                    last = nc.vector.scalar_tensor_tensor(y[b][:, h, :], y_ps[b][:, h * CW:(h + 1) * CW], b2[:, h:h + 1], fac[b][:, :], ALU.add, ALU.mult)
                last.then_inc(y_scaled, 1)
                dve.wait_ge(y_scaled, c + NOW)
                nc.vector.tensor_tensor(y[b][:, :, :], y[b][:, :, :], t[b][:, :, :], ALU.add).then_inc(y_t, 1)
                dve.wait_ge(y_t, c + NOW)
                nc.vector.tensor_tensor(y[b][:, :, :], y[b][:, :, :], x[b][:, :, :], ALU.add).then_inc(y_x, 1)
            chunks(dve, body)


def attention_weights(nc, name, sorted_d, prev_d, a_d, hist_d, base_d, max_d, pair_d, ev_d, c_d):
    FAR = -1e30
    with Phase(nc, name) as ph:
        ident = ph.sb("ident", [P, P])
        meta, pair = ph.sb("meta", [P, ET, 3]), ph.sb("pair", [P, ET, 2])
        prev, same, pen = ph.sb("prev", [P, ET]), ph.sb("same", [P, ET]), ph.sb("pen", [P, ET])
        idx = ph.sb("idx", [P, ET], I32)
        a1 = ph.sb("a1", [P, ET])
        zero = ph.sb("zero", [P, ET])
        loc, acc, mx = ph.sb("loc", [P, ET]), ph.sb("acc", [P, ET]), ph.sb("mx", [P, ET])
        fill = [ph.sb(f"fill{n}", [P, ET]) for n in range(2)]
        v, vl, d, dm, ev = (ph.sb(n, [P, ET]) for n in ("v", "vl", "d", "dm", "ev"))
        edge, rowp, rows = ph.sb("edge", [P, 2]), ph.sb("rowp", [1, 2, P]), ph.sb("rows", [1, 4, P + 1])
        cin = ph.sb("cin", [P, 3])
        ib = [ph.sb(f"ib{b}", [P, EB], I32) for b in range(2)]
        gb = [ph.sb(f"gb{b}", [P, EB]) for b in range(2)]
        base, hist, first, mask, at, amax, a0, s, sl = (ph.sb(n, [TT, NT]) for n in ("base", "hist", "first", "mask", "at", "amax", "a0", "s", "sl"))
        ends, put = ph.sb("ends", [TT, NT], I32), ph.sb("put", [TT, NT], I32)
        nodes = ph.sb("nodes", [TT, NT, 2])
        x_ps = ph.ps("x_ps", [P, 512])
        c_ps = ph.ps("c_ps", [P, 512])
        loaded, prep, gate, batches, saved = (ph.sem(n) for n in ("loaded", "prep", "gate", "batches", "saved"))
        landed = [ph.sem(f"landed{b}") for b in range(2)]
        index_in, values_out = ph.loop_sem("index_in"), ph.loop_sem("values_out")
        max_saved, max_got, put_ready, placed, pair_in, ends_ready = (ph.sem(n) for n in ("max_saved", "max_got", "put_ready", "placed", "pair_in", "ends_ready"))
        ends_of_parts = ph.sem("ends_of_parts")
        turned, line, back, carried, dv = (ph.sem(n) for n in ("turned", "line", "back", "carried", "dv"))
        exped, max_ready, ev_ready = ph.sem("exped"), ph.sem("max_ready"), ph.sem("ev_ready")
        block = ph.block()

        @block.sync
        def _(sp):
            sp.dma_start(ident[:, :], c_d["ident"]).then_inc(loaded, 16)
            sp.dma_start(meta[:, :, :], sorted_d.rearrange("(p j) c -> p j c", j=ET)).then_inc(loaded, 16)
            sp.dma_start(base[:, :], base_d[0:N].rearrange("(t p) -> p t", p=TT), allow_slow_non_contiguous=True).then_inc(loaded, 16)
            sp.dma_start(hist[:, :], hist_d[0:N].rearrange("(t p) -> p t", p=TT), allow_slow_non_contiguous=True).then_inc(loaded, 16)
            sp.dma_start(a0[:, :], a_d[1].rearrange("(t p) -> p t", p=TT), allow_slow_non_contiguous=True).then_inc(loaded, 16)
            sp.wait_ge(dv, 1)
            sp.dma_start(prev_d[1:1 + EP].rearrange("(p j) -> p j", j=ET), loc[:, :]).then_inc(saved, 16)
            sp.wait_ge(dv, 2)
            sp.dma_start(prev_d[0:1].rearrange("(a o) -> a o", a=1), cin[0:1, 0:1]).then_inc(saved, 16)
            for n in range(2):
                sp.dma_start(pair_d.rearrange("(p j) c -> p (j c)", j=ET)[:, n * ET:(n + 1) * ET], zero[:, :]).then_inc(saved, 16)
            sp.wait_ge(saved, 64)
            sp.dma_start(prev[:, :], prev_d[0:EP].rearrange("(p j) -> p j", j=ET)).then_inc(loaded, 16)
            sp.wait_ge(max_ready, 1)
            sp.dma_start(max_d.rearrange("(p j) -> p j", j=ET), mx[:, :]).then_inc(max_saved, 16)
            sp.wait_ge(placed, 16 * NT)
            sp.dma_start(pair[:, :, :], pair_d.rearrange("(p j) c -> p j c", j=ET)).then_inc(pair_in, 16)
            sp.wait_ge(ev_ready, 1)
            sp.dma_start(ev_d.rearrange("(p j) -> p j", j=ET), ev[:, :]).then_inc(pair_in, 16)
            sp.wait_ge(pair_in, 32)

        @block.gpsimd
        def _(pool):
            with pool.Fori(0, NEB // 2) as i:
                for b in range(2):
                    pool.wait_ge(index_in, i * 2 + (b + NOW))
                    pool.wait_ge(values_out, i * 2 + (b + OLD))
                    pool.sem_inc(gate, 1)
                    for j in range(EB):
                        nc.gpsimd.indirect_dma_start(gb[b][:, j:j + 1], None, a_d[0].rearrange("(n o) -> n o", o=1),
                                                     bass.IndirectOffsetOnAxis(ib[b][:, j:j + 1], 0)).then_inc(landed[b], 16)
            pool.wait_ge(max_saved, 16)
            pool.wait_ge(ends_ready, 1)
            for t in range(NT):
                nc.gpsimd.indirect_dma_start(amax[:, t:t + 1], None, max_d.rearrange("(n o) -> n o", o=1),
                                             bass.IndirectOffsetOnAxis(ends[:, t:t + 1], 0)).then_inc(max_got, 16)
            pool.wait_ge(put_ready, 1)
            pool.wait_ge(saved, 64)
            for t in range(NT):
                nc.gpsimd.indirect_dma_start(pair_d, bass.IndirectOffsetOnAxis(put[:, t:t + 1], 0), nodes[:, t, :], None,
                                             bounds_check=EP - 1, oob_is_err=False).then_inc(placed, 16)
            pool.wait_ge(placed, 16 * NT)

        @block.tensor
        def _(pe):
            pe.wait_ge(loaded, 80)
            for n in range(3):
                pe.wait_ge(ends_of_parts, n + 1)
                for k in range(2):
                    mm = nc.tensor.transpose(x_ps[0:1, k * P:(k + 1) * P], edge[:, k:k + 1], ident[:, :])
                mm.then_inc(turned, 1)
                pe.wait_ge(line, n + 1)
                nc.tensor.transpose(c_ps[:, 0:1], rows[0:1, n, 0:P], ident[0:1, 0:1]).then_inc(back, 1)

        @block.vector
        def _(dve):
            count = [0]

            def step(ins):
                count[0] += 1
                ins.then_inc(dv, 1)
                dve.wait_ge(dv, count[0])

            def join(n, op0, op1, start, change, end):
                nc.vector.tensor_copy(edge[:, 0:1], change[:, ET - 1:ET])
                nc.vector.tensor_copy(edge[:, 1:2], end[:, ET - 1:ET]).then_inc(ends_of_parts, 1)
                dve.wait_ge(turned, n + 1)
                step(nc.vector.tensor_copy(rowp[0:1, :, :], x_ps[0:1, 0:2 * P].rearrange("p (k c) -> p k c", k=2)))
                step(nc.vector.memset(rows[0:1, n, 0:1], start))
                nc.vector.tensor_tensor_scan(rows[0:1, n, 1:P + 1], rowp[0:1, 0, :], rowp[0:1, 1, :], start, op0, op1).then_inc(line, 1)
                dve.wait_ge(back, n + 1)
                step(nc.vector.tensor_copy(cin[:, n:n + 1], c_ps[:, 0:1]))

            dve.wait_ge(loaded, 80)
            nc.vector.memset(zero[:, :], 0.0)
            step(nc.vector.tensor_copy(loc[:, :], meta[:, :, 0]))
            step(nc.vector.memset(cin[:, :], -1.0))
            nc.vector.tensor_copy(idx[:, :], meta[:, :, 1]).then_inc(batches, 1)
            with dve.Fori(0, NEB // 2) as i:
                for b in range(2):
                    dve.wait_ge(landed[b], i * (16 * EB) + 16 * EB)
                    nc.vector.tensor_copy(a1[:, ds(i * (2 * EB) + b * EB, EB)], gb[b][:, :]).then_inc(values_out, 1)
            dve.wait_ge(values_out, NEB - 1 + NOW)
            dve.wait_ge(loaded, 96)
            step(nc.vector.tensor_tensor(same[:, :], meta[:, :, 0], prev[:, :], ALU.is_equal))
            step(nc.vector.tensor_scalar(pen[:, :], same[:, :], -FAR, FAR, ALU.mult, ALU.add))
            nc.vector.tensor_tensor_scan(acc[:, :], pen[:, :], pen[:, :], 0.0, ALU.add, ALU.bypass)
            nc.vector.tensor_tensor_scan(loc[:, :], pen[:, :], a1[:, :], FAR, ALU.add, ALU.max).then_inc(carried, 1)
            dve.wait_ge(carried, 1)
            join(0, ALU.add, ALU.max, FAR, acc, loc)
            nc.vector.scalar_tensor_tensor(mx[:, :], acc[:, :], cin[:, 0:1], loc[:, :], ALU.add, ALU.max).then_inc(max_ready, 1)
            step(nc.vector.tensor_scalar(mask[:, :], hist[:, :], 1.0, None, ALU.min))
            step(nc.vector.tensor_tensor(first[:, :], base[:, :], hist[:, :], ALU.add))
            nc.vector.tensor_scalar(ends[:, :], first[:, :], -1.0, 0.0, ALU.add, ALU.max).then_inc(ends_ready, 1)
            step(nc.vector.tensor_scalar(at[:, :], mask[:, :], -float(2 * EP), float(2 * EP), ALU.mult, ALU.add))
            step(nc.vector.tensor_tensor(put[:, :], at[:, :], base[:, :], ALU.add))
            dve.wait_ge(max_got, 16 * NT)
            step(nc.vector.tensor_tensor(s[:, :], amax[:, :], a0[:, :], ALU.add))
            step(nc.vector.tensor_scalar(sl[:, :], s[:, :], 0.01, None, ALU.mult))
            step(nc.vector.tensor_tensor(nodes[:, :, 1], s[:, :], sl[:, :], ALU.max))
            nc.vector.tensor_copy(nodes[:, :, 0], a0[:, :]).then_inc(put_ready, 1)
            dve.wait_ge(pair_in, 16)
            step(nc.vector.tensor_tensor_scan(acc[:, :], same[:, :], same[:, :], 1.0, ALU.mult, ALU.bypass))
            for n in range(2):
                step(nc.vector.tensor_copy(loc[:, :], pair[:, :, n]))
                step(nc.vector.tensor_tensor_scan(d[:, :], same[:, :], loc[:, :], 0.0, ALU.mult, ALU.add))
                join(n + 1, ALU.mult, ALU.add, 0.0, acc, d)
                step(nc.vector.scalar_tensor_tensor(fill[n][:, :], acc[:, :], cin[:, n + 1:n + 2], d[:, :], ALU.mult, ALU.add))
            step(nc.vector.tensor_tensor(v[:, :], fill[0][:, :], a1[:, :], ALU.add))
            step(nc.vector.tensor_scalar(vl[:, :], v[:, :], 0.01, None, ALU.mult))
            step(nc.vector.tensor_tensor(v[:, :], v[:, :], vl[:, :], ALU.max))
            step(nc.vector.tensor_tensor(dm[:, :], v[:, :], fill[1][:, :], ALU.subtract))
            nc.vector.tensor_scalar(dm[:, :], dm[:, :], 0.0, None, ALU.min).then_inc(exped, 1)

        @block.scalar
        def _(act):
            act.wait_ge(batches, 1)
            with act.Fori(0, NEB // 2) as i:
                for b in range(2):
                    act.wait_ge(values_out, i * 2 + (b + OLD))
                    nc.scalar.activation(ib[b][:, :], idx[:, ds(i * (2 * EB) + b * EB, EB)], ACT.Copy).then_inc(index_in, 1)
            act.wait_ge(exped, 1)
            nc.scalar.activation(ev[:, :], dm[:, :], ACT.Exp).then_inc(ev_ready, 1)


def network(nc, a, out_d, parts=None):
    parts = parts or {}

    def dram(name, shape):
        return parts.get(name) or nc.dram_tensor(name, shape, F32).ap()
    fm = [P, 2, N]
    c_d = {n: a[f"c_{n}"] for n in ("mean", "ident", "identb", "iota", "upper", "blocks1", "blocks2", "tri", "pick", "before")}
    xn, xn_rows = dram("xn", fm), dram("xn_rows", [N, D])
    norm_table(nc, "norm0", a["x"], xn, xn_rows, c_d)
    orders = [[dram(f"hist_{n}", [NODES]), dram(f"first_{n}", [NODES]), dram(f"sorted_{n}", [EP, 3])] for n in ("dst", "src")]
    sort_edges(nc, "sort", (a["dst"], a["src"]), a["edge_weight"], orders, c_d)

    hist, first, by_dst = orders[0]
    running, agg = nc.dram_tensor("running0", [EP, D], F32).ap(), dram("agg", fm)
    sum_edges(nc, "sum0", by_dst, None, xn_rows, running, D, c_d)
    carry = nc.dram_tensor("carry0", [ET, D], F32).ap()
    tile_carries(nc, "carry0", by_dst, running, carry, D, c_d)
    node_rows(nc, "rows0", running, carry, D, hist, first, agg, c_d)

    xs, qT = dram("mix0", fm), dram("qT0", fm)
    with Phase(nc, "copy") as ph:
        copied = ph.sem("copied")
        block = ph.block()

        @block.sync
        def _(sp):
            sp.dma_start(xs, xn).then_inc(copied, 16)
            sp.wait_ge(copied, 16)
    mixer = nc.alloc_sbuf_tensor("mixer", [P, 2, D], F32)
    with nc.Fori(0, 4) as layer:
        def of(name):
            w = a[f"L0_mix_{name}"][ds(layer, 1)]
            return w.rearrange("l p h c -> (l p) h c" if len(w.shape) == 4 else "l p h -> (l p) h")
        attend_first(nc, "attend0", 2, P, 32, 32 ** -0.25, xs, qT, mixer, c_d, of("ln1_g"), of("ln1_b"), of("Wq"), of("Wk"), of("Wv"), of("Wo"))
        attend_second(nc, "forward0", 2, P, xs, qT, mixer, xs, c_d, of("bo"), of("ln2_g"), of("ln2_b"), of("W1"), of("b1"), of("W2"), of("b2"))
    x1 = dram("x1", fm)
    g = {n: a[f"L0_gnn_{n}"] for n in ("eps_weight", "w1", "w2", "gamma1", "beta1", "gamma_h", "beta_h")}
    message_layer(nc, "message0", agg, a["x"], xn, xs, x1, dram("z", fm), dram("u", fm), hist, c_d, g["eps_weight"], g["w1"], g["w2"],
                  g["gamma1"], g["beta1"], g["gamma_h"], g["beta_h"])
    x2 = dram("x2", fm)
    experts(nc, "experts", x1, x2, c_d, *(a[f"L0_ffn_{n}"] for n in ("router_w", "w1", "b1", "w2", "b2")))

    hist, first, by_src = orders[1]
    xn1, h_rows, scores = dram("xn1", fm), dram("h_rows", [N, D]), dram("scores", [2, N])
    norm_table(nc, "norm1", x2, xn1, h_rows, c_d, a["L1_gnn_W_layer"], a["L1_gnn_b_layer"], a["L1_gnn_w_a"], a["L1_gnn_b_a"], scores)
    ev, g1 = dram("ev", [EP]), dram("g1", fm)
    attention_weights(nc, "edges1", by_src, nc.dram_tensor("prev", [EP + 1], F32).ap(), scores, hist, first, nc.dram_tensor("maxs", [EP], F32).ap(),
                      nc.dram_tensor("pairs", [EP, 2], F32).ap(), ev, c_d)
    running = nc.dram_tensor("running1", [EP, D + 1], F32).ap()
    sum_edges(nc, "sum1", by_src, ev, h_rows, running, D + 1, c_d)
    carry = nc.dram_tensor("carry1", [ET, D + 1], F32).ap()
    tile_carries(nc, "carry1", by_src, running, carry, D + 1, c_d)
    node_rows(nc, "rows1", running, carry, D + 1, hist, first, g1, c_d)

    m = {n[7:]: v for n, v in a.items() if n.startswith("L1_mix_")}
    qT1, x3 = dram("qT1", [32, 1, N]), dram("x3", fm)
    attend_first(nc, "attend1", 1, 32, 4, 1.0, xn1, qT1, mixer, c_d, m["ln1_g"], m["ln1_b"], m["Wq"], m["Wk"], m["Wv"], m["Wo"], m["Wx"], m["bx"])
    attend_second(nc, "forward1", 1, 32, xn1, qT1, mixer, x3, c_d, m["bo"], m["ln2_g"], m["ln2_b"], m["W1"], m["b1"], m["W2"], m["b2"], (x2, g1))
    t, row, factor = dram("t", fm), dram("row", [N]), dram("factor", [N])
    token_weights(nc, "tokens", x3, t, row, c_d, a["L1_ffn_wr"], a["L1_ffn_br"])
    choose_tokens(nc, "choose", row, factor, c_d)
    chosen_forward(nc, "chosen", t, x3, factor, out_d, *(a[f"L1_ffn_{n}"] for n in ("w1", "b1", "w2", "b2")))


def laid_out(inputs):
    x = {k: np.asarray(v) for k, v in inputs.items()}

    def wide(v):
        return v.reshape(*v.shape[:-2], -1, P, v.shape[-1]).swapaxes(-3, -2)

    def per_channel(v):
        return v.reshape(*v.shape[:-1], -1, P).swapaxes(-2, -1)

    def edges(v, pad):
        return np.concatenate([v, np.full(EP - E, pad, v.dtype)]).reshape(ET, P).T

    a = {"x": wide(x["x"].T), "edge_weight": edges(x["edge_weight"], 0)}
    a["src"], a["dst"] = edges(x["src"], N), edges(x["dst"], N)
    for n in ("w1", "w2"):
        a[f"L0_gnn_{n}"] = wide(x[f"L0_gnn_{n}"].T)
    for n in ("gamma1", "beta1", "gamma_h", "beta_h"):
        a[f"L0_gnn_{n}"] = per_channel(x[f"L0_gnn_{n}"])
    a["L0_gnn_eps_weight"] = x["L0_gnn_eps_weight"]
    for n in ("Wq", "Wk", "Wv", "Wo", "W1", "W2"):
        a[f"L0_mix_{n}"] = wide(x[f"L0_mix_{n}"])
    for n in ("bo", "ln1_g", "ln1_b", "b1", "b2", "ln2_g", "ln2_b"):
        a[f"L0_mix_{n}"] = per_channel(x[f"L0_mix_{n}"])
        a[f"L1_mix_{n}"] = per_channel(x[f"L1_mix_{n}"])
    a["L0_ffn_router_w"] = wide(x["L0_ffn_router_w"].T)
    for n in ("w1", "w2"):
        a[f"L0_ffn_{n}"] = wide(x[f"L0_ffn_{n}"]).transpose(1, 0, 2, 3)
    a["L0_ffn_b1"] = per_channel(x["L0_ffn_b1"]).transpose(1, 0, 2)
    a["L0_ffn_b2"] = x["L0_ffn_b2"]
    a["L1_gnn_W_layer"] = wide(x["L1_gnn_W_layer"].T)
    a["L1_gnn_b_layer"] = x["L1_gnn_b_layer"]
    a["L1_gnn_w_a"] = np.concatenate([x["L1_gnn_w_a2"], x["L1_gnn_w_a1"]])
    a["L1_gnn_b_a"] = np.concatenate([x["L1_gnn_b_a2"], x["L1_gnn_b_a1"]])
    for n in ("Wx", "Wo", "W1", "W2"):
        a[f"L1_mix_{n}"] = wide(x[f"L1_mix_{n}"])
    for n in ("Wq", "Wk", "Wv"):
        a[f"L1_mix_{n}"] = x[f"L1_mix_{n}"]
    a["L1_mix_bx"] = per_channel(x["L1_mix_bx"])
    a["L1_ffn_wr"] = per_channel(x["L1_ffn_wr"][:, 0])
    a["L1_ffn_br"] = x["L1_ffn_br"]
    for n in ("w1", "w2"):
        a[f"L1_ffn_{n}"] = wide(x[f"L1_ffn_{n}"])
    for n in ("b1", "b2"):
        a[f"L1_ffn_{n}"] = per_channel(x[f"L1_ffn_{n}"])
    p, q = np.arange(P)[:, None], np.arange(P)[None, :]
    f = np.float32
    head = (p // 32 == q // 32).astype(f)
    a["c_mean"] = np.full((P, P), 1 / D, f)
    a["c_ident"] = np.eye(P, dtype=f)
    a["c_identb"] = np.eye(P).astype(_mybir_bf16())
    a["c_iota"] = np.broadcast_to(q, (P, P)).astype(f)
    a["c_tri"], a["c_upper"] = (q < p).astype(f), (p < q).astype(f)
    a["c_blocks2"] = np.stack([head, head], 1)
    a["c_blocks1"] = (np.arange(32)[:, None] // 4 == np.arange(D)[None, :] // 32).astype(f)[:, None, :]
    e8 = np.arange(8)
    a["c_pick"] = np.broadcast_to((e8[:, None] == e8[None, :])[:, :, None], (8, 8, P)).astype(f)
    a["c_before"] = np.broadcast_to((e8[None, :] < e8[:, None])[None], (TT, 8, 8)).astype(f)
    return {k: np.ascontiguousarray(v) for k, v in a.items()}


def _mybir_bf16():
    return mybir.dt.np(BF16)


def kernel(**inputs):
    import concourse.bacc as bacc
    from concourse.bass_utils import run_bass_kernel_spmd

    nc = bacc.Bacc("TRN2", target_bir_lowering=False, num_devices=1)
    arrays = {f"in_{k}": v for k, v in laid_out(inputs).items()}
    aps = {k[3:]: nc.dram_tensor(k, v.shape, mybir.dt.from_np(v.dtype), kind="ExternalInput").ap() for k, v in arrays.items()}
    out = nc.dram_tensor("out", [P, 2, N], F32, kind="ExternalOutput").ap()
    network(nc, aps, out)
    r = run_bass_kernel_spmd(nc, [arrays], core_ids=[0])
    return r.results[0]["out"].transpose(1, 0, 2).reshape(D, N).T
```

```python
from contextlib import ExitStack, contextmanager
import numpy as np
import concourse.bass as bass
from concourse import mybir

F32 = mybir.dt.float32
I32 = mybir.dt.int32
BF16 = mybir.dt.bfloat16
ALU = mybir.AluOpType
ACT = mybir.ActivationFunctionType
AX_X = mybir.AxisListType.X
ds = bass.ds
P = 128

N = 6250
D = 256
H2 = D // P
E = 100000
TT = 125
CW = 2 * TT
NCH = N // CW
NT = N // TT
ET = 784
EP = ET * P
EB = 14
NEB = ET // EB
HI = 49
NODES = HI * P


START, NOW, PREV, OLD = 2, 3, 2, 1

CR = 2


class Phase:

    def __init__(self, nc, name):
        self.nc, self.name, self.ctx, self.sems = nc, name, ExitStack(), []
        self.loops = []

    def __enter__(self):
        self.ctx.__enter__()
        return self

    def sb(self, name, shape, dt=F32):
        return self.ctx.enter_context(self.nc.sbuf_tensor(f"{self.name}_{name}", shape, dt))

    def ps(self, name, shape, dt=F32):
        return self.ctx.enter_context(self.nc.psum_tensor(f"{self.name}_{name}", shape, dt))

    def sem(self, name):
        s = self.nc.alloc_semaphore(f"{self.name}_{name}")
        self.sems.append(s)
        return s

    def loop_sem(self, name):
        s = self.sem(name)
        self.loops.append(s)
        return s

    def block(self):
        for s in self.loops:
            self.nc.sync.sem_inc(s, START)
        self.nc.all_engine_barrier()
        return self.ctx.enter_context(self.nc.Block())

    def __exit__(self, *exc):
        self.ctx.__exit__(*exc)
        if exc[0] is None and self.sems:
            self.nc.clear_and_free_semaphores(self.sems)
            self.nc.all_engine_barrier()


SB = 32
SW = NCH * SB


class Scatter:

    def __init__(self, nc, ph, place, record, sorted_d):
        self.nc, self.place, self.record, self.sorted_d = nc, place, record, sorted_d
        self.pb = [ph.sb(f"pb{b}", [P, SB], I32) for b in range(2)]
        self.rb = [ph.sb(f"rb{b}", [P, SB, 3]) for b in range(2)]
        self.scattered = [ph.sem(f"scattered{b}") for b in range(2)]
        self.batch_in, self.batch_out = ph.loop_sem("batch_in"), ph.loop_sem("batch_out")
        self.gate = ph.sem("scatter_gate")

    def tiles(self, c):
        return min(SB, ET - c * SB) if isinstance(c, int) else SB

    def pool(self, pool, c, b, r):
        pool.wait_ge(self.batch_in, c + NOW)
        pool.sem_inc(self.gate, 1)
        for j in range(self.tiles(c)):
            self.nc.gpsimd.indirect_dma_start(self.sorted_d, bass.IndirectOffsetOnAxis(self.pb[b][:, j:j + 1], 0), self.rb[b][:, j, :],
                                              None).then_inc(self.scattered[b], 16)
        pool.wait_ge(self.scattered[b], r * (16 * SB) + 16 * self.tiles(c))
        pool.sem_inc(self.batch_out, 1)

    def dve(self, dve, c, b):
        n = SB
        dve.wait_ge(self.batch_out, c + OLD)
        self.nc.vector.tensor_copy(self.pb[b][:, 0:n], self.place[:, ds(c * SB, n)])
        self.nc.vector.tensor_copy(self.rb[b][:, 0:n, :], self.record[:, ds(c * SB, n), :]).then_inc(self.batch_in, 1)


MB = 4


def sort_edges(nc, name, keys, weights, orders, place1, record1, norm_d, xn_d, xs_d, c_d):
    S = range(2)
    with Phase(nc, name) as ph:
        kin = [ph.sb(f"kin{s}", [P, ET], I32) for s in S]
        win = ph.sb("win", [P, ET])
        hi_i, lo_i = ([ph.sb(f"{n}{s}", [P, ET], I32) for s in S] for n in ("hi_i", "lo_i"))
        meta = [ph.sb("meta0", [P, ET + EB, 3]), record1]
        lo, hi = ([ph.sb(f"{n}{s}", [P, ET + EB], BF16) for s in S] for n in ("lo", "hi"))
        iota_f, iotas, id_t, idb_t = ph.sb("iota_f", [P, P]), ph.sb("iotas", [P, P, EB], BF16), ph.sb("ident", [P, P]), ph.sb("identb", [P, P], BF16)
        tri_t, upper_t = ph.sb("tri", [P, P]), ph.sb("upper", [P, P])
        onelo = [ph.sb(f"onelo{s}", [P, 2, P, EB], BF16) for s in S]
        onehi = [ph.sb(f"onehi{s}", [P, 2, HI, EB], BF16) for s in S]
        hist, scan, base, part = ([ph.sb(f"{n}{s}", [HI, P]) for s in S] for n in ("hist", "scan", "base", "part"))
        deg, root, norm = (ph.sb(n, [HI, P]) for n in ("deg", "root", "norm"))
        hik = [ph.sb(f"hik{s}", [P, ET + EB], BF16) for s in S]
        key2 = [[ph.sb(f"key2_{s}_{b}", [P, 2, EB], BF16) for b in range(2)] for s in S]
        zero = ph.sb("zero", [P, P], BF16)
        mb = [[ph.sb(f"mb{s}_{k}", [P, EB, 3]) for k in range(MB)] for s in S]
        place = [ph.sb(f"place{k}", [P, EB], I32) for k in range(MB)]
        rank_in, rank_at = ([ph.sb(f"{n}{s}", [P, MB, EB]) for s in S] for n in ("rank_in", "rank_at"))
        hiT, hsnap = ([[ph.sb(f"{n}{s}_{q}", [HI, P]) for q in range(2)] for s in S] for n in ("hiT", "hsnap"))
        hist_ps, krow_ps, look_ps = ([ph.ps(f"{n}{s}", [P, 512]) for s in S] for n in ("hist_ps", "krow_ps", "look_ps"))
        hiT_ps = [ph.ps(f"hiT_ps{s}", [P, 1024], BF16) for s in S]
        hist_acc = [hist_ps[s][0:HI, 0:P] for s in S]
        rows_ps = [look_ps[s][0:HI, 256:257] for s in S]
        pair = lambda n: [ph.sem(f"{n}{s}") for s in S]
        loaded, zeroed, saved, gate = (ph.sem(n) for n in ("loaded", "zeroed", "saved", "gate"))
        deg_ready, rooted, normed = (ph.sem(n) for n in ("deg_ready", "rooted", "normed"))
        prep, onehot, counted, rows_before, base_ready = (pair(n) for n in ("prep", "onehot", "counted", "rows_before", "base_ready"))
        onehot2, krow, hi_turned, hi_copied, snapped, looked, added = (pair(n) for n in (
            "onehot2", "krow", "hi_turned", "hi_copied", "snapped", "looked", "added"))
        ranked_in, ranked_at, meta_b, placed = (pair(n) for n in ("ranked_in", "ranked_at", "meta_b", "placed"))
        left, scattered = ph.sem("left"), [ph.sem(f"scattered{k}") for k in range(MB)]
        block = ph.block()

        def tiles(eng, step):
            with eng.Fori(0, NEB // MB) as i:
                for k in range(MB):
                    for j in range(EB):
                        for s in S:
                            step(s, i * (MB * EB) + (k * EB + j), i * MB + k, k, j)

        @block.sync
        def _(sp):
            loads = [(kin[0], keys[0]), (kin[1], keys[1]), (win, weights), (iota_f, c_d["iota"]), (id_t, c_d["ident"]), (idb_t, c_d["identb"]), (tri_t, c_d["tri"]),
                     (upper_t, c_d["upper"])]
            for dst, src in loads:
                sp.dma_start(dst[:, :], src).then_inc(loaded, 16)
            sp.dma_start(xs_d, xn_d).then_inc(saved, 16)
            for s in S:
                hist_d, base_d, _ = orders[s]
                sp.wait_ge(base_ready[s], 4)
                sp.dma_start(hist_d.rearrange("(h l) -> h l", l=P), hist[s][:, :]).then_inc(saved, 16)
                sp.dma_start(base_d.rearrange("(h l) -> h l", l=P), base[s][:, :]).then_inc(saved, 16)
            sp.wait_ge(normed, 1)
            sp.dma_start(norm_d.rearrange("(h l) -> h l", l=P), norm[:, :]).then_inc(saved, 16)
            sp.wait_ge(saved, 96)

        @block.vector
        def _(dve):
            nc.vector.memset(zero[:, :], 0.0).then_inc(zeroed, 1)
            for s in S:
                nc.vector.memset(meta[s][:, ET:(SW if s else ET + EB), :], 0.0).then_inc(zeroed, 1)
                nc.vector.memset(lo[s][:, ET:ET + EB], 0.0).then_inc(zeroed, 1)
                nc.vector.memset(hi[s][:, ET:ET + EB], 0.0).then_inc(zeroed, 1)
                nc.vector.memset(hik[s][:, ET:ET + EB], 0.0).then_inc(zeroed, 1)
            dve.wait_ge(zeroed, 9)
            dve.wait_ge(loaded, 8 * 16)
            for s in S:
                nc.vector.tensor_scalar(hi_i[s][:, :], kin[s][:, :], 7, None, ALU.logical_shift_right).then_inc(prep[s], 1)
                nc.vector.tensor_scalar(lo_i[s][:, :], kin[s][:, :], P - 1, None, ALU.bitwise_and).then_inc(prep[s], 1)
                nc.vector.tensor_copy(meta[s][:, 0:ET, 0], kin[s][:, :]).then_inc(prep[s], 1)
                nc.vector.tensor_copy(meta[s][:, 0:ET, 2], win[:, :]).then_inc(prep[s], 1)
                nc.vector.tensor_scalar(meta[s][:, 0:ET, 1], kin[1 - s][:, :], float(N - 1), None, ALU.min).then_inc(prep[s], 1)
            nc.vector.memset(place1[:, ET:SW], 0.0).then_inc(zeroed, 1)
            nc.vector.tensor_copy(iotas[:, :, :], iota_f[:, :].unsqueeze(2).to_broadcast([P, P, EB])).then_inc(zeroed, 1)
            dve.wait_ge(zeroed, 11)
            for s in S:
                dve.wait_ge(prep[s], 5)
                nc.vector.tensor_copy(hi[s][:, 0:ET], hi_i[s][:, :]).then_inc(prep[s], 1)
                nc.vector.tensor_copy(lo[s][:, 0:ET], lo_i[s][:, :]).then_inc(prep[s], 1)
            for s in S:
                dve.wait_ge(prep[s], 7)
                nc.vector.tensor_scalar(hik[s][:, 0:ET], hi[s][:, 0:ET], float(P), None, ALU.mult).then_inc(prep[s], 1)
                dve.wait_ge(prep[s], 8)

            def one_hots(s, t0, b, done):
                for one, part, width in ((onelo, lo, P), (onehi, hi, HI)):
                    nc.vector.tensor_tensor(one[s][:, b, :, :], part[s][:, None, ds(t0, EB)].to_broadcast([P, width, EB]),
                                            iotas[:, 0:width, :], ALU.is_equal).then_inc(done, 1)

            with dve.Fori(0, NEB // 2) as i:
                for b in range(2):
                    for s in S:
                        dve.wait_ge(counted[s], i * 2 + (b + 1))
                        one_hots(s, i * (2 * EB) + b * EB, b, onehot[s])
            for s in S:
                dve.wait_ge(counted[s], CR + NEB)
                nc.vector.tensor_copy(hist[s][:, :], hist_acc[s]).then_inc(base_ready[s], 1)
                dve.wait_ge(base_ready[s], 1)
                nc.vector.tensor_tensor_scan(scan[s][:, :], hist[s][:, :], hist[s][:, :], 0.0, ALU.add, ALU.bypass).then_inc(base_ready[s], 1)
                dve.wait_ge(base_ready[s], 2)
                nc.vector.tensor_tensor(part[s][:, :], scan[s][:, :], hist[s][:, :], ALU.subtract).then_inc(base_ready[s], 1)
                dve.wait_ge(base_ready[s], 3)
                dve.wait_ge(rows_before[s], 1)
                nc.vector.tensor_scalar(base[s][:, :], part[s][:, :], rows_ps[s], None, ALU.add).then_inc(base_ready[s], 1)

            nc.vector.tensor_scalar(deg[:, :], hist[0][:, :], 1.0, None, ALU.max).then_inc(deg_ready, 1)
            dve.wait_ge(rooted, 1)
            nc.vector.reciprocal(norm[:, :], root[:, :]).then_inc(normed, 1)

            def ahead(s, t0, b, k):
                one_hots(s, t0, b, onehot2[s])
                nc.vector.tensor_copy(key2[s][b][:, 0, :], lo[s][:, ds(t0, EB)])
                nc.vector.tensor_copy(key2[s][b][:, 1, :], hik[s][:, ds(t0, EB)])
                nc.vector.tensor_copy(mb[s][k][:, :, :], meta[s][:, ds(t0, EB), :]).then_inc(meta_b[s], 1)

            def rank_inside(s, n, k, j):
                dve.wait_ge(krow[s], n)
                nc.vector.scalar_tensor_tensor(
                    krow_ps[s][:, 0:P], krow_ps[s][:, 0:P], mb[s][k][:, j, 0:1], tri_t[:, :], ALU.is_equal, ALU.mult,
                    accum_out=rank_in[s][:, k, j:j + 1]).then_inc(ranked_in[s], 1)

            for s in S:
                ahead(s, 0, 0, 0)
                dve.wait_ge(meta_b[s], 1)
                rank_inside(s, 1, 0, 0)

            def step(s, n, B, k, j):
                if j == 2:
                    dve.wait_ge(added[s], B * EB + 1)
                    dve.wait_ge(ranked_at[s], B * EB + 1)
                    if s == 0:
                        dve.wait_ge(left, B + 2)
                    ahead(s, B * EB + EB, (k + 1) % 2, (k + 1) % MB)
                j1, k1 = (j + 1, k) if j + 1 < EB else (0, (k + 1) % MB)
                if j1 == 0:
                    dve.wait_ge(meta_b[s], B + 2)
                rank_inside(s, n + 2, k1, j1)
                dve.wait_ge(looked[s], n + 3)
                nc.vector.tensor_tensor_reduce(
                    look_ps[s][:, 0:P], look_ps[s][:, 0:P], onelo[s][:, k % 2, :, j], 1.0, 0.0, ALU.mult, ALU.add,
                    rank_at[s][:, k, j:j + 1]).then_inc(ranked_at[s], 1)
                if j == EB - 1:
                    dve.wait_ge(ranked_in[s], n + 1)
                    dve.wait_ge(ranked_at[s], n + 2)
                    to = place1[:, ds(B * EB, EB)] if s else place[k][:, :]
                    nc.vector.tensor_tensor(to, rank_in[s][:, k, :], rank_at[s][:, k, :], ALU.add).then_inc(placed[s], 1)
            tiles(dve, step)

        @block.tensor
        def _(pe):
            pe.wait_ge(zeroed, 1)
            for s in S:
                nc.tensor.matmul(hist_acc[s], zero[:, 0:HI], zero[:, :], start=True, stop=False, skip_group_check=True)
                pe.sem_inc(counted[s], CR)
            with pe.Fori(0, NEB // 2) as i:
                for b in range(2):
                    for s in S:
                        pe.wait_ge(onehot[s], i * 4 + (b * 2 + 2))
                        for j in range(EB):
                            mm = nc.tensor.matmul(hist_acc[s], onehi[s][:, b, :, j], onelo[s][:, b, :, j], start=False, stop=False,
                                                  skip_group_check=True)
                        mm.then_inc(counted[s], 1)
            for s in S:
                pe.wait_ge(base_ready[s], 2)
                nc.tensor.matmul(rows_ps[s], upper_t[0:HI, 0:HI], scan[s][:, P - 1:P], start=True, stop=True).then_inc(rows_before[s], 1)
            for s in S:
                pe.wait_ge(base_ready[s], 4)
                nc.tensor.matmul(hist_acc[s], id_t[0:HI, 0:HI], base[s][:, :], start=True, stop=False, skip_group_check=True).then_inc(added[s], 1)
                pe.sem_inc(looked[s], CR)
                pe.sem_inc(ranked_at[s], 1)

            def turn(s, k, j):
                for part in range(2):
                    mm = nc.tensor.matmul(krow_ps[s][:, 0:P], key2[s][k % 2][:, part, j:j + 1].to_broadcast([P, P]), idb_t[:, :],
                                          start=(part == 0), stop=(part == 1))
                mm.then_inc(krow[s], 1)
                nc.tensor.transpose(hiT_ps[s][0:HI, 0:P], onehi[s][:, k % 2, :, j], idb_t[:, :]).then_inc(hi_turned[s], 1)

            for s in S:
                pe.wait_ge(onehot2[s], 2)
                pe.wait_ge(meta_b[s], 1)
                turn(s, 0, 0)

            def step(s, n, B, k, j):
                j1, k1 = (j + 1, k) if j + 1 < EB else (0, (k + 1) % MB)
                if j1 == 0:
                    pe.wait_ge(onehot2[s], B * 2 + 4)
                    pe.wait_ge(meta_b[s], B + 2)
                pe.wait_ge(ranked_in[s], n + 1)
                pe.wait_ge(hi_copied[s], n + 1)
                turn(s, k1, j1)
                pe.wait_ge(snapped[s], n + 1)
                pe.wait_ge(ranked_at[s], n + 1)
                nc.tensor.matmul(look_ps[s][:, 0:P], hiT[s][j % 2][:, :], hsnap[s][j % 2][:, :], start=True, stop=True).then_inc(looked[s], 1)
                nc.tensor.matmul(hist_acc[s], onehi[s][:, k % 2, :, j], onelo[s][:, k % 2, :, j], start=False, stop=False,
                                 skip_group_check=True).then_inc(added[s], 1)
            tiles(pe, step)

        @block.scalar
        def _(act):
            def copy_high(s, n, q):
                act.wait_ge(hi_turned[s], n)
                act.wait_ge(looked[s], n)
                nc.scalar.activation(hiT[s][q][:, :], hiT_ps[s][0:HI, 0:P], ACT.Copy).then_inc(hi_copied[s], 1)
            act.wait_ge(deg_ready, 1)
            nc.scalar.activation(root[:, :], deg[:, :], ACT.Sqrt).then_inc(rooted, 1)
            for s in S:
                copy_high(s, 1, 0)

            def step(s, n, B, k, j):
                act.wait_ge(looked[s], n + 1)
                act.wait_ge(added[s], n + 1)
                nc.scalar.activation(hsnap[s][j % 2][:, :], hist_acc[s], ACT.Copy).then_inc(snapped[s], 1)
                copy_high(s, n + 2, (j + 1) % 2)
            tiles(act, step)

        @block.gpsimd
        def _(pool):
            pool.sem_inc(left, MB)
            with pool.Fori(0, NEB // MB) as i:
                for k in range(MB):
                    pool.wait_ge(placed[0], i * MB + (k + 1))
                    pool.sem_inc(gate, 1)
                    for j in range(EB):
                        nc.gpsimd.indirect_dma_start(
                            orders[0][2], bass.IndirectOffsetOnAxis(place[k][:, j:j + 1], 0), mb[0][k][:, j, :], None).then_inc(scattered[k], 16)
                    for before in ([], [0], [1], [2, 3])[k]:
                        pool.wait_ge(scattered[before], i * (16 * EB) + 16 * EB)
                        pool.sem_inc(left, 1)


def chunks(eng, body, ahead=1):
    pairs = (NCH - ahead) // 2
    with eng.Fori(0, pairs) as i:
        for b in range(2):
            body(i * 2 + b, b, i, True)
    for c in range(2 * pairs, NCH):
        body(c, c % 2, c // 2, c + ahead < NCH)


def chunks_behind(eng, body, behind):
    def second(c, b, r):
        return lambda n: behind(c, b, r, n)
    body(0, 0, 0, True, lambda n: None)
    with eng.Fori(0, (NCH - 3) // 2) as i:
        body(i * 2 + 1, 1, i, True, second(i * 2, 0, i))
        body(i * 2 + 2, 0, i + 1, True, second(i * 2 + 1, 1, i))
    body(NCH - 2, 1, (NCH - 3) // 2, True, second(NCH - 3, 0, (NCH - 3) // 2))
    body(NCH - 1, 0, NCH // 2, False, second(NCH - 2, 1, (NCH - 3) // 2))
    for n in range(3):
        behind(NCH - 1, 0, NCH // 2, n)


class Norm:

    def __init__(self, nc, ph, x, ones, used, gain=None, offset=None, eps=1e-5):
        self.nc, self.x, self.ones, self.eps, self.gain, self.offset, self.used = nc, x, ones, eps, gain, offset, used
        self.stat = [ph.ps(f"stat{b}", [P, 512]) for b in range(2)]
        self.cen = [ph.sb(f"cen{b}", [P, 2, CW]) for b in range(2)]
        self.sq = [ph.sb(f"sq{b}", [P, 2, CW]) for b in range(2)]
        self.dev = [ph.sb(f"dev{b}", [P, CW]) for b in range(2)]
        self.rstd = [ph.sb(f"rstd{b}", [P, CW]) for b in range(2)]
        self.eps_t = ph.sb("eps", [P, 1])
        self.nrm = [ph.sb(f"nrm{b}", [P, 2, CW]) for b in range(2)]
        self.out = self.nrm if gain is None else [ph.sb(f"out{b}", [P, 2, CW]) for b in range(2)]
        self.mean_ready, self.centred, self.squared, self.var_ready, self.rooted, self.inverted, self.normed, self.affine = (
            ph.loop_sem(n) for n in ("mean_ready", "centred", "squared", "var_ready", "rooted", "inverted", "normed", "affine"))
        self.eps_ready = ph.sem("eps_ready")
        self.ready = self.normed if gain is None else self.affine

    def pe_mean(self, pe, n, b):
        pe.wait_ge(self.centred, n + OLD)
        for h in range(2):
            mm = self.nc.tensor.matmul(self.stat[b][:, 0:CW], self.ones[:, :], self.x[b][:, h, :], start=(h == 0), stop=(h == 1))
        mm.then_inc(self.mean_ready, 1)

    def dve_centre(self, dve, n, b):
        dve.wait_ge(self.mean_ready, n + NOW)
        dve.wait_ge(self.squared, n + OLD)
        dve.wait_ge(self.normed, n + OLD)
        self.nc.vector.tensor_tensor(self.cen[b][:, :, :], self.x[b][:, :, :],
                                     self.stat[b][:, None, 0:CW].to_broadcast([P, 2, CW]), ALU.subtract).then_inc(self.centred, 1)

    def act_square(self, act, n, b):
        act.wait_ge(self.centred, n + NOW)
        act.wait_ge(self.var_ready, n + OLD)
        self.nc.scalar.activation(self.sq[b][:, :, :], self.cen[b][:, :, :], ACT.Square).then_inc(self.squared, 1)

    def pe_var(self, pe, n, b):
        pe.wait_ge(self.squared, n + NOW)
        pe.wait_ge(self.rooted, n + OLD)
        for h in range(2):
            mm = self.nc.tensor.matmul(self.stat[b][:, CW:2 * CW], self.ones[:, :], self.sq[b][:, h, :], start=(h == 0), stop=(h == 1))
        mm.then_inc(self.var_ready, 1)

    def dve_start(self, dve):
        self.nc.vector.memset(self.eps_t[:, :], self.eps).then_inc(self.eps_ready, 1)

    def act_root(self, act, n, b):
        if isinstance(n, int) and n == 0:
            act.wait_ge(self.eps_ready, 1)
        act.wait_ge(self.var_ready, n + NOW)
        act.wait_ge(self.inverted, n + OLD)
        self.nc.scalar.activation(self.dev[b][:, :], self.stat[b][:, CW:2 * CW], ACT.Sqrt, bias=self.eps_t[:, 0:1]).then_inc(self.rooted, 1)

    def dve_norm(self, dve, n, b):
        dve.wait_ge(self.rooted, n + NOW)
        dve.wait_ge(self.normed, n + OLD)
        self.nc.vector.reciprocal(self.rstd[b][:, :], self.dev[b][:, :]).then_inc(self.inverted, 1)
        dve.wait_ge(self.inverted, n + NOW)
        for s in [self.affine] if self.gain is not None else self.used:
            dve.wait_ge(s, n + OLD)
        self.nc.vector.tensor_tensor(self.nrm[b][:, :, :], self.cen[b][:, :, :],
                                     self.rstd[b][:, None, :].to_broadcast([P, 2, CW]), ALU.mult).then_inc(self.normed, 1)

    def act_affine(self, act, n, b):
        act.wait_ge(self.normed, n + NOW)
        for s in self.used:
            act.wait_ge(s, n + OLD)
        for h in range(2):
            last = self.nc.scalar.activation(self.out[b][:, h, :], self.nrm[b][:, h, :], ACT.Identity,
                                             bias=self.offset[:, h:h + 1], scale=self.gain[:, h:h + 1])
        last.then_inc(self.affine, 1)


GB = 16
GW = (2 * NCH + 1) * GB


class Gather:

    def __init__(self, nc, ph, half, score_d, index, value):
        self.nc, self.half, self.score_d, self.index, self.value = nc, half, score_d, index, value
        self.ib, self.gb = [ph.sb(f"ib{b}", [P, GB], I32) for b in range(2)], [ph.sb(f"gb{b}", [P, GB]) for b in range(2)]
        self.landed = [ph.sem(f"gathered{b}") for b in range(2)]
        self.index_in, self.values_in, self.values_out = (ph.loop_sem(n) for n in ("index_in", "values_in", "values_out"))
        self.gate, self.cleared = ph.sem("gather_gate"), ph.sem("gather_cleared")

    def pool(self, pool, c, b, r):
        pool.wait_ge(self.index_in, c + NOW)
        pool.wait_ge(self.values_out, c + OLD)
        pool.sem_inc(self.gate, 1)
        for j in range(GB):
            self.nc.gpsimd.indirect_dma_start(self.gb[b][:, j:j + 1], None, self.score_d.rearrange("(n o) -> n o", o=1),
                                              bass.IndirectOffsetOnAxis(self.ib[b][:, j:j + 1], 0)).then_inc(self.landed[b], 16)
        pool.wait_ge(self.landed[b], r * (16 * GB) + 16 * GB)
        pool.sem_inc(self.values_in, 1)

    def dve_start(self, dve):
        if self.half:
            self.nc.vector.tensor_copy(self.gb[1][:, :], self.value[:, NCH * GB:(NCH + 1) * GB]).then_inc(self.cleared, 1)
        else:
            self.nc.vector.memset(self.gb[1][:, :], 0.0).then_inc(self.cleared, 1)
        dve.wait_ge(self.cleared, 1)
        self.nc.vector.tensor_copy(self.ib[0][:, :], self.index[:, self.half * NCH * GB:(self.half * NCH + 1) * GB]).then_inc(self.index_in, 1)

    def dve_take(self, dve, c, b):
        dve.wait_ge(self.values_in, c + PREV)
        self.nc.vector.tensor_copy(self.value[:, ds(c * GB + self.half * NCH * GB, GB)], self.gb[b][:, :]).then_inc(self.values_out, 1)

    def dve(self, dve, c, b):
        self.dve_take(dve, c, 1 - b)
        self.nc.vector.tensor_copy(self.ib[1 - b][:, :], self.index[:, ds(c * GB + (self.half * NCH + 1) * GB, GB)]).then_inc(self.index_in, 1)

    def dve_end(self, dve):
        self.dve_take(dve, NCH, 0)
        dve.wait_ge(self.values_out, NCH - 1 + NOW + 1)


def other_ends(nc, name, sorted_d, index):
    with Phase(nc, name) as ph:
        meta = ph.sb("meta", [P, ET, 3])
        loaded, done = ph.sem("loaded"), ph.sem("done")
        block = ph.block()

        @block.sync
        def _(sp):
            sp.dma_start(meta[:, :, :], sorted_d.rearrange("(p j) c -> p j c", j=ET)).then_inc(loaded, 16)

        @block.vector
        def _(dve):
            nc.vector.memset(index[:, ET:GW], 0.0).then_inc(done, 1)
            dve.wait_ge(loaded, 16)
            nc.vector.tensor_copy(index[:, 0:ET], meta[:, :, 1]).then_inc(done, 1)
            dve.wait_ge(done, 2)


def attend_first(nc, name, KH, KP, R, scale, x_d, qT_d, mixer, c_d, gain_d, offset_d, wq_d, wk_d, wv_d, wo_d, wx_d=None, bx_d=None, gather=None):
    EW = D // KH
    QW = KH * KP
    NQ = QW // R
    proj = wx_d is not None
    with Phase(nc, name) as ph:
        x = [ph.sb(f"x{b}", [P, 2, CW]) for b in range(2)]
        ones, ident = ph.sb("ones", [P, P]), ph.sb("ident", [P, P])
        blocks = ph.sb("blocks", [KP, KH, EW])
        gain, offset = ph.sb("gain", [P, 2]), ph.sb("offset", [P, 2])
        wq, wk, wv, wo = ph.sb("wq", [P, 2, QW]), ph.sb("wk", [P, 2, QW]), ph.sb("wv", [P, 2, D]), ph.sb("wo", [P, 2, D])
        if proj:
            wx, bx = ph.sb("wx", [P, 2, D]), ph.sb("bx", [P, 2])
            xm = [ph.sb(f"xm{b}", [P, 2, CW]) for b in range(2)]
        ek = [ph.sb(f"ek{b}", [KP, KH, CW]) for b in range(2)]
        ekT = [ph.sb(f"ekT{b}", [TT, 2, QW]) for b in range(2)]
        v = [ph.sb(f"v{b}", [TT, 2, D]) for b in range(2)]
        kmax, run, nbias, fade, ksum = ([ph.sb(f"{n}{b}", [KP, KH]) for b in range(2)] for n in ("kmax", "run", "nbias", "fade", "ksum"))
        total, rtotal = ph.sb("total", [KP, KH]), ph.sb("rtotal", [KP, KH])
        ctxt, ctxn = ph.sb("context", [KP, KH, EW]), ph.sb("contextn", [KP, KH, EW])
        ctxT = ph.sb("contextT", [P, 2, KP])
        qmax, qsum, qrec = ([ph.sb(f"{n}{b}", [TT, 2 * NQ]) for b in range(2)] for n in ("qmax", "qsum", "qrec"))
        qs, qe, qn = ([ph.sb(f"{n}{b}", [TT, 2 * NQ, R]) for b in range(2)] for n in ("qs", "qe", "qn"))
        qT = [ph.sb(f"qT{b}", [KP, KH, CW]) for b in range(2)]
        k_ps, q_ps, v_ps, ekT_ps, qT_ps, ctx_ps = (ph.ps(n, [P, 512]) for n in ("k_ps", "q_ps", "v_ps", "ekT_ps", "qT_ps", "ctx_ps"))
        kps = k_ps[0:KP, 0:KH * CW].rearrange("p (h c) -> p h c", h=KH)
        if proj:
            ekps = qT_ps[0:TT, 256:256 + 2 * QW].rearrange("p (t c) -> p t c", t=2)
            xm_ps = ekT_ps[:, 0:2 * CW].rearrange("p (h c) -> p h c", h=2)
        else:
            ekps = ekT_ps[0:TT, 0:2 * QW].rearrange("p (t c) -> p t c", t=2)
        qps = q_ps[0:TT, 0:2 * QW].rearrange("p (g r) -> p g r", r=R)
        vps = v_ps[0:TT, 0:2 * D].rearrange("p (t c) -> p t c", t=2)
        qTps = qT_ps[0:KP, 0:KH * CW].rearrange("p (h c) -> p h c", h=KH)
        cps = ctx_ps[0:KP, 0:KH * EW].rearrange("p (h e) -> p h e", h=KH)
        weights = ph.sem("weights")
        x_loaded = [ph.sem(f"x_loaded{b}") for b in range(2)]
        q_saved = [ph.sem(f"q_saved{b}") for b in range(2)]
        (xm_made, xm_copied, k_made, v_made, q_made, ekT_made, ctx_made, qT_made, k_maxed, k_run, k_bias, q_maxed, q_less, q_exp,
         q_summed, q_rec, q_normed, k_exp, faded, v_copied, ekT_copied, qT_copied, ctx_added, total_added) = (ph.loop_sem(n) for n in (
             "xm_made", "xm_copied", "k_made", "v_made", "q_made", "ekT_made", "ctx_made", "qT_made", "k_maxed", "k_run", "k_bias",
             "q_maxed", "q_less", "q_exp", "q_summed", "q_rec", "q_normed", "k_exp", "faded", "v_copied", "ekT_copied", "qT_copied",
             "ctx_added", "total_added"))
        started, ended, turned, turned_copied, mixed, kept = (ph.sem(n) for n in ("started", "ended", "turned", "turned_copied", "mixed", "kept"))
        ln = Norm(nc, ph, x, ones, [xm_made] if proj else [q_made], gain, offset)
        loads = [(ones, c_d["mean"]), (ident, c_d["ident"]), (blocks, c_d[f"blocks{KH}"]), (gain, gain_d), (offset, offset_d),
                 (wo, wo_d)] + ([(wx, wx_d), (bx, bx_d)] if proj else [(wq, wq_d), (wk, wk_d), (wv, wv_d)])
        side = Gather(nc, ph, *gather) if gather else None
        by_head, keys_gate = ph.sem("by_head"), ph.sem("keys_gate")
        if proj:
            for w, w_d in ((wq, wq_d), (wk, wk_d), (wv, wv_d)):
                rows, cols = w_d.shape
                for n in range(D // rows):
                    p0 = n * rows % P
                    loads.append((w[p0:p0 + rows, n * rows // P, n * cols:(n + 1) * cols], w_d))
        block = ph.block()

        @block.sync
        def _(sp):
            for b in range(2):
                sp.sem_inc(q_saved[b], 16)
            if proj:
                sp.wait_ge(by_head, 3)
            for dst, src in loads:
                sp.dma_start(dst[:], src).then_inc(weights, 16)
            for b in range(2):
                sp.dma_start(x[b][:, :, :], x_d[:, :, b * CW:(b + 1) * CW]).then_inc(x_loaded[b], 16)

            def body(c, b, r, more, behind):
                if not isinstance(c, int) or c + 2 < NCH:
                    sp.wait_ge(ln.centred, c + NOW)
                    sp.dma_start(x[b][:, :, :], x_d[:, :, ds((c + 2) * CW, CW)]).then_inc(x_loaded[b], 16)
                behind(0)

            def save(c, b, r, n):
                if n == 0:
                    sp.wait_ge(qT_copied, c + NOW)
                    sp.dma_start(qT_d[:, :, ds(c * CW, CW)], qT[b][:, :, :]).then_inc(q_saved[b], 16)
            chunks_behind(sp, body, save)
            for b in range(2):
                sp.wait_ge(q_saved[b], 16 * ((NCH + 1 - b) // 2) + 16)

        if side:
            @block.gpsimd
            def _(pool):
                chunks(pool, lambda c, b, r, more: side.pool(pool, c, b, r))

        @block.tensor
        def _(pe):
            pe.wait_ge(weights, 16 * len(loads))
            pe.wait_ge(x_loaded[0], 16)
            ln.pe_mean(pe, 0, 0)
            ln.pe_var(pe, 0, 0)

            def body(c, b, r, more, behind):
                src = xm[b] if proj else ln.out[b]
                if more:
                    pe.wait_ge(x_loaded[1 - b], r * 16 + (b * 16 + 16))
                    ln.pe_mean(pe, c + 1, 1 - b)
                pe.wait_ge(ln.affine, c + NOW)
                if proj:
                    pe.wait_ge(xm_copied, c + PREV)
                    for h in range(2):
                        for k in range(2):
                            mm = nc.tensor.matmul(xm_ps[:, h, :], wx[:, k, h * P:(h + 1) * P], ln.out[b][:, k, :], start=(k == 0), stop=(k == 1))
                    mm.then_inc(xm_made, 1)
                behind(0)
                if proj:
                    pe.wait_ge(xm_copied, c + NOW)
                pe.wait_ge(k_exp, c + PREV)
                for h in range(KH):
                    for k in range(2):
                        mm = nc.tensor.matmul(kps[:, h, :], wk[:, k, h * KP:(h + 1) * KP], src[:, k, :], start=(k == 0), stop=(k == 1))
                mm.then_inc(k_made, 1)
                pe.wait_ge(v_copied, c + PREV)
                for t in range(2):
                    for k in range(2):
                        mm = nc.tensor.matmul(vps[:, t, :], src[:, k, t * TT:(t + 1) * TT], wv[:, k, :], start=(k == 0), stop=(k == 1))
                mm.then_inc(v_made, 1)
                if more:
                    ln.pe_var(pe, c + 1, 1 - b)
                behind(1)
                pe.wait_ge(q_less, c + PREV)
                for t in range(2):
                    for k in range(2):
                        mm = nc.tensor.matmul(q_ps[0:TT, t * QW:(t + 1) * QW], src[:, k, t * TT:(t + 1) * TT], wq[:, k, :],
                                              start=(k == 0), stop=(k == 1))
                mm.then_inc(q_made, 1)
                behind(2)

            def context_part(c, b, r, n):
                if n == 0:
                    pe.wait_ge(ekT_copied, c + PREV)
                    if proj:
                        pe.wait_ge(qT_copied, c + PREV)
                    pe.wait_ge(k_exp, c + NOW)
                    pe.sem_inc(keys_gate, 1)
                    for t in range(2):
                        for h in range(KH):
                            mm = nc.tensor.transpose(ekps[:, t, h * KP:(h + 1) * KP], ek[b][:, h, t * TT:(t + 1) * TT], ident[0:KP, 0:KP])
                    mm.then_inc(ekT_made, 1)
                if n == 1:
                    pe.wait_ge(ekT_copied, c + NOW)
                    pe.wait_ge(v_copied, c + NOW)
                    pe.wait_ge(ctx_added, c + PREV)
                    for h in range(KH):
                        for t in range(2):
                            mm = nc.tensor.matmul(cps[:, h, :], ekT[b][:, t, h * KP:(h + 1) * KP], v[b][:, t, h * EW:(h + 1) * EW],
                                                  start=(t == 0), stop=(t == 1))
                    mm.then_inc(ctx_made, 1)
                if n == 2:
                    pe.wait_ge(q_normed, c + NOW)
                    pe.wait_ge(qT_copied, c + PREV)
                    for t in range(2):
                        for h in range(KH):
                            mm = nc.tensor.transpose(qTps[:, h, t * TT:(t + 1) * TT],
                                                     qn[b][:, t * NQ:(t + 1) * NQ, :].rearrange("p g r -> p (g r)")[:, h * KP:(h + 1) * KP],
                                                     ident[0:TT, 0:TT])
                    mm.then_inc(qT_made, 1)
            chunks_behind(pe, body, context_part)
            pe.wait_ge(ended, 3)
            for h in range(2):
                src = ctxn[:, h, :] if KH == 2 else ctxn[:, 0, h * P:(h + 1) * P]
                mm = nc.tensor.transpose(q_ps[:, h * P:h * P + KP], src, ident[0:KP, 0:KP])
            mm.then_inc(turned, 1)
            pe.wait_ge(turned_copied, 1)
            for h in range(2):
                mm = nc.tensor.matmul(v_ps[0:KP, h * D:(h + 1) * D] if KH == 2 else v_ps[0:KP, 0:D], ctxT[:, h, :], wo[:, h, :],
                                      start=(KH == 2 or h == 0), stop=(KH == 2 or h == 1))
            mm.then_inc(mixed, 1)

        @block.scalar
        def _(act):
            act.wait_ge(weights, 16 * len(loads))
            ln.act_square(act, 0, 0)
            ln.act_root(act, 0, 0)
            ln.act_affine(act, 0, 0)

            def body(c, b, r, more, behind):
                if proj:
                    act.wait_ge(xm_made, c + NOW)
                    act.wait_ge(q_made, c + OLD)
                    for h in range(2):
                        last = nc.scalar.activation(xm[b][:, h, :], xm_ps[:, h, :], ACT.Identity, bias=bx[:, h:h + 1])
                    last.then_inc(xm_copied, 1)
                if more:
                    ln.act_square(act, c + 1, 1 - b)
                behind(0)
                act.wait_ge(v_made, c + NOW)
                act.wait_ge(ctx_made, c + OLD)
                nc.scalar.activation(v[b][:, :, :], vps, ACT.Copy).then_inc(v_copied, 1)
                if more:
                    ln.act_root(act, c + 1, 1 - b)
                act.wait_ge(k_bias, c + NOW)
                act.wait_ge(ekT_made, c + OLD)
                act.wait_ge(total_added, c + OLD)
                for h in range(KH):
                    last = nc.scalar.activation(ek[b][:, h, :], kps[:, h, :], ACT.Exp, bias=nbias[b][:, h:h + 1], scale=scale,
                                                accum_out=ksum[b][:, h:h + 1])
                last.then_inc(k_exp, 1)
                act.wait_ge(ctx_added, c + OLD)
                for h in range(KH):
                    last = nc.scalar.activation(fade[b][:, h:h + 1], run[1 - b][:, h:h + 1], ACT.Exp, bias=nbias[b][:, h:h + 1], scale=scale)
                last.then_inc(faded, 1)
                if more:
                    ln.act_affine(act, c + 1, 1 - b)
                act.wait_ge(q_less, c + NOW)
                act.wait_ge(q_normed, c + OLD)
                nc.scalar.activation(qe[b][:], qs[b][:], ACT.Exp, scale=scale).then_inc(q_exp, 1)
                behind(1)

            def context_part(c, b, r, n):
                if n == 0:
                    act.wait_ge(ekT_made, c + NOW)
                    act.wait_ge(ctx_made, c + OLD)
                    nc.scalar.activation(ekT[b][:, :, :], ekps, ACT.Copy).then_inc(ekT_copied, 1)
                if n == 1:
                    act.wait_ge(qT_made, c + NOW)
                    act.wait_ge(q_saved[b], r * 16 + 16)
                    nc.scalar.activation(qT[b][:, :, :], qTps, ACT.Copy).then_inc(qT_copied, 1)
            chunks_behind(act, body, context_part)
            act.wait_ge(turned, 1)
            nc.scalar.activation(ctxT[:, :, :], q_ps[:, 0:2 * P].rearrange("p (h k) -> p h k", h=2)[:, :, 0:KP], ACT.Copy).then_inc(turned_copied, 1)
            act.wait_ge(mixed, 1)
            nc.scalar.activation(mixer[0:KP, 0:KH, :], v_ps[0:KP, 0:KH * D].rearrange("p (h e) -> p h e", h=KH), ACT.Copy).then_inc(kept, 1)
            act.wait_ge(kept, 1)

        @block.vector
        def _(dve):
            if proj:
                for w in (wq, wk, wv):
                    nc.vector.memset(w[:, :, :], 0.0).then_inc(by_head, 1)
            nc.vector.memset(run[1][:, :], -1e30).then_inc(started, 1)
            nc.vector.memset(total[:, :], 0.0).then_inc(started, 1)
            nc.vector.memset(ctxt[:, :, :], 0.0).then_inc(started, 1)
            dve.wait_ge(started, 3)
            ln.dve_start(dve)
            if side:
                side.dve_start(dve)
            dve.wait_ge(weights, 16 * len(loads))
            dve.wait_ge(x_loaded[0], 16)
            ln.dve_centre(dve, 0, 0)
            ln.dve_norm(dve, 0, 0)

            def body(c, b, r, more, behind):
                if more:
                    dve.wait_ge(x_loaded[1 - b], r * 16 + (b * 16 + 16))
                    ln.dve_centre(dve, c + 1, 1 - b)
                if side:
                    side.dve(dve, c, b)
                dve.wait_ge(k_made, c + NOW)
                dve.wait_ge(k_run, c + OLD)
                nc.vector.tensor_reduce(kmax[b][:, :], kps, AX_X, ALU.max).then_inc(k_maxed, 1)
                dve.wait_ge(k_maxed, c + NOW)
                dve.wait_ge(k_run, c + PREV)
                dve.wait_ge(faded, c + PREV)
                dve.wait_ge(k_bias, c + OLD)
                nc.vector.tensor_tensor(run[b][:, :], run[1 - b][:, :], kmax[b][:, :], ALU.max).then_inc(k_run, 1)
                dve.wait_ge(k_run, c + NOW)
                nc.vector.tensor_scalar(nbias[b][:, :], run[b][:, :], -scale, None, ALU.mult).then_inc(k_bias, 1)
                if more:
                    ln.dve_norm(dve, c + 1, 1 - b)
                dve.wait_ge(q_made, c + NOW)
                dve.wait_ge(q_less, c + OLD)
                nc.vector.tensor_reduce(qmax[b][:, :], qps, AX_X, ALU.max).then_inc(q_maxed, 1)
                dve.wait_ge(q_maxed, c + NOW)
                dve.wait_ge(q_exp, c + OLD)
                nc.vector.tensor_tensor(qs[b][:], qps, qmax[b][:, :].unsqueeze(2).to_broadcast([TT, 2 * NQ, R]), ALU.subtract).then_inc(q_less, 1)
                dve.wait_ge(q_exp, c + NOW)
                dve.wait_ge(q_rec, c + OLD)
                nc.vector.tensor_reduce(qsum[b][:, :], qe[b][:], AX_X, ALU.add).then_inc(q_summed, 1)
                dve.wait_ge(q_summed, c + NOW)
                dve.wait_ge(q_normed, c + OLD)
                nc.vector.reciprocal(qrec[b][:, :], qsum[b][:, :]).then_inc(q_rec, 1)
                dve.wait_ge(q_rec, c + NOW)
                dve.wait_ge(qT_made, c + OLD)
                nc.vector.tensor_tensor(qn[b][:], qe[b][:], qrec[b][:, :].unsqueeze(2).to_broadcast([TT, 2 * NQ, R]), ALU.mult).then_inc(q_normed, 1)
                dve.wait_ge(faded, c + NOW)
                dve.wait_ge(total_added, c + PREV)
                for h in range(KH):
                    last = nc.vector.scalar_tensor_tensor(total[:, h:h + 1], total[:, h:h + 1], fade[b][:, h:h + 1], ksum[b][:, h:h + 1],
                                                          ALU.mult, ALU.add)
                last.then_inc(total_added, 1)
                behind(0)

            def context_part(c, b, r, n):
                if n:
                    return
                dve.wait_ge(ctx_made, c + NOW)
                dve.wait_ge(ctx_added, c + PREV)
                for h in range(KH):
                    last = nc.vector.scalar_tensor_tensor(ctxt[:, h, :], ctxt[:, h, :], fade[b][:, h:h + 1], cps[:, h, :], ALU.mult, ALU.add)
                last.then_inc(ctx_added, 1)
            chunks_behind(dve, body, context_part)
            if side:
                side.dve_end(dve)
            dve.wait_ge(total_added, NCH - 1 + NOW)
            nc.vector.reciprocal(rtotal[:, :], total[:, :]).then_inc(ended, 1)
            dve.wait_ge(ended, 1)
            dve.wait_ge(ctx_added, NCH - 1 + NOW)
            nc.vector.tensor_tensor(ctxt[:, :, :], ctxt[:, :, :], rtotal[:, :].unsqueeze(2).to_broadcast([KP, KH, EW]), ALU.mult).then_inc(ended, 1)
            dve.wait_ge(ended, 2)
            nc.vector.tensor_tensor(ctxn[:, :, :], ctxt[:, :, :], blocks[:, :, :], ALU.mult).then_inc(ended, 1)


def attend_second(nc, name, KH, KP, x_d, qT_d, mixer, out_d, c_d, bo_d, gain_d, offset_d, w1_d, b1_d, w2_d, b2_d, add_d=(), gather=None):
    F = 4 * D
    FG = F // P
    with Phase(nc, name) as ph:
        xin = [ph.sb(f"xin{b}", [P, 2, CW]) for b in range(2)]
        q = [ph.sb(f"q{b}", [KP, KH, CW]) for b in range(2)]
        more_in = [[ph.sb(f"add{n}_{b}", [P, 2, CW]) for b in range(2)] for n in range(len(add_d))]
        x = [ph.sb(f"x{b}", [P, 2, CW]) for b in range(2)]
        g = [ph.sb(f"g{b}", [P, FG, CW]) for b in range(2)]
        y = [ph.sb(f"y{b}", [P, 2, CW]) for b in range(2)]
        ones = ph.sb("ones", [P, P])
        bo, gain, offset, b2 = (ph.sb(n, [P, 2]) for n in ("bo", "gain", "offset", "b2"))
        b1 = ph.sb("b1", [P, FG])
        w1, w2 = ph.sb("w1", [P, 2, F]), ph.sb("w2", [P, FG, D])
        a_ps, y_ps = ph.ps("a_ps", [P, 512]), ph.ps("y_ps", [P, 512])
        f_ps = [ph.ps(f"f_ps{i}", [P, 512]) for i in range(4)]
        aps = a_ps[:, 0:2 * CW].rearrange("p (h c) -> p h c", h=2)
        yps = y_ps[:, 0:2 * CW].rearrange("p (h c) -> p h c", h=2)
        weights = ph.sem("weights")
        loaded, more_loaded, saved = ([ph.sem(f"{n}{b}") for b in range(2)] for n in ("loaded", "more_loaded", "saved"))
        a_made, a_added, y_made, y_added = (ph.loop_sem(n) for n in ("a_made", "a_added", "y_made", "y_added"))
        more_added = [ph.loop_sem(f"more_added{n}") for n in range(len(add_d))]
        done = more_added[-1] if add_d else y_added
        up = [ph.loop_sem(f"up{m}") for m in range(FG // 2)]
        gelu = [ph.loop_sem(f"gelu{m}") for m in range(FG // 2)]
        ln = Norm(nc, ph, x, ones, [up[FG // 2 - 1]], gain, offset)
        loads = [(ones, c_d["mean"]), (bo, bo_d), (gain, gain_d), (offset, offset_d), (w1, w1_d), (b1, b1_d), (w2, w2_d), (b2, b2_d)]
        side = Gather(nc, ph, *gather) if gather else None
        block = ph.block()
        NL, NA = 2, len(add_d)

        @block.sync
        def _(sp):
            for b in range(2):
                sp.sem_inc(saved[b], 16)

            def load(c, b):
                for dst, src in [(xin, x_d), (q, qT_d)]:
                    sp.dma_start(dst[b][:, :, :], src[:, :, ds(c * CW, CW)]).then_inc(loaded[b], 16)

            def load_more(c, b):
                for dst, src in zip(more_in, add_d):
                    sp.dma_start(dst[b][:, :, :], src[:, :, ds(c * CW, CW)]).then_inc(more_loaded[b], 16)
            for b in range(2):
                load(b, b)
                load_more(b, b)
            for dst, src in loads:
                sp.dma_start(dst[:], src).then_inc(weights, 16)

            def body(c, b, r, more):
                if more:
                    sp.wait_ge(a_added, c + NOW)
                    load(c + 2, b)
                sp.wait_ge(done, c + NOW)
                sp.dma_start(out_d[:, :, ds(c * CW, CW)], y[b][:, :, :]).then_inc(saved[b], 16)
                if more:
                    load_more(c + 2, b)
            chunks(sp, body, 2)
            for b in range(2):
                sp.wait_ge(saved[b], 16 * ((NCH + 1 - b) // 2) + 16)

        if side:
            @block.gpsimd
            def _(pool):
                chunks(pool, lambda c, b, r, more: side.pool(pool, c, b, r))

        @block.tensor
        def _(pe):
            def attention(c, b, r):
                pe.wait_ge(loaded[b], r * (16 * NL) + 16 * NL)
                pe.wait_ge(a_added, c + PREV)
                for h in range(2):
                    for k in range(KH):
                        mm = nc.tensor.matmul(aps[:, h, :], mixer[0:KP, k, h * P:(h + 1) * P], q[b][:, k, :], start=(k == 0), stop=(k == KH - 1))
                mm.then_inc(a_made, 1)
                pe.wait_ge(a_added, c + NOW)
                ln.pe_mean(pe, c, b)

            pe.wait_ge(weights, 16 * len(loads))
            attention(0, 0, 0)
            ln.pe_var(pe, 0, 0)

            def body(c, b, r, more):
                pe.wait_ge(ln.affine, c + NOW)
                for m in range(FG // 2):
                    pe.wait_ge(gelu[m], c + PREV)
                    for h in range(2):
                        for k in range(2):
                            g0 = (2 * m + h) * P
                            mm = nc.tensor.matmul(f_ps[m][:, h * CW:(h + 1) * CW], w1[:, k, g0:g0 + P], ln.out[b][:, k, :],
                                                  start=(k == 0), stop=(k == 1))
                    mm.then_inc(up[m], 1)
                    if m == 0 and more:
                        attention(c + 1, 1 - b, r + b)
                    if m == 2 and more:
                        ln.pe_var(pe, c + 1, 1 - b)
                pe.wait_ge(y_added, c + PREV)
                for h in range(2):
                    for m in range(FG):
                        if h == 0 and m % 2 == 0:
                            pe.wait_ge(gelu[m // 2], c + NOW)
                        mm = nc.tensor.matmul(yps[:, h, :], w2[:, m, h * P:(h + 1) * P], g[b][:, m, :], start=(m == 0), stop=(m == FG - 1))
                mm.then_inc(y_made, 1)
            chunks(pe, body)

        @block.scalar
        def _(act):
            act.wait_ge(weights, 16 * len(loads))
            ln.act_square(act, 0, 0)
            ln.act_root(act, 0, 0)
            ln.act_affine(act, 0, 0)

            def body(c, b, r, more):
                act.wait_ge(y_made, c + OLD)
                for m in range(FG // 2):
                    act.wait_ge(up[m], c + NOW)
                    for h in range(2):
                        last = nc.scalar.activation(g[b][:, 2 * m + h, :], f_ps[m][:, h * CW:(h + 1) * CW], ACT.Gelu, bias=b1[:, 2 * m + h:2 * m + h + 1])
                    last.then_inc(gelu[m], 1)
                    if m == 1 and more:
                        ln.act_square(act, c + 1, 1 - b)
                if more:
                    ln.act_root(act, c + 1, 1 - b)
                    ln.act_affine(act, c + 1, 1 - b)
            chunks(act, body)

        @block.vector
        def _(dve):
            def attention(c, b, r):
                dve.wait_ge(loaded[b], r * (16 * NL) + 16 * NL)
                dve.wait_ge(a_made, c + NOW)
                dve.wait_ge(ln.mean_ready, c + OLD)
                dve.wait_ge(y_added, c + OLD)
                dve.wait_ge(ln.centred, c + OLD)
                for h in range(2):
                    last = nc.vector.scalar_tensor_tensor(x[b][:, h, :], aps[:, h, :], bo[:, h:h + 1], xin[b][:, h, :], ALU.add, ALU.add)
                last.then_inc(a_added, 1)
                dve.wait_ge(a_added, c + NOW)
                ln.dve_centre(dve, c, b)

            ln.dve_start(dve)
            if side:
                side.dve_start(dve)
            dve.wait_ge(weights, 16 * len(loads))
            attention(0, 0, 0)
            ln.dve_norm(dve, 0, 0)

            def body(c, b, r, more):
                if more:
                    attention(c + 1, 1 - b, r + b)
                    ln.dve_norm(dve, c + 1, 1 - b)
                if side:
                    side.dve(dve, c, b)
                dve.wait_ge(y_made, c + NOW)
                dve.wait_ge(saved[b], r * 16 + 16)
                for h in range(2):
                    last = nc.vector.scalar_tensor_tensor(y[b][:, h, :], yps[:, h, :], b2[:, h:h + 1], x[b][:, h, :], ALU.add, ALU.add)
                last.then_inc(y_added, 1)
                before = y_added
                if NA:
                    dve.wait_ge(more_loaded[b], r * (16 * NA) + 16 * NA)
                for n, s in enumerate(more_added):
                    dve.wait_ge(before, c + NOW)
                    nc.vector.tensor_tensor(y[b][:, :, :], y[b][:, :, :], more_in[n][b][:, :, :], ALU.add).then_inc(s, 1)
                    before = s
            chunks(dve, body)
            if side:
                side.dve_end(dve)


def feature_major(p, c0=0, n=CW):
    return p[:, c0:c0 + 2 * n].rearrange("p (h c) -> p h c", h=2)


def norm_table(nc, name, x_d, out_d, table_d, c_d, w_d=None, b_d=None, wa_d=None, ba_d=None, a_d=None):
    proj = w_d is not None
    with Phase(nc, name) as ph:
        x = [ph.sb(f"x{b}", [P, 2, CW]) for b in range(2)]
        row = [ph.sb(f"row{b}", [TT, 2, D]) for b in range(2)]
        ones, ident = ph.sb("ones", [P, P]), ph.sb("ident", [P, P])
        r_ps = [ph.ps(f"r_ps{b}", [P, 512]) for b in range(2)]
        if proj:
            w, bias, wa = ph.sb("w", [P, 2, D]), ph.sb("bias", [TT, D]), ph.sb("wa", [TT, 2, D])
            ba = ph.sb("ba", [TT, 2])
            prod = [ph.sb(f"prod{b}", [TT, 4, D]) for b in range(2)]
            dots = [ph.sb(f"dots{b}", [TT, 2, 2]) for b in range(2)]
        weights = ph.sem("weights")
        loaded, saved, a_saved = ([ph.sem(f"{n}{b}") for b in range(2)] for n in ("loaded", "saved", "a_saved"))
        rows_made, rows_copied, dotted = (ph.loop_sem(n) for n in ("rows_made", "rows_copied", "dotted"))
        out_sent = ph.sem("out_sent")
        out_saved = [ph.sem(f"out_saved{b}") for b in range(2)]
        ln = Norm(nc, ph, x, ones, [rows_made, out_sent])
        loads = [(ones, c_d["mean"]), (ident, c_d["ident"])] + ([(w, w_d), (bias, b_d.partition_broadcast(TT)), (wa, wa_d.partition_broadcast(TT)),
                                                                 (ba, ba_d.partition_broadcast(TT))] if proj else [])
        nc.sync.sem_inc(out_sent, START - 1)
        block = ph.block()

        @block.sync
        def _(sp):
            for b in range(2):
                sp.sem_inc(saved[b], 16)
                sp.sem_inc(a_saved[b], 32)
                sp.sem_inc(out_saved[b], 16)
                sp.dma_start(x[b][:, :, :], x_d[:, :, b * CW:(b + 1) * CW]).then_inc(loaded[b], 16)
            for dst, src in loads:
                sp.dma_start(dst[:], src).then_inc(weights, 16)

            def body(c, b, r, more):
                if more:
                    sp.wait_ge(ln.centred, c + NOW)
                    sp.dma_start(x[b][:, :, :], x_d[:, :, ds((c + 2) * CW, CW)]).then_inc(loaded[b], 16)
                sp.wait_ge(out_saved[1 - b], r * 16 + (b * 16 + 16))
                sp.sem_inc(out_sent, 1)
                sp.wait_ge(ln.normed, c + NOW)
                sp.dma_start(out_d[:, :, ds(c * CW, CW)], ln.out[b][:, :, :]).then_inc(out_saved[b], 16)
                sp.wait_ge(rows_copied, c + NOW)
                sp.dma_start(table_d[ds(c * CW, CW), :].rearrange("(t p) d -> p t d", t=2), row[b][:, :, :]).then_inc(saved[b], 16)
                if proj:
                    sp.wait_ge(dotted, c + NOW)
                    for n in range(2):
                        sp.dma_start(a_d[n, ds(c * CW, CW)].rearrange("(t p) -> p t", t=2), dots[b][:, :, n],
                                     allow_slow_non_contiguous=True).then_inc(a_saved[b], 16)
            chunks(sp, body, 2)
            for b in range(2):
                sp.wait_ge(out_saved[b], 16 * ((NCH + 1 - b) // 2) + 16)
                sp.wait_ge(saved[b], 16 * ((NCH + 1 - b) // 2) + 16)
                if proj:
                    sp.wait_ge(a_saved[b], 32 * ((NCH + 1 - b) // 2) + 32)

        @block.tensor
        def _(pe):
            pe.wait_ge(weights, 16 * len(loads))
            pe.wait_ge(loaded[0], 16)
            ln.pe_mean(pe, 0, 0)
            ln.pe_var(pe, 0, 0)

            def body(c, b, r, more):
                if more:
                    pe.wait_ge(loaded[1 - b], r * 16 + (b * 16 + 16))
                    ln.pe_mean(pe, c + 1, 1 - b)
                pe.wait_ge(ln.normed, c + NOW)
                pe.wait_ge(rows_copied, c + OLD)
                for t in range(2):
                    for k in range(2):
                        cols = ln.out[b][:, k, t * TT:(t + 1) * TT]
                        if proj:
                            mm = nc.tensor.matmul(r_ps[b][0:TT, t * D:(t + 1) * D], cols, w[:, k, :], start=(k == 0), stop=(k == 1))
                        else:
                            mm = nc.tensor.transpose(r_ps[b][0:TT, t * D + k * P:t * D + (k + 1) * P], cols, ident[:, :])
                mm.then_inc(rows_made, 1)
                if more:
                    ln.pe_var(pe, c + 1, 1 - b)
            chunks(pe, body)

        @block.scalar
        def _(act):
            ln.act_square(act, 0, 0)
            ln.act_root(act, 0, 0)

            def body(c, b, r, more):
                if more:
                    ln.act_square(act, c + 1, 1 - b)
                if not proj:
                    act.wait_ge(rows_made, c + NOW)
                    act.wait_ge(saved[b], r * 16 + 16)
                    nc.scalar.activation(row[b][:, :, :], r_ps[b][0:TT, :].rearrange("p (t d) -> p t d", t=2), ACT.Copy).then_inc(rows_copied, 1)
                if more:
                    ln.act_root(act, c + 1, 1 - b)
            chunks(act, body)

        @block.vector
        def _(dve):
            ln.dve_start(dve)
            dve.wait_ge(weights, 16 * len(loads))
            dve.wait_ge(loaded[0], 16)
            ln.dve_centre(dve, 0, 0)
            ln.dve_norm(dve, 0, 0)

            def body(c, b, r, more):
                if more:
                    dve.wait_ge(loaded[1 - b], r * 16 + (b * 16 + 16))
                    ln.dve_centre(dve, c + 1, 1 - b)
                if proj:
                    dve.wait_ge(rows_made, c + NOW)
                    dve.wait_ge(saved[b], r * 16 + 16)
                    dve.wait_ge(dotted, c + OLD)
                    nc.vector.tensor_tensor(row[b][:, :, :], r_ps[b][0:TT, :].rearrange("p (t d) -> p t d", t=2),
                                            bias[:, None, :].to_broadcast([TT, 2, D]), ALU.add).then_inc(rows_copied, 1)
                    dve.wait_ge(rows_copied, c + NOW)
                    dve.wait_ge(a_saved[b], r * 32 + 32)
                    for t in range(2):
                        for n in range(2):
                            last = nc.vector.tensor_tensor_reduce(prod[b][:, 2 * t + n, :], row[b][:, t, :], wa[:, n, :], 1.0, ba[:, n:n + 1], ALU.mult, ALU.add,
                                                                  dots[b][:, t, n:n + 1])
                    last.then_inc(dotted, 1)
                if more:
                    ln.dve_norm(dve, c + 1, 1 - b)
            chunks(dve, body)


RB = -(-ET // P)


def sum_edges(nc, name, sorted_d, weight_d, table_d, running_d, W, c_d):
    own = weight_d is None
    with Phase(nc, name) as ph:
        ident = ph.sb("ident", [P, P])
        rows = [ph.sb(f"rows{b}", [P, P, 3]) for b in range(2)]
        wrows = [ph.sb(f"wrows{b}", [P, P]) for b in range(2)]
        key, wgt = ph.sb("key", [P, ET + EB]), ph.sb("wgt", [P, ET + EB])
        idx = ph.sb("idx", [P, ET + EB], I32)
        kb, wb = [ph.sb(f"kb{b}", [P, EB]) for b in range(2)], [ph.sb(f"wb{b}", [P, EB]) for b in range(2)]
        ib = [ph.sb(f"ib{b}", [P, EB], I32) for b in range(2)]
        g = [ph.sb(f"g{b}", [P, EB, W]) for b in range(2)]
        run = [ph.sb(f"run{b}", [P, EB, W]) for b in range(2)]
        same = ph.sb("same", [P, 4, P])
        t_ps = [ph.ps(f"t_ps{b}", [P, 512]) for b in range(2)]
        krow_ps = [ph.ps(f"krow_ps{n}", [P, 512]) for n in range(4)]
        s_ps = [ph.ps(f"s_ps{b}", [P, 512]) for b in range(2)]
        consts, edge0, gate = ph.sem("consts"), ph.sem("edge0"), ph.sem("gate")
        rows_in = [ph.sem(f"rows_in{b}") for b in range(2)]
        turned, taken = ph.sem("turned"), ph.sem("taken")
        landed = [[ph.sem(f"landed{b}_{j}") for j in range(EB)] for b in range(2)]
        batch_in, batch_summed = ph.loop_sem("batch_in"), ph.loop_sem("batch_summed")
        krow, selected, summed, kept = (ph.loop_sem(n) for n in ("krow", "selected", "summed", "kept"))
        saved = [ph.sem(f"saved{b}") for b in range(2)]
        parts = 3 if own else 2
        per = 1 if own else 2
        blocks = [(n * P, min(P, ET - n * P)) for n in range(RB)]
        block = ph.block()

        @block.sync
        def _(sp):
            for b in range(2):
                sp.sem_inc(saved[b], 16)
            sp.dma_start(ident[:, :], c_d["ident"]).then_inc(consts, 16)
            for n, (t0, nt) in enumerate(blocks):
                if n >= 2:
                    sp.wait_ge(turned, n - 1)
                sp.dma_start(rows[n % 2][0:nt, :, :], sorted_d.rearrange("(t p) c -> t p c", p=P)[t0:t0 + nt]).then_inc(rows_in[n % 2], 16)
                if not own:
                    sp.dma_start(wrows[n % 2][0:nt, :], weight_d.rearrange("(t p) -> t p", p=P)[t0:t0 + nt]).then_inc(rows_in[n % 2], 16)
            out = running_d.rearrange("(t p) w -> p t w", p=P)
            with sp.Fori(0, NEB // 2) as i:
                for b in range(2):
                    t0 = i * (2 * EB) + b * EB
                    sp.wait_ge(kept, t0 + (EB - 1 + NOW))
                    sp.dma_start(out[:, ds(t0, EB), :], run[b][:, :, :]).then_inc(saved[b], 16)
            for b in range(2):
                sp.wait_ge(saved[b], 16 * (NEB // 2) + 16)

        @block.gpsimd
        def _(pool):
            with pool.Fori(0, NEB // 2) as i:
                for b in range(2):
                    pool.wait_ge(batch_in, i * 2 + (b + NOW))
                    pool.wait_ge(batch_summed, i * 2 + (b + OLD))
                    pool.sem_inc(gate, 1)
                    for j in range(EB):
                        nc.gpsimd.indirect_dma_start(g[b][:, j, 0:D], None, table_d, bass.IndirectOffsetOnAxis(ib[b][:, j:j + 1], 0)).then_inc(landed[b][j], 16)

        @block.tensor
        def _(pe):
            pe.wait_ge(consts, 16)
            for n, (t0, nt) in enumerate(blocks):
                pe.wait_ge(rows_in[n % 2], 16 * per * (n // 2 + 1))
                if n >= 2:
                    pe.wait_ge(taken, n - 1)
                for k in range(3):
                    src = rows[n % 2][0:nt, :, k] if k < 2 or own else wrows[n % 2][0:nt, :]
                    mm = nc.tensor.transpose(t_ps[n % 2][:, k * P:k * P + nt], src, ident[0:nt, 0:nt])
                mm.then_inc(turned, 1)

            def keys_along(t0, b, j):
                pe.wait_ge(selected, t0 + (max(j - 4, -1) + NOW))
                nc.tensor.transpose(krow_ps[j % 4][:, 0:P], kb[b][:, j:j + 1].to_broadcast([P, P]), ident[:, :]).then_inc(krow, 1)

            with pe.Fori(0, NEB // 2) as i:
                for b in range(2):
                    t0 = i * (2 * EB) + b * EB
                    pe.wait_ge(batch_in, i * 2 + (b + NOW))
                    for j in range(3):
                        keys_along(t0, b, j)
                    for j in range(EB):
                        q = (b * EB + j) % 2
                        if j + 3 < EB:
                            keys_along(t0, b, j + 3)
                        pe.wait_ge(selected, t0 + (j + NOW))
                        pe.wait_ge(kept, t0 + (j + OLD))
                        pe.wait_ge(landed[b][j], i * 16 + 16)
                        nc.tensor.matmul(s_ps[q][:, 0:W], same[:, j % 4, :], g[b][:, j, :], start=True, stop=True).then_inc(summed, 1)
                    nc.tensor.transpose(t_ps[0][:, 0:P], ident[:, :], ident[:, :]).then_inc(batch_summed, 1)

        @block.scalar
        def _(act):
            with act.Fori(0, NEB // 2) as i:
                for b in range(2):
                    t0 = i * (2 * EB) + b * EB
                    act.wait_ge(saved[b], i * 16 + 16)
                    for j in range(EB):
                        q = (b * EB + j) % 2
                        act.wait_ge(summed, t0 + (j + NOW))
                        nc.scalar.activation(run[b][:, j, :], s_ps[q][:, 0:W], ACT.Copy).then_inc(kept, 1)

        @block.vector
        def _(dve):
            for b in range(2):
                if W > D:
                    nc.vector.memset(g[b][:, :, D:W], 1.0).then_inc(edge0, 1)
            dve.wait_ge(consts, 16)
            for n, (t0, nt) in enumerate(blocks):
                dve.wait_ge(turned, n + 1)
                nc.vector.tensor_copy(key[:, t0:t0 + nt], t_ps[n % 2][:, 0:nt])
                nc.vector.tensor_copy(idx[:, t0:t0 + nt], t_ps[n % 2][:, P:P + nt])
                nc.vector.tensor_copy(wgt[:, t0:t0 + nt], t_ps[n % 2][:, 2 * P:2 * P + nt]).then_inc(taken, 1)
            dve.wait_ge(taken, RB)
            for tile in (key, wgt, idx):
                nc.vector.memset(tile[:, ET:ET + EB], 0.0).then_inc(edge0, 1)
            dve.wait_ge(edge0, 5 if W > D else 3)

            def take(B, b):
                dve.wait_ge(batch_summed, B + OLD)
                dve.wait_ge(selected, B * EB + (-EB - 1 + NOW) if not isinstance(B, int) else START)
                nc.vector.tensor_copy(kb[b][:, :], key[:, ds(B * EB, EB)])
                nc.vector.tensor_copy(wb[b][:, :], wgt[:, ds(B * EB, EB)])
                nc.vector.tensor_copy(ib[b][:, :], idx[:, ds(B * EB, EB)]).then_inc(batch_in, 1)
            take(0, 0)
            with dve.Fori(0, NEB // 2) as i:
                for b in range(2):
                    t0 = i * (2 * EB) + b * EB
                    dve.wait_ge(batch_in, i * 2 + (b + NOW))
                    for j in range(EB):
                        if j == EB // 2:
                            take(i * 2 + (b + 1), 1 - b)
                        k4 = krow_ps[j % 4][:, 0:P]
                        dve.wait_ge(krow, t0 + (j + NOW))
                        dve.wait_ge(summed, t0 + (max(j - 4, -1) + NOW))
                        nc.vector.tensor_scalar(same[:, j % 4, :], k4, kb[b][:, j:j + 1], wb[b][:, j:j + 1], ALU.is_equal, ALU.mult).then_inc(selected, 1)


def tile_carries(nc, name, sorted_d, running_d, carry_d, W, c_d):
    blocks = [(n * P, min(P, ET - n * P)) for n in range(RB)]
    groups = [(0, P), (P, P)] + ([(D, W - D)] if W > D else [])
    with Phase(nc, name) as ph:
        ident = ph.sb("ident", [P, P])
        keys = ph.sb("keys", [P, RB])
        last = ph.sb("last", [P, RB, W])
        endkey, goes_on = ph.sb("endkey", [P, ET + 1]), ph.sb("goes_on", [P, ET])
        lastT, sumT = ph.sb("lastT", [P, len(groups), ET]), ph.sb("sumT", [P, len(groups), ET])
        rows, zero = ph.sb("rows", [P, RB, W]), ph.sb("zero", [1, W])
        k_ps = [ph.ps(f"k_ps{b}", [P, 512]) for b in range(2)]
        t_ps = [ph.ps(f"t_ps{b}", [P, 512]) for b in range(2)]
        r_ps = [ph.ps(f"r_ps{b}", [P, 512]) for b in range(2)]
        loaded, cleared, along, key_taken, turned, taken, scanned, back, copied, saved = (ph.sem(n) for n in (
            "loaded", "cleared", "along", "key_taken", "turned", "taken", "scanned", "back", "copied", "saved"))
        block = ph.block()

        @block.sync
        def _(sp):
            sp.dma_start(ident[:, :], c_d["ident"]).then_inc(loaded, 16)
            for n, (t0, nt) in enumerate(blocks):
                sp.dma_start(last[0:nt, n, :], running_d.rearrange("(t p) w -> t p w", p=P)[t0:t0 + nt, P - 1, :]).then_inc(loaded, 16)
                sp.dma_start(keys[0:nt, n:n + 1], sorted_d.rearrange("(t p) c -> t p c", p=P)[t0:t0 + nt, P - 1, 0:1],
                             allow_slow_non_contiguous=True).then_inc(loaded, 16)
            for n, (t0, nt) in enumerate(blocks):
                sp.wait_ge(copied, n + 1)
                nt = min(nt, ET - 1 - t0)
                sp.dma_start(carry_d[1 + t0:1 + t0 + nt, :], rows[0:nt, n, :]).then_inc(saved, 16)
            sp.wait_ge(cleared, 1)
            sp.dma_start(carry_d[0:1, :], zero[0:1, :]).then_inc(saved, 16)
            sp.wait_ge(saved, 16 * (RB + 1))

        @block.tensor
        def _(pe):
            pe.wait_ge(loaded, 16 * (1 + 2 * RB))
            for n, (t0, nt) in enumerate(blocks):
                if n >= 2:
                    pe.wait_ge(key_taken, n - 1)
                nc.tensor.transpose(k_ps[n % 2][:, 0:nt], keys[0:nt, n:n + 1].to_broadcast([nt, P]), ident[0:nt, 0:nt]).then_inc(along, 1)
            for n, (t0, nt) in enumerate(blocks):
                if n >= 2:
                    pe.wait_ge(taken, n - 1)
                for g, (c0, cw) in enumerate(groups):
                    mm = nc.tensor.transpose(t_ps[n % 2][0:cw, g * P:g * P + nt], last[0:nt, n, c0:c0 + cw], ident[0:nt, 0:nt])
                mm.then_inc(turned, 1)
            pe.wait_ge(scanned, 1)
            for n, (t0, nt) in enumerate(blocks):
                if n >= 2:
                    pe.wait_ge(copied, n - 1)
                for g, (c0, cw) in enumerate(groups):
                    mm = nc.tensor.transpose(r_ps[n % 2][0:nt, c0:c0 + cw], sumT[0:cw, g, t0:t0 + nt], ident[0:cw, 0:cw])
                mm.then_inc(back, 1)

        @block.scalar
        def _(act):
            for n, (t0, nt) in enumerate(blocks):
                act.wait_ge(back, n + 1)
                nc.scalar.activation(rows[0:nt, n, :], r_ps[n % 2][0:nt, 0:W], ACT.Copy).then_inc(copied, 1)

        @block.vector
        def _(dve):
            nc.vector.memset(zero[:, :], 0.0).then_inc(cleared, 1)
            nc.vector.memset(endkey[:, 0:1], -1.0).then_inc(cleared, 1)
            for n, (t0, nt) in enumerate(blocks):
                dve.wait_ge(along, n + 1)
                nc.vector.tensor_copy(endkey[:, 1 + t0:1 + t0 + nt], k_ps[n % 2][:, 0:nt]).then_inc(key_taken, 1)
            dve.wait_ge(cleared, 2)
            dve.wait_ge(key_taken, RB)
            nc.vector.tensor_tensor(goes_on[:, :], endkey[:, 1:ET + 1], endkey[:, 0:ET], ALU.is_equal).then_inc(key_taken, 1)
            for n, (t0, nt) in enumerate(blocks):
                dve.wait_ge(turned, n + 1)
                for g, (c0, cw) in enumerate(groups):
                    mm = nc.vector.tensor_copy(lastT[0:cw, g, t0:t0 + nt], t_ps[n % 2][0:cw, g * P:g * P + nt])
                mm.then_inc(taken, 1)
            dve.wait_ge(key_taken, RB + 1)
            dve.wait_ge(taken, RB)
            for g, (c0, cw) in enumerate(groups):
                mm = nc.vector.tensor_tensor_scan(sumT[0:cw, g, :], goes_on[0:cw, :], lastT[0:cw, g, :], 0.0, ALU.mult, ALU.add)
            mm.then_inc(scanned, 1)


def node_ends(nc, dve, ph, base, hist, first, ends, mask, sem):
    nc.vector.tensor_scalar(mask[:, :], hist[:, :], 1.0, None, ALU.min).then_inc(sem, 1)
    nc.vector.tensor_tensor(first[:, :], base[:, :], hist[:, :], ALU.add).then_inc(sem, 1)
    dve.wait_ge(sem, 2)
    nc.vector.tensor_scalar(ends[:, :], first[:, :], -1.0, 0.0, ALU.add, ALU.max).then_inc(sem, 1)
    dve.wait_ge(sem, 3)


def node_rows(nc, name, running_d, carry_d, W, hist_d, base_d, out_d, c_d, add_d=None):
    with Phase(nc, name) as ph:
        ident = ph.sb("ident", [P, P])
        base, hist, first, mask = (ph.sb(n, [TT, NT]) for n in ("base", "hist", "first", "mask"))
        ends, tile = ph.sb("ends", [TT, NT], I32), ph.sb("tile", [TT, NT], I32)
        tile_f, cross = ph.sb("tile_f", [TT, NT]), ph.sb("cross", [TT, NT])
        eb, tb = ([ph.sb(f"{n}{b}", [TT, 2], I32) for b in range(2)] for n in ("eb", "tb"))
        cb = [ph.sb(f"cb{b}", [TT, 2]) for b in range(2)]
        last, before, row = ([ph.sb(f"{n}{b}", [TT, 2, W]) for b in range(2)] for n in ("last", "before", "row"))
        fac, floor = ([ph.sb(f"{n}{b}", [TT, 2]) for b in range(2)] for n in ("fac", "floor"))
        inv = [ph.sb(f"inv{b}", [TT, 2]) for b in range(2)]
        scaled = [ph.sb(f"scaled{b}", [TT, 2, D]) for b in range(2)]
        add = [ph.sb(f"add{b}", [P, 2, CW]) for b in range(2)] if add_d is not None else None
        add_in = [ph.sem(f"add_in{b}") for b in range(2)]
        out = [ph.sb(f"out{b}", [P, 2, CW]) for b in range(2)]
        o_ps = [ph.ps(f"o_ps{b}", [P, 512]) for b in range(2)]
        loaded, prep, gate = ph.sem("loaded"), ph.sem("prep"), ph.sem("gate")
        landed = [[ph.sem(f"landed{b}{t}") for t in range(2)] for b in range(2)]
        saved = [ph.sem(f"saved{b}") for b in range(2)]
        index_in, joined, s1, s2, factored, scaled_s, turned, copied = (ph.loop_sem(n) for n in (
            "index_in", "joined", "floored", "inverted", "factored", "scaled", "turned", "copied"))
        block = ph.block()

        @block.sync
        def _(sp):
            for b in range(2):
                sp.sem_inc(saved[b], 16)
            sp.dma_start(ident[:, :], c_d["ident"]).then_inc(loaded, 16)
            sp.dma_start(base[:, :], base_d[0:N].rearrange("(t p) -> p t", p=TT), allow_slow_non_contiguous=True).then_inc(loaded, 16)
            sp.dma_start(hist[:, :], hist_d[0:N].rearrange("(t p) -> p t", p=TT), allow_slow_non_contiguous=True).then_inc(loaded, 16)

            def load(c, b):
                if add:
                    sp.dma_start(add[b][:, :, :], add_d[:, :, ds(c * CW, CW)]).then_inc(add_in[b], 16)
            for b in range(2):
                load(b, b)

            def body(c, b, r, more):
                sp.wait_ge(copied, c + NOW)
                sp.dma_start(out_d[:, :, ds(c * CW, CW)], out[b][:, :, :]).then_inc(saved[b], 16)
                if more:
                    load(c + 2, b)
            chunks(sp, body, 2)
            for b in range(2):
                sp.wait_ge(saved[b], 16 * ((NCH + 1 - b) // 2) + 16)

        @block.gpsimd
        def _(pool):
            def body(c, b, r, more):
                pool.wait_ge(index_in, c + NOW)
                pool.wait_ge(scaled_s, c + OLD)
                pool.sem_inc(gate, 1)
                for t in range(2):
                    nc.gpsimd.indirect_dma_start(last[b][:, t, :], None, running_d, bass.IndirectOffsetOnAxis(eb[b][:, t:t + 1], 0)).then_inc(landed[b][t], 16)
                    nc.gpsimd.indirect_dma_start(before[b][:, t, :], None, carry_d, bass.IndirectOffsetOnAxis(tb[b][:, t:t + 1], 0)).then_inc(landed[b][t], 16)
            chunks(pool, body)

        @block.vector
        def _(dve):
            dve.wait_ge(loaded, 48)
            node_ends(nc, dve, ph, base, hist, first, ends, mask, prep)
            nc.vector.tensor_scalar(tile[:, :], ends[:, :], 7, None, ALU.logical_shift_right).then_inc(prep, 1)
            dve.wait_ge(prep, 4)
            nc.vector.tensor_copy(tile_f[:, :], tile[:, :]).then_inc(prep, 1)
            dve.wait_ge(prep, 5)
            nc.vector.scalar_tensor_tensor(cross[:, :], tile_f[:, :], float(P), base[:, :], ALU.mult, ALU.is_gt).then_inc(prep, 1)
            dve.wait_ge(prep, 6)

            def indices(c, b):
                dve.wait_ge(scaled_s, c + OLD)
                nc.vector.tensor_copy(eb[b][:, :], ends[:, ds(c * 2, 2)])
                nc.vector.tensor_copy(cb[b][:, :], cross[:, ds(c * 2, 2)])
                nc.vector.tensor_copy(tb[b][:, :], tile[:, ds(c * 2, 2)]).then_inc(index_in, 1)
            indices(0, 0)

            def body(c, b, r, more):
                if more:
                    indices(c + 1, 1 - b)
                dve.wait_ge(index_in, c + NOW)
                for t in range(2):
                    dve.wait_ge(landed[b][t], r * 32 + 32)
                    ins = nc.vector.scalar_tensor_tensor(row[b][:, t, :], before[b][:, t, :], cb[b][:, t:t + 1], last[b][:, t, :], ALU.mult, ALU.add)
                ins.then_inc(joined, 1)
                dve.wait_ge(joined, c + NOW)
                if W > D:
                    nc.vector.tensor_scalar(floor[b][:, :], row[b][:, :, D], 1e-30, None, ALU.max).then_inc(s1, 1)
                    dve.wait_ge(s1, c + NOW)
                    nc.vector.reciprocal(inv[b][:, :], floor[b][:, :]).then_inc(s2, 1)
                    dve.wait_ge(s2, c + NOW)
                    dve.wait_ge(scaled_s, c + OLD)
                    nc.vector.tensor_tensor(fac[b][:, :], inv[b][:, :], mask[:, ds(c * 2, 2)], ALU.mult).then_inc(factored, 1)
                else:
                    dve.wait_ge(scaled_s, c + OLD)
                    nc.vector.tensor_copy(fac[b][:, :], mask[:, ds(c * 2, 2)]).then_inc(factored, 1)
                dve.wait_ge(factored, c + NOW)
                dve.wait_ge(turned, c + OLD)
                nc.vector.tensor_tensor(scaled[b][:, :, :], row[b][:, :, 0:D], fac[b][:, :].unsqueeze(2).to_broadcast([TT, 2, D]), ALU.mult).then_inc(scaled_s, 1)
                if add:
                    dve.wait_ge(turned, c + NOW)
                    dve.wait_ge(saved[b], r * 16 + 16)
                    dve.wait_ge(add_in[b], r * 16 + 16)
                    nc.vector.tensor_tensor(out[b][:, :, :], feature_major(o_ps[b]), add[b][:, :, :], ALU.add).then_inc(copied, 1)
            chunks(dve, body)

        @block.tensor
        def _(pe):
            pe.wait_ge(loaded, 48)

            def body(c, b, r, more):
                pe.wait_ge(scaled_s, c + NOW)
                pe.wait_ge(copied, c + OLD)
                for t in range(2):
                    for h in range(2):
                        mm = nc.tensor.transpose(o_ps[b][:, h * CW + t * TT:h * CW + (t + 1) * TT], scaled[b][:, t, h * P:(h + 1) * P], ident[0:TT, 0:TT])
                mm.then_inc(turned, 1)
            chunks(pe, body)

        @block.scalar
        def _(act):
            def body(c, b, r, more):
                act.wait_ge(turned, c + NOW)
                act.wait_ge(saved[b], r * 16 + 16)
                nc.scalar.activation(out[b][:, :, :], feature_major(o_ps[b]), ACT.Copy).then_inc(copied, 1)
            if not add:
                chunks(act, body)


def batchnorm_factors(nc, dve, act, stats, mv, gain, offset, scale, shift, dev, inv, t, eps_t, sem, root):
    def on_dve():
        for h in range(2):
            nc.vector.bn_aggr(mv[:, h, :], stats[:, h, :, :].rearrange("p c s -> p (c s)")).then_inc(sem, 1)
        dve.wait_ge(root, 1)
        nc.vector.reciprocal(inv[:, :], dev[:, :]).then_inc(sem, 1)
        dve.wait_ge(sem, 3)
        nc.vector.tensor_tensor(scale[:, :], inv[:, :], gain[:, :], ALU.mult).then_inc(sem, 1)
        dve.wait_ge(sem, 4)
        nc.vector.tensor_tensor(t[:, :], mv[:, :, 0], scale[:, :], ALU.mult).then_inc(sem, 1)
        dve.wait_ge(sem, 5)
        nc.vector.tensor_tensor(shift[:, :], offset[:, :], t[:, :], ALU.subtract).then_inc(sem, 1)
        dve.wait_ge(sem, 6)

    def on_act():
        act.wait_ge(sem, 2)
        nc.scalar.activation(dev[:, :], mv[:, :, 1], ACT.Sqrt, bias=eps_t[:, 0:1]).then_inc(root, 1)
    return on_dve, on_act


def message_layer(nc, name, agg_d, x_d, xn_d, mix_d, out_d, norm_d, c_d, eps_d, w1_d, w2_d, g1_d, o1_d, g2_d, o2_d):
    common = ("gain1", "offset1", "gain2", "offset2", "scale1", "shift1", "scale2", "shift2", "dev", "inv", "t")
    with Phase(nc, name) as keep:
        tiles = {n: keep.sb(n, [P, 2]) for n in common}
        mv = keep.sb("mv", [P, 2, 2])
        zu = keep.sb("zu", [P, 2, N])
        stats = keep.sb("stats", [P, 2, NCH, 6])
        w1, w2, epsw, eps_t = keep.sb("w1", [P, 2, D]), keep.sb("w2", [P, 2, D]), keep.sb("epsw", [P, 1]), keep.sb("eps", [P, 1])
        for step in range(3):
            with Phase(nc, f"{name}{step}") as ph:
                srcs = [(agg_d, xn_d), (), (xn_d, x_d, mix_d)][step]
                ins = [[ph.sb(f"in{n}_{b}", [P, 2, CW]) for b in range(2)] for n in range(len(srcs))]
                y, res = ([ph.sb(f"{n}{b}", [P, 2, CW]) for b in range(2)] for n in ("y", "res"))
                nn = [ph.sb(f"nn{b}", [P, CW]) for b in range(2)]
                m_ps = [ph.ps(f"m_ps{b}", [P, 512]) for b in range(2)]
                loaded, saved = ([ph.sem(f"{n}{b}") for b in range(2)] for n in ("loaded", "saved"))
                y_made, mult, res_made, statted, s3, s4, s5 = (ph.loop_sem(n) for n in (
                    "y_made", "mult", "res_made", "statted", "plus_xn", "plus_x", "plus_mix"))
                weights, agg_s, root = ph.sem("weights"), ph.sem("aggregated"), ph.sem("root")
                n_in = len(srcs) + (1 if step == 1 else 0)
                loads = [] if step else [(tiles["gain1"], g1_d), (tiles["offset1"], o1_d), (tiles["gain2"], g2_d), (tiles["offset2"], o2_d),
                                         (w1, w1_d), (w2, w2_d), (epsw, eps_d.partition_broadcast(P))]
                inputs_used = (y_made, res_made, s5)[step]
                block = ph.block()

                @block.sync
                def _(sp):
                    for b in range(2):
                        sp.sem_inc(saved[b], 16)
                    for to, src in loads:
                        sp.dma_start(to[:], src).then_inc(weights, 16)

                    def load(c, b):
                        for n, src in enumerate(srcs):
                            sp.dma_start(ins[n][b][:, :, :], src[:, :, ds(c * CW, CW)]).then_inc(loaded[b], 16)
                        if step == 1:
                            sp.dma_start(nn[b][:, :], norm_d[ds(c * CW, CW)].partition_broadcast(P)).then_inc(loaded[b], 16)
                    load(0, 0)

                    def body(c, b, r, more):
                        if more:
                            sp.wait_ge(inputs_used, c + PREV)
                            load(c + 1, 1 - b)
                        if step == 2:
                            sp.wait_ge(s5, c + NOW)
                            sp.dma_start(out_d[:, :, ds(c * CW, CW)], res[b][:, :, :]).then_inc(saved[b], 16)
                    chunks(sp, body)
                    if step == 2:
                        for b in range(2):
                            sp.wait_ge(saved[b], 16 * ((NCH + 1 - b) // 2) + 16)

                @block.vector
                def _(dve):
                    if step == 0:
                        nc.vector.memset(eps_t[:, :], 1e-5).then_inc(weights, 1)
                        dve.wait_ge(weights, 16 * len(loads) + 1)

                    def before(c, b, r):
                        dve.wait_ge(loaded[b], r * (16 * n_in) + 16 * n_in)
                        if step == 0:
                            dve.wait_ge(mult, c + OLD)
                            nc.vector.scalar_tensor_tensor(y[b][:, :, :], ins[1][b][:, :, :], epsw[:, 0:1], ins[0][b][:, :, :], ALU.mult,
                                                           ALU.add).then_inc(y_made, 1)
                    if step < 2:
                        before(0, 0, 0)

                    def body(c, b, r, more):
                        zu_c = zu[:, :, ds(c * CW, CW)]
                        if step < 2:
                            if more:
                                before(c + 1, 1 - b, r + b)
                            dve.wait_ge(mult, c + NOW)
                        else:
                            dve.wait_ge(loaded[b], r * (16 * n_in) + 16 * n_in)
                        if step == 0:
                            nc.vector.tensor_copy(zu_c, feature_major(m_ps[b])).then_inc(res_made, 1)
                        if step == 1:
                            nc.vector.tensor_tensor(zu_c, feature_major(m_ps[b]), nn[b][:, None, :].to_broadcast([P, 2, CW]),
                                                    ALU.mult).then_inc(res_made, 1)
                        if step < 2:
                            dve.wait_ge(res_made, c + NOW)
                            for h in range(2):
                                last = nc.vector.bn_stats(stats[:, h, ds(c, 1), :].rearrange("p c s -> p (c s)"), zu[:, h, ds(c * CW, CW)])
                            last.then_inc(statted, 1)
                        if step == 2:
                            dve.wait_ge(y_made, c + NOW)
                            dve.wait_ge(saved[b], r * 16 + 16)
                            for n, (a, s) in enumerate(((y, s3), (res, s4), (res, s5))):
                                if n:
                                    dve.wait_ge((s3, s4)[n - 1], c + NOW)
                                nc.vector.tensor_tensor(res[b][:, :, :], a[b][:, :, :], ins[n][b][:, :, :], ALU.add).then_inc(s, 1)
                    chunks(dve, body)
                    if step < 2:
                        dve.wait_ge(statted, NCH - 1 + NOW)
                        batchnorm_factors(nc, dve, None, stats, mv, tiles[f"gain{step + 1}"], tiles[f"offset{step + 1}"], tiles[f"scale{step + 1}"],
                                          tiles[f"shift{step + 1}"], tiles["dev"], tiles["inv"], tiles["t"], eps_t, agg_s, root)[0]()

                @block.scalar
                def _(act):
                    def body(c, b, r, more):
                        if step:
                            act.wait_ge(mult if step == 1 else s3, c + OLD)
                            for h in range(2):
                                last = nc.scalar.activation(y[b][:, h, :], zu[:, h, ds(c * CW, CW)], ACT.Relu, bias=tiles[f"shift{step}"][:, h:h + 1],
                                                            scale=tiles[f"scale{step}"][:, h:h + 1])
                            last.then_inc(y_made, 1)
                    if step:
                        chunks(act, body)
                    if step < 2:
                        batchnorm_factors(nc, None, act, stats, mv, None, None, None, None, tiles["dev"], None, None, eps_t, agg_s, root)[1]()

                if step < 2:
                    @block.tensor
                    def _(pe):
                        w = (w1, w2)[step]
                        if step == 0:
                            pe.wait_ge(weights, 16 * len(loads) + 1)

                        def body(c, b, r, more):
                            pe.wait_ge(y_made, c + NOW)
                            pe.wait_ge(res_made, c + OLD)
                            for h in range(2):
                                for k in range(2):
                                    mm = nc.tensor.matmul(m_ps[b][:, h * CW:(h + 1) * CW], w[:, k, h * P:(h + 1) * P], y[b][:, k, :], start=(k == 0), stop=(k == 1))
                            mm.then_inc(mult, 1)
                        chunks(pe, body)


def experts(nc, name, x_d, out_d, c_d, router_d, w1_d, b1_d, w2_d, b2_d, scatter):
    NE = 8
    with Phase(nc, name) as ph:
        x = [ph.sb(f"x{b}", [P, 2, CW]) for b in range(2)]
        ones, ident = ph.sb("ones", [P, P]), ph.sb("ident", [P, P])
        router, pick = ph.sb("router", [P, 2, NE]), ph.sb("pick", [NE, NE, P])
        before = ph.sb("before", [TT, NE, NE])
        w1, w2 = ph.sb("w1", [P, NE, 2, D]), ph.sb("w2", [P, NE, 2, D])
        b1, b2 = ph.sb("b1", [P, NE, 2]), ph.sb("b2", [NE, D])
        lg, lmax, les, ex, esum, erec, pr, cnt, eq, sel, psel, ps, pg, pgr, comb = (
            [ph.sb(f"{n}{b}", s) for b in range(2)] for n, s in (
                ("lg", [TT, 2, NE]), ("lmax", [TT, 2]), ("les", [TT, 2, NE]), ("ex", [TT, 2, NE]), ("esum", [TT, 2]), ("erec", [TT, 2]),
                ("pr", [TT, 2, NE]), ("cnt", [TT, 2 * NE, NE]), ("eq", [TT, 2 * NE, NE]), ("sel", [TT, 2, NE]), ("psel", [TT, 2, NE]),
                ("ps", [TT, 2]), ("pg", [TT, 2]), ("pgr", [TT, 2]), ("comb", [TT, 2, NE])))
        combT = [ph.sb(f"combT{b}", [NE, CW]) for b in range(2)]
        g = [ph.sb(f"g{n}", [P, 2, CW]) for n in range(2)]
        gw = [ph.sb(f"gw{n}", [P, 2, CW]) for n in range(2)]
        t1, y = ([ph.sb(f"{n}{b}", [P, 2, CW]) for b in range(2)] for n in ("t1_", "y"))
        h_ps = [ph.ps(f"h_ps{n}", [P, 512]) for n in range(2)]
        o_ps = [ph.ps(f"o_ps{h}", [P, 512]) for h in range(2)]
        l_ps, c_ps = ph.ps("l_ps", [P, 512]), ph.ps("c_ps", [P, 512])
        weights = ph.sem("weights")
        loaded, saved = ([ph.sem(f"{n}{b}") for b in range(2)] for n in ("loaded", "saved"))
        logits, l_read, comb_ready, combT_made, combT_copied, y_made, summed_x = (ph.loop_sem(n) for n in (
            "logits", "l_read", "comb_ready", "combT_made", "combT_copied", "y_made", "summed_x"))
        route = [ph.loop_sem(f"route{n}") for n in range(16)]
        e_up, e_gelu, e_cb, e_weighted, e_down = (ph.loop_sem(n) for n in ("e_up", "e_gelu", "e_cb", "e_weighted", "e_down"))
        exped = ph.loop_sem("exped")
        ln = Norm(nc, ph, x, ones, [y_made, summed_x])
        loads = [(ones, c_d["mean"]), (ident, c_d["ident"]), (pick, c_d["pick"]), (before, c_d["before"]), (router, router_d),
                 (w1, w1_d), (b1, b1_d), (w2, w2_d), (b2, b2_d)]
        side = Scatter(nc, ph, *scatter)
        block = ph.block()

        @block.sync
        def _(sp):
            for b in range(2):
                sp.sem_inc(saved[b], 16)
            sp.dma_start(x[0][:, :, :], x_d[:, :, 0:CW]).then_inc(loaded[0], 16)
            for dst, src in loads:
                sp.dma_start(dst[:], src).then_inc(weights, 16)

            def body(c, b, r, more):
                if more:
                    sp.wait_ge(ln.centred, c + PREV)
                    sp.wait_ge(summed_x, c + PREV)
                    sp.dma_start(x[1 - b][:, :, :], x_d[:, :, ds((c + 1) * CW, CW)]).then_inc(loaded[1 - b], 16)
                sp.wait_ge(y_made, c + NOW)
                sp.dma_start(out_d[:, :, ds(c * CW, CW)], y[b][:, :, :]).then_inc(saved[b], 16)
            chunks(sp, body)
            for b in range(2):
                sp.wait_ge(saved[b], 16 * ((NCH + 1 - b) // 2) + 16)

        @block.gpsimd
        def _(pool):
            chunks(pool, lambda c, b, r, more: side.pool(pool, c, b, r))

        @block.tensor
        def _(pe):
            def scores(c, b):
                pe.wait_ge(ln.normed, c + NOW)
                pe.wait_ge(l_read, c + PREV)
                pe.wait_ge(combT_copied, c + PREV)
                for t in range(2):
                    for k in range(2):
                        mm = nc.tensor.matmul(l_ps[0:TT, t * NE:(t + 1) * NE], ln.out[b][:, k, t * TT:(t + 1) * TT], router[:, k, :], start=(k == 0), stop=(k == 1))
                mm.then_inc(logits, 1)

            def turn(c, b):
                pe.wait_ge(comb_ready, c + NOW)
                for t in range(2):
                    mm = nc.tensor.transpose(l_ps[0:NE, 256 + t * TT:256 + (t + 1) * TT], comb[b][:, t, :], ident[0:TT, 0:TT])
                mm.then_inc(combT_made, 1)

            def up(c, b, e):
                n = c * NE + e
                pe.wait_ge(e_gelu, n + OLD)
                for h in range(2):
                    for k in range(2):
                        mm = nc.tensor.matmul(h_ps[e % 2][:, h * CW:(h + 1) * CW], w1[:, e, k, h * P:(h + 1) * P], ln.out[b][:, k, :], start=(k == 0), stop=(k == 1))
                mm.then_inc(e_up, 1)
                pe.wait_ge(e_weighted, n + PREV)
                nc.tensor.matmul(c_ps[:, 0:CW], pick[:, e, :], combT[b][:, :], start=True, stop=True).then_inc(e_cb, 1)

            def down(c, b, e):
                pe.wait_ge(e_weighted, c * NE + (e + NOW))
                for h in range(2):
                    for k in range(2):
                        mm = nc.tensor.matmul(o_ps[h][:, 0:CW], w2[:, e, k, h * P:(h + 1) * P], gw[e % 2][:, k, :], start=False, stop=(e == NE - 1 and k == 1),
                                              skip_group_check=True)
                mm.then_inc(e_down, 1)

            pe.wait_ge(weights, 16 * len(loads))
            pe.wait_ge(loaded[0], 16)
            ln.pe_mean(pe, 0, 0)
            ln.pe_var(pe, 0, 0)
            scores(0, 0)
            turn(0, 0)

            def body(c, b, r, more):
                pe.wait_ge(combT_copied, c + NOW)
                pe.wait_ge(y_made, c + PREV)
                for e in range(NE):
                    up(c, b, e)
                    if e == 0:
                        for h in range(2):
                            nc.tensor.matmul(o_ps[h][:, 0:CW], b2[:, h * P:(h + 1) * P], combT[b][:, :], start=True, stop=False, skip_group_check=True)
                    else:
                        down(c, b, e - 1)
                    if more:
                        if e == 1:
                            pe.wait_ge(loaded[1 - b], r * 16 + (b * 16 + 16))
                            ln.pe_mean(pe, c + 1, 1 - b)
                        if e == 3:
                            ln.pe_var(pe, c + 1, 1 - b)
                        if e == 5:
                            scores(c + 1, 1 - b)
                        if e == 7:
                            turn(c + 1, 1 - b)
                down(c, b, NE - 1)
            chunks(pe, body)

        @block.scalar
        def _(act):
            def softmax_exp(c, b):
                act.wait_ge(route[1], c + NOW)
                act.wait_ge(route[3], c + OLD)
                act.wait_ge(route[4], c + OLD)
                nc.scalar.activation(ex[b][:, :, :], les[b][:, :, :], ACT.Exp).then_inc(exped, 1)

            def copy_turned(c, b):
                act.wait_ge(combT_made, c + NOW)
                act.wait_ge(y_made, c + OLD)
                nc.scalar.activation(combT[b][:, :], l_ps[0:NE, 256:256 + CW], ACT.Copy).then_inc(combT_copied, 1)

            act.wait_ge(weights, 16 * len(loads))
            ln.act_square(act, 0, 0)
            ln.act_root(act, 0, 0)
            softmax_exp(0, 0)
            copy_turned(0, 0)

            def body(c, b, r, more):
                for e in range(NE):
                    n = c * NE + e
                    act.wait_ge(e_up, n + NOW)
                    act.wait_ge(e_weighted, n + OLD)
                    for h in range(2):
                        last = nc.scalar.activation(g[e % 2][:, h, :], h_ps[e % 2][:, h * CW:(h + 1) * CW], ACT.Gelu, bias=b1[:, e, h:h + 1])
                    last.then_inc(e_gelu, 1)
                    if more:
                        if e == 2:
                            ln.act_square(act, c + 1, 1 - b)
                        if e == 4:
                            ln.act_root(act, c + 1, 1 - b)
                        if e == 6:
                            softmax_exp(c + 1, 1 - b)
                if more:
                    copy_turned(c + 1, 1 - b)
            chunks(act, body)

        @block.vector
        def _(dve):
            def step(c, n, ins):
                ins.then_inc(route[n], 1)
                dve.wait_ge(route[n], c + NOW)

            def routing1(c, b):
                dve.wait_ge(logits, c + NOW)
                dve.wait_ge(comb_ready, c + OLD)
                dve.wait_ge(exped, c + OLD)
                nc.vector.tensor_copy(lg[b][:, :, :], l_ps[0:TT, 0:2 * NE].rearrange("p (t e) -> p t e", t=2)).then_inc(l_read, 1)
                dve.wait_ge(l_read, c + NOW)
                step(c, 0, nc.vector.tensor_reduce(lmax[b][:, :], lg[b][:, :, :], AX_X, ALU.max))
                step(c, 1, nc.vector.tensor_tensor(les[b][:, :, :], lg[b][:, :, :], lmax[b][:, :].unsqueeze(2).to_broadcast([TT, 2, NE]), ALU.subtract))

            def routing2(c, b):
                dve.wait_ge(exped, c + NOW)
                step(c, 3, nc.vector.tensor_reduce(esum[b][:, :], ex[b][:, :, :], AX_X, ALU.add))
                step(c, 2, nc.vector.reciprocal(erec[b][:, :], esum[b][:, :]))
                step(c, 4, nc.vector.tensor_tensor(pr[b][:, :, :], ex[b][:, :, :], erec[b][:, :].unsqueeze(2).to_broadcast([TT, 2, NE]), ALU.mult))
                for t in range(2):
                    own = pr[b][:, t, :].unsqueeze(2).to_broadcast([TT, NE, NE])
                    others = pr[b][:, t, None, :].to_broadcast([TT, NE, NE])
                    nc.vector.tensor_tensor(cnt[b][:, t * NE:(t + 1) * NE, :], others, own, ALU.is_gt)
                    last = nc.vector.tensor_tensor(eq[b][:, t * NE:(t + 1) * NE, :], others, own, ALU.is_equal)
                step(c, 5, last)
                for t in range(2):
                    last = nc.vector.tensor_tensor(eq[b][:, t * NE:(t + 1) * NE, :], eq[b][:, t * NE:(t + 1) * NE, :], before[:, :, :], ALU.mult)
                step(c, 6, last)
                step(c, 7, nc.vector.tensor_tensor(cnt[b][:], cnt[b][:], eq[b][:], ALU.add))
                step(c, 8, nc.vector.tensor_reduce(sel[b][:].rearrange("p t e -> p (t e)"), cnt[b][:], AX_X, ALU.add))
                step(c, 9, nc.vector.scalar_tensor_tensor(psel[b][:], sel[b][:], 2.0, pr[b][:], ALU.is_lt, ALU.mult))
                step(c, 10, nc.vector.tensor_reduce(ps[b][:, :], psel[b][:], AX_X, ALU.add))
                step(c, 11, nc.vector.tensor_scalar(pg[b][:, :], ps[b][:, :], 1e-12, None, ALU.max))
                step(c, 12, nc.vector.reciprocal(pgr[b][:, :], pg[b][:, :]))
                dve.wait_ge(combT_made, c + OLD)
                nc.vector.tensor_tensor(comb[b][:], psel[b][:], pgr[b][:, :].unsqueeze(2).to_broadcast([TT, 2, NE]), ALU.mult).then_inc(comb_ready, 1)

            ln.dve_start(dve)
            side.dve(dve, 0, 0)
            dve.wait_ge(weights, 16 * len(loads))
            dve.wait_ge(loaded[0], 16)
            ln.dve_centre(dve, 0, 0)
            ln.dve_norm(dve, 0, 0)
            routing1(0, 0)
            routing2(0, 0)

            def body(c, b, r, more):
                for e in range(NE):
                    n = c * NE + e
                    dve.wait_ge(e_gelu, n + NOW)
                    dve.wait_ge(e_cb, n + NOW)
                    dve.wait_ge(e_down, n + OLD)
                    nc.vector.tensor_tensor(gw[e % 2][:, :, :], g[e % 2][:, :, :], c_ps[:, None, 0:CW].to_broadcast([P, 2, CW]), ALU.mult).then_inc(e_weighted, 1)
                    if more:
                        if e == 0:
                            side.dve(dve, c + 1, 1 - b)
                        if e == 1:
                            dve.wait_ge(loaded[1 - b], r * 16 + (b * 16 + 16))
                            ln.dve_centre(dve, c + 1, 1 - b)
                        if e == 4:
                            ln.dve_norm(dve, c + 1, 1 - b)
                        if e == 5:
                            routing1(c + 1, 1 - b)
                        if e == 6:
                            routing2(c + 1, 1 - b)
                dve.wait_ge(y_made, c + OLD)
                nc.vector.tensor_tensor(t1[b][:, :, :], x[b][:, :, :], ln.out[b][:, :, :], ALU.add).then_inc(summed_x, 1)
                dve.wait_ge(summed_x, c + NOW)
                dve.wait_ge(e_down, c * NE + (NE - 1 + NOW))
                dve.wait_ge(saved[b], r * 16 + 16)
                for h in range(2):
                    last = nc.vector.tensor_tensor(y[b][:, h, :], t1[b][:, h, :], o_ps[h][:, 0:CW], ALU.add)
                last.then_inc(y_made, 1)
            chunks(dve, body)


def token_weights(nc, name, x_d, t_d, row_d, c_d, wr_d, br_d):
    with Phase(nc, name) as ph:
        x = [ph.sb(f"x{b}", [P, 2, CW]) for b in range(2)]
        ones, wr, wrb, br = ph.sb("ones", [P, P]), ph.sb("wr", [P, 2]), ph.sb("wrb", [P, 2, 32]), ph.sb("br", [32, 1])
        row = [ph.sb(f"row{b}", [32, CW]) for b in range(2)]
        r_ps = [ph.ps(f"r_ps{b}", [P, 512]) for b in range(2)]
        weights, wide = ph.sem("weights"), ph.sem("wide")
        loaded, saved, out_saved = ([ph.sem(f"{n}{b}") for b in range(2)] for n in ("loaded", "saved", "out_saved"))
        made, copied = (ph.loop_sem(n) for n in ("made", "copied"))
        out_sent = ph.sem("out_sent")
        ln = Norm(nc, ph, x, ones, [made, out_sent])
        loads = [(ones, c_d["mean"]), (wr, wr_d), (br, br_d.partition_broadcast(32))]
        nc.sync.sem_inc(out_sent, START - 1)
        block = ph.block()

        @block.sync
        def _(sp):
            for b in range(2):
                sp.sem_inc(saved[b], 16)
                sp.sem_inc(out_saved[b], 16)
                sp.dma_start(x[b][:, :, :], x_d[:, :, b * CW:(b + 1) * CW]).then_inc(loaded[b], 16)
            for dst, src in loads:
                sp.dma_start(dst[:], src).then_inc(weights, 16)

            def body(c, b, r, more):
                if more:
                    sp.wait_ge(ln.centred, c + NOW)
                    sp.dma_start(x[b][:, :, :], x_d[:, :, ds((c + 2) * CW, CW)]).then_inc(loaded[b], 16)
                sp.wait_ge(out_saved[1 - b], r * 16 + (b * 16 + 16))
                sp.sem_inc(out_sent, 1)
                sp.wait_ge(ln.normed, c + NOW)
                sp.dma_start(t_d[:, :, ds(c * CW, CW)], ln.out[b][:, :, :]).then_inc(out_saved[b], 16)
                sp.wait_ge(copied, c + NOW)
                sp.dma_start(row_d[ds(c * CW, CW)].rearrange("(o n) -> o n", o=1), row[b][0:1, :]).then_inc(saved[b], 16)
            chunks(sp, body, 2)
            for b in range(2):
                sp.wait_ge(out_saved[b], 16 * ((NCH + 1 - b) // 2) + 16)
                sp.wait_ge(saved[b], 16 * ((NCH + 1 - b) // 2) + 16)

        @block.tensor
        def _(pe):
            pe.wait_ge(weights, 16 * len(loads))
            pe.wait_ge(loaded[0], 16)
            ln.pe_mean(pe, 0, 0)
            ln.pe_var(pe, 0, 0)
            pe.wait_ge(wide, 1)

            def body(c, b, r, more):
                if more:
                    pe.wait_ge(loaded[1 - b], r * 16 + (b * 16 + 16))
                    ln.pe_mean(pe, c + 1, 1 - b)
                pe.wait_ge(ln.normed, c + NOW)
                pe.wait_ge(copied, c + OLD)
                for k in range(2):
                    mm = nc.tensor.matmul(r_ps[b][0:32, 0:CW], wrb[:, k, :], ln.out[b][:, k, :], start=(k == 0), stop=(k == 1))
                mm.then_inc(made, 1)
                if more:
                    ln.pe_var(pe, c + 1, 1 - b)
            chunks(pe, body)

        @block.scalar
        def _(act):
            act.wait_ge(weights, 16 * len(loads))
            ln.act_square(act, 0, 0)
            ln.act_root(act, 0, 0)

            def body(c, b, r, more):
                if more:
                    ln.act_square(act, c + 1, 1 - b)
                act.wait_ge(made, c + NOW)
                act.wait_ge(saved[b], r * 16 + 16)
                nc.scalar.activation(row[b][:, :], r_ps[b][0:32, 0:CW], ACT.Identity, bias=br[:, 0:1]).then_inc(copied, 1)
                if more:
                    ln.act_root(act, c + 1, 1 - b)
            chunks(act, body)

        @block.vector
        def _(dve):
            ln.dve_start(dve)
            dve.wait_ge(weights, 16 * len(loads))
            nc.vector.tensor_copy(wrb[:, :, :], wr[:, :].unsqueeze(2).to_broadcast([P, 2, 32])).then_inc(wide, 1)
            dve.wait_ge(loaded[0], 16)
            ln.dve_centre(dve, 0, 0)
            ln.dve_norm(dve, 0, 0)

            def body(c, b, r, more):
                if more:
                    dve.wait_ge(loaded[1 - b], r * 16 + (b * 16 + 16))
                    ln.dve_centre(dve, c + 1, 1 - b)
                    ln.dve_norm(dve, c + 1, 1 - b)
            chunks(dve, body)


KEPT = N // 2 - 1


def chosen_forward(nc, name, t_d, x_d, row_d, factor_d, out_d, c_d, w1_d, b1_d, w2_d, b2_d):
    F = 4 * D
    FG = F // P
    with Phase(nc, name) as ph:
        row, col = ph.sb("row", [TT, N]), ph.sb("col", [TT, NT])
        tri, diag = ph.sb("tri", [TT, TT]), [ph.sb(f"diag{b}", [TT, TT]) for b in range(2)]
        junk = ph.sb("junk", [TT, N])
        parts = ph.sb("parts", [TT, 4, NT])
        total, factor = ph.sb("total", [TT, 3, NT]), ph.sb("factor", [TT, NT])
        forward = ph.sb("forward", [P, 2, N])
        t, x, y = ([ph.sb(f"{n}{b}", [P, 2, CW]) for b in range(2)] for n in ("t", "x", "y"))
        fac = [ph.sb(f"fac{b}", [P, CW]) for b in range(2)]
        g = [ph.sb(f"g{b}", [P, FG, CW]) for b in range(2)]
        w1, w2, b1, b2 = ph.sb("w1", [P, 2, F]), ph.sb("w2", [P, FG, D]), ph.sb("b1", [P, FG]), ph.sb("b2", [P, 2])
        f_ps = [ph.ps(f"f_ps{i}", [P, 512]) for i in range(4)]
        y_ps = [ph.ps(f"y_ps{b}", [P, 512]) for b in range(2)]
        weights, compare_in, step, factor_saved, done = (ph.sem(n) for n in ("weights", "compare_in", "step", "factor_saved", "compared"))
        t_in, loaded, saved = ([ph.sem(f"{n}{b}") for b in range(2)] for n in ("t_in", "loaded", "saved"))
        y_made, y_kept, y_scaled, y_t, y_x = (ph.loop_sem(n) for n in ("y_made", "y_kept", "y_scaled", "plus_t", "plus_x"))
        up = [ph.loop_sem(f"up{m}") for m in range(4)]
        gelu = [ph.loop_sem(f"gelu{m}") for m in range(4)]
        loads = [(w1, w1_d), (b1, b1_d), (w2, w2_d), (b2, b2_d)]
        block = ph.block()

        @block.sync
        def _(sp):
            for b in range(2):
                sp.sem_inc(saved[b], 16)

            def load(dst, src, c, b, sem):
                sp.dma_start(dst[b][:, :, :], src[:, :, ds(c * CW, CW)]).then_inc(sem[b], 16)
            for b in range(2):
                load(t, t_d, b, b, t_in)
            for dst, src in loads:
                sp.dma_start(dst[:], src).then_inc(weights, 16)
            sp.dma_start(row[:, :], row_d.partition_broadcast(TT)).then_inc(compare_in, 16)
            sp.dma_start(col[:, :], row_d.rearrange("(t p) -> p t", p=TT), allow_slow_non_contiguous=True).then_inc(compare_in, 16)
            sp.dma_start(tri[:, :], c_d["tri"][0:TT, 0:TT]).then_inc(compare_in, 16)

            def body(c, b, r, more):
                if more:
                    sp.wait_ge(up[3], c + NOW)
                    load(t, t_d, c + 2, b, t_in)
            chunks(sp, body, 2)
            sp.wait_ge(step, 5)
            sp.dma_start(factor_d.rearrange("(t p) -> p t", p=TT), factor[:, :], allow_slow_non_contiguous=True).then_inc(factor_saved, 16)
            sp.wait_ge(up[3], NCH - 1 + NOW)
            sp.wait_ge(factor_saved, 16)

            def load_all(c, b):
                load(t, t_d, c, b, loaded)
                load(x, x_d, c, b, loaded)
                sp.dma_start(fac[b][:, :], factor_d[ds(c * CW, CW)].partition_broadcast(P)).then_inc(loaded[b], 16)
            for b in range(2):
                load_all(b, b)

            def finish(c, b, r, more):
                sp.wait_ge(y_x, c + NOW)
                sp.dma_start(out_d[:, :, ds(c * CW, CW)], y[b][:, :, :]).then_inc(saved[b], 16)
                if more:
                    load_all(c + 2, b)
            chunks(sp, finish, 2)
            for b in range(2):
                sp.wait_ge(saved[b], 16 * ((NCH + 1 - b) // 2) + 16)

        @block.tensor
        def _(pe):
            pe.wait_ge(weights, 16 * len(loads))

            def body(c, b, r, more):
                pe.wait_ge(t_in[b], r * 16 + 16)
                for m in range(4):
                    pe.wait_ge(gelu[m], c + PREV)
                    for h in range(2):
                        for k in range(2):
                            g0 = (2 * m + h) * P
                            mm = nc.tensor.matmul(f_ps[m][:, h * CW:(h + 1) * CW], w1[:, k, g0:g0 + P], t[b][:, k, :], start=(k == 0), stop=(k == 1))
                    mm.then_inc(up[m], 1)
                pe.wait_ge(y_kept, c + OLD)
                for h in range(2):
                    for m in range(FG):
                        if h == 0 and m % 2 == 0:
                            pe.wait_ge(gelu[m // 2], c + NOW)
                        mm = nc.tensor.matmul(y_ps[b][:, h * CW:(h + 1) * CW], w2[:, m, h * P:(h + 1) * P], g[b][:, m, :], start=(m == 0), stop=(m == FG - 1))
                mm.then_inc(y_made, 1)
            chunks(pe, body)

        @block.scalar
        def _(act):
            act.wait_ge(weights, 16 * len(loads))

            def keep(c, b):
                act.wait_ge(y_made, c + NOW)
                for h in range(2):
                    last = nc.scalar.activation(forward[:, h, ds(c * CW, CW)], y_ps[b][:, h * CW:(h + 1) * CW], ACT.Identity, bias=b2[:, h:h + 1])
                last.then_inc(y_kept, 1)

            def body(c, b, r, more, behind):
                act.wait_ge(y_made, c + OLD)
                for m in range(4):
                    act.wait_ge(up[m], c + NOW)
                    for h in range(2):
                        last = nc.scalar.activation(g[b][:, 2 * m + h, :], f_ps[m][:, h * CW:(h + 1) * CW], ACT.Gelu_apprx_tanh,
                                                    bias=b1[:, 2 * m + h:2 * m + h + 1])
                    last.then_inc(gelu[m], 1)
                behind(0)

            def keep_before(c, b, r, n):
                if n == 0:
                    keep(c, b)
            chunks_behind(act, body, keep_before)

        @block.vector
        def _(dve):
            dve.wait_ge(compare_in, 48)
            nc.vector.memset(parts[:, :, :], 0.0).then_inc(step, 1)
            dve.wait_ge(step, 1)
            for n in range(NT):
                a, z = n * TT, (n + 1) * TT
                own = col[:, n:n + 1]
                if n:
                    dve.wait_ge(done, n)
                    nc.vector.tensor_scalar(junk[:, 0:a], row[:, 0:a], own, 0.0, ALU.is_ge, ALU.add, accum_out=parts[:, 0, n:n + 1])
                if z < N:
                    nc.vector.tensor_scalar(junk[:, z:N], row[:, z:N], own, 0.0, ALU.is_gt, ALU.add, accum_out=parts[:, 1, n:n + 1])
                nc.vector.tensor_scalar(junk[:, a:z], row[:, a:z], own, 0.0, ALU.is_gt, ALU.add, accum_out=parts[:, 2, n:n + 1])
                nc.vector.scalar_tensor_tensor(diag[n % 2][:, :], row[:, a:z], own, tri[:, :], ALU.is_equal, ALU.mult,
                                               accum_out=parts[:, 3, n:n + 1]).then_inc(done, 1)
            dve.wait_ge(done, NT)
            nc.vector.tensor_tensor(total[:, 0, :], parts[:, 0, :], parts[:, 1, :], ALU.add).then_inc(step, 1)
            nc.vector.tensor_tensor(total[:, 1, :], parts[:, 2, :], parts[:, 3, :], ALU.add).then_inc(step, 1)
            dve.wait_ge(step, 3)
            nc.vector.tensor_tensor(total[:, 2, :], total[:, 0, :], total[:, 1, :], ALU.add).then_inc(step, 1)
            dve.wait_ge(step, 4)
            nc.vector.scalar_tensor_tensor(factor[:, :], total[:, 2, :], float(KEPT), col[:, :], ALU.is_lt, ALU.mult).then_inc(step, 1)

            def body(c, b, r, more):
                dve.wait_ge(y_kept, c + NOW)
                dve.wait_ge(loaded[b], r * 48 + 48)
                dve.wait_ge(saved[b], r * 16 + 16)
                nc.vector.tensor_tensor(y[b][:, :, :], forward[:, :, ds(c * CW, CW)], fac[b][:, None, :].to_broadcast([P, 2, CW]), ALU.mult).then_inc(y_scaled, 1)
                dve.wait_ge(y_scaled, c + NOW)
                nc.vector.tensor_tensor(y[b][:, :, :], y[b][:, :, :], t[b][:, :, :], ALU.add).then_inc(y_t, 1)
                dve.wait_ge(y_t, c + NOW)
                nc.vector.tensor_tensor(y[b][:, :, :], y[b][:, :, :], x[b][:, :, :], ALU.add).then_inc(y_x, 1)
            chunks(dve, body)


def attention_weights(nc, name, sorted_d, prev_d, a_d, hist_d, base_d, max_d, pair_d, ev_d, value, c_d):
    FAR = -1e30
    with Phase(nc, name) as ph:
        ident = ph.sb("ident", [P, P])
        meta, pair = ph.sb("meta", [P, ET, 3]), ph.sb("pair", [P, ET, 2])
        prev, same, pen = ph.sb("prev", [P, ET]), ph.sb("same", [P, ET]), ph.sb("pen", [P, ET])
        a1 = value[:, GB:GB + ET]
        zero = ph.sb("zero", [P, ET])
        loc, acc, mx = ph.sb("loc", [P, ET]), ph.sb("acc", [P, ET]), ph.sb("mx", [P, ET])
        fill = [ph.sb(f"fill{n}", [P, ET]) for n in range(2)]
        v, vl, d, dm, ev = (ph.sb(n, [P, ET]) for n in ("v", "vl", "d", "dm", "ev"))
        edge, rowp, rows = ph.sb("edge", [P, 2]), ph.sb("rowp", [1, 2, P]), ph.sb("rows", [1, 4, P + 1])
        cin = ph.sb("cin", [P, 3])
        base, hist, first, mask, at, amax, a0, s, sl = (ph.sb(n, [TT, NT]) for n in ("base", "hist", "first", "mask", "at", "amax", "a0", "s", "sl"))
        ends, put = ph.sb("ends", [TT, NT], I32), ph.sb("put", [TT, NT], I32)
        nodes = ph.sb("nodes", [TT, NT, 2])
        x_ps = ph.ps("x_ps", [P, 512])
        c_ps = ph.ps("c_ps", [P, 512])
        loaded, saved = ph.sem("loaded"), ph.sem("saved")
        max_saved, max_got, put_ready, placed, pair_in, ends_ready = (ph.sem(n) for n in ("max_saved", "max_got", "put_ready", "placed", "pair_in", "ends_ready"))
        ends_of_parts = ph.sem("ends_of_parts")
        turned, line, back, carried, dv = (ph.sem(n) for n in ("turned", "line", "back", "carried", "dv"))
        exped, max_ready, ev_ready = ph.sem("exped"), ph.sem("max_ready"), ph.sem("ev_ready")
        block = ph.block()

        @block.sync
        def _(sp):
            sp.dma_start(ident[:, :], c_d["ident"]).then_inc(loaded, 16)
            sp.dma_start(meta[:, :, :], sorted_d.rearrange("(p j) c -> p j c", j=ET)).then_inc(loaded, 16)
            sp.dma_start(base[:, :], base_d[0:N].rearrange("(t p) -> p t", p=TT), allow_slow_non_contiguous=True).then_inc(loaded, 16)
            sp.dma_start(hist[:, :], hist_d[0:N].rearrange("(t p) -> p t", p=TT), allow_slow_non_contiguous=True).then_inc(loaded, 16)
            sp.dma_start(a0[:, :], a_d[1].rearrange("(t p) -> p t", p=TT), allow_slow_non_contiguous=True).then_inc(loaded, 16)
            sp.wait_ge(dv, 1)
            sp.dma_start(prev_d[1:1 + EP].rearrange("(p j) -> p j", j=ET), loc[:, :]).then_inc(saved, 16)
            sp.wait_ge(dv, 2)
            sp.dma_start(prev_d[0:1].rearrange("(a o) -> a o", a=1), cin[0:1, 0:1]).then_inc(saved, 16)
            for n in range(2):
                sp.dma_start(pair_d.rearrange("(p j) c -> p (j c)", j=ET)[:, n * ET:(n + 1) * ET], zero[:, :]).then_inc(saved, 16)
            sp.wait_ge(saved, 64)
            sp.dma_start(prev[:, :], prev_d[0:EP].rearrange("(p j) -> p j", j=ET)).then_inc(loaded, 16)
            sp.wait_ge(max_ready, 1)
            sp.dma_start(max_d.rearrange("(p j) -> p j", j=ET), mx[:, :]).then_inc(max_saved, 16)
            sp.wait_ge(placed, 16 * NT)
            sp.dma_start(pair[:, :, :], pair_d.rearrange("(p j) c -> p j c", j=ET)).then_inc(pair_in, 16)
            sp.wait_ge(ev_ready, 1)
            sp.dma_start(ev_d.rearrange("(p j) -> p j", j=ET), ev[:, :]).then_inc(pair_in, 16)
            sp.wait_ge(pair_in, 32)

        @block.gpsimd
        def _(pool):
            pool.wait_ge(max_saved, 16)
            pool.wait_ge(ends_ready, 1)
            for t in range(NT):
                nc.gpsimd.indirect_dma_start(amax[:, t:t + 1], None, max_d.rearrange("(n o) -> n o", o=1),
                                             bass.IndirectOffsetOnAxis(ends[:, t:t + 1], 0)).then_inc(max_got, 16)
            pool.wait_ge(put_ready, 1)
            pool.wait_ge(saved, 64)
            for t in range(NT):
                nc.gpsimd.indirect_dma_start(pair_d, bass.IndirectOffsetOnAxis(put[:, t:t + 1], 0), nodes[:, t, :], None,
                                             bounds_check=EP - 1, oob_is_err=False).then_inc(placed, 16)
            pool.wait_ge(placed, 16 * NT)

        @block.tensor
        def _(pe):
            pe.wait_ge(loaded, 80)
            for n in range(3):
                pe.wait_ge(ends_of_parts, n + 1)
                for k in range(2):
                    mm = nc.tensor.transpose(x_ps[0:1, k * P:(k + 1) * P], edge[:, k:k + 1], ident[:, :])
                mm.then_inc(turned, 1)
                pe.wait_ge(line, n + 1)
                nc.tensor.transpose(c_ps[:, 0:1], rows[0:1, n, 0:P], ident[0:1, 0:1]).then_inc(back, 1)

        @block.vector
        def _(dve):
            count = [0]

            def step(ins):
                count[0] += 1
                ins.then_inc(dv, 1)
                dve.wait_ge(dv, count[0])

            def join(n, op0, op1, start, change, end):
                nc.vector.tensor_copy(edge[:, 0:1], change[:, ET - 1:ET])
                nc.vector.tensor_copy(edge[:, 1:2], end[:, ET - 1:ET]).then_inc(ends_of_parts, 1)
                dve.wait_ge(turned, n + 1)
                step(nc.vector.tensor_copy(rowp[0:1, :, :], x_ps[0:1, 0:2 * P].rearrange("p (k c) -> p k c", k=2)))
                step(nc.vector.memset(rows[0:1, n, 0:1], start))
                nc.vector.tensor_tensor_scan(rows[0:1, n, 1:P + 1], rowp[0:1, 0, :], rowp[0:1, 1, :], start, op0, op1).then_inc(line, 1)
                dve.wait_ge(back, n + 1)
                step(nc.vector.tensor_copy(cin[:, n:n + 1], c_ps[:, 0:1]))

            dve.wait_ge(loaded, 80)
            nc.vector.memset(zero[:, :], 0.0)
            step(nc.vector.tensor_copy(loc[:, :], meta[:, :, 0]))
            step(nc.vector.memset(cin[:, :], -1.0))
            dve.wait_ge(loaded, 96)
            step(nc.vector.tensor_tensor(same[:, :], meta[:, :, 0], prev[:, :], ALU.is_equal))
            step(nc.vector.tensor_scalar(pen[:, :], same[:, :], -FAR, FAR, ALU.mult, ALU.add))
            nc.vector.tensor_tensor_scan(acc[:, :], pen[:, :], pen[:, :], 0.0, ALU.add, ALU.bypass)
            nc.vector.tensor_tensor_scan(loc[:, :], pen[:, :], a1, FAR, ALU.add, ALU.max).then_inc(carried, 1)
            dve.wait_ge(carried, 1)
            join(0, ALU.add, ALU.max, FAR, acc, loc)
            nc.vector.scalar_tensor_tensor(mx[:, :], acc[:, :], cin[:, 0:1], loc[:, :], ALU.add, ALU.max).then_inc(max_ready, 1)
            step(nc.vector.tensor_scalar(mask[:, :], hist[:, :], 1.0, None, ALU.min))
            step(nc.vector.tensor_tensor(first[:, :], base[:, :], hist[:, :], ALU.add))
            nc.vector.tensor_scalar(ends[:, :], first[:, :], -1.0, 0.0, ALU.add, ALU.max).then_inc(ends_ready, 1)
            step(nc.vector.tensor_scalar(at[:, :], mask[:, :], -float(2 * EP), float(2 * EP), ALU.mult, ALU.add))
            step(nc.vector.tensor_tensor(put[:, :], at[:, :], base[:, :], ALU.add))
            dve.wait_ge(max_got, 16 * NT)
            step(nc.vector.tensor_tensor(s[:, :], amax[:, :], a0[:, :], ALU.add))
            step(nc.vector.tensor_scalar(sl[:, :], s[:, :], 0.01, None, ALU.mult))
            step(nc.vector.tensor_tensor(nodes[:, :, 1], s[:, :], sl[:, :], ALU.max))
            nc.vector.tensor_copy(nodes[:, :, 0], a0[:, :]).then_inc(put_ready, 1)
            dve.wait_ge(pair_in, 16)
            step(nc.vector.tensor_tensor_scan(acc[:, :], same[:, :], same[:, :], 1.0, ALU.mult, ALU.bypass))
            for n in range(2):
                step(nc.vector.tensor_copy(loc[:, :], pair[:, :, n]))
                step(nc.vector.tensor_tensor_scan(d[:, :], same[:, :], loc[:, :], 0.0, ALU.mult, ALU.add))
                join(n + 1, ALU.mult, ALU.add, 0.0, acc, d)
                step(nc.vector.scalar_tensor_tensor(fill[n][:, :], acc[:, :], cin[:, n + 1:n + 2], d[:, :], ALU.mult, ALU.add))
            step(nc.vector.tensor_tensor(v[:, :], fill[0][:, :], a1, ALU.add))
            step(nc.vector.tensor_scalar(vl[:, :], v[:, :], 0.01, None, ALU.mult))
            step(nc.vector.tensor_tensor(v[:, :], v[:, :], vl[:, :], ALU.max))
            step(nc.vector.tensor_tensor(dm[:, :], v[:, :], fill[1][:, :], ALU.subtract))
            nc.vector.tensor_scalar(dm[:, :], dm[:, :], 0.0, None, ALU.min).then_inc(exped, 1)

        @block.scalar
        def _(act):
            act.wait_ge(exped, 1)
            nc.scalar.activation(ev[:, :], dm[:, :], ACT.Exp).then_inc(ev_ready, 1)


def network(nc, a, out_d, parts=None):
    parts = parts or {}

    def dram(name, shape):
        return parts.get(name) or nc.dram_tensor(name, shape, F32).ap()
    fm = [P, 2, N]
    c_d = {n: a[f"c_{n}"] for n in ("mean", "ident", "identb", "iota", "upper", "blocks1", "blocks2", "tri", "pick", "before")}
    xn, xn_rows = dram("xn", fm), dram("xn_rows", [N, D])
    norm_table(nc, "norm0", a["x"], xn, xn_rows, c_d)
    orders = [[dram(f"hist_{n}", [NODES]), dram(f"first_{n}", [NODES]), dram(f"sorted_{n}", [EP, 3])] for n in ("dst", "src")]
    xs = dram("mix0", fm)
    norm_d = dram("degree_norm", [NODES])
    mixer = nc.alloc_sbuf_tensor("mixer", [P, 2, D], F32)
    later = ExitStack()
    place1 = later.enter_context(nc.sbuf_tensor("place1", [P, SW], I32))
    record1 = later.enter_context(nc.sbuf_tensor("record1", [P, SW, 3], F32))
    sort_edges(nc, "sort", (a["dst"], a["src"]), a["edge_weight"], orders, place1, record1, norm_d, xn, xs, c_d)

    hist, first, by_dst = orders[0]
    running, agg = nc.dram_tensor("running0", [EP, D], F32).ap(), dram("agg", fm)
    sum_edges(nc, "sum0", by_dst, None, xn_rows, running, D, c_d)
    carry = nc.dram_tensor("carry0", [ET, D], F32).ap()
    tile_carries(nc, "carry0", by_dst, running, carry, D, c_d)
    node_rows(nc, "rows0", running, carry, D, hist, first, agg, c_d)

    qT = dram("qT0", fm)
    with nc.Fori(0, 4) as layer:
        def of(name):
            w = a[f"L0_mix_{name}"][ds(layer, 1)]
            return w.rearrange("l p h c -> (l p) h c" if len(w.shape) == 4 else "l p h -> (l p) h")
        attend_first(nc, "attend0", 2, P, 32, 32 ** -0.25, xs, qT, mixer, c_d, of("ln1_g"), of("ln1_b"), of("Wq"), of("Wk"), of("Wv"), of("Wo"))
        attend_second(nc, "forward0", 2, P, xs, qT, mixer, xs, c_d, of("bo"), of("ln2_g"), of("ln2_b"), of("W1"), of("b1"), of("W2"), of("b2"))
    x1 = dram("x1", fm)
    g = {n: a[f"L0_gnn_{n}"] for n in ("eps_weight", "w1", "w2", "gamma1", "beta1", "gamma_h", "beta_h")}
    message_layer(nc, "message0", agg, a["x"], xn, xs, x1, norm_d, c_d, g["eps_weight"], g["w1"], g["w2"],
                  g["gamma1"], g["beta1"], g["gamma_h"], g["beta_h"])
    x2 = dram("x2", fm)
    experts(nc, "experts", x1, x2, c_d, *(a[f"L0_ffn_{n}"] for n in ("router_w", "w1", "b1", "w2", "b2")), (place1, record1, orders[1][2]))
    later.close()

    hist, first, by_src = orders[1]
    xn1, h_rows, scores = dram("xn1", fm), dram("h_rows", [N, D]), dram("scores", [2, N])
    norm_table(nc, "norm1", x2, xn1, h_rows, c_d, a["L1_gnn_W_layer"], a["L1_gnn_b_layer"], a["L1_gnn_w_a"], a["L1_gnn_b_a"], scores)
    m = {n[7:]: v for n, v in a.items() if n.startswith("L1_mix_")}
    qT1, x2m, x3, ev = dram("qT1", [32, 1, N]), dram("x2m", fm), dram("x3", fm), dram("ev", [EP])
    with Phase(nc, "edge_scores") as ph:
        index, value = ph.sb("index", [P, GW], I32), ph.sb("value", [P, GW])
        other_ends(nc, "ends1", by_src, index)
        attend_first(nc, "attend1", 1, 32, 4, 1.0, xn1, qT1, mixer, c_d, m["ln1_g"], m["ln1_b"], m["Wq"], m["Wk"], m["Wv"], m["Wo"], m["Wx"], m["bx"],
                     (0, scores[0], index, value))
        attend_second(nc, "forward1", 1, 32, xn1, qT1, mixer, x2m, c_d, m["bo"], m["ln2_g"], m["ln2_b"], m["W1"], m["b1"], m["W2"], m["b2"], (x2,),
                      (1, scores[0], index, value))
        attention_weights(nc, "edges1", by_src, nc.dram_tensor("prev", [EP + 1], F32).ap(), scores, hist, first, nc.dram_tensor("maxs", [EP], F32).ap(),
                          nc.dram_tensor("pairs", [EP, 2], F32).ap(), ev, value, c_d)
    running, carry = nc.dram_tensor("running1", [EP, D + 1], F32).ap(), nc.dram_tensor("carry1", [ET, D + 1], F32).ap()
    sum_edges(nc, "sum1", by_src, ev, h_rows, running, D + 1, c_d)
    tile_carries(nc, "carry1", by_src, running, carry, D + 1, c_d)
    node_rows(nc, "rows1", running, carry, D + 1, hist, first, x3, c_d, x2m)

    t, row, factor = dram("t", fm), dram("row", [N]), dram("factor", [N])
    token_weights(nc, "tokens", x3, t, row, c_d, a["L1_ffn_wr"], a["L1_ffn_br"])
    chosen_forward(nc, "chosen", t, x3, row, factor, out_d, c_d, *(a[f"L1_ffn_{n}"] for n in ("w1", "b1", "w2", "b2")))


def laid_out(inputs):
    x = {k: np.asarray(v) for k, v in inputs.items()}

    def wide(v):
        return v.reshape(*v.shape[:-2], -1, P, v.shape[-1]).swapaxes(-3, -2)

    def per_channel(v):
        return v.reshape(*v.shape[:-1], -1, P).swapaxes(-2, -1)

    def edges(v, pad):
        return np.concatenate([v, np.full(EP - E, pad, v.dtype)]).reshape(ET, P).T

    a = {"x": wide(x["x"].T), "edge_weight": edges(x["edge_weight"], 0)}
    a["src"], a["dst"] = edges(x["src"], N), edges(x["dst"], N)
    for n in ("w1", "w2"):
        a[f"L0_gnn_{n}"] = wide(x[f"L0_gnn_{n}"].T)
    for n in ("gamma1", "beta1", "gamma_h", "beta_h"):
        a[f"L0_gnn_{n}"] = per_channel(x[f"L0_gnn_{n}"])
    a["L0_gnn_eps_weight"] = x["L0_gnn_eps_weight"]
    for n in ("Wq", "Wk", "Wv", "Wo", "W1", "W2"):
        a[f"L0_mix_{n}"] = wide(x[f"L0_mix_{n}"])
    for n in ("bo", "ln1_g", "ln1_b", "b1", "b2", "ln2_g", "ln2_b"):
        a[f"L0_mix_{n}"] = per_channel(x[f"L0_mix_{n}"])
        a[f"L1_mix_{n}"] = per_channel(x[f"L1_mix_{n}"])
    a["L0_ffn_router_w"] = wide(x["L0_ffn_router_w"].T)
    for n in ("w1", "w2"):
        a[f"L0_ffn_{n}"] = wide(x[f"L0_ffn_{n}"]).transpose(1, 0, 2, 3)
    a["L0_ffn_b1"] = per_channel(x["L0_ffn_b1"]).transpose(1, 0, 2)
    a["L0_ffn_b2"] = x["L0_ffn_b2"]
    a["L1_gnn_W_layer"] = wide(x["L1_gnn_W_layer"].T)
    a["L1_gnn_b_layer"] = x["L1_gnn_b_layer"]
    a["L1_gnn_w_a"] = np.concatenate([x["L1_gnn_w_a2"], x["L1_gnn_w_a1"]])
    a["L1_gnn_b_a"] = np.concatenate([x["L1_gnn_b_a2"], x["L1_gnn_b_a1"]])
    for n in ("Wx", "Wo", "W1", "W2"):
        a[f"L1_mix_{n}"] = wide(x[f"L1_mix_{n}"])
    for n in ("Wq", "Wk", "Wv"):
        a[f"L1_mix_{n}"] = x[f"L1_mix_{n}"]
    a["L1_mix_bx"] = per_channel(x["L1_mix_bx"])
    a["L1_ffn_wr"] = per_channel(x["L1_ffn_wr"][:, 0])
    a["L1_ffn_br"] = x["L1_ffn_br"]
    for n in ("w1", "w2"):
        a[f"L1_ffn_{n}"] = wide(x[f"L1_ffn_{n}"])
    for n in ("b1", "b2"):
        a[f"L1_ffn_{n}"] = per_channel(x[f"L1_ffn_{n}"])
    p, q = np.arange(P)[:, None], np.arange(P)[None, :]
    f = np.float32
    head = (p // 32 == q // 32).astype(f)
    a["c_mean"] = np.full((P, P), 1 / D, f)
    a["c_ident"] = np.eye(P, dtype=f)
    a["c_identb"] = np.eye(P).astype(_mybir_bf16())
    a["c_iota"] = np.broadcast_to(q, (P, P)).astype(f)
    a["c_tri"], a["c_upper"] = (q < p).astype(f), (p < q).astype(f)
    a["c_blocks2"] = np.stack([head, head], 1)
    a["c_blocks1"] = (np.arange(32)[:, None] // 4 == np.arange(D)[None, :] // 32).astype(f)[:, None, :]
    e8 = np.arange(8)
    a["c_pick"] = np.broadcast_to((e8[:, None] == e8[None, :])[:, :, None], (8, 8, P)).astype(f)
    a["c_before"] = np.broadcast_to((e8[None, :] < e8[:, None])[None], (TT, 8, 8)).astype(f)
    return {k: np.ascontiguousarray(v) for k, v in a.items()}


def _mybir_bf16():
    return mybir.dt.np(BF16)


def kernel(**inputs):
    import concourse.bacc as bacc
    from concourse.bass_utils import run_bass_kernel_spmd

    nc = bacc.Bacc("TRN2", target_bir_lowering=False, num_devices=1)
    arrays = {f"in_{k}": v for k, v in laid_out(inputs).items()}
    aps = {k[3:]: nc.dram_tensor(k, v.shape, mybir.dt.from_np(v.dtype), kind="ExternalInput").ap() for k, v in arrays.items()}
    out = nc.dram_tensor("out", [P, 2, N], F32, kind="ExternalOutput").ap()
    network(nc, aps, out)
    r = run_bass_kernel_spmd(nc, [arrays], core_ids=[0])
    return r.results[0]["out"].transpose(1, 0, 2).reshape(D, N).T
```
